# Optimizing a Trainium2 kernel written in Bass

```python
import numpy as np
import jax
import jax.numpy as jnp

def _softmax(x, axis=-1):
    return jax.nn.softmax(x, axis=axis)

def _gelu(x):
    return jax.nn.gelu(x, approximate=True)

def _silu(x):
    return jax.nn.silu(x)

def _sigmoid(x):
    return jax.nn.sigmoid(x)

def _layernorm(x, axis=-1, eps=1e-05):
    m = jnp.mean(x, axis=axis, keepdims=True)
    v = jnp.var(x, axis=axis, keepdims=True)
    return (x - m) / jnp.sqrt(v + eps)

def _scatter_add(tgt, idx, src, axis=0):
    return tgt.at[idx].add(src)

def _segment_sum(src, seg, n):
    return jax.ops.segment_sum(src, seg, n)
kernel_name = 'mk_decoder_postln_d2_seqx_r4_08af53'

def setup_inputs(seed: int=0):
    np.random.seed(seed)
    _w = jnp.asarray

    def _rec_inputs():
        import jax
        import jax.numpy as jnp
        _rk = jax.random.key(seed)
        x = -0.0002928 + 1 * jax.random.normal(jax.random.fold_in(_rk, 1), (4, 1024, 256), jnp.float32)
        _lenS = 1024 - jax.random.randint(jax.random.fold_in(_rk, 7), (4,), 0, max(1, 1024 // 4) + 1, jnp.int32)
        _lenS2 = 77 - jax.random.randint(jax.random.fold_in(_rk, 8), (4,), 0, max(1, 77 // 4) + 1, jnp.int32)
        _ctx_1024P = jax.random.normal(jax.random.fold_in(_rk, 11), (4, 16, 256), jnp.float32)
        _ctx_1024c = jax.random.dirichlet(jax.random.fold_in(_rk, 511), 0.3 * jnp.ones((16,), jnp.float32), (4, 77))
        _ctx_1024t = jnp.einsum('bsk,bkd->bsd', _ctx_1024c, _ctx_1024P)
        _ctx_1024t = _ctx_1024t * jax.lax.rsqrt(jnp.mean(jnp.square(_ctx_1024t)) + 1e-12) * 0.953939
        ctx_1024 = -1.78809e-06 + 0.0312453 * (_ctx_1024t + 0.3 * jax.random.normal(jax.random.fold_in(_rk, 611), (4, 77, 256), jnp.float32))
        return (x, ctx_1024)
    x, ctx_1024 = _rec_inputs()

    def _L0_attn_setup():
        import jax, jax.numpy as jnp
        import numpy as np
        import math
        B, N, D = (2, 512, 256)
        H = 16
        DH = D // H
        CG_ITERS = 30
        THRESHOLD = 0.99
        LAMBDA_INIT = 1.0
        LAMBDA_LOWER = 0.25
        NORM_EPS = 1e-05

        def l2norm(x, eps=1e-06):
            return x * jax.lax.rsqrt(jnp.sum(x * x, axis=-1, keepdims=True) + eps)

        def cg_solve(A, rhs, n_iters):
            x0 = jnp.zeros_like(rhs)
            rs0 = jnp.sum(rhs * rhs, axis=-1)

            def step(carry, _):
                x, r, p, rs = carry
                Ap = jnp.einsum('bhij,bhj->bhi', A, p)
                alpha = rs / (jnp.sum(p * Ap, axis=-1) + 1e-12)
                x = x + alpha[..., None] * p
                r = r - alpha[..., None] * Ap
                rs_new = jnp.sum(r * r, axis=-1)
                p = r + (rs_new / (rs + 1e-12))[..., None] * p
                return ((x, r, p, rs_new), None)
            (x, _, _, _), _ = jax.lax.scan(step, (x0, rhs, rhs, rs0), None, length=n_iters)
            return x
        key = jax.random.key(seed)
        ks = jax.random.split(key, 10)
        std = 0.02
        inp = {'x': jax.random.normal(ks[0], (B, N, D), dtype=jnp.float32), 'Wq': jax.random.normal(ks[1], (D, D), dtype=jnp.float32) * std, 'Wk': jax.random.normal(ks[2], (D, D), dtype=jnp.float32) * std, 'Wv': jax.random.normal(ks[3], (D, D), dtype=jnp.float32) * std, 'Wf': jax.random.normal(ks[4], (D, H), dtype=jnp.float32) * std, 'Wbet': jax.random.normal(ks[5], (D, H), dtype=jnp.float32) * std, 'Wo': jax.random.normal(ks[6], (D, D), dtype=jnp.float32) * std, 'delta': jnp.full((H,), math.log(THRESHOLD / (1.0 - THRESHOLD)), dtype=jnp.float32), 'lamb_params': jnp.full((D,), math.log(math.exp(math.exp(LAMBDA_INIT - LAMBDA_LOWER)) - 1.0), dtype=jnp.float32), 'norm_weight': jnp.ones((D,), dtype=jnp.float32), 'gate_w1': jax.random.normal(ks[7], (D, DH), dtype=jnp.float32) * std, 'gate_w2': jax.random.normal(ks[8], (DH, D), dtype=jnp.float32) * std}
        return inp
    _L0_attn_all = _L0_attn_setup()
    _L0_attn_in = {k: v for k, v in _L0_attn_all.items() if k in ('Wq', 'Wk', 'Wv', 'Wf', 'Wbet', 'Wo', 'delta', 'lamb_params', 'norm_weight', 'gate_w1', 'gate_w2')}
    del _L0_attn_all

    def _L0_xattn_setup():
        import jax, jax.numpy as jnp
        import numpy as np
        E, TPE, H, F = (64, 64, 256, 256)
        key = jax.random.key(seed)
        k1, k2, k3, k4 = jax.random.split(key, 4)
        scale = 1.0 / np.sqrt(H)
        return {'x': jax.random.normal(k1, (E, TPE, H), dtype=jnp.float32), 'w1': jax.random.normal(k2, (E, F, H), dtype=jnp.float32) * scale, 'v1': jax.random.normal(k3, (E, F, H), dtype=jnp.float32) * scale, 'w2': jax.random.normal(k4, (E, F, H), dtype=jnp.float32) * scale}
    _L0_xattn_all = _L0_xattn_setup()
    _L0_xattn_in = {k: v for k, v in _L0_xattn_all.items() if k in ()}
    del _L0_xattn_all

    def _L0_ffn_setup():
        import jax, jax.numpy as jnp
        import numpy as np
        HIDDEN = 256
        INNER = 1024

        def _weight_quant(w):
            scale = 1.0 / jnp.clip(jnp.mean(jnp.abs(w)), 1e-05)
            wq = jnp.clip(jnp.round(w * scale), -1.0, 1.0) / scale
            return w + jax.lax.stop_gradient(wq - w)

        def _act_quant(x):
            scale = 127.0 / jnp.clip(jnp.max(jnp.abs(x), axis=-1, keepdims=True), 1e-05)
            xq = jnp.clip(jnp.round(x * scale), -128.0, 127.0) / scale
            return x + jax.lax.stop_gradient(xq - x)

        def _bitlinear(x, w):
            return jnp.einsum('bsi,oi->bso', _act_quant(x), _weight_quant(w))
        key = jax.random.key(seed)
        k0, k1, k2, k3 = jax.random.split(key, 4)
        x = jax.random.normal(k0, (4, 512, HIDDEN), dtype=jnp.float32)
        w_gate = jax.random.normal(k1, (INNER, HIDDEN), dtype=jnp.float32) / np.sqrt(HIDDEN)
        w_up = jax.random.normal(k2, (INNER, HIDDEN), dtype=jnp.float32) / np.sqrt(HIDDEN)
        w_down = jax.random.normal(k3, (HIDDEN, INNER), dtype=jnp.float32) / np.sqrt(INNER)
        return {'x': x, 'w_gate': w_gate, 'w_up': w_up, 'w_down': w_down}
    _L0_ffn_all = _L0_ffn_setup()
    _L0_ffn_in = {k: v for k, v in _L0_ffn_all.items() if k in ('w_gate', 'w_up', 'w_down')}
    del _L0_ffn_all

    def _L1_attn_setup():
        import jax, jax.numpy as jnp
        import numpy as np
        B, S, DIN, DOUT, H, KVH = (2, 512, 256, 256, 16, 16)
        HD = DOUT // H
        CB = 16
        CS = 16
        SB = 8
        TOPK = 2
        WIN = 64
        SCALE = 1.0 / np.sqrt(HD)

        def _rope(x, hd):
            b, s, d = x.shape
            xh = x.reshape(b, s, d // hd, hd)
            half = hd // 2
            inv = 1.0 / 10000.0 ** (jnp.arange(half, dtype=jnp.float32) * 2.0 / hd)
            ang = jnp.arange(s, dtype=jnp.float32)[:, None] * inv[None, :]
            cos = jnp.cos(ang)[None, :, None, :]
            sin = jnp.sin(ang)[None, :, None, :]
            x1, x2 = (xh[..., 0::2], xh[..., 1::2])
            out = jnp.stack([x1 * cos - x2 * sin, x1 * sin + x2 * cos], axis=-1)
            return out.reshape(b, s, d)

        def _masked_softmax(scores, mask):
            s = jnp.where(mask, scores, -jnp.inf)
            m = jnp.max(s, axis=-1, keepdims=True)
            m = jnp.where(jnp.isfinite(m), m, jnp.zeros_like(m))
            e = jnp.exp(s - m)
            den = jnp.sum(e, axis=-1, keepdims=True)
            return jnp.where(den > 0, e / jnp.where(den > 0, den, 1.0), jnp.zeros_like(e))
        key = jax.random.key(seed)
        ks = jax.random.split(key, 12)
        sc_in = 1.0 / np.sqrt(DIN)
        sc_out = 1.0 / np.sqrt(DOUT)
        return {'x': jax.random.normal(ks[0], (B, S, DIN), jnp.float32), 'Wq': jax.random.normal(ks[1], (DIN, DOUT), jnp.float32) * sc_in, 'Wk': jax.random.normal(ks[2], (DIN, KVH * HD), jnp.float32) * sc_in, 'Wv': jax.random.normal(ks[3], (DIN, KVH * HD), jnp.float32) * sc_in, 'Wo': jax.random.normal(ks[4], (DOUT, DOUT), jnp.float32) * sc_out, 'bo': jnp.zeros((DOUT,), jnp.float32), 'wk_comp': jax.random.normal(ks[5], (CB,), jnp.float32), 'wv_comp': jax.random.normal(ks[6], (CB,), jnp.float32), 'pe': jax.random.normal(ks[7], (CB, KVH * HD), jnp.float32), 'Wg': jax.random.normal(ks[8], (DIN, 3), jnp.float32) * sc_in, 'bg': jnp.zeros((3,), jnp.float32)}
    _L1_attn_all = _L1_attn_setup()
    _L1_attn_in = {k: v for k, v in _L1_attn_all.items() if k in ('Wq', 'Wk', 'Wv', 'Wo', 'bo', 'wk_comp', 'wv_comp', 'pe', 'Wg', 'bg')}
    del _L1_attn_all

    def _L1_xattn_setup():
        import jax, jax.numpy as jnp
        import numpy as np
        D = 256
        NUM_ITERS = 3
        EPS = 1e-06
        SCALE = D ** (-0.5)

        def rmsnorm(x, w, eps=EPS):
            return x * jax.lax.rsqrt(jnp.mean(x * x, axis=-1, keepdims=True) + eps) * w

        def gru_cell(x, h, wih, whh, bih, bhh):
            gx = x @ wih.T + bih
            gh = h @ whh.T + bhh
            xr, xz, xn = jnp.split(gx, 3, axis=-1)
            hr, hz, hn = jnp.split(gh, 3, axis=-1)
            r = jax.nn.sigmoid(xr + hr)
            z = jax.nn.sigmoid(xz + hz)
            n = jnp.tanh(xn + r * hn)
            return (1.0 - z) * n + z * h
        key = jax.random.key(seed)
        ks = jax.random.split(key, 8)
        B, K, M, d = (8, 64, 1024, D)
        w_std = d ** (-0.5)
        return {'slots': jax.random.normal(ks[0], (B, K, d), jnp.float32), 'P': jax.random.normal(ks[1], (B, M, d), jnp.float32), 'Wq': jax.random.normal(ks[2], (d, d), jnp.float32) * w_std, 'Wk': jax.random.normal(ks[3], (d, d), jnp.float32) * w_std, 'Wv': jax.random.normal(ks[4], (d, d), jnp.float32) * w_std, 'gru_wih': jax.random.normal(ks[5], (3 * d, d), jnp.float32) * w_std, 'gru_whh': jax.random.normal(ks[6], (3 * d, d), jnp.float32) * w_std, 'gru_bih': jnp.zeros((3 * d,), jnp.float32), 'gru_bhh': jnp.zeros((3 * d,), jnp.float32), 'slot_norm_w': jnp.ones((d,), jnp.float32), 'input_norm_w': jnp.ones((d,), jnp.float32)}
    _L1_xattn_all = _L1_xattn_setup()
    _L1_xattn_in = {k: v for k, v in _L1_xattn_all.items() if k in ('Wq', 'Wk', 'Wv', 'gru_wih', 'gru_whh', 'gru_bih', 'gru_bhh', 'slot_norm_w', 'input_norm_w')}
    del _L1_xattn_all

    def _L1_ffn_setup():
        import jax, jax.numpy as jnp
        import numpy as np
        D_IN, D_HID = (256, 1024)

        def _ternary(key, shape):
            return jax.random.randint(key, shape, -1, 2).astype(jnp.float32)

        def _tlin(x, w, s):
            return jnp.einsum('bsi,oi->bso', x, w) * s
        key = jax.random.key(seed)
        ks = jax.random.split(key, 12)
        inv = lambda fan: 1.0 / np.sqrt(fan).astype(np.float32)
        return {'x': jax.random.normal(ks[0], (4, 512, D_IN), dtype=jnp.float32), 'w1_w': _ternary(ks[1], (D_HID, D_IN)), 'w1_s': jax.random.uniform(ks[2], (D_HID,), dtype=jnp.float32) * inv(D_IN), 'w2_w': _ternary(ks[3], (D_HID, D_IN)), 'w2_s': jax.random.uniform(ks[4], (D_HID,), dtype=jnp.float32) * inv(D_IN), 'h1_w': _ternary(ks[5], (D_HID, D_HID)), 'h1_s': jax.random.uniform(ks[6], (D_HID,), dtype=jnp.float32) * inv(D_HID), 'h2_w': _ternary(ks[7], (D_HID, D_HID)), 'h2_s': jax.random.uniform(ks[8], (D_HID,), dtype=jnp.float32) * inv(D_HID), 'w3_w': _ternary(ks[9], (D_IN, D_HID)), 'w3_s': jax.random.uniform(ks[10], (D_IN,), dtype=jnp.float32) * inv(D_HID)}
    _L1_ffn_all = _L1_ffn_setup()
    _L1_ffn_in = {k: v for k, v in _L1_ffn_all.items() if k in ('w1_w', 'w1_s', 'w2_w', 'w2_s', 'h1_w', 'h1_s', 'h2_w', 'h2_s', 'w3_w', 'w3_s')}
    del _L1_ffn_all
    return {'x': x, 'ctx_1024': ctx_1024, 'L0_attn_Wq': _L0_attn_in['Wq'], 'L0_attn_Wk': _L0_attn_in['Wk'], 'L0_attn_Wv': _L0_attn_in['Wv'], 'L0_attn_Wf': _L0_attn_in['Wf'], 'L0_attn_Wbet': _L0_attn_in['Wbet'], 'L0_attn_Wo': _L0_attn_in['Wo'], 'L0_attn_delta': _L0_attn_in['delta'], 'L0_attn_lamb_params': _L0_attn_in['lamb_params'], 'L0_attn_norm_weight': _L0_attn_in['norm_weight'], 'L0_attn_gate_w1': _L0_attn_in['gate_w1'], 'L0_attn_gate_w2': _L0_attn_in['gate_w2'], 'L0_ffn_w_gate': _L0_ffn_in['w_gate'], 'L0_ffn_w_up': _L0_ffn_in['w_up'], 'L0_ffn_w_down': _L0_ffn_in['w_down'], 'L1_attn_Wq': _L1_attn_in['Wq'], 'L1_attn_Wk': _L1_attn_in['Wk'], 'L1_attn_Wv': _L1_attn_in['Wv'], 'L1_attn_Wo': _L1_attn_in['Wo'], 'L1_attn_bo': _L1_attn_in['bo'], 'L1_attn_wk_comp': _L1_attn_in['wk_comp'], 'L1_attn_wv_comp': _L1_attn_in['wv_comp'], 'L1_attn_pe': _L1_attn_in['pe'], 'L1_attn_Wg': _L1_attn_in['Wg'], 'L1_attn_bg': _L1_attn_in['bg'], 'L1_xattn_Wq': _L1_xattn_in['Wq'], 'L1_xattn_Wk': _L1_xattn_in['Wk'], 'L1_xattn_Wv': _L1_xattn_in['Wv'], 'L1_xattn_gru_wih': _L1_xattn_in['gru_wih'], 'L1_xattn_gru_whh': _L1_xattn_in['gru_whh'], 'L1_xattn_gru_bih': _L1_xattn_in['gru_bih'], 'L1_xattn_gru_bhh': _L1_xattn_in['gru_bhh'], 'L1_xattn_slot_norm_w': _L1_xattn_in['slot_norm_w'], 'L1_xattn_input_norm_w': _L1_xattn_in['input_norm_w'], 'L1_ffn_w1_w': _L1_ffn_in['w1_w'], 'L1_ffn_w1_s': _L1_ffn_in['w1_s'], 'L1_ffn_w2_w': _L1_ffn_in['w2_w'], 'L1_ffn_w2_s': _L1_ffn_in['w2_s'], 'L1_ffn_h1_w': _L1_ffn_in['h1_w'], 'L1_ffn_h1_s': _L1_ffn_in['h1_s'], 'L1_ffn_h2_w': _L1_ffn_in['h2_w'], 'L1_ffn_h2_s': _L1_ffn_in['h2_s'], 'L1_ffn_w3_w': _L1_ffn_in['w3_w'], 'L1_ffn_w3_s': _L1_ffn_in['w3_s']}

def reference(x, ctx_1024, L0_attn_Wq, L0_attn_Wk, L0_attn_Wv, L0_attn_Wf, L0_attn_Wbet, L0_attn_Wo, L0_attn_delta, L0_attn_lamb_params, L0_attn_norm_weight, L0_attn_gate_w1, L0_attn_gate_w2, L0_ffn_w_gate, L0_ffn_w_up, L0_ffn_w_down, L1_attn_Wq, L1_attn_Wk, L1_attn_Wv, L1_attn_Wo, L1_attn_bo, L1_attn_wk_comp, L1_attn_wv_comp, L1_attn_pe, L1_attn_Wg, L1_attn_bg, L1_xattn_Wq, L1_xattn_Wk, L1_xattn_Wv, L1_xattn_gru_wih, L1_xattn_gru_whh, L1_xattn_gru_bih, L1_xattn_gru_bhh, L1_xattn_slot_norm_w, L1_xattn_input_norm_w, L1_ffn_w1_w, L1_ffn_w1_s, L1_ffn_w2_w, L1_ffn_w2_s, L1_ffn_h1_w, L1_ffn_h1_s, L1_ffn_h2_w, L1_ffn_h2_s, L1_ffn_w3_w, L1_ffn_w3_s):
    import jax
    import jax.numpy as jnp

    def _L0_attn_ref(x, Wq, Wk, Wv, Wf, Wbet, Wo, delta, lamb_params, norm_weight, gate_w1, gate_w2):
        import jax, jax.numpy as jnp
        import numpy as np
        import math
        B, N, D = (2, 512, 256)
        H = 16
        DH = D // H
        CG_ITERS = 30
        THRESHOLD = 0.99
        LAMBDA_INIT = 1.0
        LAMBDA_LOWER = 0.25
        NORM_EPS = 1e-05

        def l2norm(x, eps=1e-06):
            return x * jax.lax.rsqrt(jnp.sum(x * x, axis=-1, keepdims=True) + eps)

        def cg_solve(A, rhs, n_iters):
            x0 = jnp.zeros_like(rhs)
            rs0 = jnp.sum(rhs * rhs, axis=-1)

            def step(carry, _):
                x, r, p, rs = carry
                Ap = jnp.einsum('bhij,bhj->bhi', A, p)
                alpha = rs / (jnp.sum(p * Ap, axis=-1) + 1e-12)
                x = x + alpha[..., None] * p
                r = r - alpha[..., None] * Ap
                rs_new = jnp.sum(r * r, axis=-1)
                p = r + (rs_new / (rs + 1e-12))[..., None] * p
                return ((x, r, p, rs_new), None)
            (x, _, _, _), _ = jax.lax.scan(step, (x0, rhs, rhs, rs0), None, length=n_iters)
            return x
        b, n, d = x.shape
        h, dh = (H, DH)
        q = (x @ Wq).reshape(b, n, h, dh)
        k = (x @ Wk).reshape(b, n, h, dh)
        v = (x @ Wv).reshape(b, n, h, dh)
        log_f = jax.nn.log_sigmoid(x @ Wf + delta)
        beta = jax.nn.sigmoid(x @ Wbet)
        lamb = (jax.nn.softplus(lamb_params) + LAMBDA_LOWER).reshape(h, dh)
        q = l2norm(q)
        k = l2norm(k)
        diag_lamb = lamb[:, :, None] * jnp.eye(dh, dtype=x.dtype)
        qT = q.transpose(1, 0, 2, 3)
        kT = k.transpose(1, 0, 2, 3)
        vT = v.transpose(1, 0, 2, 3)
        fT = log_f.transpose(1, 0, 2)
        bT = beta.transpose(1, 0, 2)

        def step(carry, inp):
            h_kk, h_kv = carry
            qt, kt, vt, ft, bt = inp
            fexp = jnp.exp(ft)[..., None, None]
            bkt = bt[..., None] * kt
            h_kk = fexp * h_kk + jnp.einsum('bhi,bhj->bhij', bkt, kt)
            h_kv = fexp * h_kv + jnp.einsum('bhi,bhj->bhij', bkt, vt)
            A = h_kk + diag_lamb
            qs = cg_solve(A, qt, CG_ITERS)
            ot = jnp.einsum('bhi,bhij->bhj', qs, h_kv)
            return ((h_kk, h_kv), ot)
        init = (jnp.zeros((b, h, dh, dh), dtype=x.dtype), jnp.zeros((b, h, dh, dh), dtype=x.dtype))
        _, oT = jax.lax.scan(step, init, (qT, kT, vT, fT, bT))
        o = oT.transpose(1, 0, 2, 3)
        gate = jax.nn.sigmoid(x @ gate_w1 @ gate_w2).reshape(b, n, h, dh)
        og = o * gate
        og = og * jax.lax.rsqrt(jnp.mean(og * og, axis=-1, keepdims=True) + NORM_EPS)
        out = og.reshape(b, n, d) * norm_weight
        return out @ Wo

    def _L0_xattn_ref(x, w1, v1, w2):
        import jax, jax.numpy as jnp
        import numpy as np
        E, TPE, H, F = (64, 64, 256, 256)
        h1 = jnp.einsum('eth,efh->etf', x, w1)
        h2 = jnp.einsum('eth,efh->etf', x, v1)
        g = jax.nn.gelu(h1, approximate=False) * h2
        return jnp.einsum('etf,efh->eth', g, w2)

    def _L0_ffn_ref(x, w_gate, w_up, w_down):
        import jax, jax.numpy as jnp
        import numpy as np
        HIDDEN = 256
        INNER = 1024

        def _weight_quant(w):
            scale = 1.0 / jnp.clip(jnp.mean(jnp.abs(w)), 1e-05)
            wq = jnp.clip(jnp.round(w * scale), -1.0, 1.0) / scale
            return w + jax.lax.stop_gradient(wq - w)

        def _act_quant(x):
            scale = 127.0 / jnp.clip(jnp.max(jnp.abs(x), axis=-1, keepdims=True), 1e-05)
            xq = jnp.clip(jnp.round(x * scale), -128.0, 127.0) / scale
            return x + jax.lax.stop_gradient(xq - x)

        def _bitlinear(x, w):
            return jnp.einsum('bsi,oi->bso', _act_quant(x), _weight_quant(w))
        gate = jax.nn.silu(_bitlinear(x, w_gate))
        up = _bitlinear(x, w_up)
        return _bitlinear(gate * up, w_down)

    def _L1_attn_ref(x, Wq, Wk, Wv, Wo, bo, wk_comp, wv_comp, pe, Wg, bg):
        import jax, jax.numpy as jnp
        import numpy as np
        B, S, DIN, DOUT, H, KVH = (2, 512, 256, 256, 16, 16)
        HD = DOUT // H
        CB = 16
        CS = 16
        SB = 8
        TOPK = 2
        WIN = 64
        SCALE = 1.0 / np.sqrt(HD)

        def _rope(x, hd):
            b, s, d = x.shape
            xh = x.reshape(b, s, d // hd, hd)
            half = hd // 2
            inv = 1.0 / 10000.0 ** (jnp.arange(half, dtype=jnp.float32) * 2.0 / hd)
            ang = jnp.arange(s, dtype=jnp.float32)[:, None] * inv[None, :]
            cos = jnp.cos(ang)[None, :, None, :]
            sin = jnp.sin(ang)[None, :, None, :]
            x1, x2 = (xh[..., 0::2], xh[..., 1::2])
            out = jnp.stack([x1 * cos - x2 * sin, x1 * sin + x2 * cos], axis=-1)
            return out.reshape(b, s, d)

        def _masked_softmax(scores, mask):
            s = jnp.where(mask, scores, -jnp.inf)
            m = jnp.max(s, axis=-1, keepdims=True)
            m = jnp.where(jnp.isfinite(m), m, jnp.zeros_like(m))
            e = jnp.exp(s - m)
            den = jnp.sum(e, axis=-1, keepdims=True)
            return jnp.where(den > 0, e / jnp.where(den > 0, den, 1.0), jnp.zeros_like(e))
        b, s, _ = x.shape
        q = _rope(x @ Wq, HD)
        k = _rope(x @ Wk, HD)
        v = x @ Wv
        nb = (s - CB) // CS + 1
        kb = k[:, :nb * CS].reshape(b, nb, CB, -1) + pe[None, None]
        vb = v[:, :nb * CS].reshape(b, nb, CB, -1) + pe[None, None]
        ck = jnp.einsum('bnkd,k->bnd', kb, wk_comp)
        cv = jnp.einsum('bnkd,k->bnd', vb, wv_comp)
        q4 = q.reshape(b, s, H, HD).transpose(0, 2, 1, 3)
        k4 = k.reshape(b, s, KVH, HD).transpose(0, 2, 1, 3)
        v4 = v.reshape(b, s, KVH, HD).transpose(0, 2, 1, 3)
        ck4 = ck.reshape(b, nb, KVH, HD).transpose(0, 2, 1, 3)
        cv4 = cv.reshape(b, nb, KVH, HD).transpose(0, 2, 1, 3)
        sc = jnp.einsum('bhsd,bhnd->bhsn', q4, ck4) * SCALE
        comp_mask = (jnp.arange(nb) + 1) * CS <= jnp.arange(s)[:, None]
        a_comp = _masked_softmax(sc, comp_mask[None, None])
        out_comp = jnp.einsum('bhsn,bhnd->bhsd', a_comp, cv4).transpose(0, 2, 1, 3).reshape(b, s, DOUT)
        imp = sc.mean(axis=(1, 2))
        _, top_idx = jax.lax.top_k(imp, TOPK)
        pos = (top_idx * CS)[:, :, None] + jnp.arange(SB)[None, None, :]
        pos = pos.reshape(b, TOPK * SB)
        valid = pos < s
        posc = jnp.minimum(pos, s - 1)
        sel_k = jnp.take_along_axis(k, posc[..., None], axis=1) * valid[..., None]
        sel_v = jnp.take_along_axis(v, posc[..., None], axis=1) * valid[..., None]
        M = TOPK * SB
        ks4 = sel_k.reshape(b, M, KVH, HD).transpose(0, 2, 1, 3)
        vs4 = sel_v.reshape(b, M, KVH, HD).transpose(0, 2, 1, 3)
        ss = jnp.einsum('bhsd,bhmd->bhsm', q4, ks4) * SCALE
        causal_sel = jnp.arange(s)[None, :, None] >= pos[:, None, :]
        a_sel = _masked_softmax(ss, (causal_sel & valid[:, None, :])[:, None])
        out_sel = jnp.einsum('bhsm,bhmd->bhsd', a_sel, vs4).transpose(0, 2, 1, 3).reshape(b, s, DOUT)
        sw = jnp.einsum('bhsd,bhtd->bhst', q4, k4) * SCALE
        rows = jnp.arange(s)[:, None]
        cols = jnp.arange(s)[None, :]
        wmask = (cols <= rows) & (cols > rows - WIN)
        a_win = _masked_softmax(sw, wmask[None, None])
        out_win = jnp.einsum('bhst,bhtd->bhsd', a_win, v4).transpose(0, 2, 1, 3).reshape(b, s, DOUT)
        g = jax.nn.softmax(x @ Wg + bg, axis=-1)
        out = g[..., 0:1] * out_comp + g[..., 1:2] * out_sel + g[..., 2:3] * out_win
        return out @ Wo + bo

    def _L1_xattn_ref(slots, P, Wq, Wk, Wv, gru_wih, gru_whh, gru_bih, gru_bhh, slot_norm_w, input_norm_w):
        import jax, jax.numpy as jnp
        import numpy as np
        D = 256
        NUM_ITERS = 3
        EPS = 1e-06
        SCALE = D ** (-0.5)

        def rmsnorm(x, w, eps=EPS):
            return x * jax.lax.rsqrt(jnp.mean(x * x, axis=-1, keepdims=True) + eps) * w

        def gru_cell(x, h, wih, whh, bih, bhh):
            gx = x @ wih.T + bih
            gh = h @ whh.T + bhh
            xr, xz, xn = jnp.split(gx, 3, axis=-1)
            hr, hz, hn = jnp.split(gh, 3, axis=-1)
            r = jax.nn.sigmoid(xr + hr)
            z = jax.nn.sigmoid(xz + hz)
            n = jnp.tanh(xn + r * hn)
            return (1.0 - z) * n + z * h
        Pn = rmsnorm(P, input_norm_w)
        k_proj = Pn @ Wk.T
        v_proj = Pn @ Wv.T
        for _ in range(NUM_ITERS):
            sn = rmsnorm(slots, slot_norm_w)
            q_proj = sn @ Wq.T
            scores = jnp.einsum('bkd,bmd->bkm', q_proj, k_proj) * SCALE
            attn = jax.nn.softmax(scores, axis=-2)
            attn = attn / (jnp.sum(attn, axis=-1, keepdims=True) + EPS)
            updates = jnp.einsum('bkm,bmd->bkd', attn, v_proj)
            slots = gru_cell(updates, slots, gru_wih, gru_whh, gru_bih, gru_bhh)
        return slots

    def _L1_ffn_ref(x, w1_w, w1_s, w2_w, w2_s, h1_w, h1_s, h2_w, h2_s, w3_w, w3_s):
        import jax, jax.numpy as jnp
        import numpy as np
        D_IN, D_HID = (256, 1024)

        def _ternary(key, shape):
            return jax.random.randint(key, shape, -1, 2).astype(jnp.float32)

        def _tlin(x, w, s):
            return jnp.einsum('bsi,oi->bso', x, w) * s
        h = jax.nn.silu(_tlin(x, w1_w, w1_s)) * _tlin(x, w2_w, w2_s)
        h = jax.nn.gelu(_tlin(h, h1_w, h1_s), approximate=False)
        h = jax.nn.gelu(_tlin(h, h2_w, h2_s), approximate=False)
        return _tlin(h, w3_w, w3_s)
    x = _layernorm(x + _L0_attn_ref(x, L0_attn_Wq, L0_attn_Wk, L0_attn_Wv, L0_attn_Wf, L0_attn_Wbet, L0_attn_Wo, L0_attn_delta, L0_attn_lamb_params, L0_attn_norm_weight, L0_attn_gate_w1, L0_attn_gate_w2), axis=-1)
    x = _layernorm(x + _L0_xattn_ref(x, ctx_1024, ctx_1024, ctx_1024), axis=-1)
    x = _layernorm(x + _L0_ffn_ref(x, L0_ffn_w_gate, L0_ffn_w_up, L0_ffn_w_down), axis=-1)
    x = _layernorm(x + _L1_attn_ref(x, L1_attn_Wq, L1_attn_Wk, L1_attn_Wv, L1_attn_Wo, L1_attn_bo, L1_attn_wk_comp, L1_attn_wv_comp, L1_attn_pe, L1_attn_Wg, L1_attn_bg), axis=-1)
    x = _layernorm(x + _L1_xattn_ref(x, ctx_1024, L1_xattn_Wq, L1_xattn_Wk, L1_xattn_Wv, L1_xattn_gru_wih, L1_xattn_gru_whh, L1_xattn_gru_bih, L1_xattn_gru_bhh, L1_xattn_slot_norm_w, L1_xattn_input_norm_w), axis=-1)
    x = _layernorm(x + _L1_ffn_ref(x, L1_ffn_w1_w, L1_ffn_w1_s, L1_ffn_w2_w, L1_ffn_w2_s, L1_ffn_h1_w, L1_ffn_h1_s, L1_ffn_h2_w, L1_ffn_h2_s, L1_ffn_w3_w, L1_ffn_w3_s), axis=-1)
    return x

_drawn_inputs = setup_inputs


def setup_inputs(seed=0):
    import zlib

    import numpy as np

    out = dict(_drawn_inputs(seed))
    spreads = {'L0_attn_delta': (4.595119953155518, 0.2),
     'L0_attn_lamb_params': (1.9887207746505737, 0.2),
     'L0_attn_norm_weight': (1.0, 0.2),
     'L1_attn_bo': (0.0, 0.1),
     'L1_attn_bg': (0.0, 0.288),
     'L1_xattn_gru_bih': (0.0, 0.1),
     'L1_xattn_gru_bhh': (0.0, 0.1),
     'L1_xattn_slot_norm_w': (1.0, 0.6),
     'L1_xattn_input_norm_w': (1.0, 0.2)}
    factors = {'L0_attn_Wf': 7.568,
     'L0_attn_gate_w1': 8.0,
     'L0_attn_gate_w2': 8.0,
     'L1_ffn_w1_w': 8.0,
     'L1_ffn_w1_s': 8.0,
     'L1_ffn_w2_w': 8.0,
     'L1_ffn_w2_s': 8.0,
     'L1_ffn_h1_w': 8.0,
     'L1_ffn_h1_s': 8.0,
     'L1_ffn_h2_w': 8.0,
     'L1_ffn_h2_s': 8.0,
     'L1_ffn_w3_w': 8.0,
     'L1_ffn_w3_s': 8.0}
    for name, (base, spread) in spreads.items():
        noise = np.random.default_rng([zlib.crc32(name.encode()), seed]).standard_normal(out[name].shape)
        drawn = base * np.exp(spread * noise) if base else spread * noise
        out[name] = jnp.asarray(drawn.astype(out[name].dtype))
    for name, factor in factors.items():
        out[name] = (out[name] * factor).astype(out[name].dtype)
    return out
```

```python
from contextlib import ExitStack

import concourse.bass as bass
import numpy as np
from concourse import mybir

F32 = mybir.dt.float32
BF16 = mybir.dt.bfloat16
ALU = mybir.AluOpType
ACT = mybir.ActivationFunctionType
AX = mybir.AxisListType

P = 128
B, S, D = 4, 1024, 256
C = D // P
T = B * S
W = 512
NT = T // W
M = 77
INNER = 1024
CI = INNER // P
H, DH = 16, 16
EPS_LN = 1e-5
ONE = 1
STAGES = (1, 2, 3, 4, 5, 6)


class Stage:

    def __init__(self, nc, name):
        self.nc, self.name, self.memory, self.counters = nc, name, ExitStack(), []

    def sb(self, name, shape, dt=F32):
        return self.memory.enter_context(self.nc.sbuf_tensor(f"{self.name}_{name}", shape, dt))

    def ps(self, name, shape=(P, W), dt=F32):
        return self.memory.enter_context(self.nc.psum_tensor(f"{self.name}_{name}", list(shape), dt))

    def sem(self, name):
        self.counters.append(self.memory.enter_context(self.nc.semaphore(f"{self.name}_{name}")))
        return self.counters[-1]

    def shared_out(self, act):
        share = -(-len(self.counters) // 4)
        with self.nc.Block() as block:
            for k, engine in enumerate((block.vector, block.scalar, block.gpsimd, block.sync)):
                @engine
                def _(eng, mine=self.counters[k * share:(k + 1) * share]):
                    for sem in mine:
                        act(eng, sem)

    def start_counters(self):
        self.shared_out(lambda eng, sem: eng.sem_inc(sem, ONE))

    def close(self):
        self.shared_out(lambda eng, sem: eng.sem_clear(sem))
        self.memory.close()



def load_stream(nc, xf, x_in):
    st = Stage(nc, "load")
    x_here = st.sem("x_here")
    with nc.Block() as block:
        @block.sync
        def _(sp):
            for b in range(B):
                sp.dma_start(xf[:, :, b * S:(b + 1) * S], x_in[:, :, b * S:(b + 1) * S]).then_inc(x_here, 16)
            sp.wait_ge(x_here, 16 * B)
    st.close()


def store_stream(nc, xf, x_out):
    st = Stage(nc, "store")
    x_out_done = st.sem("x_out_done")
    with nc.Block() as block:
        @block.sync
        def _(sp):
            for b in range(B):
                sp.dma_start(x_out[:, :, b * S:(b + 1) * S], xf[:, :, b * S:(b + 1) * S]).then_inc(x_out_done, 16)
            sp.wait_ge(x_out_done, 16 * B)
    st.close()



def layer_norm(nc, name, xf, mean_w, eps_ln):
    st = Stage(nc, name)
    cen = st.sb("centred", [P, 2, C, W])
    sq = st.sb("square", [P, 2, C, W])
    sd = st.sb("deviation", [P, 2, W])
    rs = st.sb("inverse", [P, 2, W])
    ps_mean = [st.ps(f"mean{k}") for k in range(2)]
    ps_var = [st.ps(f"var{k}") for k in range(2)]
    mean_done, cen_done, sq_done, var_done = (st.sem(n) for n in ("mean_done", "cen_done", "sq_done", "var_done"))
    sd_done, rs_done, norm_done = (st.sem(n) for n in ("sd_done", "rs_done", "norm_done"))
    cols = [slice(t * W, (t + 1) * W) for t in range(NT)]
    with nc.Block() as block:
        @block.tensor
        def _(pe):
            def var(t):
                pe.wait_ge(sq_done, t + 1)
                if t >= 2:
                    pe.wait_ge(sd_done, t - 1)
                for c in range(C):
                    mm = pe.matmul(ps_var[t % 2][:], mean_w[:], sq[:, t % 2, c, :], start=c == 0, stop=c == C - 1)
                mm.then_inc(var_done, 1)
            for t in range(NT):
                if t >= 2:
                    pe.wait_ge(cen_done, t - 1)
                for c in range(C):
                    mm = pe.matmul(ps_mean[t % 2][:], mean_w[:], xf[:, c, cols[t]], start=c == 0, stop=c == C - 1)
                mm.then_inc(mean_done, 1)
                if t >= 1:
                    var(t - 1)
            var(NT - 1)

        @block.vector
        def _(dve):
            def scale(t):
                dve.wait_ge(sd_done, t + 1)
                if t >= 2:
                    dve.wait_ge(norm_done, t - 1)
                dve.reciprocal(rs[:, t % 2, :], sd[:, t % 2, :]).then_inc(rs_done, 1)
                dve.wait_ge(rs_done, t + 1)
                dve.tensor_tensor(xf[:, :, cols[t]], cen[:, t % 2, :, :],
                                  rs[:, t % 2, :].unsqueeze(1).to_broadcast([P, C, W]), ALU.mult).then_inc(norm_done, 1)
            for t in range(NT):
                dve.wait_ge(mean_done, t + 1)
                if t >= 2:
                    dve.wait_ge(norm_done, t - 1)
                    dve.wait_ge(sq_done, t - 1)
                dve.tensor_tensor(cen[:, t % 2, :, :], xf[:, :, cols[t]],
                                  ps_mean[t % 2][:].unsqueeze(1).to_broadcast([P, C, W]), ALU.subtract).then_inc(cen_done, 1)
                if t >= 1:
                    scale(t - 1)
            scale(NT - 1)

        @block.scalar
        def _(act):
            def root(t):
                act.wait_ge(var_done, t + 1)
                if t >= 2:
                    act.wait_ge(rs_done, t - 1)
                act.activation(sd[:, t % 2, :], ps_var[t % 2][:], ACT.Sqrt, bias=eps_ln[:, 0:1]).then_inc(sd_done, 1)
            for t in range(NT):
                act.wait_ge(cen_done, t + 1)
                if t >= 2:
                    act.wait_ge(var_done, t - 1)
                act.activation(sq[:, t % 2, :, :], cen[:, t % 2, :, :], ACT.Square).then_inc(sq_done, 1)
                if t >= 1:
                    root(t - 1)
            root(NT - 1)
    st.close()



def context_mixture(nc, xf, ctx, ctxT):
    st = Stage(nc, "mix")
    ctx_sb = st.sb("ctx", [M, B, D])
    ctxT_sb = st.sb("ctxT", [P, C, B * M])
    gel = st.sb("gelu", [M, 2, W])
    g = st.sb("g", [M, 2, W])
    ps_h = [st.ps(f"h{k}") for k in range(2)]
    ps_o = [[st.ps(f"o{k}{c}") for c in range(C)] for k in range(2)]
    ctx_here, h_done, gelu_done, g_done = (st.sem(n) for n in ("ctx_here", "h_done", "gelu_done", "g_done"))
    o_done, add_done = st.sem("o_done"), st.sem("add_done")
    cols = [slice(t * W, (t + 1) * W) for t in range(NT)]
    with nc.Block() as block:
        @block.sync
        def _(sp):
            sp.dma_start(ctx_sb[:], ctx).then_inc(ctx_here, 16)
            sp.dma_start(ctxT_sb[:], ctxT).then_inc(ctx_here, 16)

        @block.tensor
        def _(pe):
            pe.wait_ge(ctx_here, 32)

            def out(t):
                b = t * W // S
                pe.wait_ge(g_done, t + 1)
                if t >= 2:
                    pe.wait_ge(add_done, C * (t - 1))
                for c in range(C):
                    pe.matmul(ps_o[t % 2][c][:], ctx_sb[:, b, c * P:(c + 1) * P], g[:, t % 2, :],
                              start=True, stop=True).then_inc(o_done, 1)
            for t in range(NT):
                b = t * W // S
                if t >= 2:
                    pe.wait_ge(g_done, t - 1)
                for c in range(C):
                    mm = pe.matmul(ps_h[t % 2][0:M, :], ctxT_sb[:, c, b * M:(b + 1) * M], xf[:, c, cols[t]],
                                   start=c == 0, stop=c == C - 1)
                mm.then_inc(h_done, 1)
                if t >= 1:
                    out(t - 1)
            out(NT - 1)

        @block.scalar
        def _(act):
            for t in range(NT):
                act.wait_ge(h_done, t + 1)
                if t >= 2:
                    act.wait_ge(g_done, t - 1)
                act.activation(gel[:, t % 2, :], ps_h[t % 2][0:M, :], ACT.Gelu).then_inc(gelu_done, 1)

        @block.vector
        def _(dve):
            def add(t):
                for c in range(C):
                    dve.wait_ge(o_done, C * t + c + 1)
                    dve.tensor_tensor(xf[:, c, cols[t]], ps_o[t % 2][c][:], xf[:, c, cols[t]], ALU.add).then_inc(add_done, 1)
            for t in range(NT):
                dve.wait_ge(gelu_done, t + 1)
                if t >= 2:
                    dve.wait_ge(o_done, C * (t - 1))
                dve.tensor_tensor(g[:, t % 2, :], ps_h[t % 2][0:M, :], gel[:, t % 2, :], ALU.mult).then_inc(g_done, 1)
                if t >= 1:
                    add(t - 1)
            add(NT - 1)
    st.close()



def ternary_ffn(nc, xf, w1T, w2T, h1T, h2T, w3T, scales):
    st = Stage(nc, "ffn1")
    w1 = st.sb("w1", [P, C, INNER])
    w2 = st.sb("w2", [P, C, INNER])
    h1 = st.sb("h1", [P, CI, INNER])
    h2 = st.sb("h2", [P, CI, INNER])
    w3 = st.sb("w3", [P, CI, D])
    sc = st.sb("row_scales", [P, 4 * CI + C])
    xt = st.sb("x_tile", [P, C, W])
    silu = st.sb("silu", [P, 2, W])
    ha = st.sb("hidden_a", [P, CI, W])
    hb = st.sb("hidden_b", [P, CI, W])
    ps = [st.ps(f"bank{k}") for k in range(8)]
    w_here = [st.sem(f"w_here{k}") for k in range(5)]
    x_ready, x_added = st.sem("x_ready"), st.sem("x_added")
    gate_done, up_done, silu_done, gated = (st.sem(n) for n in ("gate_done", "up_done", "silu_done", "gated"))
    mix1_done, gelu1_done, mix2_done, gelu2_done, out_done = (
        st.sem(n) for n in ("mix1_done", "gelu1_done", "mix2_done", "gelu2_done", "out_done"))
    st.start_counters()
    with nc.Block() as block:
        @block.sync
        def _(sp):
            sp.dma_start(w1[:], w1T).then_inc(w_here[0], 16)
            sp.dma_start(w2[:], w2T).then_inc(w_here[0], 16)
            sp.dma_start(sc[:], scales).then_inc(w_here[1], 16)
            sp.dma_start(h1[:], h1T).then_inc(w_here[2], 16)
            sp.dma_start(h2[:], h2T).then_inc(w_here[3], 16)
            sp.dma_start(w3[:], w3T).then_inc(w_here[4], 16)

        @block.tensor
        def _(pe):
            pe.wait_ge(w_here[0], ONE + 32)
            for k in (2, 3, 4):
                pe.wait_ge(w_here[k], ONE + 16)
            with pe.Fori(0, NT) as t:
                pe.wait_ge(x_ready, ONE + t + 1)
                for m in range(CI):
                    rows = slice(m * P, (m + 1) * P)
                    pe.wait_ge(silu_done, ONE + t * CI + max(m - 1, 0))
                    for c in range(C):
                        mm = pe.matmul(ps[m % 2][:], w1[:, c, rows], xt[:, c, :], start=c == 0, stop=c == C - 1)
                    mm.then_inc(gate_done, 1)
                    pe.wait_ge(gated, ONE + t * CI + max(m - 1, 0))
                    for c in range(C):
                        mm = pe.matmul(ps[2 + m % 2][:], w2[:, c, rows], xt[:, c, :], start=c == 0, stop=c == C - 1)
                    mm.then_inc(up_done, 1)
                pe.wait_ge(gated, ONE + t * CI + CI)
                for m in range(CI):
                    pe.wait_ge(gelu1_done, ONE + t * CI + max(m - 1, 0))
                    for c in range(CI):
                        mm = pe.matmul(ps[4 + m % 2][:], h1[:, c, m * P:(m + 1) * P], ha[:, c, :],
                                       start=c == 0, stop=c == CI - 1)
                    mm.then_inc(mix1_done, 1)
                pe.wait_ge(gelu1_done, ONE + t * CI + CI)
                for m in range(CI):
                    pe.wait_ge(gelu2_done, ONE + t * CI + max(m - 1, 0))
                    for c in range(CI):
                        mm = pe.matmul(ps[4 + m % 2][:], h2[:, c, m * P:(m + 1) * P], hb[:, c, :],
                                       start=c == 0, stop=c == CI - 1)
                    mm.then_inc(mix2_done, 1)
                pe.wait_ge(gelu2_done, ONE + t * CI + CI)
                pe.wait_ge(x_added, ONE + t * C)
                for m in range(C):
                    for c in range(CI):
                        mm = pe.matmul(ps[6 + m][:], w3[:, c, m * P:(m + 1) * P], ha[:, c, :],
                                       start=c == 0, stop=c == CI - 1)
                    mm.then_inc(out_done, 1)

        @block.scalar
        def _(act):
            act.wait_ge(w_here[1], ONE + 16)
            with act.Fori(0, NT) as t:
                for m in range(CI):
                    act.wait_ge(gate_done, ONE + t * CI + m + 1)
                    act.wait_ge(gated, ONE + t * CI + max(m - 1, 0))
                    act.activation(silu[:, m % 2, :], ps[m % 2][:], ACT.Silu, scale=sc[:, m:m + 1]).then_inc(silu_done, 1)
                for m in range(CI):
                    act.wait_ge(mix1_done, ONE + t * CI + m + 1)
                    act.activation(hb[:, m, :], ps[4 + m % 2][:], ACT.Gelu,
                                   scale=sc[:, 2 * CI + m:2 * CI + m + 1]).then_inc(gelu1_done, 1)
                act.wait_ge(mix1_done, ONE + t * CI + CI)
                for m in range(CI):
                    act.wait_ge(mix2_done, ONE + t * CI + m + 1)
                    act.activation(ha[:, m, :], ps[4 + m % 2][:], ACT.Gelu,
                                   scale=sc[:, 3 * CI + m:3 * CI + m + 1]).then_inc(gelu2_done, 1)

        @block.vector
        def _(dve):
            dve.wait_ge(w_here[1], ONE + 16)
            with dve.Fori(0, NT) as t:
                dve.wait_ge(up_done, ONE + t * CI)
                dve.wait_ge(x_added, ONE + t * C)
                dve.tensor_copy(xt[:], xf[:, :, bass.ts(t, W)]).then_inc(x_ready, 1)
                dve.wait_ge(out_done, ONE + t * C)
                for m in range(CI):
                    dve.wait_ge(silu_done, ONE + t * CI + m + 1)
                    dve.wait_ge(up_done, ONE + t * CI + m + 1)
                    dve.scalar_tensor_tensor(out=ha[:, m, :], in0=ps[2 + m % 2][:], scalar=sc[:, CI + m:CI + m + 1],
                                             in1=silu[:, m % 2, :], op0=ALU.mult, op1=ALU.mult).then_inc(gated, 1)
                for c in range(C):
                    dve.wait_ge(out_done, ONE + t * C + c + 1)
                    dve.scalar_tensor_tensor(out=xf[:, c, bass.ts(t, W)], in0=ps[6 + c][:],
                                             scalar=sc[:, 4 * CI + c:4 * CI + c + 1], in1=xt[:, c, :],
                                             op0=ALU.mult, op1=ALU.add).then_inc(x_added, 1)
    st.close()


def slot_attention(nc, xf, io, mean_w, eps):
    G3 = 3 * D
    ROUNDS = 3
    TW = S // W
    RMS_EPS = eps[:, 1:2]
    st = Stage(nc, "slot")
    ctxT = st.sb("ctxT", [P, C, B * M])
    wkT, wq, wvT = st.sb("wkT", [P, C, D]), st.sb("wq", [P, C, D]), st.sb("wvT", [P, C, D])
    wihT, whhT = st.sb("wihT", [P, C, G3]), st.sb("whhT", [P, C, G3])
    vecs = st.sb("vectors", [P, 2 * C + 12])
    bias = st.sb("bias", [P, 8])
    sq = st.sb("ctx_square", [P, C, B * M])
    rinv = st.sb("ctx_inverse", [P, B * M])
    root = st.sb("ctx_root", [P, B * M])
    pn = st.sb("ctx_normed", [P, C, B * M])
    kT, vT = st.sb("kT", [P, C, B * M]), st.sb("vT", [P, C, B * M])
    keys = st.sb("keys", [P, C, B * M])
    vals = st.sb("values", [M, B, G3])
    key_b, val_b = st.sb("key_b", [P, C, M]), st.sb("val_b", [M, G3])
    slots = [st.sb(f"slots{k}", [P, C, S]) for k in range(2)]
    ssq = st.sb("slot_square", [P, C, S])
    sroot = st.sb("slot_root", [M, S])
    srs = st.sb("slot_inverse", [M, S])
    score = st.sb("score", [M, S])
    prob = st.sb("prob", [M, S])
    attn = st.sb("attn", [M, S])
    den = st.sb("mass", [M, S])
    mx, nmx, zsum, zinv = (st.sb(n, [M, 1]) for n in ("top", "minus_top", "sum", "sum_inverse"))
    ones_m = st.sb("ones", [M, M])
    gate_r, gate_z = st.sb("reset", [P, 2, W]), st.sb("update", [P, 2, W])
    hid, new = st.sb("hidden", [P, 2, W]), st.sb("new", [P, 2, W])
    pre, arg = st.sb("reset_hidden", [P, 2, W]), st.sb("new_argument", [P, 2, W])
    dif, dif2 = st.sb("difference", [P, 2, W]), st.sb("gated_difference", [P, 2, W])
    bank = [st.ps(f"bank{k}") for k in range(8)]
    here = st.sem("inputs_here")
    names = ("bias_ready csq_done cms_done croot_done cinv_done pn_half pn_done kv_done kv_copied keys_done keys_copied "
             "vals_done vals_copied ones_set row_ready slots_square ms_done sroot_done srs_done scores_done scaled top_done "
             "minus_done prob_done zinv_done attn_done mass_done mass_moved attn_normed hid_done reset_done update_done "
             "cell_done pre_done arg_done new_done dif_done dif2_done slots_done x_copied mass_inv_done x_added").split()
    s = {n: st.sem(n) for n in names}
    HALVES = ROUNDS * TW * C
    st.start_counters()
    with nc.Block() as block:
        @block.sync
        def _(sp):
            for dst, src in ((ctxT, "ctxT"), (wkT, "slot_wkT"), (wq, "slot_wq"), (wvT, "slot_wvT"), (wihT, "slot_wihT"),
                             (whhT, "slot_whhT"), (vecs, "slot_vectors")):
                sp.dma_start(dst[:], io[src]).then_inc(here, 16)

        @block.tensor
        def _(pe):
            pe.wait_ge(s["csq_done"], ONE + 1)
            for c in range(C):
                mm = pe.matmul(bank[0][:, 0:B * M], mean_w[:], sq[:, c, :], start=c == 0, stop=c == C - 1)
            mm.then_inc(s["cms_done"], 1)
            pe.wait_ge(s["pn_done"], ONE + C)
            for k, w in enumerate((wkT, wvT)):
                for m in range(C):
                    for c in range(C):
                        mm = pe.matmul(bank[1 + 2 * k + m][:, 0:B * M], w[:, c, m * P:(m + 1) * P], pn[:, c, :],
                                       start=c == 0, stop=c == C - 1)
                    mm.then_inc(s["kv_done"], 1)
            pe.wait_ge(s["kv_copied"], ONE + 2 * C)
            for m in range(C):
                for c in range(C):
                    mm = pe.matmul(bank[5 + m][:, 0:B * M], wq[:, c, m * P:(m + 1) * P], kT[:, c, :],
                                   start=c == 0, stop=c == C - 1)
                mm.then_inc(s["keys_done"], 1)
            for b in range(B):
                for h in range(2):
                    n = 2 * b + h
                    if n >= 2:
                        pe.wait_ge(s["vals_copied"], ONE + n - 1)
                    for c in range(C):
                        mm = pe.matmul(bank[1 + n % 2][0:M, 0:G3 // 2], vT[:, c, b * M:(b + 1) * M],
                                       wihT[:, c, h * (G3 // 2):(h + 1) * (G3 // 2)], start=c == 0, stop=c == C - 1)
                    mm.then_inc(s["vals_done"], 1)
            pe.wait_ge(s["ones_set"], ONE + 1)
            with pe.Fori(0, B) as b:
                pe.wait_ge(s["row_ready"], ONE + 2 * b + 2)
                for r in range(ROUNDS):
                    n0 = b * ROUNDS + r
                    cur = slots[(r + 1) % 2]
                    pe.wait_ge(s["slots_square"], ONE + n0 + 1)
                    pe.wait_ge(s["slots_done"], ONE + b * HALVES + r * TW * C)
                    for t in range(TW):
                        for c in range(C):
                            mm = pe.matmul(bank[t][0:M, :], mean_w[:, 0:M], ssq[:, c, t * W:(t + 1) * W],
                                           start=c == 0, stop=c == C - 1)
                        mm.then_inc(s["ms_done"], 1)
                        for c in range(C):
                            mm = pe.matmul(bank[2 + t][0:M, :], key_b[:, c, :], cur[:, c, t * W:(t + 1) * W],
                                           start=c == 0, stop=c == C - 1)
                        mm.then_inc(s["scores_done"], 1)
                    pe.wait_ge(s["attn_done"], ONE + n0 + 1)
                    for t in range(TW):
                        pe.matmul(bank[t][0:M, :], ones_m[:], attn[:, t * W:(t + 1) * W], start=True, stop=True) \
                            .then_inc(s["mass_done"], 1)
                    pe.wait_ge(s["attn_normed"], ONE + n0 + 1)
                    for t in range(TW):
                        for m in range(C):
                            k = t * C + m
                            j = b * HALVES + r * TW * C + k
                            if k >= 2:
                                pe.wait_ge(s["arg_done"], ONE + j - 1)
                                pe.wait_ge(s["update_done"], ONE + j - 1)
                            x = slice(t * W, (t + 1) * W)
                            q = bank[4 * (k % 2):4 * (k % 2) + 4]
                            for g in range(2):
                                rows = slice(g * D + m * P, g * D + (m + 1) * P)
                                for c in range(C):
                                    pe.matmul(q[g][:], whhT[:, c, rows], cur[:, c, x], start=c == 0, stop=False)
                                pe.matmul(q[g][:], val_b[:, rows], prob[:, x], start=False, stop=True).then_inc(s["cell_done"], 1)
                            rows = slice(2 * D + m * P, 2 * D + (m + 1) * P)
                            for c in range(C):
                                mm = pe.matmul(q[2][:], whhT[:, c, rows], cur[:, c, x], start=c == 0, stop=c == C - 1)
                            mm.then_inc(s["cell_done"], 1)
                            pe.matmul(q[3][:], val_b[:, rows], prob[:, x], start=True, stop=True).then_inc(s["cell_done"], 1)

        @block.scalar
        def _(act):
            act.wait_ge(here, ONE + 16 * 7)
            act.activation(sq[:], ctxT[:], ACT.Square).then_inc(s["csq_done"], 1)
            act.wait_ge(s["cms_done"], ONE + 1)
            act.activation(root[:], bank[0][:, 0:B * M], ACT.Sqrt, bias=RMS_EPS).then_inc(s["croot_done"], 1)
            for k, dst in enumerate((kT, vT)):
                for m in range(C):
                    act.wait_ge(s["kv_done"], ONE + 2 * k + m + 1)
                    act.copy(dst[:, m, :], bank[1 + 2 * k + m][:, 0:B * M]).then_inc(s["kv_copied"], 1)
            for b in range(B):
                for h in range(2):
                    n = 2 * b + h
                    act.wait_ge(s["vals_done"], ONE + n + 1)
                    act.copy(vals[:, b, h * (G3 // 2):(h + 1) * (G3 // 2)], bank[1 + n % 2][0:M, 0:G3 // 2]) \
                        .then_inc(s["vals_copied"], 1)
            act.wait_ge(s["bias_ready"], ONE + 4)
            with act.Fori(0, B) as b:
                for r in range(ROUNDS):
                    n0 = b * ROUNDS + r
                    cur = slots[(r + 1) % 2]
                    act.wait_ge(s["slots_done"], ONE + b * HALVES + r * TW * C)
                    if r == 0:
                        act.wait_ge(s["x_copied"], ONE + b + 1)
                    act.wait_ge(s["ms_done"], ONE + TW * n0)
                    act.activation(ssq[:], cur[:], ACT.Square).then_inc(s["slots_square"], 1)
                    for t in range(TW):
                        act.wait_ge(s["ms_done"], ONE + TW * n0 + t + 1)
                        act.wait_ge(s["srs_done"], ONE + TW * n0)
                        act.activation(sroot[:, t * W:(t + 1) * W], bank[t][0:M, :], ACT.Sqrt, bias=eps[0:M, 1:2]) \
                            .then_inc(s["sroot_done"], 1)
                    act.wait_ge(s["minus_done"], ONE + n0 + 1)
                    act.activation(attn[:], score[:], ACT.Exp, bias=nmx[:], accum_out=zsum[:]).then_inc(s["prob_done"], 1)
                    for k in range(TW * C):
                        j = b * HALVES + r * TW * C + k
                        q = bank[4 * (k % 2):4 * (k % 2) + 4]
                        m = k % C
                        act.wait_ge(s["cell_done"], ONE + 4 * j + 1)
                        if k >= 2:
                            act.wait_ge(s["slots_done"], ONE + j - 1)
                        act.activation(gate_r[:, k % 2, :], q[0][:], ACT.Tanh, bias=bias[:, m:m + 1], scale=0.5) \
                            .then_inc(s["reset_done"], 1)
                        act.wait_ge(s["cell_done"], ONE + 4 * j + 2)
                        act.activation(gate_z[:, k % 2, :], q[1][:], ACT.Tanh, bias=bias[:, C + m:C + m + 1], scale=0.5) \
                            .then_inc(s["update_done"], 1)
                        act.wait_ge(s["cell_done"], ONE + 4 * j + 3)
                        act.activation(hid[:, k % 2, :], q[2][:], ACT.Identity, bias=bias[:, 6 + m:7 + m], scale=0.5) \
                            .then_inc(s["hid_done"], 1)
                        act.wait_ge(s["arg_done"], ONE + j + 1)
                        act.activation(new[:, k % 2, :], arg[:, k % 2, :], ACT.Tanh).then_inc(s["new_done"], 1)

        @block.gpsimd
        def _(pool):
            with pool.Fori(0, B) as b:
                pool.wait_ge(s["keys_copied"], ONE + C)
                pool.wait_ge(s["vals_copied"], ONE + 2 * B)
                pool.wait_ge(s["scores_done"], ONE + b * ROUNDS * TW)
                pool.wait_ge(s["cell_done"], ONE + b * HALVES * 4)
                pool.tensor_copy(key_b[:], keys[:, :, bass.ts(b, M)]).then_inc(s["row_ready"], 1)
                pool.tensor_copy(val_b[:], vals[:, b, :]).then_inc(s["row_ready"], 1)
                for r in range(ROUNDS):
                    cur, nxt = slots[(r + 1) % 2], slots[r % 2]
                    for k in range(TW * C):
                        t, m = k // C, k % C
                        j = b * HALVES + r * TW * C + k
                        x = slice(t * W, (t + 1) * W)
                        pool.wait_ge(s["new_done"], ONE + j + 1)
                        if k >= 2:
                            pool.wait_ge(s["dif2_done"], ONE + j - 1)
                        pool.tensor_tensor(dif[:, k % 2, :], cur[:, m, x], new[:, k % 2, :], ALU.subtract) \
                            .then_inc(s["dif_done"], 1)

        @block.vector
        def _(dve):
            dve.wait_ge(here, ONE + 16 * 7)
            dve.memset(ones_m[:], 1.0).then_inc(s["ones_set"], 1)
            dve.tensor_tensor(bias[:, 0:4], vecs[:, 4:8], vecs[:, 10:14], ALU.add).then_inc(s["bias_ready"], 1)
            dve.wait_ge(s["bias_ready"], ONE + 1)
            dve.tensor_scalar(bias[:, 0:4], bias[:, 0:4], 0.5, None, ALU.mult).then_inc(s["bias_ready"], 1)
            dve.tensor_copy(bias[:, 4:6], vecs[:, 8:10]).then_inc(s["bias_ready"], 1)
            dve.tensor_scalar(bias[:, 6:8], vecs[:, 14:16], 0.5, None, ALU.mult).then_inc(s["bias_ready"], 1)
            dve.wait_ge(s["croot_done"], ONE + 1)
            dve.reciprocal(rinv[:], root[:]).then_inc(s["cinv_done"], 1)
            dve.wait_ge(s["cinv_done"], ONE + 1)
            for c in range(C):
                dve.scalar_tensor_tensor(out=pn[:, c, :], in0=ctxT[:, c, :], scalar=vecs[:, C + c:C + c + 1],
                                         in1=rinv[:], op0=ALU.mult, op1=ALU.mult).then_inc(s["pn_done"], 1)
            for m in range(C):
                dve.wait_ge(s["keys_done"], ONE + m + 1)
                dve.tensor_scalar(keys[:, m, :], bank[5 + m][:, 0:B * M], vecs[:, m:m + 1], float(D) ** -0.5,
                                  ALU.mult, ALU.mult).then_inc(s["keys_copied"], 1)
            dve.wait_ge(s["bias_ready"], ONE + 4)
            with dve.Fori(0, B) as b:
                dve.wait_ge(s["cell_done"], ONE + b * HALVES * 4)
                dve.wait_ge(s["dif_done"], ONE + b * HALVES)
                dve.tensor_copy(slots[1][:], xf[:, :, bass.ts(b, S)]).then_inc(s["x_copied"], 1)
                for r in range(ROUNDS):
                    n0 = b * ROUNDS + r
                    nxt = slots[r % 2]
                    for t in range(TW):
                        x = slice(t * W, (t + 1) * W)
                        dve.wait_ge(s["sroot_done"], ONE + TW * n0 + t + 1)
                        dve.reciprocal(srs[:, x], sroot[:, x]).then_inc(s["srs_done"], 1)
                        dve.wait_ge(s["srs_done"], ONE + TW * n0 + t + 1)
                        dve.wait_ge(s["scores_done"], ONE + TW * n0 + t + 1)
                        dve.tensor_tensor(score[:, x], bank[2 + t][0:M, :], srs[:, x], ALU.mult).then_inc(s["scaled"], 1)
                    dve.wait_ge(s["scaled"], ONE + TW * (n0 + 1))
                    dve.tensor_reduce(mx[:], score[:], AX.X, ALU.max).then_inc(s["top_done"], 1)
                    dve.wait_ge(s["top_done"], ONE + n0 + 1)
                    dve.tensor_scalar(nmx[:], mx[:], -1.0, None, ALU.mult).then_inc(s["minus_done"], 1)
                    dve.wait_ge(s["prob_done"], ONE + n0 + 1)
                    dve.reciprocal(zinv[:], zsum[:]).then_inc(s["zinv_done"], 1)
                    dve.wait_ge(s["zinv_done"], ONE + n0 + 1)
                    dve.tensor_scalar(attn[:], attn[:], zinv[:], None, ALU.mult).then_inc(s["attn_done"], 1)
                    for t in range(TW):
                        x = slice(t * W, (t + 1) * W)
                        dve.wait_ge(s["mass_done"], ONE + TW * n0 + t + 1)
                        dve.tensor_scalar(den[:, x], bank[t][0:M, :], 1e-6, None, ALU.add).then_inc(s["mass_moved"], 1)
                    dve.wait_ge(s["mass_moved"], ONE + TW * (n0 + 1))
                    dve.reciprocal(srs[:], den[:]).then_inc(s["mass_inv_done"], 1)
                    dve.wait_ge(s["mass_inv_done"], ONE + n0 + 1)
                    dve.tensor_tensor(prob[:], attn[:], srs[:], ALU.mult).then_inc(s["attn_normed"], 1)
                    for k in range(TW * C):
                        t, m = k // C, k % C
                        j = b * HALVES + r * TW * C + k
                        x = slice(t * W, (t + 1) * W)
                        q = bank[4 * (k % 2):4 * (k % 2) + 4]
                        dve.wait_ge(s["reset_done"], ONE + j + 1)
                        dve.wait_ge(s["hid_done"], ONE + j + 1)
                        dve.scalar_tensor_tensor(out=pre[:, k % 2, :], in0=gate_r[:, k % 2, :], scalar=1.0,
                                                 in1=hid[:, k % 2, :], op0=ALU.add, op1=ALU.mult).then_inc(s["pre_done"], 1)
                        dve.wait_ge(s["pre_done"], ONE + j + 1)
                        dve.wait_ge(s["cell_done"], ONE + 4 * j + 4)
                        dve.scalar_tensor_tensor(out=arg[:, k % 2, :], in0=q[3][:], scalar=bias[:, 4 + m:5 + m],
                                                 in1=pre[:, k % 2, :], op0=ALU.add, op1=ALU.add).then_inc(s["arg_done"], 1)
                        dve.wait_ge(s["dif_done"], ONE + j + 1)
                        dve.wait_ge(s["update_done"], ONE + j + 1)
                        dve.scalar_tensor_tensor(out=dif2[:, k % 2, :], in0=gate_z[:, k % 2, :], scalar=1.0,
                                                 in1=dif[:, k % 2, :], op0=ALU.add, op1=ALU.mult).then_inc(s["dif2_done"], 1)
                        dve.wait_ge(s["dif2_done"], ONE + j + 1)
                        dve.scalar_tensor_tensor(out=nxt[:, m, x], in0=dif2[:, k % 2, :], scalar=0.5,
                                                 in1=new[:, k % 2, :], op0=ALU.mult, op1=ALU.add).then_inc(s["slots_done"], 1)
                dve.wait_ge(s["slots_done"], ONE + (b + 1) * HALVES)
                dve.tensor_tensor(xf[:, :, bass.ts(b, S)], xf[:, :, bass.ts(b, S)], slots[0][:], ALU.add) \
                    .then_inc(s["x_added"], 1)
            dve.wait_ge(s["x_added"], ONE + B)
    st.close()


def quantised_ffn(nc, xf, io, eps):
    TT = 128
    N = T // TT
    HALF = INNER // 2
    MAGIC = 1.5 * 2.0 ** 23
    st = Stage(nc, "ffn0")
    wf = [st.sb(f"w_float{k}", [P, 2 * INNER]) for k in range(3)]
    wq = [st.sb(f"w_tern{k}", [P, 2 * INNER], BF16) for k in range(3)]
    wabs = st.sb("w_abs", [P, 2 * INNER])
    wr = st.sb("w_rounded", [P, 2 * INNER])
    wsum, wmean, wscale = st.sb("w_sum", [P, 3]), st.sb("w_mean", [P, 3]), st.sb("w_scale", [P, 3])
    wmean127 = st.sb("w_mean_127", [P, 3])
    count_w = st.sb("count_w", [P, P])
    magic = st.sb("magic", [P, 1])
    identf, identb = st.sb("identity", [P, P]), st.sb("identity_b", [P, P], BF16)
    xc = st.sb("x_tile", [P, 2, C, TT])
    xr, xq = st.sb("x_rounded", [P, D]), st.sb("x_quantised", [P, D], BF16)
    xqT = st.sb("x_quantisedT", [P, 2, C, TT], BF16)
    sg, h = st.sb("silu", [P, INNER]), st.sb("h", [P, INNER])
    hr, hq = st.sb("h_rounded", [P, INNER]), st.sb("h_quantised", [P, INNER], BF16)
    hqT = st.sb("h_quantisedT", [P, CI, TT], BF16)
    o = st.sb("o", [P, D])
    xm = st.sb("x_scales", [P, 2, 6])
    hm = st.sb("h_scales", [P, 2, 5])
    ps_x = st.ps("xT", [P, D])
    ps_q = st.ps("xqT_bank", [P, C, TT], BF16)
    ps_g = [st.ps(f"gate{k}") for k in range(2)]
    ps_u = [st.ps(f"up{k}") for k in range(2)]
    ps_h = st.ps("hqT_bank", [P, CI, TT], BF16)
    ps_o = st.ps("out", [P, 2, D])
    names = ("here consts wsum_done wtot_done wm_done wstep wq_done x_copied x_turned xmax xstep xr_done xq_done xq_turned "
             "xqT_done gu_done silu_done h_done hmax hstep hr_done hq_done h_turned hqT_done down_done o_done o_turned "
             "added h_half hq_turn").split()
    s = {n: st.sem(n) for n in names}

    def cols(n):
        return bass.ts(n, TT)

    st.start_counters()
    with nc.Block() as block:
        @block.sync
        def _(sp):
            for k, name in enumerate(("q_gateT", "q_upT", "q_downT")):
                sp.dma_start(wf[k][:], io[name].rearrange("p c n -> p (c n)")).then_inc(s["here"], 16)
            sp.dma_start(identf[:], io["identity"]).then_inc(s["here"], 16)

        @block.tensor
        def _(pe):
            pe.wait_ge(s["wsum_done"], ONE + 3)
            pe.wait_ge(s["consts"], ONE + 3)
            pe.matmul(ps_x[:, 0:3], count_w[:], wsum[:], start=True, stop=True).then_inc(s["wtot_done"], 1)
            pe.wait_ge(s["wq_done"], ONE + 3)
            pe.wait_ge(s["wm_done"], ONE + 1)

            def turn_x(n, u):
                pe.wait_ge(s["x_copied"], ONE + n + 1)
                pe.wait_ge(s["xr_done"], ONE + n)
                pe.wait_ge(s["xmax"], ONE + n)
                for c in range(C):
                    mm = pe.transpose(ps_x[:, c * TT:(c + 1) * TT], xc[:, u, c, :], identf[:])
                mm.then_inc(s["x_turned"], 1)

            def turn_xq(n):
                pe.wait_ge(s["xq_done"], ONE + n + 1)
                pe.wait_ge(s["xqT_done"], ONE + n)
                for c in range(C):
                    mm = pe.transpose(ps_q[:, c, :], xq[:, c * TT:(c + 1) * TT], identb[:])
                mm.then_inc(s["xq_turned"], 1)

            def gate_up(n, u):
                pe.wait_ge(s["xqT_done"], ONE + n + 1)
                pe.wait_ge(s["h_done"], ONE + n)
                pe.wait_ge(s["silu_done"], ONE + 2 * n)
                for bank, w in ((ps_g, wq[0]), (ps_u, wq[1])):
                    for f in range(2):
                        for c in range(C):
                            mm = pe.matmul(bank[f][:], xqT[:, u, c, :], w[:, c * INNER + f * HALF:c * INNER + (f + 1) * HALF],
                                           start=c == 0, stop=c == C - 1)
                        mm.then_inc(s["gu_done"], 1)

            def turn_hq(n):
                pe.wait_ge(s["hq_done"], ONE + n + 1)
                pe.wait_ge(s["hqT_done"], ONE + n)
                for c in range(CI):
                    mm = pe.transpose(ps_h[:, c, :], hq[:, c * TT:(c + 1) * TT], identb[:])
                mm.then_inc(s["h_turned"], 1)

            def down(n):
                pe.wait_ge(s["hqT_done"], ONE + n + 1)
                pe.wait_ge(s["o_done"], ONE + n)
                pe.wait_ge(s["added"], ONE + n)
                for c in range(CI):
                    mm = pe.matmul(ps_o[:, 0, :], hqT[:, c, :], wq[2][:, c * D:(c + 1) * D], start=c == 0, stop=c == CI - 1)
                mm.then_inc(s["down_done"], 1)

            def turn_o(n):
                pe.wait_ge(s["o_done"], ONE + n + 1)
                for c in range(C):
                    mm = pe.transpose(ps_o[:, 1, c * TT:(c + 1) * TT], o[:, c * TT:(c + 1) * TT], identf[:])
                mm.then_inc(s["o_turned"], 1)

            def first(n, u):
                turn_x(n, u)
                turn_xq(n)

            def step(n, u):
                first(n + 1, 1 - u)
                turn_hq(n)
                down(n)
                gate_up(n + 1, 1 - u)
                turn_o(n)

            first(0, 0)
            gate_up(0, 0)
            with pe.Fori(0, N // 2 - 1) as i:
                step(2 * i, 0)
                step(2 * i + 1, 1)
            step(N - 2, 0)
            turn_hq(N - 1)
            down(N - 1)
            turn_o(N - 1)

        @block.scalar
        def _(act):
            for k in range(3):
                act.wait_ge(s["here"], ONE + 16 * 4)
                if k:
                    act.wait_ge(s["wsum_done"], ONE + k)
                act.activation(wabs[:], wf[k][:], ACT.Abs, accum_out=wsum[:, k:k + 1]).then_inc(s["wsum_done"], 1)
            act.wait_ge(s["consts"], ONE + 4)

            def copy_x(n, u):
                act.wait_ge(s["x_turned"], ONE + n)
                act.copy(xc[:, u, :, :], xf[:, :, cols(n)]).then_inc(s["x_copied"], 1)

            def round_x(n, u):
                act.wait_ge(s["xstep"], ONE + 5 * n + 5)
                act.wait_ge(s["xq_done"], ONE + n)
                act.activation(xr[:], ps_x[:], ACT.Identity, bias=magic[:], scale=xm[:, u, 3:4]).then_inc(s["xr_done"], 1)

            def copy_xq(n, u):
                act.wait_ge(s["xq_turned"], ONE + n + 1)
                act.copy(xqT[:, u, :, :], ps_q[:]).then_inc(s["xqT_done"], 1)

            def silu(n, u):
                act.wait_ge(s["h_done"], ONE + n)
                for f in range(2):
                    act.wait_ge(s["gu_done"], ONE + 4 * n + f + 1)
                    act.activation(sg[:, f * HALF:(f + 1) * HALF], ps_g[f][:], ACT.Silu, scale=xm[:, u, 4:5]) \
                        .then_inc(s["silu_done"], 1)

            def round_h(n, u):
                act.wait_ge(s["hstep"], ONE + 4 * n + 4)
                act.wait_ge(s["hq_done"], ONE + n)
                act.activation(hr[:], h[:], ACT.Identity, bias=magic[:], scale=hm[:, u, 3:4]).then_inc(s["hr_done"], 1)

            def copy_hq(n):
                act.wait_ge(s["h_turned"], ONE + n + 1)
                act.wait_ge(s["down_done"], ONE + n)
                act.copy(hqT[:], ps_h[:]).then_inc(s["hqT_done"], 1)

            def scale_o(n, u):
                act.wait_ge(s["down_done"], ONE + n + 1)
                act.wait_ge(s["o_turned"], ONE + n)
                act.activation(o[:], ps_o[:, 0, :], ACT.Copy, scale=hm[:, u, 4:5]).then_inc(s["o_done"], 1)

            def first(n, u):
                copy_x(n, u)
                round_x(n, u)
                copy_xq(n, u)

            def step(n, u):
                first(n + 1, 1 - u)
                round_h(n, u)
                copy_hq(n)
                silu(n + 1, 1 - u)
                scale_o(n, u)

            first(0, 0)
            silu(0, 0)
            with act.Fori(0, N // 2 - 1) as i:
                step(2 * i, 0)
                step(2 * i + 1, 1)
            step(N - 2, 0)
            round_h(N - 1, 1)
            copy_hq(N - 1)
            scale_o(N - 1, 1)

        @block.gpsimd
        def _(pool):
            pool.memset(count_w[:], 1.0 / (INNER * D)).then_inc(s["consts"], 1)
            pool.memset(magic[:], MAGIC).then_inc(s["consts"], 1)
            pool.wait_ge(s["here"], ONE + 16 * 4)
            pool.tensor_copy(identb[:], identf[:]).then_inc(s["consts"], 1)

            def quant_h(n):
                pool.wait_ge(s["hr_done"], ONE + n + 1)
                pool.wait_ge(s["h_turned"], ONE + n)
                pool.sem_inc(s["hq_turn"], 1)
                pool.tensor_scalar(hq[:], hr[:], -MAGIC, 127.0, ALU.add, ALU.min).then_inc(s["hq_done"], 1)
            with pool.Fori(0, N) as n:
                quant_h(n)

        @block.vector
        def _(dve):
            dve.wait_ge(s["wtot_done"], ONE + 1)
            dve.tensor_scalar(wmean[:], ps_x[:, 0:3], 1e-5, None, ALU.max).then_inc(s["wm_done"], 1)
            dve.wait_ge(s["wm_done"], ONE + 1)
            dve.reciprocal(wscale[:], wmean[:]).then_inc(s["wstep"], 1)
            dve.tensor_scalar(wmean127[:], wmean[:], 1.0 / 127.0, None, ALU.mult).then_inc(s["wstep"], 1)
            dve.wait_ge(s["wstep"], ONE + 2)
            for k in range(3):
                if k:
                    dve.wait_ge(s["wq_done"], ONE + k)
                dve.tensor_scalar(wr[:], wf[k][:], wscale[:, k:k + 1], MAGIC, ALU.mult, ALU.add).then_inc(s["wstep"], 1)
                dve.wait_ge(s["wstep"], ONE + 3 + 2 * k)
                dve.tensor_scalar(wr[:], wr[:], -MAGIC, 1.0, ALU.add, ALU.min).then_inc(s["wstep"], 1)
                dve.wait_ge(s["wstep"], ONE + 4 + 2 * k)
                dve.tensor_scalar(wq[k][:], wr[:], -1.0, None, ALU.max).then_inc(s["wq_done"], 1)
            dve.memset(xm[:], 1.0).then_inc(s["consts"], 1)
            dve.wait_ge(s["consts"], ONE + 4)

            def scales(n, u, m, mx, step, outs):
                k = 3 + len(outs)
                def next_step(a, c):
                    a.then_inc(step, 1)
                    dve.wait_ge(step, ONE + k * n + c)
                next_step(dve.tensor_scalar(m[:, u, 1:2], m[:, u, 0:1], 1e-5, None, ALU.max), 1)
                next_step(dve.reciprocal(m[:, u, 2:3], m[:, u, 1:2]), 2)
                dve.tensor_scalar(m[:, u, 3:4], m[:, u, 2:3], 127.0, None, ALU.mult).then_inc(step, 1)
                for i, w in enumerate(outs):
                    dve.tensor_scalar(m[:, u, 4 + i:5 + i], m[:, u, 1:2], wmean127[:, w:w + 1], None, ALU.mult).then_inc(step, 1)

            def quant_x(n, u):
                dve.wait_ge(s["x_turned"], ONE + n + 1)
                dve.tensor_reduce(xm[:, u, 0:1], ps_x[:], AX.X, ALU.max, apply_absolute_value=True).then_inc(s["xmax"], 1)
                dve.wait_ge(s["xmax"], ONE + n + 1)
                scales(n, u, xm, s["xmax"], s["xstep"], (0, 1))
                dve.wait_ge(s["xr_done"], ONE + n + 1)
                dve.wait_ge(s["xq_turned"], ONE + n)
                dve.tensor_scalar(xq[:], xr[:], -MAGIC, 127.0, ALU.add, ALU.min).then_inc(s["xq_done"], 1)

            def gated(n, u):
                dve.wait_ge(s["hr_done"], ONE + n)
                dve.wait_ge(s["hmax"], ONE + n)
                dve.wait_ge(s["xstep"], ONE + 5 * n + 5)
                for f in range(2):
                    dve.wait_ge(s["gu_done"], ONE + 4 * n + 3 + f)
                    dve.wait_ge(s["silu_done"], ONE + 2 * n + f + 1)
                    half = slice(f * HALF, (f + 1) * HALF)
                    mm = dve.scalar_tensor_tensor(out=h[:, half], in0=ps_u[f][:], scalar=xm[:, u, 5:6], in1=sg[:, half],
                                                  op0=ALU.mult, op1=ALU.mult)
                    mm.then_inc(s["h_done" if f else "h_half"], 1)
                dve.wait_ge(s["h_half"], ONE + n + 1)
                dve.wait_ge(s["h_done"], ONE + n + 1)
                dve.tensor_reduce(hm[:, u, 0:1], h[:], AX.X, ALU.max, apply_absolute_value=True).then_inc(s["hmax"], 1)
                dve.wait_ge(s["hmax"], ONE + n + 1)
                scales(n, u, hm, s["hmax"], s["hstep"], (2,))

            def add(n):
                dve.wait_ge(s["o_turned"], ONE + n + 1)
                dve.tensor_tensor(xf[:, :, cols(n)], xf[:, :, cols(n)],
                                  ps_o[:, 1, :].rearrange("p (c t) -> p c t", c=C), ALU.add).then_inc(s["added"], 1)

            def step(n, u):
                quant_x(n + 1, 1 - u)
                gated(n + 1, 1 - u)
                add(n)

            quant_x(0, 0)
            gated(0, 0)
            with dve.Fori(0, N // 2 - 1) as i:
                step(2 * i, 0)
                step(2 * i + 1, 1)
            step(N - 2, 0)
            add(N - 1)
    st.close()


def sparse_attention(nc, xf, io, eps):
    QT, NQ, PAD = 128, S // 128, 64
    NB, SEL = S // 16, 16
    CS, WK = NB + SEL, PAD + QT
    KEYS = CS + WK
    G = 4
    UQ = 4
    NG = H // G
    VA = DH + 1
    NEG = -1e30
    st = Stage(nc, "nsa")
    names_w = ("wq", "wqs", "wk", "wks", "wv", "wo")
    w = {n: st.sb(n, [P, C, D]) for n in names_w}
    wg, bg = st.sb("wg", [P, C, 3]), st.sb("bg", [P, 3])
    bo = st.sb("bo", [P, C])
    cos, sin = st.sb("cos", [P, S]), st.sb("sin", [P, S])
    wkc, wvc = st.sb("wk_comp", [P, 16]), st.sb("wv_comp", [P, 1])
    pe, peT = st.sb("pe", [16, D]), st.sb("peT", [P, C, 16])
    parity = st.sb("head_parity", [P, 2])
    mask_f = st.sb("mask_float", [P, KEYS])
    mask = st.sb("mask", [P, NQ, KEYS], BF16)
    ident, identb = st.sb("identity", [P, P]), st.sb("identity_b", [P, P], BF16)
    block_of = st.sb("block_of", [P, NQ, NB])
    comp_w = st.sb("comp_w", [P, NQ, NB])
    pe_w = st.sb("pe_w", [16, NB])
    token_no = st.sb("token_number", [P, NQ])
    offset = st.sb("sel_offset", [P, SEL])
    ones = st.sb("ones", [1, P])
    xb = st.sb("x_row", [P, C, PAD + S])
    t1, t2 = st.sb("rope_cos", [P, 2, W]), st.sb("rope_sin", [P, 2, W])
    qT = st.sb("qT", [P, C, S])
    kr = st.sb("kT", [P, C, S])
    keo = st.sb("k_even_odd", [P, C, 2, PAD + S])
    kc = st.sb("k_comp_sel", [P, C, 2, CS])
    kcomp = st.sb("k_comp", [P, C, CS])
    kw_prod = st.sb("k_weighted", [P, S])
    pe_k = st.sb("pe_weighted", [P, C, 16])
    pe_sum = st.sb("pe_sum", [P, C])
    ktok = st.sb("k_token", [P, NQ, D])
    v = st.sb("v", [P, NQ, H, VA])
    vprev = st.sb("v_before", [PAD, NQ, H, VA])
    vcs = st.sb("v_comp_sel", [CS, H, 2 * VA])
    qsum = st.sb("q_sum", [P, C])
    imp = st.sb("importance", [1, NB])
    top = st.sb("top_values", [1, 8])
    top_i = st.sb("top_index", [1, 8], mybir.dt.uint32)
    pos0 = st.sb("top_start", [1, 2])
    pos = st.sb("sel_position", [P, SEL])
    sel = st.sb("sel_onehot", [P, NQ, SEL])
    gl, ge = st.sb("gate_logit", [P, NQ, 3]), st.sb("gate_exp", [P, NQ, 3])
    gmx, gsum, ginv = (st.sb(n, [P, NQ]) for n in ("gate_top", "gate_sum", "gate_inverse"))
    gate = st.sb("gate", [P, NQ, 3])
    q_t = st.sb("q_tile", [P, 2, C, QT])
    k_t = st.sb("k_tile", [P, 2, C * 2, WK])
    v_t, vp_t = st.sb("v_tile", [P, 2, H, VA]), st.sb("v_before_tile", [PAD, 2, H, VA])
    m_t = st.sb("mask_tile", [P, 2, KEYS], BF16)
    mx = st.sb("top", [P, 2, 3, G])
    prob = st.sb("prob", [P, 2, G * KEYS])
    pT = st.sb("probT", [P, 2, 3, G * QT])
    den, rden, rg = (st.sb(n, [P, H, 3]) for n in ("sum", "sum_inverse", "branch_weight"))
    wo3 = st.sb("weighted", [P, H, 3, DH])
    att = st.sb("attention", [P, D])
    attT = st.sb("attentionT", [P, C, QT])
    S_ = st.ps("scores", [P, 3, W])
    T_ = st.ps("turned", [P, 3, W])
    O_ = st.ps("out", [P, 2, W])
    loads = ([(w[n][:], "nsa_" + n) for n in names_w] + [(wg[:], "nsa_wg"), (bg[:], "nsa_bg"), (bo[:], "nsa_bo"), (cos[:], "nsa_cos"),
             (sin[:], "nsa_sin"), (wkc[:], "nsa_wk_comp"), (wvc[:], "nsa_wv_comp"), (pe[:], "nsa_pe"), (peT[:], "nsa_peT"),
             (parity[:], "nsa_parity"), (ident[:], "identity"), (block_of[:], "nsa_block_of"), (token_no[:], "nsa_token"),
             (offset[:], "nsa_offset")])
    names = ("here mask_here mask_cast consts cw pew x_copied rope_mm ropec ropes roped k_split v_mm v_moved kc_w kc_red kc_added "
             "cv_mm cv_moved qsum_done imp_mm imp_moved top_done topi_done posf pos_mm pos_done sel_done mask_done ktok_mm ktok_moved "
             "selk_mm selk_moved kc_split g_mm g_logit g_top g_shift g_exp g_sum g_inv gate_done vcs_mm vcs_moved tile_copied scores_done "
             "max_done clamp_done shifted exp_done turned pT_moved pv_done den_done rden_done rg_done weighted att_done att_turned "
             "attT_moved wo_done x_added peT_w pe_sum pew0 ones_set carrier").split()
    s = {n: st.sem(n) for n in names}

    def head(g, j):
        return j // 2, 8 * (j // 2) + 2 * g + j % 2, j % 2

    st.start_counters()
    AHEAD = ONE + NG

    with nc.Block() as block:
        @block.sync
        def _(sp):
            for dst, src in loads:
                sp.dma_start(dst, io[src]).then_inc(s["here"], 16)
            with sp.Fori(0, NQ) as i:
                sp.wait_ge(s["mask_cast"], ONE + i)
                sp.dma_start(mask_f[:], io["nsa_mask"][:, i, :]).then_inc(s["mask_here"], 16)

        @block.tensor
        def _(pe_):
            pe_.wait_ge(s["here"], ONE + 16 * len(loads))
            pe_.wait_ge(s["consts"], ONE + 8)
            pe_.wait_ge(s["cw"], ONE + NQ)
            pe_.wait_ge(s["pew"], ONE + 1)
            with pe_.Fori(0, B) as b:
                pe_.wait_ge(s["x_copied"], ONE + b + 1)
                for r in range(8):
                    which, m, t = r // 4, (r // 2) % 2, r % 2
                    if r >= 2:
                        pe_.wait_ge(s["ropes"], ONE + b * 8 + r - 1)
                    for k, name in enumerate((("wq", "wqs"), ("wk", "wks"))[which]):
                        for c in range(C):
                            mm = pe_.matmul((S_ if r % 2 else T_)[:, k, :], w[name][:, c, m * P:(m + 1) * P],
                                            xb[:, c, PAD + t * W:PAD + (t + 1) * W], start=c == 0, stop=c == C - 1)
                    mm.then_inc(s["rope_mm"], 1)
                for i in range(NQ):
                    if i >= 2:
                        pe_.wait_ge(s["v_moved"], ONE + b * 2 * NQ + 2 * (i - 1))
                    for c in range(C):
                        mm = pe_.matmul(O_[:, i % 2, 0:D], xb[:, c, PAD + i * QT:PAD + (i + 1) * QT], w["wv"][:, c, :],
                                        start=c == 0, stop=c == C - 1)
                    mm.then_inc(s["v_mm"], 1)
                    for c in range(C):
                        mm = pe_.matmul(O_[0:PAD, i % 2, D:2 * D], xb[:, c, i * QT:i * QT + PAD], w["wv"][:, c, :],
                                        start=c == 0, stop=c == C - 1)
                    mm.then_inc(s["v_mm"], 1)
                pe_.wait_ge(s["ropes"], ONE + b * 8 + 8)
                for i in range(NQ):
                    for c in range(C):
                        mm = pe_.matmul(S_[:, 2, 3 * i:3 * i + 3], xb[:, c, PAD + i * QT:PAD + (i + 1) * QT], wg[:, c, :],
                                        start=c == 0, stop=c == C - 1)
                mm.then_inc(s["g_mm"], 1)
                pe_.wait_ge(s["qsum_done"], ONE + b * C + C)
                pe_.wait_ge(s["kc_added"], ONE + b * C + C)
                for c in range(C):
                    mm = pe_.matmul(S_[0:1, 0, 0:NB], qsum[:, c:c + 1], kcomp[:, c, 0:NB], start=c == 0, stop=c == C - 1)
                mm.then_inc(s["imp_mm"], 1)
                pe_.wait_ge(s["roped"], ONE + b * 8 + 8)
                for i in range(NQ):
                    if i >= 2:
                        pe_.wait_ge(s["ktok_moved"], ONE + b * NQ + i - 1)
                    for c in range(C):
                        mm = pe_.transpose(T_[:, i % 2, c * P:(c + 1) * P], kr[:, c, i * QT:(i + 1) * QT], ident[:])
                    mm.then_inc(s["ktok_mm"], 1)
                pe_.wait_ge(s["posf"], ONE + b + 1)
                pe_.matmul(S_[:, 1, 0:2], ones[:], pos0[:], start=True, stop=True).then_inc(s["pos_mm"], 1)
                pe_.wait_ge(s["v_moved"], ONE + (b + 1) * 2 * NQ)
                for i in range(NQ):
                    pe_.matmul(O_[0:NB, 0, 0:D], comp_w[:, i, :], v[:, i, :, 0:DH], start=i == 0, stop=False)
                pe_.matmul(O_[0:NB, 0, 0:D], pe_w[:], pe[:], start=False, stop=True).then_inc(s["cv_mm"], 1)
                pe_.wait_ge(s["sel_done"], ONE + b * NQ + NQ)
                pe_.wait_ge(s["ktok_moved"], ONE + (b + 1) * NQ)
                for i in range(NQ):
                    mm = pe_.matmul(O_[NB:CS, 1, 0:D], sel[:, i, :], v[:, i, :, 0:DH], start=i == 0, stop=i == NQ - 1)
                mm.then_inc(s["cv_mm"], 1)
                for c in range(C):
                    for i in range(NQ):
                        mm = pe_.matmul(T_[:, 2, c * SEL:(c + 1) * SEL], ktok[:, i, c * P:(c + 1) * P], sel[:, i, :],
                                        start=i == 0, stop=i == NQ - 1)
                mm.then_inc(s["selk_mm"], 1)
                pe_.wait_ge(s["kc_split"], ONE + 2 * C * (b + 1))
                pe_.wait_ge(s["vcs_moved"], ONE + 2 * (b + 1))
                pe_.wait_ge(s["mask_done"], ONE + b * NQ + NQ)
                pe_.wait_ge(s["gate_done"], ONE + b + 1)

                pe_.sem_inc(s["carrier"], 1)
                with pe_.Fori(0, NQ // UQ) as i:
                    n0 = b * NQ + i * UQ
                    k0 = n0 * NG

                    def scores(k):
                        t, g, u = k // NG, k % NG, k // NG % 2
                        if g == 0:
                            pe_.wait_ge(s["tile_copied"], ONE + (n0 + t) * 5 + 5)
                        pe_.wait_ge(s["shifted"], ONE + 3 * (k0 + k))
                        for j in range(G):
                            c, _, par = head(g, j)
                            p0 = 32 * g
                            qh = q_t[p0:p0 + 32, u, c, :]
                            cs_o, w_o = slice(j * CS, (j + 1) * CS), slice((j % 2) * WK, (j % 2 + 1) * WK)
                            pe_.matmul(S_[:, 0, cs_o], qh, kc[p0:p0 + 32, c, par, :], start=True, stop=False)
                            pe_.matmul(S_[:, 0, cs_o], identb[:], m_t[:, u, 0:CS], start=False, stop=True)
                            pe_.matmul(S_[:, 1 + j // 2, w_o], qh, k_t[p0:p0 + 32, u, 2 * c + par, :], start=True, stop=False)
                            mm = pe_.matmul(S_[:, 1 + j // 2, w_o], identb[:], m_t[:, u, CS:KEYS], start=False, stop=True)
                        mm.then_inc(s["scores_done"], 1)

                    def turn(k):
                        u = k % 2
                        pe_.wait_ge(s["exp_done"], ONE + k0 + k + 1)
                        pe_.wait_ge(s["pT_moved"], ONE + 3 * (k0 + k))
                        for j in range(G):
                            pe_.transpose(T_[0:CS, 0, j * QT:(j + 1) * QT], prob[:, u, j * CS:(j + 1) * CS], ident[:])
                        for part, (a, z) in enumerate(((0, PAD), (PAD, WK))):
                            for j in range(G):
                                o = G * CS + j * WK
                                mm = pe_.transpose(T_[0:z - a, 1 + part, j * QT:(j + 1) * QT], prob[:, u, o + a:o + z], ident[:])
                        mm.then_inc(s["turned"], 1)

                    def weigh(k):
                        t, g, u = k // NG, k % NG, k // NG % 2
                        pe_.wait_ge(s["pT_moved"], ONE + 3 * (k0 + k) + 3)
                        if g == 0:
                            pe_.wait_ge(s["weighted"], ONE + (n0 + t) * 2)
                            pe_.wait_ge(s["den_done"], ONE + n0 + t)
                        for j in range(G):
                            _, h, _ = head(g, j)
                            o = (h % 8) * 3 * VA
                            q = slice(j * QT, (j + 1) * QT)
                            bank = O_[:, h // 8, :]
                            pe_.matmul(bank[:, o:o + 2 * VA], pT[0:CS, k % 2, 0, q], vcs[:, h, :], start=True, stop=True)
                            pe_.matmul(bank[:, o + 2 * VA:o + 3 * VA], pT[0:PAD, k % 2, 1, q], vp_t[:, u, h, :], start=True, stop=False)
                            mm = pe_.matmul(bank[:, o + 2 * VA:o + 3 * VA], pT[:, k % 2, 2, q], v_t[:, u, h, :], start=False, stop=True)
                        mm.then_inc(s["pv_done"], 1)

                    def turn_out(t, k):
                        pe_.wait_ge(s["att_done"], ONE + n0 + t + 1)
                        pe_.wait_ge(s["pT_moved"], ONE + 3 * (k0 + k) + 3)
                        for c in range(C):
                            mm = pe_.transpose(T_[:, 0, c * QT:(c + 1) * QT], att[:, c * P:(c + 1) * P], ident[:])
                        mm.then_inc(s["att_turned"], 1)

                    def through_wo(t):
                        pe_.wait_ge(s["attT_moved"], ONE + n0 + t + 1)
                        for m in range(C):
                            for c in range(C):
                                mm = pe_.matmul(T_[:, 1, m * QT:(m + 1) * QT], w["wo"][:, c, m * P:(m + 1) * P], attT[:, c, :],
                                                start=c == 0, stop=c == C - 1)
                        mm.then_inc(s["wo_done"], 1)

                    last = UQ * NG - 1
                    for k in range(last + 5):
                        if k <= last:
                            scores(k)
                        if k >= 7 and (k - 7) % NG == 0:
                            through_wo((k - 7) // NG)
                        if 2 <= k <= last + 2:
                            weigh(k - 2)
                        if 1 <= k <= last + 1:
                            if k >= 7 and (k - 7) % NG == 0:
                                pe_.wait_ge(s["x_added"], ONE + C * (n0 + (k - 7) // NG + 1))
                            turn(k - 1)
                        if k >= 6 and (k - 6) % NG == 0:
                            turn_out((k - 6) // NG, min(k - 1, last))
                    pe_.wait_ge(s["x_added"], ONE + C * (n0 + UQ))

        @block.scalar
        def _(act):
            act.wait_ge(s["here"], ONE + 16 * len(loads))
            act.wait_ge(s["consts"], ONE + 8)
            with act.Fori(0, B) as b:
                act.wait_ge(s["x_added"], ONE + b * C * NQ)
                act.copy(xb[:, :, PAD:], xf[:, :, bass.ts(b, S)]).then_inc(s["x_copied"], 1)
                for r in range(4):
                    m, t = r // 2, r % 2
                    x = slice(t * W, (t + 1) * W)
                    act.wait_ge(s["roped"], ONE + b * 8 + 5 + r)
                    for par in range(2):
                        act.activation(keo[:, m, par, PAD + t * W:PAD + (t + 1) * W], kr[:, m, x], ACT.Copy,
                                       scale=parity[:, par:par + 1]).then_inc(s["k_split"], 1)
                for i in range(NQ):
                    act.wait_ge(s["v_mm"], ONE + b * 2 * NQ + 2 * i + 2)
                    act.copy(v[:, i, :, 0:DH], O_[:, i % 2, 0:D].rearrange("p (h d) -> p h d", h=H)).then_inc(s["v_moved"], 1)
                    act.copy(vprev[:, i, :, 0:DH], O_[0:PAD, i % 2, D:2 * D].rearrange("p (h d) -> p h d", h=H)).then_inc(s["v_moved"], 1)
                act.wait_ge(s["imp_mm"], ONE + b + 1)
                act.copy(imp[:], S_[0:1, 0, 0:NB]).then_inc(s["imp_moved"], 1)
                for i in range(NQ):
                    act.wait_ge(s["ktok_mm"], ONE + b * NQ + i + 1)
                    act.copy(ktok[:, i, :], T_[:, i % 2, 0:D]).then_inc(s["ktok_moved"], 1)
                act.wait_ge(s["g_shift"], ONE + b + 1)
                act.activation(ge[:], gl[:], ACT.Exp).then_inc(s["g_exp"], 1)
                act.wait_ge(s["cv_mm"], ONE + 2 * b + 1)
                act.copy(vcs[0:NB, :, 0:DH], O_[0:NB, 0, 0:D].rearrange("p (h d) -> p h d", h=H)).then_inc(s["vcs_moved"], 1)
                act.wait_ge(s["cv_mm"], ONE + 2 * b + 2)
                act.copy(vcs[NB:CS, :, VA:VA + DH], O_[NB:CS, 1, 0:D].rearrange("p (h d) -> p h d", h=H)).then_inc(s["vcs_moved"], 1)
                act.wait_ge(s["selk_mm"], ONE + b + 1)
                act.copy(kcomp[:, :, NB:CS], T_[:, 2, 0:C * SEL].rearrange("p (c m) -> p c m", c=C)).then_inc(s["selk_moved"], 1)
                act.wait_ge(s["selk_moved"], ONE + b + 1)
                act.wait_ge(s["kc_added"], ONE + (b + 1) * C)
                for c in range(C):
                    for par in range(2):
                        act.activation(kc[:, c, par, :], kcomp[:, c, :], ACT.Copy, scale=parity[:, par:par + 1]).then_inc(s["kc_split"], 1)
                act.sem_inc(s["carrier"], 1)
                with act.Fori(0, NQ // UQ) as i:
                    n0 = b * NQ + i * UQ
                    k0 = n0 * NG

                    def exps(k):
                        act.wait_ge(s["shifted"], ONE + 3 * (k0 + k) + 3)
                        act.activation(prob[:, k % 2, :], prob[:, k % 2, :], ACT.Exp, scale=float(DH) ** -0.5).then_inc(s["exp_done"], 1)

                    def move(k):
                        act.wait_ge(s["turned"], ONE + k0 + k + 1)
                        act.wait_ge(s["pv_done"], AHEAD + k0 + max(k - 1, 0))
                        act.copy(pT[0:CS, k % 2, 0, :], T_[0:CS, 0, :]).then_inc(s["pT_moved"], 1)
                        act.copy(pT[0:PAD, k % 2, 1, :], T_[0:PAD, 1, :]).then_inc(s["pT_moved"], 1)
                        act.copy(pT[:, k % 2, 2, :], T_[:, 2, :]).then_inc(s["pT_moved"], 1)

                    def move_out(t):
                        act.wait_ge(s["att_turned"], ONE + n0 + t + 1)
                        act.copy(attT[:], T_[:, 0, 0:C * QT].rearrange("p (c q) -> p c q", c=C)).then_inc(s["attT_moved"], 1)

                    last = UQ * NG - 1
                    for k in range(last + 4):
                        if k <= last:
                            exps(k)
                        if 1 <= k <= last + 1:
                            move(k - 1)
                        if k >= 6 and (k - 6) % NG == 0:
                            move_out((k - 6) // NG)

        @block.gpsimd
        def _(pool):
            pool.sem_inc(s["pv_done"], AHEAD - ONE)
            pool.memset(v[:, :, :, DH:VA], 1.0).then_inc(s["consts"], 1)
            pool.memset(vprev[:, :, :, DH:VA], 1.0).then_inc(s["consts"], 1)
            pool.memset(vcs[:], 0.0).then_inc(s["consts"], 1)
            pool.memset(xb[:, :, 0:PAD], 0.0).then_inc(s["consts"], 1)
            pool.memset(keo[:, :, :, 0:PAD], 0.0).then_inc(s["consts"], 1)
            pool.wait_ge(s["consts"], ONE + 5)
            pool.memset(vcs[0:NB, :, DH:VA], 1.0).then_inc(s["consts"], 1)
            pool.wait_ge(s["consts"], ONE + 6)
            pool.memset(vcs[NB:CS, :, VA + DH:2 * VA], 1.0).then_inc(s["consts"], 1)
            pool.wait_ge(s["consts"], ONE + 7)
            pool.wait_ge(s["here"], ONE + 16 * len(loads))
            pool.tensor_copy(identb[:], ident[:]).then_inc(s["consts"], 1)
            with pool.Fori(0, B) as b:
                pool.wait_ge(s["k_split"], ONE + 8 * b + 8)
                pool.wait_ge(s["roped"], ONE + 8 * b + 8)
                pool.wait_ge(s["v_moved"], ONE + 2 * NQ * (b + 1))
                pool.wait_ge(s["mask_done"], ONE + b * NQ + NQ)
                pool.wait_ge(s["gate_done"], ONE + b + 1)
                pool.sem_inc(s["carrier"], 1)
                with pool.Fori(0, NQ // 2) as i:
                    for u in range(2):
                        t = i * 2 + u
                        n = b * NQ + t
                        pool.wait_ge(s["pv_done"], AHEAD + n * NG - NG)
                        pool.sem_inc(s["carrier"], 1)
                        pool.tensor_copy(q_t[:, u], qT[:, :, bass.ts(t, QT)]).then_inc(s["tile_copied"], 1)
                        pool.tensor_copy(k_t[:, u], keo[:].rearrange("p c e k -> p (c e) k")[:, :, bass.ds(t * QT, WK)]).then_inc(s["tile_copied"], 1)
                        pool.tensor_copy(v_t[:, u], v[:, bass.ds(t, 1), :, :].rearrange("p o h d -> p (o h) d")).then_inc(s["tile_copied"], 1)
                        pool.tensor_copy(vp_t[:, u], vprev[:, bass.ds(t, 1), :, :].rearrange("p o h d -> p (o h) d")).then_inc(s["tile_copied"], 1)
                        pool.tensor_copy(m_t[:, u], mask[:, bass.ds(t, 1), :].rearrange("p o k -> p (o k)")).then_inc(s["tile_copied"], 1)

        @block.vector
        def _(dve):
            dve.memset(ones[:], 1.0).then_inc(s["ones_set"], 1)
            dve.wait_ge(s["ones_set"], ONE + 1)
            dve.wait_ge(s["here"], ONE + 16 * len(loads))
            with dve.Fori(0, NQ) as i:
                dve.wait_ge(s["mask_here"], ONE + 16 * i + 16)
                dve.tensor_copy(mask[:, bass.ds(i, 1), :].rearrange("p o k -> p (o k)"), mask_f[:]).then_inc(s["mask_cast"], 1)
            dve.tensor_scalar(comp_w[:].rearrange("p i n -> p (i n)"), block_of[:].rearrange("p i n -> p (i n)"), wvc[:, 0:1], None,
                              ALU.mult).then_inc(s["cw"], NQ)
            dve.wait_ge(s["cw"], ONE + NQ)
            dve.memset(pe_w[:], 1.0).then_inc(s["pew0"], 1)
            dve.wait_ge(s["pew0"], ONE + 1)
            dve.tensor_scalar(pe_w[:], pe_w[:], wvc[0:16, 0:1], None, ALU.mult).then_inc(s["pew"], 1)
            dve.tensor_tensor(pe_k[:], peT[:], wkc[:].unsqueeze(1).to_broadcast([P, C, 16]), ALU.mult).then_inc(s["peT_w"], 1)
            dve.wait_ge(s["peT_w"], ONE + 1)
            dve.tensor_reduce(pe_sum[:], pe_k[:], AX.X, ALU.add).then_inc(s["pe_sum"], 1)
            dve.wait_ge(s["pe_sum"], ONE + 1)
            dve.wait_ge(s["mask_cast"], ONE + NQ)
            with dve.Fori(0, B) as b:
                for r in range(8):
                    which, m, t = r // 4, (r // 2) % 2, r % 2
                    x = slice(t * W, (t + 1) * W)
                    src = S_ if r % 2 else T_
                    dve.wait_ge(s["rope_mm"], ONE + b * 8 + r + 1)
                    dve.wait_ge(s["roped"], ONE + b * 8 + max(r - 1, 0))
                    dve.tensor_tensor(t1[:, r % 2, :], src[:, 0, :], cos[:, x], ALU.mult).then_inc(s["ropec"], 1)
                    dve.tensor_tensor(t2[:, r % 2, :], src[:, 1, :], sin[:, x], ALU.mult).then_inc(s["ropes"], 1)
                    dve.wait_ge(s["ropes"], ONE + b * 8 + r + 1)
                    dve.wait_ge(s["ropec"], ONE + b * 8 + r + 1)
                    dve.tensor_tensor((kr if which else qT)[:, m, x], t1[:, r % 2, :], t2[:, r % 2, :], ALU.add).then_inc(s["roped"], 1)
                dve.wait_ge(s["roped"], ONE + b * 8 + 8)
                dve.wait_ge(s["imp_mm"], ONE + b)
                dve.wait_ge(s["kc_split"], ONE + 2 * C * b)
                for c in range(C):
                    dve.tensor_reduce(qsum[:, c:c + 1], qT[:, c, :], AX.X, ALU.add).then_inc(s["qsum_done"], 1)
                    dve.wait_ge(s["kc_red"], ONE + b * C + c)
                    dve.tensor_tensor(kw_prod[:].rearrange("p (n k) -> p n k", k=16), kr[:, c, :].rearrange("p (n k) -> p n k", k=16),
                                      wkc[:].unsqueeze(1).to_broadcast([P, NB, 16]), ALU.mult).then_inc(s["kc_w"], 1)
                    dve.wait_ge(s["kc_w"], ONE + b * C + c + 1)
                    dve.tensor_reduce(kcomp[:, c, 0:NB], kw_prod[:].rearrange("p (n k) -> p n k", k=16), AX.X, ALU.add).then_inc(s["kc_red"], 1)
                    dve.wait_ge(s["kc_red"], ONE + b * C + c + 1)
                    dve.tensor_scalar(kcomp[:, c, 0:NB], kcomp[:, c, 0:NB], pe_sum[:, c:c + 1], None, ALU.add).then_inc(s["kc_added"], 1)
                dve.wait_ge(s["g_mm"], ONE + b + 1)
                dve.tensor_tensor(gl[:], S_[:, 2, 0:3 * NQ].rearrange("p (i g) -> p i g", g=3), bg[:].unsqueeze(1).to_broadcast([P, NQ, 3]),
                                  ALU.add).then_inc(s["g_logit"], 1)
                dve.wait_ge(s["g_logit"], ONE + b + 1)
                dve.tensor_reduce(gmx[:], gl[:], AX.X, ALU.max).then_inc(s["g_top"], 1)
                dve.wait_ge(s["g_top"], ONE + b + 1)
                dve.tensor_tensor(gl[:], gl[:], gmx[:].unsqueeze(2).to_broadcast([P, NQ, 3]), ALU.subtract).then_inc(s["g_shift"], 1)
                dve.wait_ge(s["imp_moved"], ONE + b + 1)
                dve.sem_inc(s["carrier"], 1)
                dve.max(top[:], imp[:]).then_inc(s["top_done"], 1)
                dve.wait_ge(s["top_done"], ONE + b + 1)
                dve.sem_inc(s["carrier"], 1)
                dve.max_index(top_i[:], top[:], imp[:]).then_inc(s["topi_done"], 1)
                dve.wait_ge(s["topi_done"], ONE + b + 1)
                dve.tensor_scalar(pos0[:], top_i[:, 0:2], 16.0, None, ALU.mult).then_inc(s["posf"], 1)
                dve.wait_ge(s["pos_mm"], ONE + b + 1)
                dve.tensor_tensor(pos[:].rearrange("p (a e) -> p a e", a=2), offset[:].rearrange("p (a e) -> p a e", a=2),
                                  S_[:, 1, 0:2].unsqueeze(2).to_broadcast([P, 2, SEL // 2]), ALU.add).then_inc(s["pos_done"], 1)
                dve.wait_ge(s["pos_done"], ONE + b + 1)
                for i in range(NQ):
                    dve.tensor_scalar(sel[:, i, :], pos[:], token_no[:, i:i + 1], None, ALU.is_equal).then_inc(s["sel_done"], 1)
                for i in range(NQ):
                    dve.tensor_scalar(mask[:, i, NB:CS], pos[:], token_no[:, i:i + 1], NEG, ALU.is_gt, ALU.mult).then_inc(s["mask_done"], 1)
                dve.wait_ge(s["g_exp"], ONE + b + 1)
                dve.tensor_reduce(gsum[:], ge[:], AX.X, ALU.add).then_inc(s["g_sum"], 1)
                dve.wait_ge(s["g_sum"], ONE + b + 1)
                dve.reciprocal(ginv[:], gsum[:]).then_inc(s["g_inv"], 1)
                dve.wait_ge(s["g_inv"], ONE + b + 1)
                dve.tensor_tensor(gate[:], ge[:], ginv[:].unsqueeze(2).to_broadcast([P, NQ, 3]), ALU.mult).then_inc(s["gate_done"], 1)
                dve.wait_ge(s["gate_done"], ONE + b + 1)
                dve.sem_inc(s["carrier"], 1)
                with dve.Fori(0, NQ // UQ) as i:
                    n0 = b * NQ + i * UQ
                    k0 = n0 * NG
                    o5 = O_[:, :, 0:8 * 3 * VA].rearrange("p b (h x) -> p b h x", x=VA)
                    rgf, wof = rg[:].rearrange("p h r -> p (h r)"), wo3[:].rearrange("p h r d -> p (h r) d")

                    def shift(k):
                        u = k % 2
                        dve.wait_ge(s["scores_done"], ONE + k0 + k + 1)
                        dve.wait_ge(s["shifted"], ONE + 3 * (k0 + k))
                        dve.wait_ge(s["turned"], ONE + k0 + max(k - 1, 0))
                        cs3 = S_[:, 0, 0:G * CS].rearrange("p (h k) -> p h k", h=G)
                        win4 = S_[:, 1:3, 0:2 * WK].rearrange("p b (h k) -> p b h k", h=2)
                        dve.tensor_reduce(mx[:, u, 0, :], cs3[:, :, 0:NB], AX.X, ALU.max).then_inc(s["max_done"], 1)
                        dve.tensor_reduce(mx[:, u, 1, :], cs3[:, :, NB:CS], AX.X, ALU.max).then_inc(s["max_done"], 1)
                        dve.tensor_reduce(mx[:, u, 2, :].rearrange("p (b h) -> p b h", b=2), win4, AX.X, ALU.max).then_inc(s["max_done"], 1)
                        dve.wait_ge(s["max_done"], ONE + 3 * (k0 + k) + 3)
                        dve.tensor_scalar(mx[:, u, :, :], mx[:, u, :, :], NEG / 10, None, ALU.max).then_inc(s["clamp_done"], 1)
                        dve.wait_ge(s["clamp_done"], ONE + k0 + k + 1)
                        pcs = prob[:, u, 0:G * CS].rearrange("p (h k) -> p h k", h=G)
                        pwin = prob[:, u, G * CS:].rearrange("p (b h k) -> p b h k", b=2, h=2)
                        dve.tensor_tensor(pcs[:, :, 0:NB], cs3[:, :, 0:NB], mx[:, u, 0, :].unsqueeze(2).to_broadcast([P, G, NB]),
                                          ALU.subtract).then_inc(s["shifted"], 1)
                        dve.tensor_tensor(pcs[:, :, NB:CS], cs3[:, :, NB:CS], mx[:, u, 1, :].unsqueeze(2).to_broadcast([P, G, SEL]),
                                          ALU.subtract).then_inc(s["shifted"], 1)
                        dve.tensor_tensor(pwin, win4, mx[:, u, 2, :].rearrange("p (b h) -> p b h", b=2).unsqueeze(3).to_broadcast([P, 2, 2, WK]),
                                          ALU.subtract).then_inc(s["shifted"], 1)

                    def combine(t):
                        n = n0 + t
                        dve.wait_ge(s["pv_done"], AHEAD + (n + 1) * NG)
                        dve.tensor_scalar(den[:].rearrange("p (b h) r -> p b (h r)", b=2), o5[:, :, :, DH], 1e-30, None, ALU.max).then_inc(s["den_done"], 1)
                        dve.wait_ge(s["den_done"], ONE + n + 1)
                        dve.reciprocal(rden[:], den[:]).then_inc(s["rden_done"], 1)
                        dve.wait_ge(s["rden_done"], ONE + n + 1)
                        dve.tensor_tensor(rg[:], rden[:], gate[:, bass.ds(i * UQ + t, 1), :].to_broadcast([P, H, 3]), ALU.mult).then_inc(s["rg_done"], 1)
                        dve.wait_ge(s["rg_done"], ONE + n + 1)
                        for k in range(2):
                            dve.tensor_tensor(wof[:, 24 * k:24 * k + 24, :], o5[:, k, :, 0:DH],
                                              rgf[:, 24 * k:24 * k + 24].unsqueeze(2).to_broadcast([P, 24, DH]), ALU.mult).then_inc(s["weighted"], 1)
                        dve.wait_ge(s["weighted"], ONE + 2 * n + 2)
                        dve.wait_ge(s["att_turned"], ONE + n)
                        dve.tensor_reduce(att[:].rearrange("p (h d) -> p h d", h=H), wo3[:].rearrange("p h r d -> p h d r"), AX.X,
                                          ALU.add).then_inc(s["att_done"], 1)

                    def add(t):
                        dve.wait_ge(s["wo_done"], ONE + n0 + t + 1)
                        for c in range(C):
                            x = xf[:, c, bass.ds((n0 + t) * QT, QT)]
                            dve.scalar_tensor_tensor(out=x, in0=T_[:, 1, c * QT:(c + 1) * QT], scalar=bo[:, c:c + 1], in1=x,
                                                     op0=ALU.add, op1=ALU.add).then_inc(s["x_added"], 1)

                    last = UQ * NG - 1
                    for k in range(last + 5):
                        if k <= last:
                            shift(k)
                        if k >= 5 and (k - 5) % NG == 0:
                            combine((k - 5) // NG)
                        if k >= 7 and (k - 7) % NG == 0:
                            add((k - 7) // NG)
    st.close()


def mesa_attention(nc, xf, io, eps):
    L = 128
    SEG = 2
    NGRP = T // (L * SEG)
    SYS = SEG * H
    TRI = DH * (DH + 1) // 2

    def off(i):
        return DH * i - i * (i - 1) // 2

    st = Stage(nc, "mesa")
    wqk, wv = st.sb("wqk", [P, C, 2 * D]), st.sb("wv", [P, C, D])
    wfb, gw1, gw2 = st.sb("wfb", [P, C, 2 * H]), st.sb("gw1", [P, C, DH]), st.sb("gw2", [DH, D])
    wo_raw, wo = st.sb("wo_raw", [P, C, D]), st.sb("wo_n", [P, C, D])
    normw = st.sb("norm_w", [P, C])
    delta, restart = st.sb("delta", [P, H]), st.sb("restart", [P, T // L])
    delta_n = st.sb("delta_segment", [P, T // L, H])
    lam = st.sb("lambda", [P, DH, H])
    la, lb = st.sb("lambda_a", [P, DH, H]), st.sb("lambda_b", [P, DH, H])
    upto, after = st.sb("upto", [P, L]), st.sb("after", [P, L])
    negf, negb = st.sb("neg_float", [P, L]), st.sb("neg", [P, L], BF16)
    ident, identb = st.sb("identity", [P, P]), st.sb("identity_b", [P, P], BF16)
    parity, expand = st.sb("parity", [P, 2]), st.sb("expand", [H, C, P])
    own = st.sb("own_block", [P, C, P])
    c_small = st.sb("small", [P, 2 * H])
    c_half = st.sb("minus_half", [P, 2 * H])
    c_one = st.sb("one", [P, H])
    c_minus = st.sb("minus_one", [P, H])
    c_eps4 = st.sb("eps4", [P, H])
    xs = st.sb("x_seg", [P, C, L])
    sqk = st.sb("qk_square", [P, 2 * H, DH])
    qk, z16 = st.sb("qk", [P, 2 * D]), st.sb("z_f", [P, H])
    ta, tb, tc_, ssum = (st.sb(n, [P, 2 * H, k]) for n, k in (("sum8", 8), ("sum4", 4), ("sum2", 2), ("sum1", 1)))
    rn = st.sb("qk_inverse", [P, 2 * H])
    g1T = st.sb("g1T", [DH, L])
    zf, zabs, zexp, zln, zmin, zneg = (st.sb(n, [P, H]) for n in ("zf", "zf_abs", "zf_exp", "zf_ln", "zf_relu", "zf_sum"))
    eb, eb1, beta = (st.sb(n, [P, H]) for n in ("eb", "eb1", "beta"))
    gt = st.sb("gate_tanh", [P, D])
    kn = st.sb("k", [P, H, DH])
    eG = st.sb("decay_to_end", [P, H])
    kk = st.sb("kk", [P, H, TRI])
    lfU = st.sb("log_f_upto", [P, H, L])
    dec = st.sb("decay", [P, 4, 4, L])
    ef_row = st.sb("decay_row", [1, H, L])
    h_rows = st.sb("state_rows", [P, H, TRI])
    h_last, h_row = h_rows[96:P], h_rows[0:1]
    kb = st.sb("k_beta", [P, 2, SEG, D])
    kd = st.sb("k_decayed", [P, 2, SEG, D])
    vs = st.sb("v", [P, 2, SEG, D])
    g1p = st.sb("gate", [P, 2, SEG, D])
    lf = st.sb("log_f", [P, 2, SEG, H])
    eF = st.sb("decay_from_start", [P, 2, SEG, H])
    eFT = st.sb("decay_from_startT", [H, 2, SEG, L])
    A = st.sb("A", [P, 2, TRI, SYS])
    Y = st.sb("Y", [P, 2, DH, SYS])
    mult = st.sb("multipliers", [P, 2, DH, SYS])
    prod = st.sb("product", [P, 2, DH, SYS])
    prod_y = st.sb("product_y", [P, DH, SYS])
    piv, rinv = st.sb("pivot", [P, SYS]), st.sb("pivot_inverse", [P, DH, SYS])
    red, num = st.sb("known_part", [P, SYS]), st.sb("numerator", [P, SYS])
    qs = st.sb("solution", [P, D])
    kbT, qsT = st.sb("k_betaT", [P, C, 2, L]), st.sb("solutionT", [P, C, L])
    e2, pm = st.sb("decay2", [P, 2, 4 * L]), st.sb("weights", [P, 2, 4 * L])
    oi, o, og, osq, on = (st.sb(n, [P, H, DH]) for n in ("o_inter", "o", "o_gated", "o_square", "o_normed"))
    t8, t4, t2, t1 = (st.sb(n, [P, H, k]) for n, k in (("osum8", 8), ("osum4", 4), ("osum2", 2), ("osum1", 1)))
    oms, orn = st.sb("o_mean", [P, H]), st.sb("o_inverse", [P, H])
    onT = st.sb("o_normedT", [P, C, L])
    state, s_own, s_dec = (st.sb(n, [P, C, P]) for n in ("state", "state_new", "state_decayed"))
    ssb, o7 = st.sb("scores", [P, 2, 4 * L]), st.sb("o_parts", [P, 2, H, DH])
    st5, wo6 = st.sb("state_parts", [P, D + C]), st.sb("wo_out", [P, C, L])
    c16 = st.sb("sixteenth", [P, H])
    bk = [st.ps(f"bank{k}") for k in range(8)]
    loads = [(wqk[:], "mesa_wqk"), (wv[:], "mesa_wv"), (wfb[:], "mesa_wfb"), (gw1[:], "mesa_gw1"), (gw2[:], "mesa_gw2"),
             (wo_raw[:], "mesa_wo"), (normw[:], "mesa_norm"), (delta[:], "mesa_delta"), (restart[:], "mesa_restart"), (la[:], "mesa_lambda"),
             (upto[:], "mesa_upto"), (after[:], "mesa_after"), (negf[:], "mesa_neg"), (ident[:], "identity"),
             (parity[:], "nsa_parity"), (expand[:], "mesa_expand"), (own[:], "mesa_own")]
    names = ("here consts lam1 lam2 lam_done wo_ready carrier "
             "xs_done qk_mm proj_mm gate_mm sqk_done g1_moved eb_done v_moved tanh_done zf_done zabs_done zexp_done zln_done zmin_done "
             "zneg_done lf_done eb1_done beta_done sum8 sum4 sum2 sum1 sume rn_done y_done kn_done kb_done kk_done f_mm ef_done eg_done eft_done "
             "ef_row_here kd_done lfu_done gate1_done d_mm dec_done a_mm a_moved h_row_here "
             "solved e "
             "o_lfu qs_done o_turned kbt_done qst_done o_dmm o_smm e2_done pm_done intra_mm inter_mm oi_done o_done og_done osq_done "
             "qk_moved z_moved s_moved o7_moved st_moved wo_moved os8 os4 os2 os1 osm ose orn_done on_done on_turned ont_done wo_mm x_added st_mm st_own st_dec st_done").split()
    s = {n: st.sem(n) for n in names}

    def head(g, j):
        return 8 * (j // 2) + 2 * g + j % 2

    def grouped(t, g):
        return t.rearrange("p (c a e) t -> p c a e t", c=2, a=4)[:, :, g, :, :]

    NP_ = 4

    def schedule(eng, prepare, complete):
        prepare(0, 0)
        prepare(1, 1)
        eng.sem_inc(s["carrier"], 1)
        with eng.Fori(0, NGRP // 2 - 1) as i:
            for u in range(2):
                complete(2 * i + u, u)
                prepare(2 * i + 2 + u, u)
        complete(NGRP - 2, 0)
        complete(NGRP - 1, 1)

    st.start_counters()
    with nc.Block() as block:
        @block.sync
        def _(sp):
            for dst, src in loads:
                sp.dma_start(dst, io[src]).then_inc(s["here"], 16)

            def carry(g, u, q):
                n = g * SEG + q
                sp.wait_ge(s["a_mm"], ONE + 8 * n)
                sp.sem_inc(s["carrier"], 1)
                sp.wait_ge(s["eft_done"], ONE + n + 1)
                sp.sem_inc(s["carrier"], 1)
                sp.dma_start(ef_row[:], eFT[:, u, q, :]).then_inc(s["ef_row_here"], 16)
                sp.wait_ge(s["a_mm"], ONE + 8 * n + 8)
                sp.sem_inc(s["carrier"], 1)
                sp.wait_ge(s["a_moved"], ONE + 16 * n + 16)
                sp.dma_start(h_row, h_last[31:32, :, :]).then_inc(s["h_row_here"], 16)
            with sp.Fori(0, NGRP // 2) as i:
                for u in range(2):
                    for q in range(SEG):
                        carry(2 * i + u, u, q)
            sp.wait_ge(s["h_row_here"], ONE + 16 * NGRP * SEG)

        @block.tensor
        def _(pe):
            pe.wait_ge(s["here"], ONE + 16 * len(loads))
            pe.wait_ge(s["consts"], ONE + 11)
            pe.wait_ge(s["wo_ready"], ONE + C)

            def prepare(g, u):
                for q in range(SEG):
                    n = g * SEG + q
                    pe.wait_ge(s["xs_done"], ONE + n + 1)
                    pe.wait_ge(s["dec_done"], ONE + NP_ * n)
                    for c in range(C):
                        mm = pe.matmul(bk[0][:], xs[:, c, :], wqk[:, c, :], start=c == 0, stop=c == C - 1)
                    mm.then_inc(s["qk_mm"], 1)
                    for c in range(C):
                        pe.matmul(bk[1][:, 0:D], xs[:, c, :], wv[:, c, :], start=c == 0, stop=c == C - 1)
                    pe.wait_ge(s["a_moved"], ONE + 16 * n)
                    for c in range(C):
                        pe.matmul(bk[2][:, 0:2 * H], xs[:, c, :], wfb[:, c, :], start=c == 0, stop=c == C - 1)
                    for c in range(C):
                        mm = pe.matmul(bk[3][0:DH, 0:L], gw1[:, c, :], xs[:, c, :], start=c == 0, stop=c == C - 1)
                    mm.then_inc(s["proj_mm"], 1)
                    pe.wait_ge(s["g1_moved"], ONE + n + 1)
                    pe.matmul(bk[1][:, D:2 * D], g1T[:], gw2[:], start=True, stop=True).then_inc(s["gate_mm"], 1)
                    pe.wait_ge(s["lf_done"], ONE + n + 1)
                    pe.matmul(bk[3][:, 0:H], upto[:], lf[:, u, q, :], start=True, stop=True)
                    pe.matmul(bk[3][:, H:2 * H], after[:], lf[:, u, q, :], start=True, stop=True)
                    pe.matmul(bk[3][0:H, 2 * H:2 * H + L], lf[:, u, q, :], upto[:], start=True, stop=True).then_inc(s["f_mm"], 1)
                    pe.wait_ge(s["lfu_done"], ONE + n + 1)
                    for d in range(4):
                        if d == 0:
                            pe.wait_ge(s["qk_moved"], ONE + n + 1)
                            pe.wait_ge(s["sqk_done"], ONE + n + 1)
                        elif d == 1:
                            pe.wait_ge(s["v_moved"], ONE + n + 1)
                            pe.wait_ge(s["tanh_done"], ONE + n + 1)
                        else:
                            pe.wait_ge(s["dec_done"], ONE + NP_ * n + d - 1)
                        pe.matmul(bk[d % 2][:], after[:], grouped(lfU[:], d), start=True, stop=False)
                        pe.matmul(bk[d % 2][:], identb[:], negb[:].unsqueeze(1).to_broadcast([P, 4, L]), start=False, stop=True) \
                            .then_inc(s["d_mm"], 1)
                    pe.wait_ge(s["kk_done"], ONE + DH * (n + 1))
                    pe.wait_ge(s["eft_done"], ONE + n + 1)
                    pe.wait_ge(s["eb_done"], ONE + n + 1)
                    pe.wait_ge(s["ef_row_here"], ONE + 16 * (n + 1))
                    pe.wait_ge(s["h_row_here"], ONE + 16 * n)
                    for k in range(8):
                        g4, j0 = k // 2, 2 * (k % 2)
                        pe.wait_ge(s["dec_done"], ONE + NP_ * n + g4 + 1)
                        if k >= 2:
                            pe.wait_ge(s["a_moved"], ONE + 16 * n + 2 * (k - 1))
                        for e in range(2):
                            h = head(g4, j0 + e)
                            dst = bk[2 + k % 2][:, e * TRI:(e + 1) * TRI]
                            pe.matmul(dst, dec[:, g4, j0 + e, :], kk[:, h, :], start=True, stop=False)
                            mm = pe.matmul(dst, ef_row[:, h, :], h_row[:, h, :], start=False, stop=True)
                        mm.then_inc(s["a_mm"], 1)

            def complete(g, u):
                for q in range(SEG):
                    n = g * SEG + q
                    pe.wait_ge(s["wo_moved"], ONE + n)
                    pe.wait_ge(s["qs_done"], ONE + n + 1)
                    for c in range(C):
                        pe.transpose(bk[6][:, c * P:(c + 1) * P], kb[:, u, q, c * P:(c + 1) * P], ident[:])
                    for c in range(C):
                        mm = pe.transpose(bk[6][:, D + c * P:D + (c + 1) * P], qs[:, c * P:(c + 1) * P], ident[:])
                    mm.then_inc(s["o_turned"], 1)
                    pe.wait_ge(s["o_lfu"], ONE + n + 1)

                    def intra(d):
                        pe.wait_ge(s["pm_done"], ONE + 4 * n + d + 1)
                        for j in range(4):
                            h = head(d, j)
                            mm = pe.matmul(bk[7][:, D + h * DH:D + (h + 1) * DH], pm[:, d % 2, j * L:(j + 1) * L],
                                           vs[:, u, q, h * DH:(h + 1) * DH], start=True, stop=True)
                        mm.then_inc(s["intra_mm"], 1)
                    for d in range(4):
                        pe.wait_ge(s["e2_done"], ONE + 4 * n + d)
                        pe.matmul(bk[4][:], after[:], grouped(lfU[:], d), start=True, stop=False)
                        pe.matmul(bk[4][:], identb[:], negb[:].unsqueeze(1).to_broadcast([P, 4, L]), start=False, stop=True) \
                            .then_inc(s["o_dmm"], 1)
                        if d == 0:
                            pe.wait_ge(s["kbt_done"], ONE + 2 * n + 2)
                            pe.wait_ge(s["qst_done"], ONE + n + 1)
                            pe.wait_ge(s["st_moved"], ONE + n)
                        pe.wait_ge(s["s_moved"], ONE + 4 * n + d)
                        for j in range(4):
                            mm = pe.matmul(bk[5][:, j * L:(j + 1) * L], kbT[32 * d:32 * d + 32, j // 2, j % 2, :],
                                           qsT[32 * d:32 * d + 32, j // 2, :], start=True, stop=True)
                        mm.then_inc(s["o_smm"], 1)
                        if d == 0:
                            pe.wait_ge(s["o7_moved"], ONE + n)
                            pe.wait_ge(s["st_done"], ONE + n)
                            for c in range(C):
                                mm = pe.matmul(bk[7][:, c * P:(c + 1) * P], qsT[:, c, :], state[:, c, :], start=True, stop=True)
                            mm.then_inc(s["inter_mm"], 1)
                        else:
                            intra(d - 1)
                    intra(3)
                    pe.wait_ge(s["s_moved"], ONE + 4 * n + 4)
                    for c in range(C):
                        pe.matmul(bk[5][:, c * P:(c + 1) * P], kd[:, u, q, c * P:(c + 1) * P], vs[:, u, q, c * P:(c + 1) * P],
                                  start=True, stop=True)
                    for c in range(C):
                        mm = pe.matmul(bk[5][:, D + c:D + c + 1], expand[:, c, :], eFT[:, u, q, L - 1:L], start=True, stop=True)
                    mm.then_inc(s["st_mm"], 1)
                    pe.wait_ge(s["on_done"], ONE + n + 1)
                    for c in range(C):
                        mm = pe.transpose(bk[6][:, c * P:(c + 1) * P], on[:].rearrange("p h d -> p (h d)")[:, c * P:(c + 1) * P], ident[:])
                    mm.then_inc(s["on_turned"], 1)
                    pe.wait_ge(s["ont_done"], ONE + n + 1)
                    for m in range(C):
                        for c in range(C):
                            mm = pe.matmul(bk[6][:, D + m * L:D + (m + 1) * L], wo[:, c, m * P:(m + 1) * P], onT[:, c, :],
                                           start=c == 0, stop=c == C - 1)
                    mm.then_inc(s["wo_mm"], 1)

            schedule(pe, prepare, complete)

        @block.scalar
        def _(act):
            act.wait_ge(s["here"], ONE + 16 * len(loads))
            act.wait_ge(s["consts"], ONE + 11)
            act.activation(lb[:], la[:], ACT.Abs).then_inc(s["lam1"], 1)
            act.wait_ge(s["lam1"], ONE + 1)
            act.activation(lb[:], lb[:], ACT.Exp, scale=-1.0).then_inc(s["lam1"], 1)
            act.wait_ge(s["lam1"], ONE + 2)
            act.activation(lb[:], lb[:], ACT.Ln, bias=eps[:, 3:4]).then_inc(s["lam1"], 1)
            for c in range(C):
                act.activation(wo[:, c, :], wo_raw[:, c, :], ACT.Copy, scale=normw[:, c:c + 1]).then_inc(s["wo_ready"], 1)

            def prepare(g, u):
                for q in range(SEG):
                    n = g * SEG + q
                    act.wait_ge(s["proj_mm"], ONE + n)
                    act.copy(xs[:], xf[:, :, bass.ts(n, L)]).then_inc(s["xs_done"], 1)
                    act.wait_ge(s["qk_mm"], ONE + n + 1)
                    act.wait_ge(s["sum8"], ONE + n)
                    act.activation(sqk[:].rearrange("p h d -> p (h d)"), bk[0][:], ACT.Square).then_inc(s["sqk_done"], 1)
                    act.wait_ge(s["y_done"], ONE + n)
                    act.wait_ge(s["kn_done"], ONE + n)
                    act.copy(qk[:], bk[0][:]).then_inc(s["qk_moved"], 1)
                    act.wait_ge(s["proj_mm"], ONE + n + 1)
                    act.wait_ge(s["zf_done"], ONE + n)
                    act.copy(z16[:], bk[2][:, 0:H]).then_inc(s["z_moved"], 1)
                    act.wait_ge(s["gate_mm"], ONE + n)
                    act.copy(g1T[:], bk[3][0:DH, 0:L]).then_inc(s["g1_moved"], 1)
                    act.wait_ge(s["eb1_done"], ONE + n)
                    act.activation(eb[:], bk[2][:, H:2 * H], ACT.Exp, scale=-1.0).then_inc(s["eb_done"], 1)
                    act.wait_ge(s["zf_done"], ONE + n + 1)
                    act.activation(zabs[:], zf[:], ACT.Abs).then_inc(s["zabs_done"], 1)
                    act.wait_ge(s["zneg_done"], ONE + n)
                    act.activation(zmin[:], zf[:], ACT.Relu, scale=-1.0).then_inc(s["zmin_done"], 1)
                    act.wait_ge(s["zabs_done"], ONE + n + 1)
                    act.activation(zexp[:], zabs[:], ACT.Exp, scale=-1.0).then_inc(s["zexp_done"], 1)
                    act.wait_ge(s["zexp_done"], ONE + n + 1)
                    act.activation(zln[:], zexp[:], ACT.Ln, bias=eps[:, 3:4]).then_inc(s["zln_done"], 1)
                    act.wait_ge(s["gate_mm"], ONE + n + 1)
                    if q == 0:
                        act.wait_ge(s["x_added"], ONE + SEG * prior(g))
                    act.copy(vs[:, u, q, :], bk[1][:, 0:D]).then_inc(s["v_moved"], 1)
                    act.wait_ge(s["gate1_done"], ONE + n)
                    act.activation(gt[:], bk[1][:, D:2 * D], ACT.Tanh, scale=0.5).then_inc(s["tanh_done"], 1)
                    act.wait_ge(s["f_mm"], ONE + n + 1)
                    act.activation(eF[:, u, q, :], bk[3][:, 0:H], ACT.Exp).then_inc(s["ef_done"], 1)
                    act.wait_ge(s["kd_done"], ONE + n)
                    act.activation(eG[:], bk[3][:, H:2 * H], ACT.Exp).then_inc(s["eg_done"], 1)
                    act.activation(eFT[:, u, q, :], bk[3][0:H, 2 * H:2 * H + L], ACT.Exp).then_inc(s["eft_done"], 1)
                    act.wait_ge(s["a_mm"], ONE + 8 * n)
                    for d in range(4):
                        act.wait_ge(s["d_mm"], ONE + 4 * n + d + 1)
                        act.activation(dec[:, d, :, :].rearrange("p j t -> p (j t)"), bk[d % 2][:], ACT.Exp).then_inc(s["dec_done"], 1)
                    if q == 0:
                        act.wait_ge(s["solved"], ONE + prior(g))
                    act.wait_ge(s["h_row_here"], ONE + 16 * n)
                    for k in range(8):
                        h0 = head(k // 2, 2 * (k % 2))
                        act.wait_ge(s["a_mm"], ONE + 8 * n + k + 1)
                        src = bk[2 + k % 2][:, 0:2 * TRI].rearrange("p (e m) -> p e m", e=2)
                        act.copy(A[:, u, :, q * H + h0:q * H + h0 + 2].rearrange("p m e -> p e m"), src).then_inc(s["a_moved"], 1)
                        act.copy(h_last[:, h0:h0 + 2, :], src[96:P]).then_inc(s["a_moved"], 1)

            def prior(g):
                return g - 1 if not isinstance(g, int) else max(g - 1, 0)

            def complete(g, u):
                for q in range(SEG):
                    n = g * SEG + q
                    if q == 0:
                        act.wait_ge(s["solved"], ONE + g + 1)
                    act.wait_ge(s["o_turned"], ONE + n)
                    act.copy(qs[:].rearrange("p (h d) -> p h d", h=H), Y[:, u, :, q * H:(q + 1) * H].rearrange("p d h -> p h d")) \
                        .then_inc(s["qs_done"], 1)
                    act.wait_ge(s["o_turned"], ONE + n + 1)
                    act.wait_ge(s["o_smm"], ONE + 4 * n)
                    act.wait_ge(s["inter_mm"], ONE + n)
                    for e in range(2):
                        act.activation(kbT[:, :, e, :], bk[6][:, 0:D].rearrange("p (c t) -> p c t", c=C), ACT.Copy,
                                       scale=parity[:, e:e + 1]).then_inc(s["kbt_done"], 1)
                    act.copy(qsT[:], bk[6][:, D:2 * D].rearrange("p (c t) -> p c t", c=C)).then_inc(s["qst_done"], 1)
                    for d in range(4):
                        act.wait_ge(s["o_dmm"], ONE + 4 * n + d + 1)
                        act.wait_ge(s["pm_done"], ONE + 4 * n + max(d - 1, 0))
                        act.activation(e2[:, d % 2, :], bk[4][:], ACT.Exp).then_inc(s["e2_done"], 1)
                        act.wait_ge(s["o_smm"], ONE + 4 * n + d + 1)
                        act.copy(ssb[:, d % 2, :], bk[5][:]).then_inc(s["s_moved"], 1)
                    act.wait_ge(s["intra_mm"], ONE + 4 * n + 4)
                    act.wait_ge(s["inter_mm"], ONE + n + 1)
                    act.wait_ge(s["o_done"], ONE + n)
                    act.copy(o7[:].rearrange("p a h d -> p (a h d)"), bk[7][:]).then_inc(s["o7_moved"], 1)
                    act.wait_ge(s["st_mm"], ONE + n + 1)
                    act.wait_ge(s["st_done"], ONE + n)
                    act.copy(st5[:], bk[5][:, 0:D + C]).then_inc(s["st_moved"], 1)
                    act.wait_ge(s["og_done"], ONE + n + 1)
                    act.wait_ge(s["os8"], ONE + n)
                    act.activation(osq[:], og[:], ACT.Square).then_inc(s["osq_done"], 1)
                    act.wait_ge(s["on_turned"], ONE + n + 1)
                    act.wait_ge(s["wo_mm"], ONE + n)
                    act.copy(onT[:], bk[6][:, 0:D].rearrange("p (c t) -> p c t", c=C)).then_inc(s["ont_done"], 1)
                    act.wait_ge(s["wo_mm"], ONE + n + 1)
                    act.wait_ge(s["x_added"], ONE + n)
                    act.copy(wo6[:], bk[6][:, D:2 * D].rearrange("p (c t) -> p c t", c=C)).then_inc(s["wo_moved"], 1)
            schedule(act, prepare, complete)

        @block.gpsimd
        def _(pool):
            pool.memset(c_small[:], 1e-6).then_inc(s["consts"], 1)
            pool.memset(c_half[:], -0.5).then_inc(s["consts"], 1)
            pool.memset(c_one[:], 1.0).then_inc(s["consts"], 1)
            pool.memset(c_minus[:], -1.0).then_inc(s["consts"], 1)
            pool.memset(c_eps4[:], 4e-5).then_inc(s["consts"], 1)
            pool.memset(c16[:], 1.0 / DH).then_inc(s["consts"], 1)
            pool.wait_ge(s["here"], ONE + 16 * len(loads))
            pool.tensor_copy(negb[:], negf[:]).then_inc(s["consts"], 1)
            pool.tensor_copy(identb[:], ident[:]).then_inc(s["consts"], 1)
            pool.memset(h_row, 0.0).then_inc(s["consts"], 1)
            pool.memset(state[:], 0.0).then_inc(s["consts"], 1)
            pool.wait_ge(s["consts"], ONE + 10)
            pool.tensor_tensor(delta_n[:], delta[:].unsqueeze(1).to_broadcast([P, T // L, H]),
                               restart[:].unsqueeze(2).to_broadcast([P, T // L, H]), ALU.add).then_inc(s["consts"], 1)
            pool.wait_ge(s["consts"], ONE + 11)

            def op(out, a, b, alu, done, n=None):
                pool.tensor_tensor(out, a, b, alu).then_inc(s[done], 1)
                if n is not None:
                    pool.wait_ge(s[done], ONE + n)

            def bc(t, k):
                return t.unsqueeze(2).to_broadcast([P, t.shape[1], k])

            def prepare(g, u):
                for q in range(SEG):
                    n = g * SEG + q
                    sysm = slice(q * H, (q + 1) * H)
                    pool.wait_ge(s["z_moved"], ONE + n + 1)
                    pool.sem_inc(s["carrier"], 1)
                    op(zf[:], z16[:], delta_n[:, bass.ds(n, 1), :].rearrange("p o h -> p (o h)"), ALU.add, "zf_done", n + 1)
                    pool.wait_ge(s["sqk_done"], ONE + n + 1)
                    op(ta[:], sqk[:, :, 0:8], sqk[:, :, 8:16], ALU.add, "sum8", n + 1)
                    op(tb[:], ta[:, :, 0:4], ta[:, :, 4:8], ALU.add, "sum4", n + 1)
                    op(tc_[:], tb[:, :, 0:2], tb[:, :, 2:4], ALU.add, "sum2", n + 1)
                    op(ssum[:], tc_[:, :, 0:1], tc_[:, :, 1:2], ALU.add, "sum1", n + 1)
                    flat = ssum[:].rearrange("p h o -> p (h o)")
                    op(flat, flat, c_small[:], ALU.add, "sume", n + 1)
                    op(rn[:], flat, c_half[:], ALU.pow, "rn_done", n + 1)
                    pool.wait_ge(s["zln_done"], ONE + n + 1)
                    pool.wait_ge(s["zmin_done"], ONE + n + 1)
                    if q == 0:
                        wait_prior(g)
                    op(zneg[:], zmin[:], zln[:], ALU.add, "zneg_done", n + 1)
                    op(lf[:, u, q, :], zneg[:], c_minus[:], ALU.mult, "lf_done", n + 1)
                    pool.wait_ge(s["eb_done"], ONE + n + 1)
                    op(eb1[:], eb[:], c_one[:], ALU.add, "eb1_done", n + 1)
                    op(beta[:], eb1[:], c_minus[:], ALU.pow, "beta_done", n + 1)
                    pool.wait_ge(s["d_mm"], ONE + 4 * n)
                    pool.wait_ge(s["o_dmm"], ONE + lfu_before_prepare(g, q))
                    op(lfU[:], upto[:].unsqueeze(1).to_broadcast([P, H, L]), bc(lf[:, u, q, :], L), ALU.mult, "lfu_done")
                    pool.wait_ge(s["qk_moved"], ONE + n + 1)
                    if q == 0:
                        pool.wait_ge(s["qs_done"], ONE + prior(g) * SEG)
                    op(Y[:, u, :, sysm].rearrange("p d h -> p h d"), qk[:, 0:D].rearrange("p (h d) -> p h d", h=H),
                       bc(rn[:, 0:H], DH), ALU.mult, "y_done")
                    op(kn[:], qk[:, D:2 * D].rearrange("p (h d) -> p h d", h=H), bc(rn[:, H:2 * H], DH), ALU.mult, "kn_done", n + 1)
                    kbv = kb[:, u, q, :].rearrange("p (h d) -> p h d", h=H)
                    op(kbv, kn[:], bc(beta[:], DH), ALU.mult, "kb_done", n + 1)
                    pool.wait_ge(s["a_mm"], ONE + 8 * n)
                    for i in range(DH):
                        op(kk[:, :, off(i):off(i) + DH - i], kbv[:, :, i:i + 1].to_broadcast([P, H, DH - i]), kn[:, :, i:], ALU.mult, "kk_done")
                    pool.wait_ge(s["eg_done"], ONE + n + 1)
                    op(kd[:, u, q, :].rearrange("p (h d) -> p h d", h=H), kbv, bc(eG[:], DH), ALU.mult, "kd_done")
                    pool.wait_ge(s["tanh_done"], ONE + n + 1)
                    op(g1p[:, u, q, :].rearrange("p (h d) -> p h d", h=H), gt[:].rearrange("p (h d) -> p h d", h=H),
                       bc(c_one[:], DH), ALU.add, "gate1_done", n + 1)
                    pool.wait_ge(s["kk_done"], ONE + DH * (n + 1))
                    pool.wait_ge(s["y_done"], ONE + n + 1)
                    pool.wait_ge(s["kd_done"], ONE + n + 1)
                    pool.wait_ge(s["lfu_done"], ONE + n + 1)

            def prior(g):
                return g - 1 if not isinstance(g, int) else max(g - 1, 0)

            def lfu_before_prepare(g, q):
                return 4 * SEG * prior(g)

            def wait_prior(g):
                pool.wait_ge(s["wo_mm"], ONE + SEG * prior(g))

            def complete(g, u):
                for q in range(SEG):
                    n = g * SEG + q
                    pool.wait_ge(s["o_dmm"], ONE + 4 * n)
                    pool.wait_ge(s["d_mm"], ONE + prepared(g))
                    op(lfU[:], upto[:].unsqueeze(1).to_broadcast([P, H, L]), bc(lf[:, u, q, :], L), ALU.mult, "o_lfu", n + 1)
                    for d in range(4):
                        pool.wait_ge(s["e2_done"], ONE + 4 * n + d + 1)
                        pool.wait_ge(s["s_moved"], ONE + 4 * n + d + 1)
                        pool.wait_ge(s["intra_mm"], ONE + 4 * n + max(d - 1, 0))
                        op(pm[:, d % 2, :], ssb[:, d % 2, :], e2[:, d % 2, :], ALU.mult, "pm_done")
                    pool.wait_ge(s["o7_moved"], ONE + n + 1)
                    flat7 = o7
                    op(oi[:], flat7[:, 0], bc(eF[:, u, q, :], DH), ALU.mult, "oi_done", n + 1)
                    op(o[:], flat7[:, 1], oi[:], ALU.add, "o_done", n + 1)
                    op(og[:], o[:], g1p[:, u, q, :].rearrange("p (h d) -> p h d", h=H), ALU.mult, "og_done", n + 1)
                    pool.wait_ge(s["st_moved"], ONE + n + 1)
                    op(s_own[:], st5[:, 0:D].rearrange("p (c k) -> p c k", c=C), own[:], ALU.mult, "st_own", n + 1)
                    op(s_dec[:], state[:], st5[:, D:D + C].unsqueeze(2).to_broadcast([P, C, P]), ALU.mult, "st_dec", n + 1)
                    op(state[:], s_dec[:], s_own[:], ALU.add, "st_done", n + 1)
                    pool.wait_ge(s["osq_done"], ONE + n + 1)
                    op(t8[:], osq[:, :, 0:8], osq[:, :, 8:16], ALU.add, "os8", n + 1)
                    op(t4[:], t8[:, :, 0:4], t8[:, :, 4:8], ALU.add, "os4", n + 1)
                    op(t2[:], t4[:, :, 0:2], t4[:, :, 2:4], ALU.add, "os2", n + 1)
                    op(t1[:], t2[:, :, 0:1], t2[:, :, 1:2], ALU.add, "os1", n + 1)
                    op(oms[:], t1[:].rearrange("p h o -> p (h o)"), c16[:], ALU.mult, "osm", n + 1)
                    op(oms[:], oms[:], c_eps4[:], ALU.add, "ose", n + 1)
                    op(orn[:], oms[:], c_half[:, 0:H], ALU.pow, "orn_done", n + 1)
                    pool.wait_ge(s["on_turned"], ONE + n)
                    op(on[:], og[:], bc(orn[:], DH), ALU.mult, "on_done", n + 1)
                    pool.wait_ge(s["wo_moved"], ONE + n + 1)
                    pool.sem_inc(s["carrier"], 1)
                    x = xf[:, :, bass.ts(n, L)]
                    pool.tensor_tensor(x, wo6[:], x, ALU.add).then_inc(s["x_added"], 1)

            def prepared(g):
                if isinstance(g, int):
                    return 4 * SEG * min(g + 2, NGRP)
                return 4 * SEG * (g + 2)
            schedule(pool, prepare, complete)

        @block.vector
        def _(dve):
            dve.wait_ge(s["lam1"], ONE + 3)
            dve.scalar_tensor_tensor(out=lam[:], in0=la[:], scalar=0.0, in1=lb[:], op0=ALU.max, op1=ALU.add).then_inc(s["lam2"], 1)
            dve.wait_ge(s["lam2"], ONE + 1)
            dve.tensor_scalar(lam[:], lam[:], 0.25, None, ALU.add).then_inc(s["lam_done"], 1)
            dve.wait_ge(s["lam_done"], ONE + 1)

            def solve(g, u, base):
                count = [0]

                def step(ins):
                    ins.then_inc(s["e"], 1)
                    count[0] += 1
                    return count[0]

                def upto_step(k):
                    dve.wait_ge(s["e"], ONE + base + k)

                Au, Yu = A[:, u], Y[:, u]
                dve.wait_ge(s["a_moved"], ONE + (g + 1) * SEG * 16)
                dve.wait_ge(s["y_done"], ONE + (g + 1) * SEG)
                row_done = {}
                y_last = 0
                for k in range(DH):
                    row = Au[:, off(k):off(k) + DH - k, :]
                    if k:
                        upto_step(row_done[k])
                    a = step(dve.tensor_tensor(piv[:].rearrange("p (q h) -> p q h", h=H), row[:, 0, :].rearrange("p (q h) -> p q h", h=H),
                                               lam[:, k:k + 1, :].to_broadcast([P, SEG, H]), ALU.add))
                    upto_step(a)
                    a = step(dve.reciprocal(rinv[:, k, :], piv[:]))
                    if k == DH - 1:
                        break
                    m = DH - 1 - k
                    mu = mult[:, k % 2]
                    upto_step(a)
                    a = step(dve.tensor_tensor(mu[:, 0:m, :], row[:, 1:, :], rinv[:, k:k + 1, :].to_broadcast([P, m, SYS]), ALU.mult))
                    upto_step(a)
                    if y_last:
                        upto_step(y_last)
                    py = step(dve.tensor_tensor(prod_y[:, 0:m, :], mu[:, 0:m, :], Yu[:, k:k + 1, :].to_broadcast([P, m, SYS]), ALU.mult))
                    waiting = None
                    for i in range(k + 1, DH + 1):
                        if i < DH:
                            w_ = DH - i
                            pr = prod[:, i % 2, 0:w_, :]
                            if i >= k + 3:
                                upto_step(row_done[i - 2])
                            elif k:
                                upto_step(row_done[DH - 1] if (DH - 1) % 2 == i % 2 else row_done[DH - 1])
                            a = step(dve.tensor_tensor(pr, row[:, i - k:, :], mu[:, i - k - 1:i - k, :].to_broadcast([P, w_, SYS]), ALU.mult))
                        if waiting is not None:
                            wi, wa, wp = waiting
                            upto_step(wa)
                            dst = Au[:, off(wi):off(wi) + DH - wi, :]
                            row_done[wi] = step(dve.tensor_tensor(dst, dst, wp, ALU.subtract))
                        if i < DH:
                            waiting = (i, a, pr)
                    upto_step(py)
                    y_last = step(dve.tensor_tensor(Yu[:, k + 1:, :], Yu[:, k + 1:, :], prod_y[:, 0:m, :], ALU.subtract))
                upto_step(a)
                upto_step(y_last)
                x_done = step(dve.tensor_tensor(Yu[:, DH - 1, :], Yu[:, DH - 1, :], rinv[:, DH - 1, :], ALU.mult))
                for k in range(DH - 2, -1, -1):
                    m = DH - 1 - k
                    upto_step(x_done)
                    a = step(dve.tensor_tensor(prod[:, 0, 0:m, :], Au[:, off(k) + 1:off(k) + DH - k, :], Yu[:, k + 1:, :], ALU.mult))
                    upto_step(a)
                    a = step(dve.tensor_reduce(red[:], prod[:, 0, 0:m, :].rearrange("p j s -> p s j"), AX.X, ALU.add))
                    upto_step(a)
                    a = step(dve.tensor_tensor(num[:], Yu[:, k, :], red[:], ALU.subtract))
                    upto_step(a)
                    x_done = step(dve.tensor_tensor(Yu[:, k, :], num[:], rinv[:, k, :], ALU.mult))
                upto_step(x_done)
                dve.sem_inc(s["solved"], 1)
                return count[0]

            STEPS = sum(2 + (k < DH - 1) * (2 + 2 * (DH - 1 - k) + 1) for k in range(DH)) + 1 + 4 * (DH - 1)
            with dve.Fori(0, NGRP // 2) as i:
                for u in range(2):
                    assert solve(2 * i + u, u, (2 * i + u) * STEPS) == STEPS
    st.close()



def decoder(nc, io, x_out):
    whole = Stage(nc, "all")
    xf = whole.sb("x", [P, C, T])
    mean_w = whole.sb("mean_w", [P, P])
    eps = whole.sb("eps", [P, 4])
    const_set = whole.sem("const_set")
    with nc.Block() as block:
        @block.vector
        def _(dve):
            dve.memset(mean_w[:], 1.0 / D).then_inc(const_set, 1)
            dve.memset(eps[:, 0:1], EPS_LN).then_inc(const_set, 1)
            dve.memset(eps[:, 1:2], 1e-6).then_inc(const_set, 1)
            dve.memset(eps[:, 2:3], 0.0).then_inc(const_set, 1)
            dve.memset(eps[:, 3:4], 1.0).then_inc(const_set, 1)
    load_stream(nc, xf, io["x"])
    if 1 in STAGES:
        mesa_attention(nc, xf, io, eps)
        layer_norm(nc, "ln0a", xf, mean_w, eps)
    if 2 in STAGES:
        context_mixture(nc, xf, io["ctx"], io["ctxT"])
        layer_norm(nc, "ln0b", xf, mean_w, eps)
    if 3 in STAGES:
        quantised_ffn(nc, xf, io, eps)
        layer_norm(nc, "ln0c", xf, mean_w, eps)
    if 4 in STAGES:
        sparse_attention(nc, xf, io, eps)
        layer_norm(nc, "ln1a", xf, mean_w, eps)
    if 5 in STAGES:
        slot_attention(nc, xf, io, mean_w, eps)
        layer_norm(nc, "ln1b", xf, mean_w, eps)
    if 6 in STAGES:
        ternary_ffn(nc, xf, io["w1T"], io["w2T"], io["h1T"], io["h2T"], io["w3T"], io["ffn1_scales"])
        layer_norm(nc, "ln1c", xf, mean_w, eps)
    store_stream(nc, xf, x_out)
    whole.close()



def rows_in_chunks(w):
    k, n = w.shape
    return np.ascontiguousarray(w.reshape(k // P, P, n).transpose(1, 0, 2))


def columns(v):
    return v.reshape(-1, P).T


def lay_out(a):
    n = {k: np.asarray(v) for k, v in a.items()}
    io = {
        "x": np.ascontiguousarray(n["x"].reshape(T, C, P).transpose(2, 1, 0)),
        "ctx": np.ascontiguousarray(n["ctx_1024"].transpose(1, 0, 2)),
        "ctxT": np.ascontiguousarray(n["ctx_1024"].reshape(B * M, C, P).transpose(2, 1, 0)),
    }
    if 6 in STAGES:
        for k, w in (("w1T", "w1_w"), ("w2T", "w2_w"), ("h1T", "h1_w"), ("h2T", "h2_w"), ("w3T", "w3_w")):
            io[k] = rows_in_chunks(n["L1_ffn_" + w].T)
        io["ffn1_scales"] = np.ascontiguousarray(np.concatenate(
            [columns(n["L1_ffn_" + w]) for w in ("w1_s", "w2_s", "h1_s", "h2_s", "w3_s")], axis=1))
    if 5 in STAGES:
        for k, w in (("slot_wkT", "Wk"), ("slot_wvT", "Wv"), ("slot_wihT", "gru_wih"), ("slot_whhT", "gru_whh")):
            io[k] = rows_in_chunks(n["L1_xattn_" + w].T)
        io["slot_wq"] = rows_in_chunks(n["L1_xattn_Wq"])
        io["slot_vectors"] = np.ascontiguousarray(np.concatenate(
            [columns(n["L1_xattn_" + w]) for w in ("slot_norm_w", "input_norm_w", "gru_bih", "gru_bhh")], axis=1))
    if 3 in STAGES:
        for k, w in (("q_gateT", "w_gate"), ("q_upT", "w_up"), ("q_downT", "w_down")):
            io[k] = rows_in_chunks(n["L0_ffn_" + w].T)
    io["identity"] = np.eye(P, dtype=np.float32)
    if 4 in STAGES:
        for k, w in (("nsa_wq", "Wq"), ("nsa_wk", "Wk"), ("nsa_wv", "Wv"), ("nsa_wo", "Wo"), ("nsa_wg", "Wg")):
            io[k] = rows_in_chunks(n["L1_attn_" + w])
        swapped = np.arange(D) ^ 1
        io["nsa_wqs"], io["nsa_wks"] = io["nsa_wq"][:, :, swapped], io["nsa_wk"][:, :, swapped]
        io["nsa_bg"] = np.ascontiguousarray(np.broadcast_to(n["L1_attn_bg"], (P, 3)))
        io["nsa_bo"] = np.ascontiguousarray(columns(n["L1_attn_bo"]))
        io["nsa_wk_comp"] = np.ascontiguousarray(np.broadcast_to(n["L1_attn_wk_comp"], (P, 16)))
        io["nsa_wv_comp"] = np.ascontiguousarray(np.tile(n["L1_attn_wv_comp"], P // 16)[:, None])
        io["nsa_pe"] = n["L1_attn_pe"]
        io["nsa_peT"] = rows_in_chunks(n["L1_attn_pe"].T)
        inv = (1.0 / np.float32(10000.0) ** (np.arange(DH // 2, dtype=np.float32) * np.float32(2.0) / np.float32(DH))).astype(np.float32)
        ang = np.arange(S, dtype=np.float32)[None, :] * np.repeat(inv, 2)[:, None]
        io["nsa_cos"] = np.tile(np.cos(ang), (P // DH, 1)).astype(np.float32)
        sign = np.tile(np.array([-1.0, 1.0], np.float32), DH // 2)[:, None]
        io["nsa_sin"] = np.tile(sign * np.sin(ang), (P // DH, 1)).astype(np.float32)
        token = np.arange(P)[:, None] + P * np.arange(S // P)[None, :]
        io["nsa_token"] = token.astype(np.float32)
        io["nsa_offset"] = np.tile(np.arange(8, dtype=np.float32), (P, 2))
        io["nsa_block_of"] = (token[:, :, None] // 16 == np.arange(S // 16)).astype(np.float32)
        seen = np.zeros((P, S // P, 64 + 16 + 192), bool)
        seen[:, :, 0:64] = (np.arange(64) + 1) * 16 <= token[:, :, None]
        key = 128 * np.arange(S // P)[None, :, None] - 64 + np.arange(192)
        seen[:, :, 80:] = (key >= 0) & (key <= token[:, :, None]) & (key > token[:, :, None] - 64)
        io["nsa_mask"] = np.where(seen, 0.0, -1e30).astype(np.float32)
    if 1 in STAGES:
        io["mesa_wqk"] = rows_in_chunks(np.concatenate([n["L0_attn_Wq"], n["L0_attn_Wk"]], axis=1))
        io["mesa_wfb"] = rows_in_chunks(np.concatenate([n["L0_attn_Wf"], n["L0_attn_Wbet"]], axis=1))
        for k, w in (("mesa_wv", "Wv"), ("mesa_gw1", "gate_w1"), ("mesa_wo", "Wo")):
            io[k] = rows_in_chunks(n["L0_attn_" + w])
        io["mesa_gw2"] = n["L0_attn_gate_w2"]
        io["mesa_norm"] = np.ascontiguousarray(columns(n["L0_attn_norm_weight"]))
        io["mesa_delta"] = np.ascontiguousarray(np.broadcast_to(n["L0_attn_delta"], (P, H)))
        io["mesa_restart"] = np.where((np.arange(P)[:, None] == 0) & (np.arange(T // P) % (S // P) == 0), -30000.0, 0.0).astype(np.float32)
        io["mesa_lambda"] = np.ascontiguousarray(np.broadcast_to(n["L0_attn_lamb_params"].reshape(H, DH).T, (P, DH, H)))
        r, c = np.arange(P)[:, None], np.arange(P)[None, :]
        io["mesa_upto"] = (r <= c).astype(np.float32)
        io["mesa_after"] = (r > c).astype(np.float32)
        io["mesa_neg"] = np.where(r <= c, 0.0, -30000.0).astype(np.float32)
        io["mesa_own"] = np.ascontiguousarray(np.broadcast_to(((r // DH) == (c // DH)).astype(np.float32)[:, None, :], (P, C, P)))
        io["mesa_expand"] = (np.arange(H)[:, None, None] == 8 * np.arange(C)[:, None] + np.arange(P) // DH).astype(np.float32)
    io["nsa_parity"] = ((np.arange(P)[:, None] // DH) % 2 == np.arange(2)).astype(np.float32)
    return io


def kernel(**inputs):
    import concourse.bacc as bacc
    from concourse.bass_utils import run_bass_kernel_spmd

    nc = bacc.Bacc("TRN2", target_bir_lowering=False, num_devices=1)
    arrays = lay_out(inputs)
    io = {k: nc.dram_tensor("in_" + k, v.shape, mybir.dt.from_np(v.dtype), kind="ExternalInput").ap() for k, v in arrays.items()}
    x_out = nc.dram_tensor("x_out", (P, C, T), F32, kind="ExternalOutput").ap()
    decoder(nc, io, x_out)
    r = run_bass_kernel_spmd(nc, [{"in_" + k: v for k, v in arrays.items()}], core_ids=[0])
    y = r.results[0]["x_out"]
    return y.transpose(2, 1, 0).reshape(B, S, D)
```

```python
from contextlib import ExitStack

import concourse.bass as bass
import numpy as np
from concourse import mybir

F32 = mybir.dt.float32
BF16 = mybir.dt.bfloat16
ALU = mybir.AluOpType
ACT = mybir.ActivationFunctionType
AX = mybir.AxisListType

P = 128
B, S, D = 4, 1024, 256
C = D // P
T = B * S
W = 512
NT = T // W
M = 77
INNER = 1024
CI = INNER // P
H, DH = 16, 16
EPS_LN = 1e-5
ONE = 1
STAGES = (1, 2, 3, 4, 5, 6)


class Stage:

    def __init__(self, nc, name):
        self.nc, self.name, self.memory, self.counters = nc, name, ExitStack(), []

    def sb(self, name, shape, dt=F32):
        return self.memory.enter_context(self.nc.sbuf_tensor(f"{self.name}_{name}", shape, dt))

    def ps(self, name, shape=(P, W), dt=F32):
        return self.memory.enter_context(self.nc.psum_tensor(f"{self.name}_{name}", list(shape), dt))

    def sem(self, name):
        self.counters.append(self.memory.enter_context(self.nc.semaphore(f"{self.name}_{name}")))
        return self.counters[-1]

    def shared_out(self, act):
        share = -(-len(self.counters) // 4)
        with self.nc.Block() as block:
            for k, engine in enumerate((block.vector, block.scalar, block.gpsimd, block.sync)):
                @engine
                def _(eng, mine=self.counters[k * share:(k + 1) * share]):
                    for sem in mine:
                        act(eng, sem)

    def start_counters(self):
        self.shared_out(lambda eng, sem: eng.sem_inc(sem, ONE))

    def close(self):
        self.shared_out(lambda eng, sem: eng.sem_clear(sem))
        self.memory.close()



def load_stream(nc, xf, x_in):
    st = Stage(nc, "load")
    x_here = st.sem("x_here")
    with nc.Block() as block:
        @block.sync
        def _(sp):
            for b in range(B):
                sp.dma_start(xf[:, :, b * S:(b + 1) * S], x_in[:, :, b * S:(b + 1) * S]).then_inc(x_here, 16)
            sp.wait_ge(x_here, 16 * B)
    st.close()


def store_stream(nc, xf, x_out):
    st = Stage(nc, "store")
    x_out_done = st.sem("x_out_done")
    with nc.Block() as block:
        @block.sync
        def _(sp):
            for b in range(B):
                sp.dma_start(x_out[:, :, b * S:(b + 1) * S], xf[:, :, b * S:(b + 1) * S]).then_inc(x_out_done, 16)
            sp.wait_ge(x_out_done, 16 * B)
    st.close()



def layer_norm(nc, name, xf, mean_w, eps_ln):
    st = Stage(nc, name)
    cen = st.sb("centred", [P, 2, C, W])
    sq = st.sb("square", [P, 2, C, W])
    sd = st.sb("deviation", [P, 2, W])
    rs = st.sb("inverse", [P, 2, W])
    ps_mean = [st.ps(f"mean{k}") for k in range(2)]
    ps_var = [st.ps(f"var{k}") for k in range(2)]
    mean_done, cen_done, sq_done, var_done = (st.sem(n) for n in ("mean_done", "cen_done", "sq_done", "var_done"))
    sd_done, rs_done, norm_done = (st.sem(n) for n in ("sd_done", "rs_done", "norm_done"))
    cols = [slice(t * W, (t + 1) * W) for t in range(NT)]
    with nc.Block() as block:
        @block.tensor
        def _(pe):
            def var(t):
                pe.wait_ge(sq_done, t + 1)
                if t >= 2:
                    pe.wait_ge(sd_done, t - 1)
                for c in range(C):
                    mm = pe.matmul(ps_var[t % 2][:], mean_w[:], sq[:, t % 2, c, :], start=c == 0, stop=c == C - 1)
                mm.then_inc(var_done, 1)
            for t in range(NT):
                if t >= 2:
                    pe.wait_ge(cen_done, t - 1)
                for c in range(C):
                    mm = pe.matmul(ps_mean[t % 2][:], mean_w[:], xf[:, c, cols[t]], start=c == 0, stop=c == C - 1)
                mm.then_inc(mean_done, 1)
                if t >= 1:
                    var(t - 1)
            var(NT - 1)

        @block.vector
        def _(dve):
            def scale(t):
                dve.wait_ge(sd_done, t + 1)
                if t >= 2:
                    dve.wait_ge(norm_done, t - 1)
                dve.reciprocal(rs[:, t % 2, :], sd[:, t % 2, :]).then_inc(rs_done, 1)
                dve.wait_ge(rs_done, t + 1)
                dve.tensor_tensor(xf[:, :, cols[t]], cen[:, t % 2, :, :],
                                  rs[:, t % 2, :].unsqueeze(1).to_broadcast([P, C, W]), ALU.mult).then_inc(norm_done, 1)
            for t in range(NT):
                dve.wait_ge(mean_done, t + 1)
                if t >= 2:
                    dve.wait_ge(norm_done, t - 1)
                    dve.wait_ge(sq_done, t - 1)
                dve.tensor_tensor(cen[:, t % 2, :, :], xf[:, :, cols[t]],
                                  ps_mean[t % 2][:].unsqueeze(1).to_broadcast([P, C, W]), ALU.subtract).then_inc(cen_done, 1)
                if t >= 1:
                    scale(t - 1)
            scale(NT - 1)

        @block.scalar
        def _(act):
            def root(t):
                act.wait_ge(var_done, t + 1)
                if t >= 2:
                    act.wait_ge(rs_done, t - 1)
                act.activation(sd[:, t % 2, :], ps_var[t % 2][:], ACT.Sqrt, bias=eps_ln[:, 0:1]).then_inc(sd_done, 1)
            for t in range(NT):
                act.wait_ge(cen_done, t + 1)
                if t >= 2:
                    act.wait_ge(var_done, t - 1)
                act.activation(sq[:, t % 2, :, :], cen[:, t % 2, :, :], ACT.Square).then_inc(sq_done, 1)
                if t >= 1:
                    root(t - 1)
            root(NT - 1)
    st.close()



def context_mixture(nc, xf, ctx, ctxT):
    st = Stage(nc, "mix")
    ctx_sb = st.sb("ctx", [M, B, D])
    ctxT_sb = st.sb("ctxT", [P, C, B * M])
    gel = st.sb("gelu", [M, 2, W])
    g = st.sb("g", [M, 2, W])
    ps_h = [st.ps(f"h{k}") for k in range(2)]
    ps_o = [[st.ps(f"o{k}{c}") for c in range(C)] for k in range(2)]
    ctx_here, h_done, gelu_done, g_done = (st.sem(n) for n in ("ctx_here", "h_done", "gelu_done", "g_done"))
    o_done, add_done = st.sem("o_done"), st.sem("add_done")
    cols = [slice(t * W, (t + 1) * W) for t in range(NT)]
    with nc.Block() as block:
        @block.sync
        def _(sp):
            sp.dma_start(ctx_sb[:], ctx).then_inc(ctx_here, 16)
            sp.dma_start(ctxT_sb[:], ctxT).then_inc(ctx_here, 16)

        @block.tensor
        def _(pe):
            pe.wait_ge(ctx_here, 32)

            def out(t):
                b = t * W // S
                pe.wait_ge(g_done, t + 1)
                if t >= 2:
                    pe.wait_ge(add_done, C * (t - 1))
                for c in range(C):
                    pe.matmul(ps_o[t % 2][c][:], ctx_sb[:, b, c * P:(c + 1) * P], g[:, t % 2, :],
                              start=True, stop=True).then_inc(o_done, 1)
            for t in range(NT):
                b = t * W // S
                if t >= 2:
                    pe.wait_ge(g_done, t - 1)
                for c in range(C):
                    mm = pe.matmul(ps_h[t % 2][0:M, :], ctxT_sb[:, c, b * M:(b + 1) * M], xf[:, c, cols[t]],
                                   start=c == 0, stop=c == C - 1)
                mm.then_inc(h_done, 1)
                if t >= 1:
                    out(t - 1)
            out(NT - 1)

        @block.scalar
        def _(act):
            for t in range(NT):
                act.wait_ge(h_done, t + 1)
                if t >= 2:
                    act.wait_ge(g_done, t - 1)
                act.activation(gel[:, t % 2, :], ps_h[t % 2][0:M, :], ACT.Gelu).then_inc(gelu_done, 1)

        @block.vector
        def _(dve):
            def add(t):
                for c in range(C):
                    dve.wait_ge(o_done, C * t + c + 1)
                    dve.tensor_tensor(xf[:, c, cols[t]], ps_o[t % 2][c][:], xf[:, c, cols[t]], ALU.add).then_inc(add_done, 1)
            for t in range(NT):
                dve.wait_ge(gelu_done, t + 1)
                if t >= 2:
                    dve.wait_ge(o_done, C * (t - 1))
                dve.tensor_tensor(g[:, t % 2, :], ps_h[t % 2][0:M, :], gel[:, t % 2, :], ALU.mult).then_inc(g_done, 1)
                if t >= 1:
                    add(t - 1)
            add(NT - 1)
    st.close()



def ternary_ffn(nc, xf, w1T, w2T, h1T, h2T, w3T, scales):
    st = Stage(nc, "ffn1")
    w1 = st.sb("w1", [P, C, INNER])
    w2 = st.sb("w2", [P, C, INNER])
    h1 = st.sb("h1", [P, CI, INNER])
    h2 = st.sb("h2", [P, CI, INNER])
    w3 = st.sb("w3", [P, CI, D])
    sc = st.sb("row_scales", [P, 4 * CI + C])
    xt = st.sb("x_tile", [P, C, W])
    silu = st.sb("silu", [P, 2, W])
    ha = st.sb("hidden_a", [P, CI, W])
    hb = st.sb("hidden_b", [P, CI, W])
    ps = [st.ps(f"bank{k}") for k in range(8)]
    w_here = [st.sem(f"w_here{k}") for k in range(5)]
    x_ready, x_added = st.sem("x_ready"), st.sem("x_added")
    gate_done, up_done, silu_done, gated = (st.sem(n) for n in ("gate_done", "up_done", "silu_done", "gated"))
    mix1_done, gelu1_done, mix2_done, gelu2_done, out_done = (
        st.sem(n) for n in ("mix1_done", "gelu1_done", "mix2_done", "gelu2_done", "out_done"))
    st.start_counters()
    with nc.Block() as block:
        @block.sync
        def _(sp):
            sp.dma_start(w1[:], w1T).then_inc(w_here[0], 16)
            sp.dma_start(w2[:], w2T).then_inc(w_here[0], 16)
            sp.dma_start(sc[:], scales).then_inc(w_here[1], 16)
            sp.dma_start(h1[:], h1T).then_inc(w_here[2], 16)
            sp.dma_start(h2[:], h2T).then_inc(w_here[3], 16)
            sp.dma_start(w3[:], w3T).then_inc(w_here[4], 16)

        @block.tensor
        def _(pe):
            pe.wait_ge(w_here[0], ONE + 32)
            for k in (2, 3, 4):
                pe.wait_ge(w_here[k], ONE + 16)
            with pe.Fori(0, NT) as t:
                pe.wait_ge(x_ready, ONE + t + 1)
                for m in range(CI):
                    rows = slice(m * P, (m + 1) * P)
                    pe.wait_ge(silu_done, ONE + t * CI + max(m - 1, 0))
                    for c in range(C):
                        mm = pe.matmul(ps[m % 2][:], w1[:, c, rows], xt[:, c, :], start=c == 0, stop=c == C - 1)
                    mm.then_inc(gate_done, 1)
                    pe.wait_ge(gated, ONE + t * CI + max(m - 1, 0))
                    for c in range(C):
                        mm = pe.matmul(ps[2 + m % 2][:], w2[:, c, rows], xt[:, c, :], start=c == 0, stop=c == C - 1)
                    mm.then_inc(up_done, 1)
                pe.wait_ge(gated, ONE + t * CI + CI)
                for m in range(CI):
                    pe.wait_ge(gelu1_done, ONE + t * CI + max(m - 1, 0))
                    for c in range(CI):
                        mm = pe.matmul(ps[4 + m % 2][:], h1[:, c, m * P:(m + 1) * P], ha[:, c, :],
                                       start=c == 0, stop=c == CI - 1)
                    mm.then_inc(mix1_done, 1)
                pe.wait_ge(gelu1_done, ONE + t * CI + CI)
                for m in range(CI):
                    pe.wait_ge(gelu2_done, ONE + t * CI + max(m - 1, 0))
                    for c in range(CI):
                        mm = pe.matmul(ps[4 + m % 2][:], h2[:, c, m * P:(m + 1) * P], hb[:, c, :],
                                       start=c == 0, stop=c == CI - 1)
                    mm.then_inc(mix2_done, 1)
                pe.wait_ge(gelu2_done, ONE + t * CI + CI)
                pe.wait_ge(x_added, ONE + t * C)
                for m in range(C):
                    for c in range(CI):
                        mm = pe.matmul(ps[6 + m][:], w3[:, c, m * P:(m + 1) * P], ha[:, c, :],
                                       start=c == 0, stop=c == CI - 1)
                    mm.then_inc(out_done, 1)

        @block.scalar
        def _(act):
            act.wait_ge(w_here[1], ONE + 16)
            with act.Fori(0, NT) as t:
                for m in range(CI):
                    act.wait_ge(gate_done, ONE + t * CI + m + 1)
                    act.wait_ge(gated, ONE + t * CI + max(m - 1, 0))
                    act.activation(silu[:, m % 2, :], ps[m % 2][:], ACT.Silu, scale=sc[:, m:m + 1]).then_inc(silu_done, 1)
                for m in range(CI):
                    act.wait_ge(mix1_done, ONE + t * CI + m + 1)
                    act.activation(hb[:, m, :], ps[4 + m % 2][:], ACT.Gelu,
                                   scale=sc[:, 2 * CI + m:2 * CI + m + 1]).then_inc(gelu1_done, 1)
                act.wait_ge(mix1_done, ONE + t * CI + CI)
                for m in range(CI):
                    act.wait_ge(mix2_done, ONE + t * CI + m + 1)
                    act.activation(ha[:, m, :], ps[4 + m % 2][:], ACT.Gelu,
                                   scale=sc[:, 3 * CI + m:3 * CI + m + 1]).then_inc(gelu2_done, 1)

        @block.vector
        def _(dve):
            dve.wait_ge(w_here[1], ONE + 16)
            with dve.Fori(0, NT) as t:
                dve.wait_ge(up_done, ONE + t * CI)
                dve.wait_ge(x_added, ONE + t * C)
                dve.tensor_copy(xt[:], xf[:, :, bass.ts(t, W)]).then_inc(x_ready, 1)
                dve.wait_ge(out_done, ONE + t * C)
                for m in range(CI):
                    dve.wait_ge(silu_done, ONE + t * CI + m + 1)
                    dve.wait_ge(up_done, ONE + t * CI + m + 1)
                    dve.scalar_tensor_tensor(out=ha[:, m, :], in0=ps[2 + m % 2][:], scalar=sc[:, CI + m:CI + m + 1],
                                             in1=silu[:, m % 2, :], op0=ALU.mult, op1=ALU.mult).then_inc(gated, 1)
                for c in range(C):
                    dve.wait_ge(out_done, ONE + t * C + c + 1)
                    dve.scalar_tensor_tensor(out=xf[:, c, bass.ts(t, W)], in0=ps[6 + c][:],
                                             scalar=sc[:, 4 * CI + c:4 * CI + c + 1], in1=xt[:, c, :],
                                             op0=ALU.mult, op1=ALU.add).then_inc(x_added, 1)
    st.close()


def slot_attention(nc, xf, io, mean_w, eps):
    G3 = 3 * D
    ROUNDS = 3
    TW = S // W
    RMS_EPS = eps[:, 1:2]
    st = Stage(nc, "slot")
    ctxT = st.sb("ctxT", [P, C, B * M])
    wkT, wq, wvT = st.sb("wkT", [P, C, D]), st.sb("wq", [P, C, D]), st.sb("wvT", [P, C, D])
    wihT, whhT = st.sb("wihT", [P, C, G3]), st.sb("whhT", [P, C, G3])
    vecs = st.sb("vectors", [P, 2 * C + 12])
    bias = st.sb("bias", [P, 8])
    sq = st.sb("ctx_square", [P, C, B * M])
    rinv = st.sb("ctx_inverse", [P, B * M])
    root = st.sb("ctx_root", [P, B * M])
    pn = st.sb("ctx_normed", [P, C, B * M])
    kT, vT = st.sb("kT", [P, C, B * M]), st.sb("vT", [P, C, B * M])
    keys = st.sb("keys", [P, C, B * M])
    vals = st.sb("values", [M, B, G3])
    key_b, val_b = st.sb("key_b", [P, C, M]), st.sb("val_b", [M, G3])
    slots = [st.sb(f"slots{k}", [P, C, S]) for k in range(2)]
    ssq = st.sb("slot_square", [P, C, S])
    sroot = st.sb("slot_root", [M, S])
    srs = st.sb("slot_inverse", [M, S])
    score = st.sb("score", [M, S])
    prob = st.sb("prob", [M, S])
    attn = st.sb("attn", [M, S])
    den = st.sb("mass", [M, S])
    mx, nmx, zsum, zinv = (st.sb(n, [M, 1]) for n in ("top", "minus_top", "sum", "sum_inverse"))
    ones_m = st.sb("ones", [M, M])
    gate_r, gate_z = st.sb("reset", [P, 2, W]), st.sb("update", [P, 2, W])
    hid, new = st.sb("hidden", [P, 2, W]), st.sb("new", [P, 2, W])
    pre, arg = st.sb("reset_hidden", [P, 2, W]), st.sb("new_argument", [P, 2, W])
    dif, dif2 = st.sb("difference", [P, 2, W]), st.sb("gated_difference", [P, 2, W])
    bank = [st.ps(f"bank{k}") for k in range(8)]
    here = st.sem("inputs_here")
    names = ("bias_ready csq_done cms_done croot_done cinv_done pn_half pn_done kv_done kv_copied keys_done keys_copied "
             "vals_done vals_copied ones_set row_ready slots_square ms_done sroot_done srs_done scores_done scaled top_done "
             "minus_done prob_done zinv_done attn_done mass_done mass_moved attn_normed hid_done reset_done update_done "
             "cell_done pre_done arg_done new_done dif_done dif2_done slots_done x_copied mass_inv_done x_added").split()
    s = {n: st.sem(n) for n in names}
    HALVES = ROUNDS * TW * C
    st.start_counters()
    with nc.Block() as block:
        @block.sync
        def _(sp):
            for dst, src in ((ctxT, "ctxT"), (wkT, "slot_wkT"), (wq, "slot_wq"), (wvT, "slot_wvT"), (wihT, "slot_wihT"),
                             (whhT, "slot_whhT"), (vecs, "slot_vectors")):
                sp.dma_start(dst[:], io[src]).then_inc(here, 16)

        @block.tensor
        def _(pe):
            pe.wait_ge(s["csq_done"], ONE + 1)
            for c in range(C):
                mm = pe.matmul(bank[0][:, 0:B * M], mean_w[:], sq[:, c, :], start=c == 0, stop=c == C - 1)
            mm.then_inc(s["cms_done"], 1)
            pe.wait_ge(s["pn_done"], ONE + C)
            for k, w in enumerate((wkT, wvT)):
                for m in range(C):
                    for c in range(C):
                        mm = pe.matmul(bank[1 + 2 * k + m][:, 0:B * M], w[:, c, m * P:(m + 1) * P], pn[:, c, :],
                                       start=c == 0, stop=c == C - 1)
                    mm.then_inc(s["kv_done"], 1)
            pe.wait_ge(s["kv_copied"], ONE + 2 * C)
            for m in range(C):
                for c in range(C):
                    mm = pe.matmul(bank[5 + m][:, 0:B * M], wq[:, c, m * P:(m + 1) * P], kT[:, c, :],
                                   start=c == 0, stop=c == C - 1)
                mm.then_inc(s["keys_done"], 1)
            for b in range(B):
                for h in range(2):
                    n = 2 * b + h
                    if n >= 2:
                        pe.wait_ge(s["vals_copied"], ONE + n - 1)
                    for c in range(C):
                        mm = pe.matmul(bank[1 + n % 2][0:M, 0:G3 // 2], vT[:, c, b * M:(b + 1) * M],
                                       wihT[:, c, h * (G3 // 2):(h + 1) * (G3 // 2)], start=c == 0, stop=c == C - 1)
                    mm.then_inc(s["vals_done"], 1)
            pe.wait_ge(s["ones_set"], ONE + 1)
            with pe.Fori(0, B) as b:
                pe.wait_ge(s["row_ready"], ONE + 2 * b + 2)
                for r in range(ROUNDS):
                    n0 = b * ROUNDS + r
                    cur = slots[(r + 1) % 2]
                    pe.wait_ge(s["slots_square"], ONE + n0 + 1)
                    pe.wait_ge(s["slots_done"], ONE + b * HALVES + r * TW * C)
                    for t in range(TW):
                        for c in range(C):
                            mm = pe.matmul(bank[t][0:M, :], mean_w[:, 0:M], ssq[:, c, t * W:(t + 1) * W],
                                           start=c == 0, stop=c == C - 1)
                        mm.then_inc(s["ms_done"], 1)
                        for c in range(C):
                            mm = pe.matmul(bank[2 + t][0:M, :], key_b[:, c, :], cur[:, c, t * W:(t + 1) * W],
                                           start=c == 0, stop=c == C - 1)
                        mm.then_inc(s["scores_done"], 1)
                    pe.wait_ge(s["attn_done"], ONE + n0 + 1)
                    for t in range(TW):
                        pe.matmul(bank[t][0:M, :], ones_m[:], attn[:, t * W:(t + 1) * W], start=True, stop=True) \
                            .then_inc(s["mass_done"], 1)
                    pe.wait_ge(s["attn_normed"], ONE + n0 + 1)
                    for t in range(TW):
                        for m in range(C):
                            k = t * C + m
                            j = b * HALVES + r * TW * C + k
                            if k >= 2:
                                pe.wait_ge(s["arg_done"], ONE + j - 1)
                                pe.wait_ge(s["update_done"], ONE + j - 1)
                            x = slice(t * W, (t + 1) * W)
                            q = bank[4 * (k % 2):4 * (k % 2) + 4]
                            for g in range(2):
                                rows = slice(g * D + m * P, g * D + (m + 1) * P)
                                for c in range(C):
                                    pe.matmul(q[g][:], whhT[:, c, rows], cur[:, c, x], start=c == 0, stop=False)
                                pe.matmul(q[g][:], val_b[:, rows], prob[:, x], start=False, stop=True).then_inc(s["cell_done"], 1)
                            rows = slice(2 * D + m * P, 2 * D + (m + 1) * P)
                            for c in range(C):
                                mm = pe.matmul(q[2][:], whhT[:, c, rows], cur[:, c, x], start=c == 0, stop=c == C - 1)
                            mm.then_inc(s["cell_done"], 1)
                            pe.matmul(q[3][:], val_b[:, rows], prob[:, x], start=True, stop=True).then_inc(s["cell_done"], 1)

        @block.scalar
        def _(act):
            act.wait_ge(here, ONE + 16 * 7)
            act.activation(sq[:], ctxT[:], ACT.Square).then_inc(s["csq_done"], 1)
            act.wait_ge(s["cms_done"], ONE + 1)
            act.activation(root[:], bank[0][:, 0:B * M], ACT.Sqrt, bias=RMS_EPS).then_inc(s["croot_done"], 1)
            for k, dst in enumerate((kT, vT)):
                for m in range(C):
                    act.wait_ge(s["kv_done"], ONE + 2 * k + m + 1)
                    act.copy(dst[:, m, :], bank[1 + 2 * k + m][:, 0:B * M]).then_inc(s["kv_copied"], 1)
            for b in range(B):
                for h in range(2):
                    n = 2 * b + h
                    act.wait_ge(s["vals_done"], ONE + n + 1)
                    act.copy(vals[:, b, h * (G3 // 2):(h + 1) * (G3 // 2)], bank[1 + n % 2][0:M, 0:G3 // 2]) \
                        .then_inc(s["vals_copied"], 1)
            act.wait_ge(s["bias_ready"], ONE + 4)
            with act.Fori(0, B) as b:
                for r in range(ROUNDS):
                    n0 = b * ROUNDS + r
                    cur = slots[(r + 1) % 2]
                    act.wait_ge(s["slots_done"], ONE + b * HALVES + r * TW * C)
                    if r == 0:
                        act.wait_ge(s["x_copied"], ONE + b + 1)
                    act.wait_ge(s["ms_done"], ONE + TW * n0)
                    act.activation(ssq[:], cur[:], ACT.Square).then_inc(s["slots_square"], 1)
                    for t in range(TW):
                        act.wait_ge(s["ms_done"], ONE + TW * n0 + t + 1)
                        act.wait_ge(s["srs_done"], ONE + TW * n0)
                        act.activation(sroot[:, t * W:(t + 1) * W], bank[t][0:M, :], ACT.Sqrt, bias=eps[0:M, 1:2]) \
                            .then_inc(s["sroot_done"], 1)
                    act.wait_ge(s["minus_done"], ONE + n0 + 1)
                    act.activation(attn[:], score[:], ACT.Exp, bias=nmx[:], accum_out=zsum[:]).then_inc(s["prob_done"], 1)
                    for k in range(TW * C):
                        j = b * HALVES + r * TW * C + k
                        q = bank[4 * (k % 2):4 * (k % 2) + 4]
                        m = k % C
                        act.wait_ge(s["cell_done"], ONE + 4 * j + 1)
                        if k >= 2:
                            act.wait_ge(s["slots_done"], ONE + j - 1)
                        act.activation(gate_r[:, k % 2, :], q[0][:], ACT.Tanh, bias=bias[:, m:m + 1], scale=0.5) \
                            .then_inc(s["reset_done"], 1)
                        act.wait_ge(s["cell_done"], ONE + 4 * j + 2)
                        act.activation(gate_z[:, k % 2, :], q[1][:], ACT.Tanh, bias=bias[:, C + m:C + m + 1], scale=0.5) \
                            .then_inc(s["update_done"], 1)
                        act.wait_ge(s["cell_done"], ONE + 4 * j + 3)
                        act.activation(hid[:, k % 2, :], q[2][:], ACT.Identity, bias=bias[:, 6 + m:7 + m], scale=0.5) \
                            .then_inc(s["hid_done"], 1)
                        act.wait_ge(s["arg_done"], ONE + j + 1)
                        act.activation(new[:, k % 2, :], arg[:, k % 2, :], ACT.Tanh).then_inc(s["new_done"], 1)

        @block.gpsimd
        def _(pool):
            with pool.Fori(0, B) as b:
                pool.wait_ge(s["keys_copied"], ONE + C)
                pool.wait_ge(s["vals_copied"], ONE + 2 * B)
                pool.wait_ge(s["scores_done"], ONE + b * ROUNDS * TW)
                pool.wait_ge(s["cell_done"], ONE + b * HALVES * 4)
                pool.tensor_copy(key_b[:], keys[:, :, bass.ts(b, M)]).then_inc(s["row_ready"], 1)
                pool.tensor_copy(val_b[:], vals[:, b, :]).then_inc(s["row_ready"], 1)
                for r in range(ROUNDS):
                    cur, nxt = slots[(r + 1) % 2], slots[r % 2]
                    for k in range(TW * C):
                        t, m = k // C, k % C
                        j = b * HALVES + r * TW * C + k
                        x = slice(t * W, (t + 1) * W)
                        pool.wait_ge(s["new_done"], ONE + j + 1)
                        if k >= 2:
                            pool.wait_ge(s["dif2_done"], ONE + j - 1)
                        pool.tensor_tensor(dif[:, k % 2, :], cur[:, m, x], new[:, k % 2, :], ALU.subtract) \
                            .then_inc(s["dif_done"], 1)

        @block.vector
        def _(dve):
            dve.wait_ge(here, ONE + 16 * 7)
            dve.memset(ones_m[:], 1.0).then_inc(s["ones_set"], 1)
            dve.tensor_tensor(bias[:, 0:4], vecs[:, 4:8], vecs[:, 10:14], ALU.add).then_inc(s["bias_ready"], 1)
            dve.wait_ge(s["bias_ready"], ONE + 1)
            dve.tensor_scalar(bias[:, 0:4], bias[:, 0:4], 0.5, None, ALU.mult).then_inc(s["bias_ready"], 1)
            dve.tensor_copy(bias[:, 4:6], vecs[:, 8:10]).then_inc(s["bias_ready"], 1)
            dve.tensor_scalar(bias[:, 6:8], vecs[:, 14:16], 0.5, None, ALU.mult).then_inc(s["bias_ready"], 1)
            dve.wait_ge(s["croot_done"], ONE + 1)
            dve.reciprocal(rinv[:], root[:]).then_inc(s["cinv_done"], 1)
            dve.wait_ge(s["cinv_done"], ONE + 1)
            for c in range(C):
                dve.scalar_tensor_tensor(out=pn[:, c, :], in0=ctxT[:, c, :], scalar=vecs[:, C + c:C + c + 1],
                                         in1=rinv[:], op0=ALU.mult, op1=ALU.mult).then_inc(s["pn_done"], 1)
            for m in range(C):
                dve.wait_ge(s["keys_done"], ONE + m + 1)
                dve.tensor_scalar(keys[:, m, :], bank[5 + m][:, 0:B * M], vecs[:, m:m + 1], float(D) ** -0.5,
                                  ALU.mult, ALU.mult).then_inc(s["keys_copied"], 1)
            dve.wait_ge(s["bias_ready"], ONE + 4)
            with dve.Fori(0, B) as b:
                dve.wait_ge(s["cell_done"], ONE + b * HALVES * 4)
                dve.wait_ge(s["dif_done"], ONE + b * HALVES)
                dve.tensor_copy(slots[1][:], xf[:, :, bass.ts(b, S)]).then_inc(s["x_copied"], 1)
                for r in range(ROUNDS):
                    n0 = b * ROUNDS + r
                    nxt = slots[r % 2]
                    for t in range(TW):
                        x = slice(t * W, (t + 1) * W)
                        dve.wait_ge(s["sroot_done"], ONE + TW * n0 + t + 1)
                        dve.reciprocal(srs[:, x], sroot[:, x]).then_inc(s["srs_done"], 1)
                        dve.wait_ge(s["srs_done"], ONE + TW * n0 + t + 1)
                        dve.wait_ge(s["scores_done"], ONE + TW * n0 + t + 1)
                        dve.tensor_tensor(score[:, x], bank[2 + t][0:M, :], srs[:, x], ALU.mult).then_inc(s["scaled"], 1)
                    dve.wait_ge(s["scaled"], ONE + TW * (n0 + 1))
                    dve.tensor_reduce(mx[:], score[:], AX.X, ALU.max).then_inc(s["top_done"], 1)
                    dve.wait_ge(s["top_done"], ONE + n0 + 1)
                    dve.tensor_scalar(nmx[:], mx[:], -1.0, None, ALU.mult).then_inc(s["minus_done"], 1)
                    dve.wait_ge(s["prob_done"], ONE + n0 + 1)
                    dve.reciprocal(zinv[:], zsum[:]).then_inc(s["zinv_done"], 1)
                    dve.wait_ge(s["zinv_done"], ONE + n0 + 1)
                    dve.tensor_scalar(attn[:], attn[:], zinv[:], None, ALU.mult).then_inc(s["attn_done"], 1)
                    for t in range(TW):
                        x = slice(t * W, (t + 1) * W)
                        dve.wait_ge(s["mass_done"], ONE + TW * n0 + t + 1)
                        dve.tensor_scalar(den[:, x], bank[t][0:M, :], 1e-6, None, ALU.add).then_inc(s["mass_moved"], 1)
                    dve.wait_ge(s["mass_moved"], ONE + TW * (n0 + 1))
                    dve.reciprocal(srs[:], den[:]).then_inc(s["mass_inv_done"], 1)
                    dve.wait_ge(s["mass_inv_done"], ONE + n0 + 1)
                    dve.tensor_tensor(prob[:], attn[:], srs[:], ALU.mult).then_inc(s["attn_normed"], 1)
                    for k in range(TW * C):
                        t, m = k // C, k % C
                        j = b * HALVES + r * TW * C + k
                        x = slice(t * W, (t + 1) * W)
                        q = bank[4 * (k % 2):4 * (k % 2) + 4]
                        dve.wait_ge(s["reset_done"], ONE + j + 1)
                        dve.wait_ge(s["hid_done"], ONE + j + 1)
                        dve.scalar_tensor_tensor(out=pre[:, k % 2, :], in0=gate_r[:, k % 2, :], scalar=1.0,
                                                 in1=hid[:, k % 2, :], op0=ALU.add, op1=ALU.mult).then_inc(s["pre_done"], 1)
                        dve.wait_ge(s["pre_done"], ONE + j + 1)
                        dve.wait_ge(s["cell_done"], ONE + 4 * j + 4)
                        dve.scalar_tensor_tensor(out=arg[:, k % 2, :], in0=q[3][:], scalar=bias[:, 4 + m:5 + m],
                                                 in1=pre[:, k % 2, :], op0=ALU.add, op1=ALU.add).then_inc(s["arg_done"], 1)
                        dve.wait_ge(s["dif_done"], ONE + j + 1)
                        dve.wait_ge(s["update_done"], ONE + j + 1)
                        dve.scalar_tensor_tensor(out=dif2[:, k % 2, :], in0=gate_z[:, k % 2, :], scalar=1.0,
                                                 in1=dif[:, k % 2, :], op0=ALU.add, op1=ALU.mult).then_inc(s["dif2_done"], 1)
                        dve.wait_ge(s["dif2_done"], ONE + j + 1)
                        dve.scalar_tensor_tensor(out=nxt[:, m, x], in0=dif2[:, k % 2, :], scalar=0.5,
                                                 in1=new[:, k % 2, :], op0=ALU.mult, op1=ALU.add).then_inc(s["slots_done"], 1)
                dve.wait_ge(s["slots_done"], ONE + (b + 1) * HALVES)
                dve.tensor_tensor(xf[:, :, bass.ts(b, S)], xf[:, :, bass.ts(b, S)], slots[0][:], ALU.add) \
                    .then_inc(s["x_added"], 1)
            dve.wait_ge(s["x_added"], ONE + B)
    st.close()


def quantised_ffn(nc, xf, io, eps):
    TT = 128
    N = T // TT
    HALF = INNER // 2
    MAGIC = 1.5 * 2.0 ** 23
    st = Stage(nc, "ffn0")
    wf = [st.sb(f"w_float{k}", [P, 2 * INNER]) for k in range(3)]
    wq = [st.sb(f"w_tern{k}", [P, 2 * INNER], BF16) for k in range(3)]
    wabs = st.sb("w_abs", [P, 2 * INNER])
    wr = st.sb("w_rounded", [P, 2 * INNER])
    wsum, wmean, wscale = st.sb("w_sum", [P, 3]), st.sb("w_mean", [P, 3]), st.sb("w_scale", [P, 3])
    wmean127 = st.sb("w_mean_127", [P, 3])
    count_w = st.sb("count_w", [P, P])
    magic = st.sb("magic", [P, 1])
    identf, identb = st.sb("identity", [P, P]), st.sb("identity_b", [P, P], BF16)
    xc = st.sb("x_tile", [P, 2, C, TT])
    xr, xq = st.sb("x_rounded", [P, D]), st.sb("x_quantised", [P, D], BF16)
    xqT = st.sb("x_quantisedT", [P, 2, C, TT], BF16)
    sg, h = st.sb("silu", [P, INNER]), st.sb("h", [P, INNER])
    hr, hq = st.sb("h_rounded", [P, INNER]), st.sb("h_quantised", [P, INNER], BF16)
    hqT = st.sb("h_quantisedT", [P, CI, TT], BF16)
    o = st.sb("o", [P, D])
    xm = st.sb("x_scales", [P, 2, 6])
    hm = st.sb("h_scales", [P, 2, 5])
    ps_x = st.ps("xT", [P, D])
    ps_q = st.ps("xqT_bank", [P, C, TT], BF16)
    ps_g = [st.ps(f"gate{k}") for k in range(2)]
    ps_u = [st.ps(f"up{k}") for k in range(2)]
    ps_h = st.ps("hqT_bank", [P, CI, TT], BF16)
    ps_o = st.ps("out", [P, 2, D])
    names = ("here consts wsum_done wtot_done wm_done wstep wq_done x_copied x_turned xmax xstep xr_done xq_done xq_turned "
             "xqT_done gu_done silu_done h_done hmax hstep hr_done hq_done h_turned hqT_done down_done o_done o_turned "
             "added h_half").split()
    s = {n: st.sem(n) for n in names}

    def cols(n):
        return bass.ts(n, TT)

    st.start_counters()
    with nc.Block() as block:
        @block.sync
        def _(sp):
            for k, name in enumerate(("q_gateT", "q_upT", "q_downT")):
                sp.dma_start(wf[k][:], io[name].rearrange("p c n -> p (c n)")).then_inc(s["here"], 16)
            sp.dma_start(identf[:], io["identity"]).then_inc(s["here"], 16)

        @block.tensor
        def _(pe):
            pe.wait_ge(s["wsum_done"], ONE + 3)
            pe.wait_ge(s["consts"], ONE + 3)
            pe.matmul(ps_x[:, 0:3], count_w[:], wsum[:], start=True, stop=True).then_inc(s["wtot_done"], 1)
            pe.wait_ge(s["wq_done"], ONE + 3)
            pe.wait_ge(s["wm_done"], ONE + 1)

            def turn_x(n, u):
                pe.wait_ge(s["x_copied"], ONE + n + 1)
                pe.wait_ge(s["xr_done"], ONE + n)
                pe.wait_ge(s["xmax"], ONE + n)
                for c in range(C):
                    mm = pe.transpose(ps_x[:, c * TT:(c + 1) * TT], xc[:, u, c, :], identf[:])
                mm.then_inc(s["x_turned"], 1)

            def turn_xq(n):
                pe.wait_ge(s["xq_done"], ONE + n + 1)
                pe.wait_ge(s["xqT_done"], ONE + n)
                for c in range(C):
                    mm = pe.transpose(ps_q[:, c, :], xq[:, c * TT:(c + 1) * TT], identb[:])
                mm.then_inc(s["xq_turned"], 1)

            def gate_up(n, u):
                pe.wait_ge(s["xqT_done"], ONE + n + 1)
                pe.wait_ge(s["h_done"], ONE + n)
                pe.wait_ge(s["silu_done"], ONE + 2 * n)
                for bank, w in ((ps_g, wq[0]), (ps_u, wq[1])):
                    for f in range(2):
                        for c in range(C):
                            mm = pe.matmul(bank[f][:], xqT[:, u, c, :], w[:, c * INNER + f * HALF:c * INNER + (f + 1) * HALF],
                                           start=c == 0, stop=c == C - 1)
                        mm.then_inc(s["gu_done"], 1)

            def turn_hq(n):
                pe.wait_ge(s["hq_done"], ONE + n + 1)
                pe.wait_ge(s["hqT_done"], ONE + n)
                for c in range(CI):
                    mm = pe.transpose(ps_h[:, c, :], hq[:, c * TT:(c + 1) * TT], identb[:])
                mm.then_inc(s["h_turned"], 1)

            def down(n):
                pe.wait_ge(s["hqT_done"], ONE + n + 1)
                pe.wait_ge(s["o_done"], ONE + n)
                pe.wait_ge(s["added"], ONE + n)
                for c in range(CI):
                    mm = pe.matmul(ps_o[:, 0, :], hqT[:, c, :], wq[2][:, c * D:(c + 1) * D], start=c == 0, stop=c == CI - 1)
                mm.then_inc(s["down_done"], 1)

            def turn_o(n):
                pe.wait_ge(s["o_done"], ONE + n + 1)
                for c in range(C):
                    mm = pe.transpose(ps_o[:, 1, c * TT:(c + 1) * TT], o[:, c * TT:(c + 1) * TT], identf[:])
                mm.then_inc(s["o_turned"], 1)

            def step(n, u, ahead=2):
                if ahead >= 1:
                    gate_up(n + 1, 1 - u)
                if ahead >= 2:
                    turn_x(n + 2, u)
                turn_hq(n)
                down(n)
                if ahead >= 2:
                    turn_xq(n + 2)
                turn_o(n)

            turn_x(0, 0)
            turn_xq(0)
            turn_x(1, 1)
            turn_xq(1)
            gate_up(0, 0)
            with pe.Fori(0, N // 2 - 2) as i:
                step(2 * i, 0)
                step(2 * i + 1, 1)
            step(N - 4, 0)
            step(N - 3, 1)
            step(N - 2, 0, ahead=1)
            step(N - 1, 1, ahead=0)

        @block.scalar
        def _(act):
            for k in range(3):
                act.wait_ge(s["here"], ONE + 16 * 4)
                if k:
                    act.wait_ge(s["wsum_done"], ONE + k)
                act.activation(wabs[:], wf[k][:], ACT.Abs, accum_out=wsum[:, k:k + 1]).then_inc(s["wsum_done"], 1)
            act.wait_ge(s["consts"], ONE + 4)

            def copy_x(n, u):
                act.wait_ge(s["x_turned"], ONE + n)
                act.copy(xc[:, u, :, :], xf[:, :, cols(n)]).then_inc(s["x_copied"], 1)

            def round_x(n, u):
                act.wait_ge(s["xstep"], ONE + 5 * n + 5)
                act.wait_ge(s["xq_done"], ONE + n)
                act.activation(xr[:], ps_x[:], ACT.Identity, bias=magic[:], scale=xm[:, u, 3:4]).then_inc(s["xr_done"], 1)

            def copy_xq(n, u):
                act.wait_ge(s["xq_turned"], ONE + n + 1)
                act.copy(xqT[:, u, :, :], ps_q[:]).then_inc(s["xqT_done"], 1)

            def silu(n, u):
                act.wait_ge(s["h_done"], ONE + n)
                for f in range(2):
                    act.wait_ge(s["gu_done"], ONE + 4 * n + f + 1)
                    act.activation(sg[:, f * HALF:(f + 1) * HALF], ps_g[f][:], ACT.Silu, scale=xm[:, u, 4:5]) \
                        .then_inc(s["silu_done"], 1)

            def round_h(n, u):
                act.wait_ge(s["hstep"], ONE + 4 * n + 4)
                act.wait_ge(s["hq_done"], ONE + n)
                act.activation(hr[:], h[:], ACT.Identity, bias=magic[:], scale=hm[:, u, 3:4]).then_inc(s["hr_done"], 1)

            def copy_hq(n):
                act.wait_ge(s["h_turned"], ONE + n + 1)
                act.wait_ge(s["down_done"], ONE + n)
                act.copy(hqT[:], ps_h[:]).then_inc(s["hqT_done"], 1)

            def scale_o(n, u):
                act.wait_ge(s["down_done"], ONE + n + 1)
                act.wait_ge(s["o_turned"], ONE + n)
                act.activation(o[:], ps_o[:, 0, :], ACT.Copy, scale=hm[:, u, 4:5]).then_inc(s["o_done"], 1)

            def step(n, u, ahead=3):
                if ahead >= 1:
                    silu(n + 1, 1 - u)
                copy_hq(n)
                if ahead >= 3:
                    copy_x(n + 3, 1 - u)
                if ahead >= 1:
                    round_h(n + 1, 1 - u)
                if ahead >= 2:
                    round_x(n + 2, u)
                scale_o(n, u)
                if ahead >= 2:
                    copy_xq(n + 2, u)

            copy_x(0, 0)
            round_x(0, 0)
            copy_xq(0, 0)
            copy_x(1, 1)
            round_x(1, 1)
            copy_xq(1, 1)
            copy_x(2, 0)
            silu(0, 0)
            round_h(0, 0)
            with act.Fori(0, N // 2 - 2) as i:
                step(2 * i, 0)
                step(2 * i + 1, 1)
            step(N - 4, 0)
            step(N - 3, 1, ahead=2)
            step(N - 2, 0, ahead=1)
            step(N - 1, 1, ahead=0)

        @block.gpsimd
        def _(pool):
            pool.memset(count_w[:], 1.0 / (INNER * D)).then_inc(s["consts"], 1)
            pool.memset(magic[:], MAGIC).then_inc(s["consts"], 1)
            pool.wait_ge(s["here"], ONE + 16 * 4)
            pool.tensor_copy(identb[:], identf[:]).then_inc(s["consts"], 1)

        @block.vector
        def _(dve):
            dve.wait_ge(s["wtot_done"], ONE + 1)
            dve.tensor_scalar(wmean[:], ps_x[:, 0:3], 1e-5, None, ALU.max).then_inc(s["wm_done"], 1)
            dve.wait_ge(s["wm_done"], ONE + 1)
            dve.reciprocal(wscale[:], wmean[:]).then_inc(s["wstep"], 1)
            dve.tensor_scalar(wmean127[:], wmean[:], 1.0 / 127.0, None, ALU.mult).then_inc(s["wstep"], 1)
            dve.wait_ge(s["wstep"], ONE + 2)
            for k in range(3):
                if k:
                    dve.wait_ge(s["wq_done"], ONE + k)
                dve.tensor_scalar(wr[:], wf[k][:], wscale[:, k:k + 1], MAGIC, ALU.mult, ALU.add).then_inc(s["wstep"], 1)
                dve.wait_ge(s["wstep"], ONE + 3 + 2 * k)
                dve.tensor_scalar(wr[:], wr[:], -MAGIC, 1.0, ALU.add, ALU.min).then_inc(s["wstep"], 1)
                dve.wait_ge(s["wstep"], ONE + 4 + 2 * k)
                dve.tensor_scalar(wq[k][:], wr[:], -1.0, None, ALU.max).then_inc(s["wq_done"], 1)
            dve.memset(xm[:], 1.0).then_inc(s["consts"], 1)
            dve.wait_ge(s["consts"], ONE + 4)

            def scales(n, u, m, mx, step, outs):
                k = 3 + len(outs)
                def next_step(a, c):
                    a.then_inc(step, 1)
                    dve.wait_ge(step, ONE + k * n + c)
                next_step(dve.tensor_scalar(m[:, u, 1:2], m[:, u, 0:1], 1e-5, None, ALU.max), 1)
                next_step(dve.reciprocal(m[:, u, 2:3], m[:, u, 1:2]), 2)
                dve.tensor_scalar(m[:, u, 3:4], m[:, u, 2:3], 127.0, None, ALU.mult).then_inc(step, 1)
                for i, w in enumerate(outs):
                    dve.tensor_scalar(m[:, u, 4 + i:5 + i], m[:, u, 1:2], wmean127[:, w:w + 1], None, ALU.mult).then_inc(step, 1)

            def scale_x(n, u):
                dve.wait_ge(s["x_turned"], ONE + n + 1)
                dve.tensor_reduce(xm[:, u, 0:1], ps_x[:], AX.X, ALU.max, apply_absolute_value=True).then_inc(s["xmax"], 1)
                dve.wait_ge(s["xmax"], ONE + n + 1)
                scales(n, u, xm, s["xmax"], s["xstep"], (0, 1))

            def quant_x(n):
                dve.wait_ge(s["xr_done"], ONE + n + 1)
                dve.wait_ge(s["xq_turned"], ONE + n)
                dve.tensor_scalar(xq[:], xr[:], -MAGIC, 127.0, ALU.add, ALU.min).then_inc(s["xq_done"], 1)

            def gated(n, u):
                dve.wait_ge(s["hr_done"], ONE + n)
                dve.wait_ge(s["hmax"], ONE + n)
                dve.wait_ge(s["xstep"], ONE + 5 * n + 5)
                for f in range(2):
                    dve.wait_ge(s["gu_done"], ONE + 4 * n + 3 + f)
                    dve.wait_ge(s["silu_done"], ONE + 2 * n + f + 1)
                    half = slice(f * HALF, (f + 1) * HALF)
                    mm = dve.scalar_tensor_tensor(out=h[:, half], in0=ps_u[f][:], scalar=xm[:, u, 5:6], in1=sg[:, half],
                                                  op0=ALU.mult, op1=ALU.mult)
                    mm.then_inc(s["h_done" if f else "h_half"], 1)
                dve.wait_ge(s["h_half"], ONE + n + 1)
                dve.wait_ge(s["h_done"], ONE + n + 1)
                dve.tensor_reduce(hm[:, u, 0:1], h[:], AX.X, ALU.max, apply_absolute_value=True).then_inc(s["hmax"], 1)
                dve.wait_ge(s["hmax"], ONE + n + 1)
                scales(n, u, hm, s["hmax"], s["hstep"], (2,))

            def add(n):
                dve.wait_ge(s["o_turned"], ONE + n + 1)
                dve.tensor_tensor(xf[:, :, cols(n)], xf[:, :, cols(n)],
                                  ps_o[:, 1, :].rearrange("p (c t) -> p c t", c=C), ALU.add).then_inc(s["added"], 1)

            def quant_h(n):
                dve.wait_ge(s["hr_done"], ONE + n + 1)
                dve.wait_ge(s["h_turned"], ONE + n)
                dve.tensor_scalar(hq[:], hr[:], -MAGIC, 127.0, ALU.add, ALU.min).then_inc(s["hq_done"], 1)

            def step(n, u, ahead=2):
                if ahead >= 1:
                    gated(n + 1, 1 - u)
                if ahead >= 2:
                    scale_x(n + 2, u)
                if ahead >= 1:
                    quant_h(n + 1)
                if ahead >= 2:
                    quant_x(n + 2)
                add(n)

            scale_x(0, 0)
            quant_x(0)
            scale_x(1, 1)
            quant_x(1)
            gated(0, 0)
            quant_h(0)
            with dve.Fori(0, N // 2 - 2) as i:
                step(2 * i, 0)
                step(2 * i + 1, 1)
            step(N - 4, 0)
            step(N - 3, 1)
            step(N - 2, 0, ahead=1)
            step(N - 1, 1, ahead=0)
    st.close()


def sparse_attention(nc, xf, io, eps):
    QT, NQ, PAD = 128, S // 128, 64
    NB, SEL = S // 16, 16
    CS, WK = NB + SEL, PAD + QT
    KEYS = CS + WK
    G = 4
    UQ = 4
    NG = H // G
    VA = DH + 1
    NEG = -1e30
    st = Stage(nc, "nsa")
    names_w = ("wq", "wqs", "wk", "wks", "wv", "wo")
    w = {n: st.sb(n, [P, C, D]) for n in names_w}
    wg, bg = st.sb("wg", [P, C, 3]), st.sb("bg", [P, 3])
    bo = st.sb("bo", [P, C])
    cos, sin = st.sb("cos", [P, S]), st.sb("sin", [P, S])
    wkc, wvc = st.sb("wk_comp", [P, 16]), st.sb("wv_comp", [P, 1])
    pe, peT = st.sb("pe", [16, D]), st.sb("peT", [P, C, 16])
    parity = st.sb("head_parity", [P, 2])
    mask_f = st.sb("mask_float", [P, KEYS])
    mask = st.sb("mask", [P, NQ, KEYS], BF16)
    ident, identb = st.sb("identity", [P, P]), st.sb("identity_b", [P, P], BF16)
    block_of = st.sb("block_of", [P, NQ, NB])
    comp_w = st.sb("comp_w", [P, NQ, NB])
    pe_w = st.sb("pe_w", [16, NB])
    token_no = st.sb("token_number", [P, NQ])
    offset = st.sb("sel_offset", [P, SEL])
    ones = st.sb("ones", [1, P])
    xb = st.sb("x_row", [P, C, PAD + S])
    t1, t2 = st.sb("rope_cos", [P, 2, W]), st.sb("rope_sin", [P, 2, W])
    qT = st.sb("qT", [P, C, S])
    kr = st.sb("kT", [P, C, S])
    keo = st.sb("k_even_odd", [P, C, 2, PAD + S])
    kc = st.sb("k_comp_sel", [P, C, 2, CS])
    kcomp = st.sb("k_comp", [P, C, CS])
    kw_prod = st.sb("k_weighted", [P, S])
    pe_k = st.sb("pe_weighted", [P, C, 16])
    pe_sum = st.sb("pe_sum", [P, C])
    ktok = st.sb("k_token", [P, NQ, D])
    v = st.sb("v", [P, NQ, H, VA])
    vprev = st.sb("v_before", [PAD, NQ, H, VA])
    vcs = st.sb("v_comp_sel", [CS, H, 2 * VA])
    qsum = st.sb("q_sum", [P, C])
    imp = st.sb("importance", [1, NB])
    top = st.sb("top_values", [1, 8])
    top_i = st.sb("top_index", [1, 8], mybir.dt.uint32)
    pos0 = st.sb("top_start", [1, 2])
    pos = st.sb("sel_position", [P, SEL])
    sel = st.sb("sel_onehot", [P, NQ, SEL])
    gl, ge = st.sb("gate_logit", [P, NQ, 3]), st.sb("gate_exp", [P, NQ, 3])
    gmx, gsum, ginv = (st.sb(n, [P, NQ]) for n in ("gate_top", "gate_sum", "gate_inverse"))
    gate = st.sb("gate", [P, NQ, 3])
    q_t = st.sb("q_tile", [P, 2, C, QT])
    k_t = st.sb("k_tile", [P, 2, C * 2, WK])
    v_t, vp_t = st.sb("v_tile", [P, 2, H, VA]), st.sb("v_before_tile", [PAD, 2, H, VA])
    m_t = st.sb("mask_tile", [P, 2, KEYS], BF16)
    mx = st.sb("top", [P, 2, 3, G])
    prob = st.sb("prob", [P, 2, G * KEYS])
    pT = st.sb("probT", [P, 2, 3, G * QT])
    den, rden, rg = (st.sb(n, [P, H, 3]) for n in ("sum", "sum_inverse", "branch_weight"))
    wo3 = st.sb("weighted", [P, H, 3, DH])
    att = st.sb("attention", [P, D])
    attT = st.sb("attentionT", [P, C, QT])
    S_ = st.ps("scores", [P, 3, W])
    T_ = st.ps("turned", [P, 3, W])
    O_ = st.ps("out", [P, 2, W])
    loads = ([(w[n][:], "nsa_" + n) for n in names_w] + [(wg[:], "nsa_wg"), (bg[:], "nsa_bg"), (bo[:], "nsa_bo"), (cos[:], "nsa_cos"),
             (sin[:], "nsa_sin"), (wkc[:], "nsa_wk_comp"), (wvc[:], "nsa_wv_comp"), (pe[:], "nsa_pe"), (peT[:], "nsa_peT"),
             (parity[:], "nsa_parity"), (ident[:], "identity"), (block_of[:], "nsa_block_of"), (token_no[:], "nsa_token"),
             (offset[:], "nsa_offset")])
    names = ("here mask_here mask_cast consts cw pew x_copied rope_mm ropec ropes roped k_split v_mm v_moved kc_w kc_red kc_added "
             "cv_mm cv_moved qsum_done imp_mm imp_moved top_done topi_done posf pos_mm pos_done sel_done mask_done ktok_mm ktok_moved "
             "selk_mm selk_moved kc_split g_mm g_logit g_top g_shift g_exp g_sum g_inv gate_done vcs_mm vcs_moved tile_copied scores_done "
             "max_done clamp_done shifted exp_done turned pT_moved pv_done den_done rden_done rg_done weighted att_done att_turned "
             "attT_moved wo_done x_added peT_w pe_sum pew0 ones_set carrier").split()
    s = {n: st.sem(n) for n in names}

    def head(g, j):
        return j // 2, 8 * (j // 2) + 2 * g + j % 2, j % 2

    st.start_counters()
    AHEAD = ONE + NG

    with nc.Block() as block:
        @block.sync
        def _(sp):
            for dst, src in loads:
                sp.dma_start(dst, io[src]).then_inc(s["here"], 16)
            with sp.Fori(0, NQ) as i:
                sp.wait_ge(s["mask_cast"], ONE + i)
                sp.dma_start(mask_f[:], io["nsa_mask"][:, i, :]).then_inc(s["mask_here"], 16)

        @block.tensor
        def _(pe_):
            pe_.wait_ge(s["here"], ONE + 16 * len(loads))
            pe_.wait_ge(s["consts"], ONE + 8)
            pe_.wait_ge(s["cw"], ONE + NQ)
            pe_.wait_ge(s["pew"], ONE + 1)
            with pe_.Fori(0, B) as b:
                pe_.wait_ge(s["x_copied"], ONE + b + 1)
                for r in range(8):
                    which, m, t = r // 4, (r // 2) % 2, r % 2
                    if r >= 2:
                        pe_.wait_ge(s["ropes"], ONE + b * 8 + r - 1)
                    for k, name in enumerate((("wq", "wqs"), ("wk", "wks"))[which]):
                        for c in range(C):
                            mm = pe_.matmul((S_ if r % 2 else T_)[:, k, :], w[name][:, c, m * P:(m + 1) * P],
                                            xb[:, c, PAD + t * W:PAD + (t + 1) * W], start=c == 0, stop=c == C - 1)
                    mm.then_inc(s["rope_mm"], 1)
                for i in range(NQ):
                    if i >= 2:
                        pe_.wait_ge(s["v_moved"], ONE + b * 2 * NQ + 2 * (i - 1))
                    for c in range(C):
                        mm = pe_.matmul(O_[:, i % 2, 0:D], xb[:, c, PAD + i * QT:PAD + (i + 1) * QT], w["wv"][:, c, :],
                                        start=c == 0, stop=c == C - 1)
                    mm.then_inc(s["v_mm"], 1)
                    for c in range(C):
                        mm = pe_.matmul(O_[0:PAD, i % 2, D:2 * D], xb[:, c, i * QT:i * QT + PAD], w["wv"][:, c, :],
                                        start=c == 0, stop=c == C - 1)
                    mm.then_inc(s["v_mm"], 1)
                pe_.wait_ge(s["ropes"], ONE + b * 8 + 8)
                for i in range(NQ):
                    for c in range(C):
                        mm = pe_.matmul(S_[:, 2, 3 * i:3 * i + 3], xb[:, c, PAD + i * QT:PAD + (i + 1) * QT], wg[:, c, :],
                                        start=c == 0, stop=c == C - 1)
                mm.then_inc(s["g_mm"], 1)
                pe_.wait_ge(s["qsum_done"], ONE + b * C + C)
                pe_.wait_ge(s["kc_added"], ONE + b * C + C)
                for c in range(C):
                    mm = pe_.matmul(S_[0:1, 0, 0:NB], qsum[:, c:c + 1], kcomp[:, c, 0:NB], start=c == 0, stop=c == C - 1)
                mm.then_inc(s["imp_mm"], 1)
                pe_.wait_ge(s["roped"], ONE + b * 8 + 8)
                for i in range(NQ):
                    if i >= 2:
                        pe_.wait_ge(s["ktok_moved"], ONE + b * NQ + i - 1)
                    for c in range(C):
                        mm = pe_.transpose(T_[:, i % 2, c * P:(c + 1) * P], kr[:, c, i * QT:(i + 1) * QT], ident[:])
                    mm.then_inc(s["ktok_mm"], 1)
                pe_.wait_ge(s["posf"], ONE + b + 1)
                pe_.matmul(S_[:, 1, 0:2], ones[:], pos0[:], start=True, stop=True).then_inc(s["pos_mm"], 1)
                pe_.wait_ge(s["v_moved"], ONE + (b + 1) * 2 * NQ)
                for i in range(NQ):
                    pe_.matmul(O_[0:NB, 0, 0:D], comp_w[:, i, :], v[:, i, :, 0:DH], start=i == 0, stop=False)
                pe_.matmul(O_[0:NB, 0, 0:D], pe_w[:], pe[:], start=False, stop=True).then_inc(s["cv_mm"], 1)
                pe_.wait_ge(s["sel_done"], ONE + b * NQ + NQ)
                pe_.wait_ge(s["ktok_moved"], ONE + (b + 1) * NQ)
                for i in range(NQ):
                    mm = pe_.matmul(O_[NB:CS, 1, 0:D], sel[:, i, :], v[:, i, :, 0:DH], start=i == 0, stop=i == NQ - 1)
                mm.then_inc(s["cv_mm"], 1)
                for c in range(C):
                    for i in range(NQ):
                        mm = pe_.matmul(T_[:, 2, c * SEL:(c + 1) * SEL], ktok[:, i, c * P:(c + 1) * P], sel[:, i, :],
                                        start=i == 0, stop=i == NQ - 1)
                mm.then_inc(s["selk_mm"], 1)
                pe_.wait_ge(s["kc_split"], ONE + 2 * C * (b + 1))
                pe_.wait_ge(s["vcs_moved"], ONE + 2 * (b + 1))
                pe_.wait_ge(s["mask_done"], ONE + b * NQ + NQ)
                pe_.wait_ge(s["gate_done"], ONE + b + 1)

                pe_.sem_inc(s["carrier"], 1)
                with pe_.Fori(0, NQ // UQ) as i:
                    n0 = b * NQ + i * UQ
                    k0 = n0 * NG

                    def scores(k):
                        t, g, u = k // NG, k % NG, k // NG % 2
                        if g == 0:
                            pe_.wait_ge(s["tile_copied"], ONE + (n0 + t) * 5 + 5)
                        pe_.wait_ge(s["shifted"], ONE + 3 * (k0 + k))
                        for j in range(G):
                            c, _, par = head(g, j)
                            p0 = 32 * g
                            qh = q_t[p0:p0 + 32, u, c, :]
                            cs_o, w_o = slice(j * CS, (j + 1) * CS), slice((j % 2) * WK, (j % 2 + 1) * WK)
                            pe_.matmul(S_[:, 0, cs_o], qh, kc[p0:p0 + 32, c, par, :], start=True, stop=False)
                            pe_.matmul(S_[:, 0, cs_o], identb[:], m_t[:, u, 0:CS], start=False, stop=True)
                            pe_.matmul(S_[:, 1 + j // 2, w_o], qh, k_t[p0:p0 + 32, u, 2 * c + par, :], start=True, stop=False)
                            mm = pe_.matmul(S_[:, 1 + j // 2, w_o], identb[:], m_t[:, u, CS:KEYS], start=False, stop=True)
                        mm.then_inc(s["scores_done"], 1)

                    def turn(k):
                        u = k % 2
                        pe_.wait_ge(s["exp_done"], ONE + k0 + k + 1)
                        pe_.wait_ge(s["pT_moved"], ONE + 3 * (k0 + k))
                        for j in range(G):
                            pe_.transpose(T_[0:CS, 0, j * QT:(j + 1) * QT], prob[:, u, j * CS:(j + 1) * CS], ident[:])
                        for part, (a, z) in enumerate(((0, PAD), (PAD, WK))):
                            for j in range(G):
                                o = G * CS + j * WK
                                mm = pe_.transpose(T_[0:z - a, 1 + part, j * QT:(j + 1) * QT], prob[:, u, o + a:o + z], ident[:])
                        mm.then_inc(s["turned"], 1)

                    def weigh(k):
                        t, g, u = k // NG, k % NG, k // NG % 2
                        pe_.wait_ge(s["pT_moved"], ONE + 3 * (k0 + k) + 3)
                        if g == 0:
                            pe_.wait_ge(s["weighted"], ONE + (n0 + t) * 2)
                            pe_.wait_ge(s["den_done"], ONE + n0 + t)
                        for j in range(G):
                            _, h, _ = head(g, j)
                            o = (h % 8) * 3 * VA
                            q = slice(j * QT, (j + 1) * QT)
                            bank = O_[:, h // 8, :]
                            pe_.matmul(bank[:, o:o + 2 * VA], pT[0:CS, k % 2, 0, q], vcs[:, h, :], start=True, stop=True)
                            pe_.matmul(bank[:, o + 2 * VA:o + 3 * VA], pT[0:PAD, k % 2, 1, q], vp_t[:, u, h, :], start=True, stop=False)
                            mm = pe_.matmul(bank[:, o + 2 * VA:o + 3 * VA], pT[:, k % 2, 2, q], v_t[:, u, h, :], start=False, stop=True)
                        mm.then_inc(s["pv_done"], 1)

                    def turn_out(t, k):
                        pe_.wait_ge(s["att_done"], ONE + n0 + t + 1)
                        pe_.wait_ge(s["pT_moved"], ONE + 3 * (k0 + k) + 3)
                        for c in range(C):
                            mm = pe_.transpose(T_[:, 0, c * QT:(c + 1) * QT], att[:, c * P:(c + 1) * P], ident[:])
                        mm.then_inc(s["att_turned"], 1)

                    def through_wo(t):
                        pe_.wait_ge(s["attT_moved"], ONE + n0 + t + 1)
                        for m in range(C):
                            for c in range(C):
                                mm = pe_.matmul(T_[:, 1, m * QT:(m + 1) * QT], w["wo"][:, c, m * P:(m + 1) * P], attT[:, c, :],
                                                start=c == 0, stop=c == C - 1)
                        mm.then_inc(s["wo_done"], 1)

                    last = UQ * NG - 1
                    for k in range(last + 5):
                        if k <= last:
                            scores(k)
                        if k >= 7 and (k - 7) % NG == 0:
                            through_wo((k - 7) // NG)
                        if 2 <= k <= last + 2:
                            weigh(k - 2)
                        if 1 <= k <= last + 1:
                            if k >= 7 and (k - 7) % NG == 0:
                                pe_.wait_ge(s["x_added"], ONE + C * (n0 + (k - 7) // NG + 1))
                            turn(k - 1)
                        if k >= 6 and (k - 6) % NG == 0:
                            turn_out((k - 6) // NG, min(k - 1, last))
                    pe_.wait_ge(s["x_added"], ONE + C * (n0 + UQ))

        @block.scalar
        def _(act):
            act.wait_ge(s["here"], ONE + 16 * len(loads))
            act.wait_ge(s["consts"], ONE + 8)
            with act.Fori(0, B) as b:
                act.wait_ge(s["x_added"], ONE + b * C * NQ)
                act.copy(xb[:, :, PAD:], xf[:, :, bass.ts(b, S)]).then_inc(s["x_copied"], 1)
                for r in range(4):
                    m, t = r // 2, r % 2
                    x = slice(t * W, (t + 1) * W)
                    act.wait_ge(s["roped"], ONE + b * 8 + 5 + r)
                    for par in range(2):
                        act.activation(keo[:, m, par, PAD + t * W:PAD + (t + 1) * W], kr[:, m, x], ACT.Copy,
                                       scale=parity[:, par:par + 1]).then_inc(s["k_split"], 1)
                for i in range(NQ):
                    act.wait_ge(s["v_mm"], ONE + b * 2 * NQ + 2 * i + 2)
                    act.copy(v[:, i, :, 0:DH], O_[:, i % 2, 0:D].rearrange("p (h d) -> p h d", h=H)).then_inc(s["v_moved"], 1)
                    act.copy(vprev[:, i, :, 0:DH], O_[0:PAD, i % 2, D:2 * D].rearrange("p (h d) -> p h d", h=H)).then_inc(s["v_moved"], 1)
                act.wait_ge(s["imp_mm"], ONE + b + 1)
                act.copy(imp[:], S_[0:1, 0, 0:NB]).then_inc(s["imp_moved"], 1)
                for i in range(NQ):
                    act.wait_ge(s["ktok_mm"], ONE + b * NQ + i + 1)
                    act.copy(ktok[:, i, :], T_[:, i % 2, 0:D]).then_inc(s["ktok_moved"], 1)
                act.wait_ge(s["g_shift"], ONE + b + 1)
                act.activation(ge[:], gl[:], ACT.Exp).then_inc(s["g_exp"], 1)
                act.wait_ge(s["cv_mm"], ONE + 2 * b + 1)
                act.copy(vcs[0:NB, :, 0:DH], O_[0:NB, 0, 0:D].rearrange("p (h d) -> p h d", h=H)).then_inc(s["vcs_moved"], 1)
                act.wait_ge(s["cv_mm"], ONE + 2 * b + 2)
                act.copy(vcs[NB:CS, :, VA:VA + DH], O_[NB:CS, 1, 0:D].rearrange("p (h d) -> p h d", h=H)).then_inc(s["vcs_moved"], 1)
                act.wait_ge(s["selk_mm"], ONE + b + 1)
                act.copy(kcomp[:, :, NB:CS], T_[:, 2, 0:C * SEL].rearrange("p (c m) -> p c m", c=C)).then_inc(s["selk_moved"], 1)
                act.wait_ge(s["selk_moved"], ONE + b + 1)
                act.wait_ge(s["kc_added"], ONE + (b + 1) * C)
                for c in range(C):
                    for par in range(2):
                        act.activation(kc[:, c, par, :], kcomp[:, c, :], ACT.Copy, scale=parity[:, par:par + 1]).then_inc(s["kc_split"], 1)
                act.sem_inc(s["carrier"], 1)
                with act.Fori(0, NQ // UQ) as i:
                    n0 = b * NQ + i * UQ
                    k0 = n0 * NG

                    def exps(k):
                        act.wait_ge(s["shifted"], ONE + 3 * (k0 + k) + 3)
                        act.activation(prob[:, k % 2, :], prob[:, k % 2, :], ACT.Exp, scale=float(DH) ** -0.5).then_inc(s["exp_done"], 1)

                    def move(k):
                        act.wait_ge(s["turned"], ONE + k0 + k + 1)
                        act.wait_ge(s["pv_done"], AHEAD + k0 + max(k - 1, 0))
                        act.copy(pT[0:CS, k % 2, 0, :], T_[0:CS, 0, :]).then_inc(s["pT_moved"], 1)
                        act.copy(pT[0:PAD, k % 2, 1, :], T_[0:PAD, 1, :]).then_inc(s["pT_moved"], 1)
                        act.copy(pT[:, k % 2, 2, :], T_[:, 2, :]).then_inc(s["pT_moved"], 1)

                    def move_out(t):
                        act.wait_ge(s["att_turned"], ONE + n0 + t + 1)
                        act.copy(attT[:], T_[:, 0, 0:C * QT].rearrange("p (c q) -> p c q", c=C)).then_inc(s["attT_moved"], 1)

                    last = UQ * NG - 1
                    for k in range(last + 4):
                        if k <= last:
                            exps(k)
                        if 1 <= k <= last + 1:
                            move(k - 1)
                        if k >= 6 and (k - 6) % NG == 0:
                            move_out((k - 6) // NG)

        @block.gpsimd
        def _(pool):
            pool.sem_inc(s["pv_done"], AHEAD - ONE)
            pool.memset(v[:, :, :, DH:VA], 1.0).then_inc(s["consts"], 1)
            pool.memset(vprev[:, :, :, DH:VA], 1.0).then_inc(s["consts"], 1)
            pool.memset(vcs[:], 0.0).then_inc(s["consts"], 1)
            pool.memset(xb[:, :, 0:PAD], 0.0).then_inc(s["consts"], 1)
            pool.memset(keo[:, :, :, 0:PAD], 0.0).then_inc(s["consts"], 1)
            pool.wait_ge(s["consts"], ONE + 5)
            pool.memset(vcs[0:NB, :, DH:VA], 1.0).then_inc(s["consts"], 1)
            pool.wait_ge(s["consts"], ONE + 6)
            pool.memset(vcs[NB:CS, :, VA + DH:2 * VA], 1.0).then_inc(s["consts"], 1)
            pool.wait_ge(s["consts"], ONE + 7)
            pool.wait_ge(s["here"], ONE + 16 * len(loads))
            pool.tensor_copy(identb[:], ident[:]).then_inc(s["consts"], 1)
            with pool.Fori(0, B) as b:
                pool.wait_ge(s["k_split"], ONE + 8 * b + 8)
                pool.wait_ge(s["roped"], ONE + 8 * b + 8)
                pool.wait_ge(s["v_moved"], ONE + 2 * NQ * (b + 1))
                pool.wait_ge(s["mask_done"], ONE + b * NQ + NQ)
                pool.wait_ge(s["gate_done"], ONE + b + 1)
                pool.sem_inc(s["carrier"], 1)
                with pool.Fori(0, NQ // 2) as i:
                    for u in range(2):
                        t = i * 2 + u
                        n = b * NQ + t
                        pool.wait_ge(s["pv_done"], AHEAD + n * NG - NG)
                        pool.sem_inc(s["carrier"], 1)
                        pool.tensor_copy(q_t[:, u], qT[:, :, bass.ts(t, QT)]).then_inc(s["tile_copied"], 1)
                        pool.tensor_copy(k_t[:, u], keo[:].rearrange("p c e k -> p (c e) k")[:, :, bass.ds(t * QT, WK)]).then_inc(s["tile_copied"], 1)
                        pool.tensor_copy(v_t[:, u], v[:, bass.ds(t, 1), :, :].rearrange("p o h d -> p (o h) d")).then_inc(s["tile_copied"], 1)
                        pool.tensor_copy(vp_t[:, u], vprev[:, bass.ds(t, 1), :, :].rearrange("p o h d -> p (o h) d")).then_inc(s["tile_copied"], 1)
                        pool.tensor_copy(m_t[:, u], mask[:, bass.ds(t, 1), :].rearrange("p o k -> p (o k)")).then_inc(s["tile_copied"], 1)

        @block.vector
        def _(dve):
            dve.memset(ones[:], 1.0).then_inc(s["ones_set"], 1)
            dve.wait_ge(s["ones_set"], ONE + 1)
            dve.wait_ge(s["here"], ONE + 16 * len(loads))
            with dve.Fori(0, NQ) as i:
                dve.wait_ge(s["mask_here"], ONE + 16 * i + 16)
                dve.tensor_copy(mask[:, bass.ds(i, 1), :].rearrange("p o k -> p (o k)"), mask_f[:]).then_inc(s["mask_cast"], 1)
            dve.tensor_scalar(comp_w[:].rearrange("p i n -> p (i n)"), block_of[:].rearrange("p i n -> p (i n)"), wvc[:, 0:1], None,
                              ALU.mult).then_inc(s["cw"], NQ)
            dve.wait_ge(s["cw"], ONE + NQ)
            dve.memset(pe_w[:], 1.0).then_inc(s["pew0"], 1)
            dve.wait_ge(s["pew0"], ONE + 1)
            dve.tensor_scalar(pe_w[:], pe_w[:], wvc[0:16, 0:1], None, ALU.mult).then_inc(s["pew"], 1)
            dve.tensor_tensor(pe_k[:], peT[:], wkc[:].unsqueeze(1).to_broadcast([P, C, 16]), ALU.mult).then_inc(s["peT_w"], 1)
            dve.wait_ge(s["peT_w"], ONE + 1)
            dve.tensor_reduce(pe_sum[:], pe_k[:], AX.X, ALU.add).then_inc(s["pe_sum"], 1)
            dve.wait_ge(s["pe_sum"], ONE + 1)
            dve.wait_ge(s["mask_cast"], ONE + NQ)
            with dve.Fori(0, B) as b:
                for r in range(8):
                    which, m, t = r // 4, (r // 2) % 2, r % 2
                    x = slice(t * W, (t + 1) * W)
                    src = S_ if r % 2 else T_
                    dve.wait_ge(s["rope_mm"], ONE + b * 8 + r + 1)
                    dve.wait_ge(s["roped"], ONE + b * 8 + max(r - 1, 0))
                    dve.tensor_tensor(t1[:, r % 2, :], src[:, 0, :], cos[:, x], ALU.mult).then_inc(s["ropec"], 1)
                    dve.tensor_tensor(t2[:, r % 2, :], src[:, 1, :], sin[:, x], ALU.mult).then_inc(s["ropes"], 1)
                    dve.wait_ge(s["ropes"], ONE + b * 8 + r + 1)
                    dve.wait_ge(s["ropec"], ONE + b * 8 + r + 1)
                    dve.tensor_tensor((kr if which else qT)[:, m, x], t1[:, r % 2, :], t2[:, r % 2, :], ALU.add).then_inc(s["roped"], 1)
                dve.wait_ge(s["roped"], ONE + b * 8 + 8)
                dve.wait_ge(s["imp_mm"], ONE + b)
                dve.wait_ge(s["kc_split"], ONE + 2 * C * b)
                for c in range(C):
                    dve.tensor_reduce(qsum[:, c:c + 1], qT[:, c, :], AX.X, ALU.add).then_inc(s["qsum_done"], 1)
                    dve.wait_ge(s["kc_red"], ONE + b * C + c)
                    dve.tensor_tensor(kw_prod[:].rearrange("p (n k) -> p n k", k=16), kr[:, c, :].rearrange("p (n k) -> p n k", k=16),
                                      wkc[:].unsqueeze(1).to_broadcast([P, NB, 16]), ALU.mult).then_inc(s["kc_w"], 1)
                    dve.wait_ge(s["kc_w"], ONE + b * C + c + 1)
                    dve.tensor_reduce(kcomp[:, c, 0:NB], kw_prod[:].rearrange("p (n k) -> p n k", k=16), AX.X, ALU.add).then_inc(s["kc_red"], 1)
                    dve.wait_ge(s["kc_red"], ONE + b * C + c + 1)
                    dve.tensor_scalar(kcomp[:, c, 0:NB], kcomp[:, c, 0:NB], pe_sum[:, c:c + 1], None, ALU.add).then_inc(s["kc_added"], 1)
                dve.wait_ge(s["g_mm"], ONE + b + 1)
                dve.tensor_tensor(gl[:], S_[:, 2, 0:3 * NQ].rearrange("p (i g) -> p i g", g=3), bg[:].unsqueeze(1).to_broadcast([P, NQ, 3]),
                                  ALU.add).then_inc(s["g_logit"], 1)
                dve.wait_ge(s["g_logit"], ONE + b + 1)
                dve.tensor_reduce(gmx[:], gl[:], AX.X, ALU.max).then_inc(s["g_top"], 1)
                dve.wait_ge(s["g_top"], ONE + b + 1)
                dve.tensor_tensor(gl[:], gl[:], gmx[:].unsqueeze(2).to_broadcast([P, NQ, 3]), ALU.subtract).then_inc(s["g_shift"], 1)
                dve.wait_ge(s["imp_moved"], ONE + b + 1)
                dve.sem_inc(s["carrier"], 1)
                dve.max(top[:], imp[:]).then_inc(s["top_done"], 1)
                dve.wait_ge(s["top_done"], ONE + b + 1)
                dve.sem_inc(s["carrier"], 1)
                dve.max_index(top_i[:], top[:], imp[:]).then_inc(s["topi_done"], 1)
                dve.wait_ge(s["topi_done"], ONE + b + 1)
                dve.tensor_scalar(pos0[:], top_i[:, 0:2], 16.0, None, ALU.mult).then_inc(s["posf"], 1)
                dve.wait_ge(s["pos_mm"], ONE + b + 1)
                dve.tensor_tensor(pos[:].rearrange("p (a e) -> p a e", a=2), offset[:].rearrange("p (a e) -> p a e", a=2),
                                  S_[:, 1, 0:2].unsqueeze(2).to_broadcast([P, 2, SEL // 2]), ALU.add).then_inc(s["pos_done"], 1)
                dve.wait_ge(s["pos_done"], ONE + b + 1)
                for i in range(NQ):
                    dve.tensor_scalar(sel[:, i, :], pos[:], token_no[:, i:i + 1], None, ALU.is_equal).then_inc(s["sel_done"], 1)
                for i in range(NQ):
                    dve.tensor_scalar(mask[:, i, NB:CS], pos[:], token_no[:, i:i + 1], NEG, ALU.is_gt, ALU.mult).then_inc(s["mask_done"], 1)
                dve.wait_ge(s["g_exp"], ONE + b + 1)
                dve.tensor_reduce(gsum[:], ge[:], AX.X, ALU.add).then_inc(s["g_sum"], 1)
                dve.wait_ge(s["g_sum"], ONE + b + 1)
                dve.reciprocal(ginv[:], gsum[:]).then_inc(s["g_inv"], 1)
                dve.wait_ge(s["g_inv"], ONE + b + 1)
                dve.tensor_tensor(gate[:], ge[:], ginv[:].unsqueeze(2).to_broadcast([P, NQ, 3]), ALU.mult).then_inc(s["gate_done"], 1)
                dve.wait_ge(s["gate_done"], ONE + b + 1)
                dve.sem_inc(s["carrier"], 1)
                with dve.Fori(0, NQ // UQ) as i:
                    n0 = b * NQ + i * UQ
                    k0 = n0 * NG
                    o5 = O_[:, :, 0:8 * 3 * VA].rearrange("p b (h x) -> p b h x", x=VA)
                    rgf, wof = rg[:].rearrange("p h r -> p (h r)"), wo3[:].rearrange("p h r d -> p (h r) d")

                    def shift(k):
                        u = k % 2
                        dve.wait_ge(s["scores_done"], ONE + k0 + k + 1)
                        dve.wait_ge(s["shifted"], ONE + 3 * (k0 + k))
                        dve.wait_ge(s["turned"], ONE + k0 + max(k - 1, 0))
                        cs3 = S_[:, 0, 0:G * CS].rearrange("p (h k) -> p h k", h=G)
                        win4 = S_[:, 1:3, 0:2 * WK].rearrange("p b (h k) -> p b h k", h=2)
                        dve.tensor_reduce(mx[:, u, 0, :], cs3[:, :, 0:NB], AX.X, ALU.max).then_inc(s["max_done"], 1)
                        dve.tensor_reduce(mx[:, u, 1, :], cs3[:, :, NB:CS], AX.X, ALU.max).then_inc(s["max_done"], 1)
                        dve.tensor_reduce(mx[:, u, 2, :].rearrange("p (b h) -> p b h", b=2), win4, AX.X, ALU.max).then_inc(s["max_done"], 1)
                        dve.wait_ge(s["max_done"], ONE + 3 * (k0 + k) + 3)
                        dve.tensor_scalar(mx[:, u, :, :], mx[:, u, :, :], NEG / 10, None, ALU.max).then_inc(s["clamp_done"], 1)
                        dve.wait_ge(s["clamp_done"], ONE + k0 + k + 1)
                        pcs = prob[:, u, 0:G * CS].rearrange("p (h k) -> p h k", h=G)
                        pwin = prob[:, u, G * CS:].rearrange("p (b h k) -> p b h k", b=2, h=2)
                        dve.tensor_tensor(pcs[:, :, 0:NB], cs3[:, :, 0:NB], mx[:, u, 0, :].unsqueeze(2).to_broadcast([P, G, NB]),
                                          ALU.subtract).then_inc(s["shifted"], 1)
                        dve.tensor_tensor(pcs[:, :, NB:CS], cs3[:, :, NB:CS], mx[:, u, 1, :].unsqueeze(2).to_broadcast([P, G, SEL]),
                                          ALU.subtract).then_inc(s["shifted"], 1)
                        dve.tensor_tensor(pwin, win4, mx[:, u, 2, :].rearrange("p (b h) -> p b h", b=2).unsqueeze(3).to_broadcast([P, 2, 2, WK]),
                                          ALU.subtract).then_inc(s["shifted"], 1)

                    def combine(t):
                        n = n0 + t
                        dve.wait_ge(s["pv_done"], AHEAD + (n + 1) * NG)
                        dve.tensor_scalar(den[:].rearrange("p (b h) r -> p b (h r)", b=2), o5[:, :, :, DH], 1e-30, None, ALU.max).then_inc(s["den_done"], 1)
                        dve.wait_ge(s["den_done"], ONE + n + 1)
                        dve.reciprocal(rden[:], den[:]).then_inc(s["rden_done"], 1)
                        dve.wait_ge(s["rden_done"], ONE + n + 1)
                        dve.tensor_tensor(rg[:], rden[:], gate[:, bass.ds(i * UQ + t, 1), :].to_broadcast([P, H, 3]), ALU.mult).then_inc(s["rg_done"], 1)
                        dve.wait_ge(s["rg_done"], ONE + n + 1)
                        for k in range(2):
                            dve.tensor_tensor(wof[:, 24 * k:24 * k + 24, :], o5[:, k, :, 0:DH],
                                              rgf[:, 24 * k:24 * k + 24].unsqueeze(2).to_broadcast([P, 24, DH]), ALU.mult).then_inc(s["weighted"], 1)
                        dve.wait_ge(s["weighted"], ONE + 2 * n + 2)
                        dve.wait_ge(s["att_turned"], ONE + n)
                        dve.tensor_reduce(att[:].rearrange("p (h d) -> p h d", h=H), wo3[:].rearrange("p h r d -> p h d r"), AX.X,
                                          ALU.add).then_inc(s["att_done"], 1)

                    def add(t):
                        dve.wait_ge(s["wo_done"], ONE + n0 + t + 1)
                        for c in range(C):
                            x = xf[:, c, bass.ds((n0 + t) * QT, QT)]
                            dve.scalar_tensor_tensor(out=x, in0=T_[:, 1, c * QT:(c + 1) * QT], scalar=bo[:, c:c + 1], in1=x,
                                                     op0=ALU.add, op1=ALU.add).then_inc(s["x_added"], 1)

                    last = UQ * NG - 1
                    for k in range(last + 5):
                        if k <= last:
                            shift(k)
                        if k >= 5 and (k - 5) % NG == 0:
                            combine((k - 5) // NG)
                        if k >= 7 and (k - 7) % NG == 0:
                            add((k - 7) // NG)
    st.close()


def mesa_attention(nc, xf, io, eps):
    L = 128
    SEG = 2
    NGRP = T // (L * SEG)
    SYS = SEG * H
    TRI = DH * (DH + 1) // 2

    def off(i):
        return DH * i - i * (i - 1) // 2

    st = Stage(nc, "mesa")
    wqk, wv = st.sb("wqk", [P, C, 2 * D]), st.sb("wv", [P, C, D])
    wfb, gw1, gw2 = st.sb("wfb", [P, C, 2 * H]), st.sb("gw1", [P, C, DH]), st.sb("gw2", [DH, D])
    wo = st.sb("wo_n", [P, C, D])
    normw = st.sb("norm_w", [P, C])
    delta, restart = st.sb("delta", [P, H]), st.sb("restart", [P, T // L])
    delta_n = st.sb("delta_segment", [P, T // L, H])
    la, lb = st.sb("lambda_a", [P, DH, H]), st.sb("lambda", [P, DH, H])
    lam = lb
    upto, after = st.sb("upto", [P, L]), st.sb("after", [P, L])
    negf, negb = st.sb("neg_float", [P, L]), st.sb("neg", [P, L], BF16)
    ident, identb = st.sb("identity", [P, P]), st.sb("identity_b", [P, P], BF16)
    parity, expand = st.sb("parity", [P, 2]), st.sb("expand", [H, C, P])
    own = st.sb("own_block", [P, C, P])
    c_small = st.sb("small", [P, 2 * H])
    c_one = st.sb("one", [P, H])
    c_minus = st.sb("minus_one", [P, H])
    c_eps4 = st.sb("eps4", [P, H])
    xs = st.sb("x_seg", [P, C, L])
    sqk = st.sb("qk_square", [P, 2 * H, DH])
    qk, z16 = st.sb("qk", [P, 2 * D]), st.sb("z_f", [P, H])
    ta, tb, tc_, ssum = (st.sb(n, [P, 2 * H, k]) for n, k in (("sum8", 8), ("sum4", 4), ("sum2", 2), ("sum1", 1)))
    rln, rn = st.sb("qk_norm_ln", [P, 2 * H]), st.sb("qk_inverse", [P, 2 * H])
    g1T = st.sb("g1T", [DH, L])
    zf, zabs, zexp, zln, zmin, zneg = (st.sb(n, [P, H]) for n in ("zf", "zf_abs", "zf_exp", "zf_ln", "zf_relu", "zf_sum"))
    eb, eb1, beta = (st.sb(n, [P, H]) for n in ("eb", "eb1", "beta"))
    kn = st.sb("k", [P, H, DH])
    eG = st.sb("decay_to_end", [P, H])
    kk = st.sb("kk", [P, H, TRI])
    lfU = st.sb("log_f_upto", [P, H, L])
    ef_row = lfU[0:1]
    h_rows = st.sb("state_rows", [P, H, TRI])
    h_last, h_row = h_rows[96:P], h_rows[0:1]
    dec = st.sb("decay", [P, 2, SEG, 4, 4, L])
    kb = st.sb("k_beta", [P, 2, SEG, D])
    kd = st.sb("k_decayed", [P, 2, SEG, D])
    vs = st.sb("v", [P, 2, SEG, D])
    g1p = st.sb("gate", [P, 2, SEG, D])
    lf = st.sb("log_f", [P, 2, SEG, H])
    eF = st.sb("decay_from_start", [P, 2, SEG, H])
    eFT = st.sb("decay_from_startT", [H, 2, SEG, L])
    A = st.sb("A", [P, 2, TRI, SYS])
    Y = st.sb("Y", [P, 2, DH, SYS])
    mult = st.sb("multipliers", [P, 2, DH, SYS])
    prod = st.sb("product", [P, 3, DH, SYS])
    prod_y = st.sb("product_y", [P, DH, SYS])
    piv, rinv = st.sb("pivot", [P, SYS]), st.sb("pivot_inverse", [P, DH, SYS])
    red, num = st.sb("known_part", [P, SYS]), st.sb("numerator", [P, SYS])
    qs = st.sb("solution", [P, D])
    kbT, qsT = st.sb("k_betaT", [P, C, 2, L]), st.sb("solutionT", [P, C, L])
    oi, o, og = (st.sb(n, [P, H, DH]) for n in ("o_inter", "o", "o_gated"))
    on, osq = oi, o
    t8, t4, t2, t1 = (st.sb(n, [P, H, k]) for n, k in (("osum8", 8), ("osum4", 4), ("osum2", 2), ("osum1", 1)))
    oln, orn = st.sb("o_mean_ln", [P, H]), st.sb("o_inverse", [P, H])
    onT = st.sb("o_normedT", [P, C, L])
    state, s_own = (st.sb(n, [P, C, P]) for n in ("state", "state_new"))
    pm, o7 = st.sb("weights", [P, 2, 4 * L]), st.sb("o_parts", [P, 2, H, DH])
    st5, wo6 = st.sb("state_parts", [P, D + C]), st.sb("wo_out", [P, C, L])
    bk = [st.ps(f"bank{k}") for k in range(8)]
    loads = [(wqk[:], "mesa_wqk"), (wv[:], "mesa_wv"), (wfb[:], "mesa_wfb"), (gw1[:], "mesa_gw1"), (gw2[:], "mesa_gw2"),
             (wo[:], "mesa_wo"), (normw[:], "mesa_norm"), (delta[:], "mesa_delta"), (restart[:], "mesa_restart"), (la[:], "mesa_lambda"),
             (upto[:], "mesa_upto"), (after[:], "mesa_after"), (negf[:], "mesa_neg"), (ident[:], "identity"),
             (parity[:], "nsa_parity"), (expand[:], "mesa_expand"), (own[:], "mesa_own")]
    names = ("here consts lam1 lam2 lam_done wo_ready carrier "
             "xs_done v_mm qk_mm proj_mm gate_mm sqk_done g1_moved eb_done v_moved tanh_done zf_done zabs_done zexp_done zln_done zmin_done "
             "zneg_done lf_done eb1_done beta_done sum8 sum4 sum2 sum1 rln_done rn_done y_done kn_done kb_done kk_done f_mm ef_done eg_done eft_done "
             "ef_row_here kd_done lfu_done gate1_done d_mm dec_done a_mm a_moved h_row_here "
             "solved e "
             "qs_done o_turned kbt_done qst_done o_smm pm_done intra_mm inter_mm oi_done o_done og_done osq_done "
             "qk_moved z_moved s_moved o7_moved st_moved wo_moved os8 os4 os2 os1 oln_done orn_done on_done on_turned ont_done wo_mm x_added st_mm st_own st_dec st_done").split()
    s = {n: st.sem(n) for n in names}

    def head(g, j):
        return 8 * (j // 2) + 2 * g + j % 2

    def grouped(t, g):
        return t.rearrange("p (c a e) t -> p c a e t", c=2, a=4)[:, :, g, :, :]

    NP_ = 4

    def schedule(eng, core, ends):
        def group(g, ahead, u):
            n = None if g is None else g * SEG
            p = None if ahead is None else ahead * SEG
            plus = lambda m, k: None if m is None else m + k
            core(n, None, p, u, 0, None, g, None)
            ends(n, p, u, 0, n)
            core(plus(n, 1), p, plus(p, 1), u, 1, 0, g, g)
            ends(plus(n, 1), plus(p, 1), u, 1, plus(n, 1))
            core(None, plus(p, 1), None, u, None, 1, g, None)

        group(None, 0, 0)
        group(None, 1, 1)
        eng.sem_inc(s["carrier"], 1)
        with eng.Fori(0, NGRP // 2 - 1) as i:
            for u in range(2):
                group(2 * i + u, 2 * i + 2 + u, u)
        group(NGRP - 2, None, 0)
        group(NGRP - 1, None, 1)

    st.start_counters()
    with nc.Block() as block:
        @block.sync
        def _(sp):
            for dst, src in loads:
                sp.dma_start(dst, io[src]).then_inc(s["here"], 16)

            def carry(g, u, q):
                n = g * SEG + q
                sp.wait_ge(s["a_mm"], ONE + 8 * n)
                sp.sem_inc(s["carrier"], 1)
                sp.wait_ge(s["eft_done"], ONE + n + 1)
                sp.sem_inc(s["carrier"], 1)
                sp.wait_ge(s["d_mm"], ONE + 4 * n + 4)
                sp.sem_inc(s["carrier"], 1)
                sp.dma_start(ef_row, eFT[:, u, q, :]).then_inc(s["ef_row_here"], 16)
                sp.wait_ge(s["a_mm"], ONE + 8 * n + 8)
                sp.sem_inc(s["carrier"], 1)
                sp.wait_ge(s["a_moved"], ONE + 16 * n + 16)
                sp.dma_start(h_row, h_last[31:32, :, :]).then_inc(s["h_row_here"], 16)
            with sp.Fori(0, NGRP // 2) as i:
                for u in range(2):
                    for q in range(SEG):
                        carry(2 * i + u, u, q)
            sp.wait_ge(s["h_row_here"], ONE + 16 * NGRP * SEG)

        @block.tensor
        def _(pe):
            pe.wait_ge(s["here"], ONE + 16 * len(loads))
            pe.wait_ge(s["consts"], ONE + 9)
            pe.wait_ge(s["wo_ready"], ONE + C)

            def project(n):
                pe.wait_ge(s["xs_done"], ONE + n + 1)
                pe.wait_ge(s["dec_done"], ONE + NP_ * n)
                for c in range(C):
                    mm = pe.matmul(bk[0][:], xs[:, c, :], wqk[:, c, :], start=c == 0, stop=c == C - 1)
                mm.then_inc(s["qk_mm"], 1)
                for c in range(C):
                    mm = pe.matmul(bk[1][:, 0:D], xs[:, c, :], wv[:, c, :], start=c == 0, stop=c == C - 1)
                mm.then_inc(s["v_mm"], 1)

            def project_small(n):
                pe.wait_ge(s["a_moved"], ONE + 16 * n)
                for c in range(C):
                    pe.matmul(bk[2][:, 0:2 * H], xs[:, c, :], wfb[:, c, :], start=c == 0, stop=c == C - 1)
                for c in range(C):
                    mm = pe.matmul(bk[3][0:DH, 0:L], gw1[:, c, :], xs[:, c, :], start=c == 0, stop=c == C - 1)
                mm.then_inc(s["proj_mm"], 1)

            def gate_and_sums(n, u, q):
                pe.wait_ge(s["g1_moved"], ONE + n + 1)
                pe.matmul(bk[1][:, D:2 * D], g1T[:], gw2[:], start=True, stop=True).then_inc(s["gate_mm"], 1)
                pe.wait_ge(s["lf_done"], ONE + n + 1)
                pe.matmul(bk[3][:, 0:H], upto[:], lf[:, u, q, :], start=True, stop=True)
                pe.matmul(bk[3][:, H:2 * H], after[:], lf[:, u, q, :], start=True, stop=True)
                pe.matmul(bk[3][0:H, 2 * H:2 * H + L], lf[:, u, q, :], upto[:], start=True, stop=True).then_inc(s["f_mm"], 1)

            def log_decay(n, d):
                if d == 0:
                    pe.wait_ge(s["qk_moved"], ONE + n + 1)
                    pe.wait_ge(s["sqk_done"], ONE + n + 1)
                elif d == 1:
                    pe.wait_ge(s["v_moved"], ONE + n + 1)
                    pe.wait_ge(s["tanh_done"], ONE + n + 1)
                else:
                    pe.wait_ge(s["dec_done"], ONE + NP_ * n + d - 1)
                pe.wait_ge(s["lfu_done"], ONE + H * n + 4 * (d + 1))
                pe.matmul(bk[d % 2][:], after[:], grouped(lfU[:], d), start=True, stop=False)
                pe.matmul(bk[d % 2][:], identb[:], negb[:].unsqueeze(1).to_broadcast([P, 4, L]), start=False, stop=True) \
                    .then_inc(s["d_mm"], 1)

            def matrices(n, u, q, d):
                if d == 0:
                    pe.wait_ge(s["kk_done"], ONE + DH * (n + 1))
                    pe.wait_ge(s["eft_done"], ONE + n + 1)
                    pe.wait_ge(s["eb_done"], ONE + n + 1)
                    pe.wait_ge(s["ef_row_here"], ONE + 16 * (n + 1))
                    pe.wait_ge(s["h_row_here"], ONE + 16 * n)
                pe.wait_ge(s["dec_done"], ONE + NP_ * n + d + 1)
                for k in (2 * d, 2 * d + 1):
                    if k >= 2:
                        pe.wait_ge(s["a_moved"], ONE + 16 * n + 2 * (k - 1))
                    for e in range(2):
                        j = 2 * (k % 2) + e
                        h = head(d, j)
                        dst = bk[2 + k % 2][:, e * TRI:(e + 1) * TRI]
                        pe.matmul(dst, dec[:, u, q, d, j, :], kk[:, h, :], start=True, stop=False)
                        mm = pe.matmul(dst, ef_row[:, h, :], h_row[:, h, :], start=False, stop=True)
                    mm.then_inc(s["a_mm"], 1)

            def turn_solution(n, u, q):
                pe.wait_ge(s["wo_moved"], ONE + n)
                pe.wait_ge(s["qs_done"], ONE + n + 1)
                for c in range(C):
                    pe.transpose(bk[6][:, c * P:(c + 1) * P], kb[:, u, q, c * P:(c + 1) * P], ident[:])
                for c in range(C):
                    mm = pe.transpose(bk[6][:, D + c * P:D + (c + 1) * P], qs[:, c * P:(c + 1) * P], ident[:])
                mm.then_inc(s["o_turned"], 1)

            def scores(n, d):
                if d == 0:
                    pe.wait_ge(s["kbt_done"], ONE + 2 * n + 2)
                    pe.wait_ge(s["qst_done"], ONE + n + 1)
                    pe.wait_ge(s["st_moved"], ONE + n)
                    pe.wait_ge(s["s_moved"], ONE + 4 * n)
                elif d >= 2:
                    pe.wait_ge(s["s_moved"], ONE + 4 * n + d - 1)
                for j in range(4):
                    mm = pe.matmul(bk[4 + d % 2][:, j * L:(j + 1) * L], kbT[32 * d:32 * d + 32, j // 2, j % 2, :],
                                   qsT[32 * d:32 * d + 32, j // 2, :], start=True, stop=True)
                mm.then_inc(s["o_smm"], 1)

            def from_state(n):
                pe.wait_ge(s["o7_moved"], ONE + n)
                pe.wait_ge(s["st_done"], ONE + n)
                for c in range(C):
                    mm = pe.matmul(bk[7][:, c * P:(c + 1) * P], qsT[:, c, :], state[:, c, :], start=True, stop=True)
                mm.then_inc(s["inter_mm"], 1)

            def from_segment(n, u, q, d):
                pe.wait_ge(s["pm_done"], ONE + 4 * n + d + 1)
                for j in range(4):
                    h = head(d, j)
                    mm = pe.matmul(bk[7][:, D + h * DH:D + (h + 1) * DH], pm[:, d % 2, j * L:(j + 1) * L],
                                   vs[:, u, q, h * DH:(h + 1) * DH], start=True, stop=True)
                mm.then_inc(s["intra_mm"], 1)

            def next_state(n, u, q):
                pe.wait_ge(s["s_moved"], ONE + 4 * n + 4)
                for c in range(C):
                    pe.matmul(bk[5][:, c * P:(c + 1) * P], kd[:, u, q, c * P:(c + 1) * P], vs[:, u, q, c * P:(c + 1) * P],
                              start=True, stop=True)
                for c in range(C):
                    mm = pe.matmul(bk[5][:, D + c:D + c + 1], expand[:, c, :], eFT[:, u, q, L - 1:L], start=True, stop=True)
                mm.then_inc(s["st_mm"], 1)

            def turn_out(n):
                pe.wait_ge(s["on_done"], ONE + n + 1)
                for c in range(C):
                    mm = pe.transpose(bk[6][:, c * P:(c + 1) * P], on[:].rearrange("p h d -> p (h d)")[:, c * P:(c + 1) * P], ident[:])
                mm.then_inc(s["on_turned"], 1)

            def through_wo(n):
                pe.wait_ge(s["ont_done"], ONE + n + 1)
                for m in range(C):
                    for c in range(C):
                        mm = pe.matmul(bk[6][:, D + m * L:D + (m + 1) * L], wo[:, c, m * P:(m + 1) * P], onT[:, c, :],
                                       start=c == 0, stop=c == C - 1)
                mm.then_inc(s["wo_mm"], 1)

            def core(n, p, a, u, q, pq, group, solved_before):
                if n is not None:
                    turn_solution(n, u, q)
                if p is not None:
                    for d in range(4):
                        log_decay(p, d)
                        if n is not None and d == 1:
                            scores(n, 0)
                elif n is not None:
                    scores(n, 0)
                if n is not None:
                    from_state(n)
                for d in range(4):
                    if n is not None and d < 3:
                        scores(n, d + 1)
                    if p is not None:
                        matrices(p, u, pq, d)
                    if n is not None:
                        from_segment(n, u, q, d)
                    if a is not None and d == 1:
                        project(a)
                if n is not None:
                    next_state(n, u, q)

            def ends(n, p, u, q, before):
                if p is not None:
                    project_small(p)
                    gate_and_sums(p, u, q)
                if n is not None:
                    turn_out(n)
                    through_wo(n)

            schedule(pe, core, ends)

        @block.scalar
        def _(act):
            act.wait_ge(s["here"], ONE + 16 * len(loads))
            act.wait_ge(s["consts"], ONE + 9)
            act.activation(lb[:], la[:], ACT.Abs).then_inc(s["lam1"], 1)
            act.wait_ge(s["lam1"], ONE + 1)
            act.activation(lb[:], lb[:], ACT.Exp, scale=-1.0).then_inc(s["lam1"], 1)
            act.wait_ge(s["lam1"], ONE + 2)
            act.activation(lb[:], lb[:], ACT.Ln, bias=eps[:, 3:4]).then_inc(s["lam1"], 1)
            for c in range(C):
                act.activation(wo[:, c, :], wo[:, c, :], ACT.Copy, scale=normw[:, c:c + 1]).then_inc(s["wo_ready"], 1)

            def take_x(n):
                act.wait_ge(s["v_mm"], ONE + n)
                act.wait_ge(s["proj_mm"], ONE + n)
                act.copy(xs[:], xf[:, :, bass.ts(n, L)]).then_inc(s["xs_done"], 1)

            def project(n):
                act.wait_ge(s["qk_mm"], ONE + n + 1)
                act.wait_ge(s["sum8"], ONE + n)
                act.activation(sqk[:].rearrange("p h d -> p (h d)"), bk[0][:], ACT.Square).then_inc(s["sqk_done"], 1)
                act.wait_ge(s["proj_mm"], ONE + n + 1)
                act.wait_ge(s["zf_done"], ONE + n)
                act.copy(z16[:], bk[2][:, 0:H]).then_inc(s["z_moved"], 1)
                act.wait_ge(s["gate_mm"], ONE + n)
                act.copy(g1T[:], bk[3][0:DH, 0:L]).then_inc(s["g1_moved"], 1)
                act.wait_ge(s["eb1_done"], ONE + n)
                act.activation(eb[:], bk[2][:, H:2 * H], ACT.Exp, scale=-1.0).then_inc(s["eb_done"], 1)
                act.wait_ge(s["zf_done"], ONE + n + 1)
                act.activation(zabs[:], zf[:], ACT.Abs).then_inc(s["zabs_done"], 1)
                act.wait_ge(s["zneg_done"], ONE + n)
                act.activation(zmin[:], zf[:], ACT.Relu, scale=-1.0).then_inc(s["zmin_done"], 1)
                act.wait_ge(s["zabs_done"], ONE + n + 1)
                act.activation(zexp[:], zabs[:], ACT.Exp, scale=-1.0).then_inc(s["zexp_done"], 1)
                act.wait_ge(s["y_done"], ONE + n)
                act.wait_ge(s["kn_done"], ONE + n)
                act.copy(qk[:], bk[0][:]).then_inc(s["qk_moved"], 1)

            def logs(n):
                act.wait_ge(s["zexp_done"], ONE + n + 1)
                act.activation(zln[:], zexp[:], ACT.Ln, bias=eps[:, 3:4]).then_inc(s["zln_done"], 1)
                act.wait_ge(s["eb_done"], ONE + n + 1)
                act.wait_ge(s["beta_done"], ONE + n)
                act.activation(eb1[:], eb[:], ACT.Ln, bias=eps[:, 3:4]).then_inc(s["eb1_done"], 1)
                act.wait_ge(s["sum1"], ONE + n + 1)
                act.wait_ge(s["rn_done"], ONE + n)
                act.activation(rln[:], ssum[:].rearrange("p h o -> p (h o)"), ACT.Ln, bias=c_small[:, 0:1]).then_inc(s["rln_done"], 1)

            def exps(n):
                act.wait_ge(s["eb1_done"], ONE + n + 1)
                act.wait_ge(s["kb_done"], ONE + n)
                act.activation(beta[:], eb1[:], ACT.Exp, scale=-1.0).then_inc(s["beta_done"], 1)
                act.wait_ge(s["rln_done"], ONE + n + 1)
                act.activation(rn[:], rln[:], ACT.Exp, scale=-0.5).then_inc(s["rn_done"], 1)

            def from_logs(n, u, q, before):
                act.wait_ge(s["a_mm"], ONE + 8 * n)
                act.wait_ge(s["lf_done"], ONE + n + 1)
                for h in [head(d, j) for d in range(4) for j in range(4)]:
                    act.activation(lfU[:, h, :], upto[:], ACT.Copy, scale=lf[:, u, q, h:h + 1]).then_inc(s["lfu_done"], 1)
                act.wait_ge(s["gate_mm"], ONE + n + 1)
                act.wait_ge(s["v_mm"], ONE + n + 1)
                if before is not None:
                    act.wait_ge(s["st_mm"], ONE + before + 1)
                    act.wait_ge(s["intra_mm"], ONE + 4 * (before + 1))
                    act.wait_ge(s["og_done"], ONE + before + 1)
                act.copy(vs[:, u, q, :], bk[1][:, 0:D]).then_inc(s["v_moved"], 1)
                act.activation(g1p[:, u, q, :], bk[1][:, D:2 * D], ACT.Tanh, scale=0.5).then_inc(s["tanh_done"], 1)
                act.wait_ge(s["f_mm"], ONE + n + 1)
                act.activation(eF[:, u, q, :], bk[3][:, 0:H], ACT.Exp).then_inc(s["ef_done"], 1)
                act.wait_ge(s["kd_done"], ONE + n)
                act.activation(eG[:], bk[3][:, H:2 * H], ACT.Exp).then_inc(s["eg_done"], 1)
                act.activation(eFT[:, u, q, :], bk[3][0:H, 2 * H:2 * H + L], ACT.Exp).then_inc(s["eft_done"], 1)

            def decays(n, u, q, d):
                if d == 0:
                    act.wait_ge(s["a_mm"], ONE + 8 * n)
                act.wait_ge(s["d_mm"], ONE + 4 * n + d + 1)
                act.activation(dec[:, u, q, d, :, :].rearrange("p j t -> p (j t)"), bk[d % 2][:], ACT.Exp).then_inc(s["dec_done"], 1)

            def matrices(n, u, q, d, solved_before):
                if d == 0:
                    if solved_before is not None:
                        act.wait_ge(s["solved"], ONE + solved_before + 1)
                    act.wait_ge(s["h_row_here"], ONE + 16 * n)
                for k in (2 * d, 2 * d + 1):
                    h0 = head(d, 2 * (k % 2))
                    act.wait_ge(s["a_mm"], ONE + 8 * n + k + 1)
                    src = bk[2 + k % 2][:, 0:2 * TRI].rearrange("p (e m) -> p e m", e=2)
                    act.copy(A[:, u, :, q * H + h0:q * H + h0 + 2].rearrange("p m e -> p e m"), src).then_inc(s["a_moved"], 1)
                    act.copy(h_last[:, h0:h0 + 2, :], src[96:P]).then_inc(s["a_moved"], 1)

            def take_solution(n, u, q):
                act.wait_ge(s["o_turned"], ONE + n)
                act.copy(qs[:].rearrange("p (h d) -> p h d", h=H), Y[:, u, :, q * H:(q + 1) * H].rearrange("p d h -> p h d")) \
                    .then_inc(s["qs_done"], 1)

            def turn_solution(n):
                act.wait_ge(s["o_turned"], ONE + n + 1)
                act.wait_ge(s["o_smm"], ONE + 4 * n)
                act.wait_ge(s["inter_mm"], ONE + n)
                for e in range(2):
                    act.activation(kbT[:, :, e, :], bk[6][:, 0:D].rearrange("p (c t) -> p c t", c=C), ACT.Copy,
                                   scale=parity[:, e:e + 1]).then_inc(s["kbt_done"], 1)
                act.copy(qsT[:], bk[6][:, D:2 * D].rearrange("p (c t) -> p c t", c=C)).then_inc(s["qst_done"], 1)

            def scores(n, d):
                act.wait_ge(s["o_smm"], ONE + 4 * n + d + 1)
                act.wait_ge(s["intra_mm"], ONE + 4 * n + max(d - 1, 0))
                act.copy(pm[:, d % 2, :], bk[4 + d % 2][:]).then_inc(s["s_moved"], 1)

            def outputs(n):
                act.wait_ge(s["intra_mm"], ONE + 4 * n + 4)
                act.wait_ge(s["inter_mm"], ONE + n + 1)
                act.wait_ge(s["o_done"], ONE + n)
                act.copy(o7[:].rearrange("p a h d -> p (a h d)"), bk[7][:]).then_inc(s["o7_moved"], 1)
                act.wait_ge(s["st_mm"], ONE + n + 1)
                act.wait_ge(s["st_done"], ONE + n)
                act.copy(st5[:], bk[5][:, 0:D + C]).then_inc(s["st_moved"], 1)

            def square(n):
                act.wait_ge(s["og_done"], ONE + n + 1)
                act.wait_ge(s["os8"], ONE + n)
                act.activation(osq[:], og[:], ACT.Square).then_inc(s["osq_done"], 1)

            def norm_log(n):
                act.wait_ge(s["os1"], ONE + n + 1)
                act.wait_ge(s["orn_done"], ONE + n)
                act.activation(oln[:], t1[:].rearrange("p h o -> p (h o)"), ACT.Ln, bias=c_eps4[:, 0:1], scale=1.0 / DH) \
                    .then_inc(s["oln_done"], 1)

            def norm_exp(n):
                act.wait_ge(s["oln_done"], ONE + n + 1)
                act.wait_ge(s["on_done"], ONE + n)
                act.activation(orn[:], oln[:], ACT.Exp, scale=-0.5).then_inc(s["orn_done"], 1)

            def out(n):
                act.wait_ge(s["on_turned"], ONE + n + 1)
                act.wait_ge(s["wo_mm"], ONE + n)
                act.copy(onT[:], bk[6][:, 0:D].rearrange("p (c t) -> p c t", c=C)).then_inc(s["ont_done"], 1)
                act.wait_ge(s["wo_mm"], ONE + n + 1)
                act.wait_ge(s["x_added"], ONE + n)
                act.copy(wo6[:], bk[6][:, D:2 * D].rearrange("p (c t) -> p c t", c=C)).then_inc(s["wo_moved"], 1)

            def core(n, p, a, u, q, pq, group, solved_before):
                if n is not None:
                    if q == 0:
                        act.wait_ge(s["solved"], ONE + group + 1)
                    take_solution(n, u, q)
                    turn_solution(n)
                if a is not None:
                    take_x(a)
                if p is not None:
                    for d in range(4):
                        decays(p, u, pq, d)
                        if n is not None and d == 1:
                            scores(n, 0)
                elif n is not None:
                    scores(n, 0)
                for d in range(4):
                    if n is not None and d < 3:
                        scores(n, d + 1)
                    if p is not None:
                        matrices(p, u, pq, d, solved_before)
                if n is not None:
                    outputs(n)

            def ends(n, p, u, q, before):
                if n is not None:
                    square(n)
                if p is not None:
                    project(p)
                    logs(p)
                if n is not None:
                    norm_log(n)
                if p is not None:
                    exps(p)
                if n is not None:
                    norm_exp(n)
                if p is not None:
                    from_logs(p, u, q, before)
                if n is not None:
                    out(n)

            schedule(act, core, ends)

        @block.gpsimd
        def _(pool):
            pool.memset(c_small[:], 1e-6).then_inc(s["consts"], 1)
            pool.memset(c_one[:], 1.0).then_inc(s["consts"], 1)
            pool.memset(c_minus[:], -1.0).then_inc(s["consts"], 1)
            pool.memset(c_eps4[:], 4e-5).then_inc(s["consts"], 1)
            pool.wait_ge(s["here"], ONE + 16 * len(loads))
            pool.tensor_copy(negb[:], negf[:]).then_inc(s["consts"], 1)
            pool.tensor_copy(identb[:], ident[:]).then_inc(s["consts"], 1)
            pool.memset(h_row, 0.0).then_inc(s["consts"], 1)
            pool.memset(state[:], 0.0).then_inc(s["consts"], 1)
            pool.wait_ge(s["consts"], ONE + 8)
            pool.tensor_tensor(delta_n[:], delta[:].unsqueeze(1).to_broadcast([P, T // L, H]),
                               restart[:].unsqueeze(2).to_broadcast([P, T // L, H]), ALU.add).then_inc(s["consts"], 1)
            pool.wait_ge(s["consts"], ONE + 9)

            def op(out, a, b, alu, done, n=None):
                pool.tensor_tensor(out, a, b, alu).then_inc(s[done], 1)
                if n is not None:
                    pool.wait_ge(s[done], ONE + n)

            def bc(t, k):
                return t.unsqueeze(2).to_broadcast([P, t.shape[1], k])

            def by_head(t):
                return t.rearrange("p (h d) -> p h d", h=H)

            def project(n, u, q):
                pool.wait_ge(s["z_moved"], ONE + n + 1)
                pool.sem_inc(s["carrier"], 1)
                op(zf[:], z16[:], delta_n[:, bass.ds(n, 1), :].rearrange("p o h -> p (o h)"), ALU.add, "zf_done", n + 1)
                pool.wait_ge(s["sqk_done"], ONE + n + 1)
                op(ta[:], sqk[:, :, 0:8], sqk[:, :, 8:16], ALU.add, "sum8", n + 1)
                op(tb[:], ta[:, :, 0:4], ta[:, :, 4:8], ALU.add, "sum4", n + 1)
                op(tc_[:], tb[:, :, 0:2], tb[:, :, 2:4], ALU.add, "sum2", n + 1)
                op(ssum[:], tc_[:, :, 0:1], tc_[:, :, 1:2], ALU.add, "sum1", n + 1)

            def log_forget(n, u, q):
                pool.wait_ge(s["zln_done"], ONE + n + 1)
                pool.wait_ge(s["zmin_done"], ONE + n + 1)
                op(zneg[:], zmin[:], zln[:], ALU.add, "zneg_done", n + 1)
                op(lf[:, u, q, :], zneg[:], c_minus[:], ALU.mult, "lf_done", n + 1)

            def keys(n, u, q, before):
                sysm = slice(q * H, (q + 1) * H)
                pool.wait_ge(s["qk_moved"], ONE + n + 1)
                pool.wait_ge(s["rn_done"], ONE + n + 1)
                if before is not None:
                    pool.wait_ge(s["qs_done"], ONE + before + 1)
                    pool.wait_ge(s["o_turned"], ONE + before + 1)
                    pool.wait_ge(s["st_mm"], ONE + before + 1)
                op(Y[:, u, :, sysm].rearrange("p d h -> p h d"), by_head(qk[:, 0:D]), bc(rn[:, 0:H], DH), ALU.mult, "y_done")
                op(kn[:], by_head(qk[:, D:2 * D]), bc(rn[:, H:2 * H], DH), ALU.mult, "kn_done", n + 1)
                pool.wait_ge(s["beta_done"], ONE + n + 1)
                kbv = by_head(kb[:, u, q, :])
                op(kbv, kn[:], bc(beta[:], DH), ALU.mult, "kb_done", n + 1)
                pool.wait_ge(s["a_mm"], ONE + 8 * n)
                for i in range(DH):
                    op(kk[:, :, off(i):off(i) + DH - i], kbv[:, :, i:i + 1].to_broadcast([P, H, DH - i]), kn[:, :, i:], ALU.mult, "kk_done")
                pool.wait_ge(s["eg_done"], ONE + n + 1)
                op(by_head(kd[:, u, q, :]), kbv, bc(eG[:], DH), ALU.mult, "kd_done")
                pool.wait_ge(s["tanh_done"], ONE + n + 1)
                op(by_head(g1p[:, u, q, :]), by_head(g1p[:, u, q, :]), bc(c_one[:], DH), ALU.add, "gate1_done", n + 1)
                pool.wait_ge(s["kk_done"], ONE + DH * (n + 1))
                pool.wait_ge(s["y_done"], ONE + n + 1)
                pool.wait_ge(s["kd_done"], ONE + n + 1)

            def weights(n, u, q):
                for d in range(4):
                    pool.wait_ge(s["s_moved"], ONE + 4 * n + d + 1)
                    op(pm[:, d % 2, :], pm[:, d % 2, :], dec[:, u, q, d, :, :].rearrange("p j t -> p (j t)"), ALU.mult, "pm_done")

            def outputs(n, u, q):
                pool.wait_ge(s["o7_moved"], ONE + n + 1)
                pool.wait_ge(s["on_turned"], ONE + n)
                op(oi[:], o7[:, 0], bc(eF[:, u, q, :], DH), ALU.mult, "oi_done", n + 1)
                op(o[:], o7[:, 1], oi[:], ALU.add, "o_done", n + 1)
                op(og[:], o[:], by_head(g1p[:, u, q, :]), ALU.mult, "og_done", n + 1)
                pool.wait_ge(s["st_moved"], ONE + n + 1)
                pool.wait_ge(s["inter_mm"], ONE + n + 1)
                op(s_own[:], st5[:, 0:D].rearrange("p (c k) -> p c k", c=C), own[:], ALU.mult, "st_own", n + 1)
                op(state[:], state[:], st5[:, D:D + C].unsqueeze(2).to_broadcast([P, C, P]), ALU.mult, "st_dec", n + 1)
                op(state[:], state[:], s_own[:], ALU.add, "st_done", n + 1)

            def square_sums(n):
                pool.wait_ge(s["osq_done"], ONE + n + 1)
                op(t8[:], osq[:, :, 0:8], osq[:, :, 8:16], ALU.add, "os8", n + 1)
                op(t4[:], t8[:, :, 0:4], t8[:, :, 4:8], ALU.add, "os4", n + 1)
                op(t2[:], t4[:, :, 0:2], t4[:, :, 2:4], ALU.add, "os2", n + 1)
                op(t1[:], t2[:, :, 0:1], t2[:, :, 1:2], ALU.add, "os1", n + 1)

            def normed(n):
                pool.wait_ge(s["orn_done"], ONE + n + 1)
                op(on[:], og[:], bc(orn[:], DH), ALU.mult, "on_done", n + 1)

            def add(n):
                pool.wait_ge(s["wo_moved"], ONE + n + 1)
                pool.sem_inc(s["carrier"], 1)
                x = xf[:, :, bass.ts(n, L)]
                pool.tensor_tensor(x, wo6[:], x, ALU.add).then_inc(s["x_added"], 1)

            def core(n, p, a, u, q, pq, group, solved_before):
                if n is not None:
                    weights(n, u, q)
                    outputs(n, u, q)

            def ends(n, p, u, q, before):
                if p is not None:
                    project(p, u, q)
                if n is not None:
                    square_sums(n)
                if p is not None:
                    log_forget(p, u, q)
                if n is not None:
                    normed(n)
                if p is not None:
                    keys(p, u, q, before)
                if n is not None:
                    add(n)

            schedule(pool, core, ends)

        @block.vector
        def _(dve):
            dve.wait_ge(s["lam1"], ONE + 3)
            dve.scalar_tensor_tensor(out=lam[:], in0=la[:], scalar=0.0, in1=lb[:], op0=ALU.max, op1=ALU.add).then_inc(s["lam2"], 1)
            dve.wait_ge(s["lam2"], ONE + 1)
            dve.tensor_scalar(lam[:], lam[:], 0.25, None, ALU.add).then_inc(s["lam_done"], 1)
            dve.wait_ge(s["lam_done"], ONE + 1)

            def solve(g, u, base):
                count = [0]

                def step(ins):
                    ins.then_inc(s["e"], 1)
                    count[0] += 1
                    return count[0]

                def upto_step(k):
                    dve.wait_ge(s["e"], ONE + base + k)

                Au, Yu = A[:, u], Y[:, u]
                dve.wait_ge(s["a_moved"], ONE + (g + 1) * SEG * 16)
                dve.wait_ge(s["y_done"], ONE + (g + 1) * SEG)
                row_done = {}
                y_last = 0
                free = {}

                def row(k):
                    return Au[:, off(k):off(k) + DH - k, :]

                def pivot(k):
                    upto_step(row_done.get(k, 0))
                    a = step(dve.tensor_tensor(piv[:].rearrange("p (q h) -> p q h", h=H), row(k)[:, 0, :].rearrange("p (q h) -> p q h", h=H),
                                               lam[:, k:k + 1, :].to_broadcast([P, SEG, H]), ALU.add))
                    yield
                    upto_step(a)
                    a = step(dve.reciprocal(rinv[:, k, :], piv[:]))
                    yield
                    m = DH - 1 - k
                    upto_step(a)
                    if m:
                        a = step(dve.tensor_tensor(mult[:, k % 2, 0:m, :], row(k)[:, 1:, :], rinv[:, k:k + 1, :].to_broadcast([P, m, SYS]), ALU.mult))
                    pivot_done[k] = a

                pivot_done = {}
                for _ in pivot(0):
                    pass
                for k in range(DH - 1):
                    m = DH - 1 - k
                    mu = mult[:, k % 2]
                    upto_step(pivot_done[k])
                    if y_last:
                        upto_step(y_last)
                    py = step(dve.tensor_tensor(prod_y[:, 0:m, :], mu[:, 0:m, :], Yu[:, k:k + 1, :].to_broadcast([P, m, SYS]), ALU.mult))
                    ahead = pivot(k + 1)
                    waiting = None
                    for i in range(k + 1, DH + 1):
                        if i < DH:
                            w_ = DH - i
                            pr = prod[:, i % 3, 0:w_, :]
                            if i % 3 in free:
                                upto_step(free[i % 3])
                            a = step(dve.tensor_tensor(pr, row(k)[:, i - k:, :], mu[:, i - k - 1:i - k, :].to_broadcast([P, w_, SYS]), ALU.mult))
                        if waiting is not None:
                            wi, wa, wp = waiting
                            upto_step(wa)
                            dst = row(wi)
                            row_done[wi] = step(dve.tensor_tensor(dst, dst, wp, ALU.subtract))
                            free[wi % 3] = row_done[wi]
                            if wi == k + 1:
                                upto_step(py)
                                y_last = step(dve.tensor_tensor(Yu[:, k + 1:, :], Yu[:, k + 1:, :], prod_y[:, 0:m, :], ALU.subtract))
                            else:
                                next(ahead, None)
                        if i < DH:
                            waiting = (i, a, pr)
                    for _ in ahead:
                        pass
                a = pivot_done[DH - 1]
                upto_step(a)
                upto_step(y_last)
                x_done = step(dve.tensor_tensor(Yu[:, DH - 1, :], Yu[:, DH - 1, :], rinv[:, DH - 1, :], ALU.mult))
                known = part = y_last
                for k in range(DH - 2, -1, -1):
                    m = DH - 1 - k
                    upto_step(x_done)
                    near = step(dve.tensor_tensor(piv[:], Au[:, off(k) + 1, :], Yu[:, k + 1, :], ALU.mult))
                    if k:
                        fa = step(dve.tensor_tensor(prod[:, k % 2, 0:m, :], Au[:, off(k - 1) + 2:off(k - 1) + DH - k + 1, :], Yu[:, k + 1:, :], ALU.mult))
                    upto_step(max(near, part))
                    a = step(dve.tensor_tensor(num[:], Yu[:, k, :], piv[:], ALU.subtract))
                    if k:
                        upto_step(fa)
                        known = step(dve.tensor_reduce(red[:], prod[:, k % 2, 0:m, :].rearrange("p j s -> p s j"), AX.X, ALU.add))
                    upto_step(a)
                    x_done = step(dve.tensor_tensor(Yu[:, k, :], num[:], rinv[:, k, :], ALU.mult))
                    if k:
                        upto_step(known)
                        part = step(dve.tensor_tensor(Yu[:, k - 1, :], Yu[:, k - 1, :], red[:], ALU.subtract))
                upto_step(x_done)
                dve.sem_inc(s["solved"], 1)
                return count[0]

            STEPS = sum(2 + (k < DH - 1) * (2 + 2 * (DH - 1 - k) + 1) for k in range(DH)) + 1 + 6 * (DH - 1) - 3
            with dve.Fori(0, NGRP // 2) as i:
                for u in range(2):
                    assert solve(2 * i + u, u, (2 * i + u) * STEPS) == STEPS
    st.close()



def decoder(nc, io, x_out):
    whole = Stage(nc, "all")
    xf = whole.sb("x", [P, C, T])
    mean_w = whole.sb("mean_w", [P, P])
    eps = whole.sb("eps", [P, 4])
    const_set = whole.sem("const_set")
    with nc.Block() as block:
        @block.vector
        def _(dve):
            dve.memset(mean_w[:], 1.0 / D).then_inc(const_set, 1)
            dve.memset(eps[:, 0:1], EPS_LN).then_inc(const_set, 1)
            dve.memset(eps[:, 1:2], 1e-6).then_inc(const_set, 1)
            dve.memset(eps[:, 2:3], 0.0).then_inc(const_set, 1)
            dve.memset(eps[:, 3:4], 1.0).then_inc(const_set, 1)
    load_stream(nc, xf, io["x"])
    if 1 in STAGES:
        mesa_attention(nc, xf, io, eps)
        layer_norm(nc, "ln0a", xf, mean_w, eps)
    if 2 in STAGES:
        context_mixture(nc, xf, io["ctx"], io["ctxT"])
        layer_norm(nc, "ln0b", xf, mean_w, eps)
    if 3 in STAGES:
        quantised_ffn(nc, xf, io, eps)
        layer_norm(nc, "ln0c", xf, mean_w, eps)
    if 4 in STAGES:
        sparse_attention(nc, xf, io, eps)
        layer_norm(nc, "ln1a", xf, mean_w, eps)
    if 5 in STAGES:
        slot_attention(nc, xf, io, mean_w, eps)
        layer_norm(nc, "ln1b", xf, mean_w, eps)
    if 6 in STAGES:
        ternary_ffn(nc, xf, io["w1T"], io["w2T"], io["h1T"], io["h2T"], io["w3T"], io["ffn1_scales"])
        layer_norm(nc, "ln1c", xf, mean_w, eps)
    store_stream(nc, xf, x_out)
    whole.close()



def rows_in_chunks(w):
    k, n = w.shape
    return np.ascontiguousarray(w.reshape(k // P, P, n).transpose(1, 0, 2))


def columns(v):
    return v.reshape(-1, P).T


def lay_out(a):
    n = {k: np.asarray(v) for k, v in a.items()}
    io = {
        "x": np.ascontiguousarray(n["x"].reshape(T, C, P).transpose(2, 1, 0)),
        "ctx": np.ascontiguousarray(n["ctx_1024"].transpose(1, 0, 2)),
        "ctxT": np.ascontiguousarray(n["ctx_1024"].reshape(B * M, C, P).transpose(2, 1, 0)),
    }
    if 6 in STAGES:
        for k, w in (("w1T", "w1_w"), ("w2T", "w2_w"), ("h1T", "h1_w"), ("h2T", "h2_w"), ("w3T", "w3_w")):
            io[k] = rows_in_chunks(n["L1_ffn_" + w].T)
        io["ffn1_scales"] = np.ascontiguousarray(np.concatenate(
            [columns(n["L1_ffn_" + w]) for w in ("w1_s", "w2_s", "h1_s", "h2_s", "w3_s")], axis=1))
    if 5 in STAGES:
        for k, w in (("slot_wkT", "Wk"), ("slot_wvT", "Wv"), ("slot_wihT", "gru_wih"), ("slot_whhT", "gru_whh")):
            io[k] = rows_in_chunks(n["L1_xattn_" + w].T)
        io["slot_wq"] = rows_in_chunks(n["L1_xattn_Wq"])
        io["slot_vectors"] = np.ascontiguousarray(np.concatenate(
            [columns(n["L1_xattn_" + w]) for w in ("slot_norm_w", "input_norm_w", "gru_bih", "gru_bhh")], axis=1))
    if 3 in STAGES:
        for k, w in (("q_gateT", "w_gate"), ("q_upT", "w_up"), ("q_downT", "w_down")):
            io[k] = rows_in_chunks(n["L0_ffn_" + w].T)
    io["identity"] = np.eye(P, dtype=np.float32)
    if 4 in STAGES:
        for k, w in (("nsa_wq", "Wq"), ("nsa_wk", "Wk"), ("nsa_wv", "Wv"), ("nsa_wo", "Wo"), ("nsa_wg", "Wg")):
            io[k] = rows_in_chunks(n["L1_attn_" + w])
        swapped = np.arange(D) ^ 1
        io["nsa_wqs"], io["nsa_wks"] = io["nsa_wq"][:, :, swapped], io["nsa_wk"][:, :, swapped]
        io["nsa_bg"] = np.ascontiguousarray(np.broadcast_to(n["L1_attn_bg"], (P, 3)))
        io["nsa_bo"] = np.ascontiguousarray(columns(n["L1_attn_bo"]))
        io["nsa_wk_comp"] = np.ascontiguousarray(np.broadcast_to(n["L1_attn_wk_comp"], (P, 16)))
        io["nsa_wv_comp"] = np.ascontiguousarray(np.tile(n["L1_attn_wv_comp"], P // 16)[:, None])
        io["nsa_pe"] = n["L1_attn_pe"]
        io["nsa_peT"] = rows_in_chunks(n["L1_attn_pe"].T)
        inv = (1.0 / np.float32(10000.0) ** (np.arange(DH // 2, dtype=np.float32) * np.float32(2.0) / np.float32(DH))).astype(np.float32)
        ang = np.arange(S, dtype=np.float32)[None, :] * np.repeat(inv, 2)[:, None]
        io["nsa_cos"] = np.tile(np.cos(ang), (P // DH, 1)).astype(np.float32)
        sign = np.tile(np.array([-1.0, 1.0], np.float32), DH // 2)[:, None]
        io["nsa_sin"] = np.tile(sign * np.sin(ang), (P // DH, 1)).astype(np.float32)
        token = np.arange(P)[:, None] + P * np.arange(S // P)[None, :]
        io["nsa_token"] = token.astype(np.float32)
        io["nsa_offset"] = np.tile(np.arange(8, dtype=np.float32), (P, 2))
        io["nsa_block_of"] = (token[:, :, None] // 16 == np.arange(S // 16)).astype(np.float32)
        seen = np.zeros((P, S // P, 64 + 16 + 192), bool)
        seen[:, :, 0:64] = (np.arange(64) + 1) * 16 <= token[:, :, None]
        key = 128 * np.arange(S // P)[None, :, None] - 64 + np.arange(192)
        seen[:, :, 80:] = (key >= 0) & (key <= token[:, :, None]) & (key > token[:, :, None] - 64)
        io["nsa_mask"] = np.where(seen, 0.0, -1e30).astype(np.float32)
    if 1 in STAGES:
        io["mesa_wqk"] = rows_in_chunks(np.concatenate([n["L0_attn_Wq"], n["L0_attn_Wk"]], axis=1))
        io["mesa_wfb"] = rows_in_chunks(np.concatenate([n["L0_attn_Wf"], n["L0_attn_Wbet"]], axis=1))
        for k, w in (("mesa_wv", "Wv"), ("mesa_gw1", "gate_w1"), ("mesa_wo", "Wo")):
            io[k] = rows_in_chunks(n["L0_attn_" + w])
        io["mesa_gw2"] = n["L0_attn_gate_w2"]
        io["mesa_norm"] = np.ascontiguousarray(columns(n["L0_attn_norm_weight"]))
        io["mesa_delta"] = np.ascontiguousarray(np.broadcast_to(n["L0_attn_delta"], (P, H)))
        io["mesa_restart"] = np.where((np.arange(P)[:, None] == 0) & (np.arange(T // P) % (S // P) == 0), -30000.0, 0.0).astype(np.float32)
        io["mesa_lambda"] = np.ascontiguousarray(np.broadcast_to(n["L0_attn_lamb_params"].reshape(H, DH).T, (P, DH, H)))
        r, c = np.arange(P)[:, None], np.arange(P)[None, :]
        io["mesa_upto"] = (r <= c).astype(np.float32)
        io["mesa_after"] = (r > c).astype(np.float32)
        io["mesa_neg"] = np.where(r <= c, 0.0, -30000.0).astype(np.float32)
        io["mesa_own"] = np.ascontiguousarray(np.broadcast_to(((r // DH) == (c // DH)).astype(np.float32)[:, None, :], (P, C, P)))
        io["mesa_expand"] = (np.arange(H)[:, None, None] == 8 * np.arange(C)[:, None] + np.arange(P) // DH).astype(np.float32)
    io["nsa_parity"] = ((np.arange(P)[:, None] // DH) % 2 == np.arange(2)).astype(np.float32)
    return io


def kernel(**inputs):
    import concourse.bacc as bacc
    from concourse.bass_utils import run_bass_kernel_spmd

    nc = bacc.Bacc("TRN2", target_bir_lowering=False, num_devices=1)
    arrays = lay_out(inputs)
    io = {k: nc.dram_tensor("in_" + k, v.shape, mybir.dt.from_np(v.dtype), kind="ExternalInput").ap() for k, v in arrays.items()}
    x_out = nc.dram_tensor("x_out", (P, C, T), F32, kind="ExternalOutput").ap()
    decoder(nc, io, x_out)
    r = run_bass_kernel_spmd(nc, [{"in_" + k: v for k, v in arrays.items()}], core_ids=[0])
    y = r.results[0]["x_out"]
    return y.transpose(2, 1, 0).reshape(B, S, D)
```

```python
from contextlib import ExitStack

import concourse.bass as bass
import numpy as np
from concourse import mybir

F32 = mybir.dt.float32
BF16 = mybir.dt.bfloat16
ALU = mybir.AluOpType
ACT = mybir.ActivationFunctionType
AX = mybir.AxisListType

P = 128
B, S, D = 4, 1024, 256
C = D // P
T = B * S
W = 512
NT = T // W
M = 77
INNER = 1024
CI = INNER // P
H, DH = 16, 16
EPS_LN = 1e-5
ONE = 1
STAGES = (1, 2, 3, 4, 5, 6)


class Stage:

    def __init__(self, nc, name):
        self.nc, self.name, self.memory, self.counters = nc, name, ExitStack(), []

    def sb(self, name, shape, dt=F32):
        return self.memory.enter_context(self.nc.sbuf_tensor(f"{self.name}_{name}", shape, dt))

    def ps(self, name, shape=(P, W), dt=F32):
        return self.memory.enter_context(self.nc.psum_tensor(f"{self.name}_{name}", list(shape), dt))

    def sem(self, name):
        self.counters.append(self.memory.enter_context(self.nc.semaphore(f"{self.name}_{name}")))
        return self.counters[-1]

    def shared_out(self, act):
        share = -(-len(self.counters) // 4)
        with self.nc.Block() as block:
            for k, engine in enumerate((block.vector, block.scalar, block.gpsimd, block.sync)):
                @engine
                def _(eng, mine=self.counters[k * share:(k + 1) * share]):
                    for sem in mine:
                        act(eng, sem)

    def start_counters(self):
        self.shared_out(lambda eng, sem: eng.sem_inc(sem, ONE))

    def close(self):
        self.shared_out(lambda eng, sem: eng.sem_clear(sem))
        self.memory.close()



def load_stream(nc, xf, x_in):
    st = Stage(nc, "load")
    x_here = st.sem("x_here")
    with nc.Block() as block:
        @block.sync
        def _(sp):
            for b in range(B):
                sp.dma_start(xf[:, :, b * S:(b + 1) * S], x_in[:, :, b * S:(b + 1) * S]).then_inc(x_here, 16)
            sp.wait_ge(x_here, 16 * B)
    st.close()


def store_stream(nc, xf, x_out):
    st = Stage(nc, "store")
    x_out_done = st.sem("x_out_done")
    with nc.Block() as block:
        @block.sync
        def _(sp):
            for b in range(B):
                sp.dma_start(x_out[:, :, b * S:(b + 1) * S], xf[:, :, b * S:(b + 1) * S]).then_inc(x_out_done, 16)
            sp.wait_ge(x_out_done, 16 * B)
    st.close()



def layer_norm(nc, name, xf, mean_w, eps_ln):
    st = Stage(nc, name)
    sq = st.sb("square", [P, 2, C, W])
    ln = st.sb("var_log", [P, NT, W])
    rs = st.sb("inverse", [P, 2, W])
    ps_mean = [st.ps(f"mean{k}") for k in range(3)]
    ps_var = [st.ps(f"var{k}") for k in range(3)]
    mean_done, cen_done, sq_done, var_done = (st.sem(n) for n in ("mean_done", "cen_done", "sq_done", "var_done"))
    ln_done, rs_done, norm_done = (st.sem(n) for n in ("ln_done", "rs_done", "norm_done"))
    cols = [slice(t * W, (t + 1) * W) for t in range(NT)]
    with nc.Block() as block:
        @block.tensor
        def _(pe):
            def var(t):
                pe.wait_ge(sq_done, t + 1)
                if t >= 3:
                    pe.wait_ge(ln_done, t - 2)
                for c in range(C):
                    mm = pe.matmul(ps_var[t % 3][:], mean_w[:], sq[:, t % 2, c, :], start=c == 0, stop=c == C - 1)
                mm.then_inc(var_done, 1)
            for t in range(NT):
                if t >= 3:
                    pe.wait_ge(cen_done, t - 2)
                for c in range(C):
                    mm = pe.matmul(ps_mean[t % 3][:], mean_w[:], xf[:, c, cols[t]], start=c == 0, stop=c == C - 1)
                mm.then_inc(mean_done, 1)
                if t >= 2:
                    var(t - 2)
            var(NT - 2)
            var(NT - 1)

        @block.vector
        def _(dve):
            for t in range(NT):
                dve.wait_ge(mean_done, t + 1)
                dve.tensor_tensor(xf[:, :, cols[t]], xf[:, :, cols[t]],
                                  ps_mean[t % 3][:].unsqueeze(1).to_broadcast([P, C, W]), ALU.subtract).then_inc(cen_done, 1)
            for t in range(NT):
                dve.wait_ge(rs_done, t + 1)
                dve.wait_ge(cen_done, t + 1)
                dve.tensor_tensor(xf[:, :, cols[t]], xf[:, :, cols[t]],
                                  rs[:, t % 2, :].unsqueeze(1).to_broadcast([P, C, W]), ALU.mult).then_inc(norm_done, 1)

        @block.scalar
        def _(act):
            for t in range(NT):
                act.wait_ge(cen_done, t + 1)
                if t >= 2:
                    act.wait_ge(var_done, t - 1)
                act.activation(sq[:, t % 2, :, :], xf[:, :, cols[t]], ACT.Square).then_inc(sq_done, 1)
                if t >= 2:
                    act.activation(ln[:, t - 2, :], ps_var[(t - 2) % 3][:], ACT.Ln, bias=eps_ln[:, 0:1]).then_inc(ln_done, 1)
            for t in (NT - 2, NT - 1):
                act.wait_ge(var_done, t + 1)
                act.activation(ln[:, t, :], ps_var[t % 3][:], ACT.Ln, bias=eps_ln[:, 0:1]).then_inc(ln_done, 1)
            for t in range(NT):
                act.wait_ge(ln_done, t + 1)
                if t >= 2:
                    act.wait_ge(norm_done, t - 1)
                act.activation(rs[:, t % 2, :], ln[:, t, :], ACT.Exp, scale=-0.5).then_inc(rs_done, 1)
    st.close()



def context_mixture(nc, xf, ctx, ctxT):
    st = Stage(nc, "mix")
    ctx_sb = st.sb("ctx", [M, B, D])
    ctxT_sb = st.sb("ctxT", [P, C, B * M])
    gel = st.sb("gelu", [M, 2, W])
    g = st.sb("g", [M, 2, W])
    ps_h = [st.ps(f"h{k}") for k in range(2)]
    ps_o = [[st.ps(f"o{k}{c}") for c in range(C)] for k in range(2)]
    ctx_here, h_done, gelu_done, g_done = (st.sem(n) for n in ("ctx_here", "h_done", "gelu_done", "g_done"))
    o_done, add_done = st.sem("o_done"), st.sem("add_done")
    cols = [slice(t * W, (t + 1) * W) for t in range(NT)]
    with nc.Block() as block:
        @block.sync
        def _(sp):
            sp.dma_start(ctx_sb[:], ctx).then_inc(ctx_here, 16)
            sp.dma_start(ctxT_sb[:], ctxT).then_inc(ctx_here, 16)

        @block.tensor
        def _(pe):
            pe.wait_ge(ctx_here, 32)

            def out(t):
                b = t * W // S
                pe.wait_ge(g_done, t + 1)
                if t >= 2:
                    pe.wait_ge(add_done, C * (t - 1))
                for c in range(C):
                    pe.matmul(ps_o[t % 2][c][:], ctx_sb[:, b, c * P:(c + 1) * P], g[:, t % 2, :],
                              start=True, stop=True).then_inc(o_done, 1)
            for t in range(NT):
                b = t * W // S
                if t >= 2:
                    pe.wait_ge(g_done, t - 1)
                for c in range(C):
                    mm = pe.matmul(ps_h[t % 2][0:M, :], ctxT_sb[:, c, b * M:(b + 1) * M], xf[:, c, cols[t]],
                                   start=c == 0, stop=c == C - 1)
                mm.then_inc(h_done, 1)
                if t >= 1:
                    out(t - 1)
            out(NT - 1)

        @block.scalar
        def _(act):
            for t in range(NT):
                act.wait_ge(h_done, t + 1)
                if t >= 2:
                    act.wait_ge(g_done, t - 1)
                act.activation(gel[:, t % 2, :], ps_h[t % 2][0:M, :], ACT.Gelu).then_inc(gelu_done, 1)

        @block.vector
        def _(dve):
            def add(t):
                for c in range(C):
                    dve.wait_ge(o_done, C * t + c + 1)
                    dve.tensor_tensor(xf[:, c, cols[t]], ps_o[t % 2][c][:], xf[:, c, cols[t]], ALU.add).then_inc(add_done, 1)
            for t in range(NT):
                dve.wait_ge(gelu_done, t + 1)
                if t >= 2:
                    dve.wait_ge(o_done, C * (t - 1))
                dve.tensor_tensor(g[:, t % 2, :], ps_h[t % 2][0:M, :], gel[:, t % 2, :], ALU.mult).then_inc(g_done, 1)
                if t >= 1:
                    add(t - 1)
            add(NT - 1)
    st.close()



def ternary_ffn(nc, xf, w1T, w2T, h1T, h2T, w3T, scales):
    st = Stage(nc, "ffn1")
    w1 = st.sb("w1", [P, C, INNER])
    w2 = st.sb("w2", [P, C, INNER])
    h1 = st.sb("h1", [P, CI, INNER])
    h2 = st.sb("h2", [P, CI, INNER])
    w3 = st.sb("w3", [P, CI, D])
    sc = st.sb("row_scales", [P, 4 * CI + C])
    xt = st.sb("x_tile", [P, 2, C, W])
    silu = st.sb("silu", [P, 2, W])
    ha = st.sb("hidden_a", [P, CI, W])
    hb = st.sb("hidden_b", [P, CI, W])
    ps = [st.ps(f"bank{k}") for k in range(8)]
    w_here = [st.sem(f"w_here{k}") for k in range(5)]
    x_ready, x_added = st.sem("x_ready"), st.sem("x_added")
    gate_done, up_done, silu_done, gated = (st.sem(n) for n in ("gate_done", "up_done", "silu_done", "gated"))
    mix1_done, gelu1_done, mix2_done, gelu2_done, out_done = (
        st.sem(n) for n in ("mix1_done", "gelu1_done", "mix2_done", "gelu2_done", "out_done"))

    def schedule(eng, tile):
        with eng.Fori(0, NT // 2 - 1) as i:
            for u in range(2):
                tile(2 * i + u, u, True)
        tile(NT - 2, 0, True)
        tile(NT - 1, 1, False)

    st.start_counters()
    with nc.Block() as block:
        @block.sync
        def _(sp):
            sp.dma_start(w1[:], w1T).then_inc(w_here[0], 16)
            sp.dma_start(w2[:], w2T).then_inc(w_here[0], 16)
            sp.dma_start(sc[:], scales).then_inc(w_here[1], 16)
            sp.dma_start(h1[:], h1T).then_inc(w_here[2], 16)
            sp.dma_start(h2[:], h2T).then_inc(w_here[3], 16)
            sp.dma_start(w3[:], w3T).then_inc(w_here[4], 16)

        @block.tensor
        def _(pe):
            pe.wait_ge(w_here[0], ONE + 32)

            def tile(t, u, more):
                pe.wait_ge(x_ready, ONE + t + 1)
                for m in range(CI):
                    rows = slice(m * P, (m + 1) * P)
                    pe.wait_ge(silu_done, ONE + t * CI + max(m - 1, 0))
                    for c in range(C):
                        mm = pe.matmul(ps[m % 2][:], w1[:, c, rows], xt[:, u, c, :], start=c == 0, stop=c == C - 1)
                    mm.then_inc(gate_done, 1)
                    pe.wait_ge(gated, ONE + t * CI + max(m - 1, 0))
                    for c in range(C):
                        mm = pe.matmul(ps[2 + m % 2][:], w2[:, c, rows], xt[:, u, c, :], start=c == 0, stop=c == C - 1)
                    mm.then_inc(up_done, 1)
                pe.wait_ge(w_here[2], ONE + 16)
                for m in range(CI):
                    pe.wait_ge(gelu1_done, ONE + t * CI + max(m - 1, 0))
                    for c in range(CI):
                        if m == 0:
                            pe.wait_ge(gated, ONE + t * CI + c + 1)
                        mm = pe.matmul(ps[4 + m % 2][:], h1[:, c, m * P:(m + 1) * P], ha[:, c, :],
                                       start=c == 0, stop=c == CI - 1)
                    mm.then_inc(mix1_done, 1)
                pe.wait_ge(w_here[3], ONE + 16)
                for m in range(CI):
                    if m <= 1:
                        pe.wait_ge(gelu1_done, ONE + t * CI + CI - 1 + m)
                    else:
                        pe.wait_ge(gelu2_done, ONE + t * CI + m - 1)
                    for c in range(CI):
                        if m == 0 and c == CI - 1:
                            pe.wait_ge(gelu1_done, ONE + t * CI + CI)
                        mm = pe.matmul(ps[4 + m % 2][:], h2[:, c, m * P:(m + 1) * P], hb[:, c, :],
                                       start=c == 0, stop=c == CI - 1)
                    mm.then_inc(mix2_done, 1)
                pe.wait_ge(w_here[4], ONE + 16)
                pe.wait_ge(x_added, ONE + t * C)
                for m in range(C):
                    for c in range(CI):
                        if m == 0:
                            pe.wait_ge(gelu2_done, ONE + t * CI + c + 1)
                        mm = pe.matmul(ps[6 + m][:], w3[:, c, m * P:(m + 1) * P], ha[:, c, :],
                                       start=c == 0, stop=c == CI - 1)
                    mm.then_inc(out_done, 1)

            schedule(pe, tile)

        @block.scalar
        def _(act):
            act.wait_ge(w_here[1], ONE + 16)

            def tile(t, u, more):
                for m in range(CI):
                    act.wait_ge(gate_done, ONE + t * CI + m + 1)
                    act.wait_ge(gated, ONE + t * CI + max(m - 1, 0))
                    act.activation(silu[:, m % 2, :], ps[m % 2][:], ACT.Silu, scale=sc[:, m:m + 1]).then_inc(silu_done, 1)
                for m in range(CI):
                    act.wait_ge(mix1_done, ONE + t * CI + m + 1)
                    act.activation(hb[:, m, :], ps[4 + m % 2][:], ACT.Gelu,
                                   scale=sc[:, 2 * CI + m:2 * CI + m + 1]).then_inc(gelu1_done, 1)
                act.wait_ge(mix1_done, ONE + t * CI + CI)
                for m in range(CI):
                    act.wait_ge(mix2_done, ONE + t * CI + m + 1)
                    act.activation(ha[:, m, :], ps[4 + m % 2][:], ACT.Gelu,
                                   scale=sc[:, 3 * CI + m:3 * CI + m + 1]).then_inc(gelu2_done, 1)

            schedule(act, tile)

        @block.vector
        def _(dve):
            dve.wait_ge(w_here[1], ONE + 16)
            dve.tensor_copy(xt[:, 0], xf[:, :, 0:W]).then_inc(x_ready, 1)

            def tile(t, u, more):
                dve.wait_ge(out_done, ONE + t * C)
                for m in range(CI):
                    dve.wait_ge(silu_done, ONE + t * CI + m + 1)
                    dve.wait_ge(up_done, ONE + t * CI + m + 1)
                    dve.scalar_tensor_tensor(out=ha[:, m, :], in0=ps[2 + m % 2][:], scalar=sc[:, CI + m:CI + m + 1],
                                             in1=silu[:, m % 2, :], op0=ALU.mult, op1=ALU.mult).then_inc(gated, 1)
                if more:
                    dve.tensor_copy(xt[:, 1 - u], xf[:, :, bass.ds((t + 1) * W, W)]).then_inc(x_ready, 1)
                for c in range(C):
                    x = xf[:, c, bass.ds(t * W, W)]
                    dve.wait_ge(out_done, ONE + t * C + c + 1)
                    dve.scalar_tensor_tensor(out=x, in0=ps[6 + c][:], scalar=sc[:, 4 * CI + c:4 * CI + c + 1], in1=x,
                                             op0=ALU.mult, op1=ALU.add).then_inc(x_added, 1)

            schedule(dve, tile)
    st.close()


def slot_attention(nc, xf, io, mean_w, eps):
    G3 = 3 * D
    ROUNDS = 3
    TW = S // W
    RMS_EPS = eps[:, 1:2]
    st = Stage(nc, "slot")
    ctxT = st.sb("ctxT", [P, C, B * M])
    wkT, wq, wvT = st.sb("wkT", [P, C, D]), st.sb("wq", [P, C, D]), st.sb("wvT", [P, C, D])
    wihT, whhT = st.sb("wihT", [P, C, G3]), st.sb("whhT", [P, C, G3])
    vecs = st.sb("vectors", [P, 2 * C + 12])
    bias = st.sb("bias", [P, 8])
    sq = st.sb("ctx_square", [P, C, B * M])
    rinv = st.sb("ctx_inverse", [P, B * M])
    root = st.sb("ctx_root", [P, B * M])
    pn = st.sb("ctx_normed", [P, C, B * M])
    kT, vT = st.sb("kT", [P, C, B * M]), st.sb("vT", [P, C, B * M])
    keys = st.sb("keys", [P, C, B * M])
    vals = st.sb("values", [M, B, G3])
    key_b, val_b = st.sb("key_b", [P, C, M]), st.sb("val_b", [M, G3])
    slots = [st.sb(f"slots{k}", [P, C, T]) for k in range(2)]
    ssq = st.sb("slot_square", [P, C, S])
    srs = st.sb("slot_inverse", [M, S])
    score = st.sb("score", [M, S])
    prob = st.sb("prob", [M, S])
    attn = st.sb("attn", [M, S])
    minv = st.sb("mass_inverse", [M, S])
    mx, nmx, zsum, zinv = (st.sb(n, [M, 1]) for n in ("top", "minus_top", "sum", "sum_inverse"))
    ones_m = st.sb("ones", [M, M])
    gate_r, gate_z = st.sb("reset", [P, 2, W]), st.sb("update", [P, 2, W])
    hid, new = st.sb("hidden", [P, 2, W]), st.sb("new", [P, 2, W])
    pre, arg = st.sb("reset_hidden", [P, 2, W]), st.sb("new_argument", [P, 2, W])
    dif, dif2 = st.sb("difference", [P, 2, W]), st.sb("gated_difference", [P, 2, W])
    bank = [st.ps(f"bank{k}") for k in range(8)]
    here = st.sem("inputs_here")
    names = ("bias_ready csq_done cms_done croot_done cinv_done pn_half pn_done kv_done kv_copied keys_done keys_copied "
             "vals_done vals_copied ones_set key_ready val_ready carrier slots_square ms_done ms_ln srs_done scores_done scaled top_done "
             "minus_done prob_done zinv_done attn_done mass_done mass_ln minv_done attn_normed hid_done reset_done update_done "
             "cell_done pre_done arg_done new_done dif_done dif2_done slots_done x_added").split()
    s = {n: st.sem(n) for n in names}
    HALVES = TW * C
    LATE = ONE + 1
    current = [xf] + slots

    def half_tile(b, k):
        t, m = k // C, k % C
        return m, bass.ds(b * S + t * W, W)

    def schedule(eng, attention, cell):
        def unit(n, r, b, a, ra, ba):
            if a is not None:
                attention(0, a, ra, ba)
            for k in range(HALVES):
                cell(n, r, b, k)
                if a is not None:
                    attention(k + 1, a, ra, ba)
        for part in range(HALVES + 1):
            attention(part, 0, 0, 0)
        for r in range(ROUNDS):
            eng.sem_inc(s["carrier"], 1)
            with eng.Fori(0, B - 1) as b:
                unit(r * B + b, r, b, r * B + b + 1, r, b + 1)
            if r < ROUNDS - 1:
                unit(r * B + B - 1, r, B - 1, (r + 1) * B, r + 1, 0)
            else:
                unit(r * B + B - 1, r, B - 1, None, None, None)
    st.start_counters()
    with nc.Block() as block:
        @block.sync
        def _(sp):
            for dst, src in ((ctxT, "ctxT"), (wkT, "slot_wkT"), (wq, "slot_wq"), (wvT, "slot_wvT"), (wihT, "slot_wihT"),
                             (whhT, "slot_whhT"), (vecs, "slot_vectors")):
                sp.dma_start(dst[:], io[src]).then_inc(here, 16)

        @block.tensor
        def _(pe):
            pe.wait_ge(s["csq_done"], ONE + 1)
            for c in range(C):
                mm = pe.matmul(bank[0][:, 0:B * M], mean_w[:], sq[:, c, :], start=c == 0, stop=c == C - 1)
            mm.then_inc(s["cms_done"], 1)
            pe.wait_ge(s["pn_done"], ONE + C)
            for k, w in enumerate((wkT, wvT)):
                for m in range(C):
                    for c in range(C):
                        mm = pe.matmul(bank[1 + 2 * k + m][:, 0:B * M], w[:, c, m * P:(m + 1) * P], pn[:, c, :],
                                       start=c == 0, stop=c == C - 1)
                    mm.then_inc(s["kv_done"], 1)
            pe.wait_ge(s["kv_copied"], ONE + 2 * C)
            for m in range(C):
                for c in range(C):
                    mm = pe.matmul(bank[5 + m][:, 0:B * M], wq[:, c, m * P:(m + 1) * P], kT[:, c, :],
                                   start=c == 0, stop=c == C - 1)
                mm.then_inc(s["keys_done"], 1)
            for b in range(B):
                for h in range(2):
                    n = 2 * b + h
                    if n >= 2:
                        pe.wait_ge(s["vals_copied"], ONE + n - 1)
                    for c in range(C):
                        mm = pe.matmul(bank[1 + n % 2][0:M, 0:G3 // 2], vT[:, c, b * M:(b + 1) * M],
                                       wihT[:, c, h * (G3 // 2):(h + 1) * (G3 // 2)], start=c == 0, stop=c == C - 1)
                    mm.then_inc(s["vals_done"], 1)
            pe.wait_ge(s["ones_set"], ONE + 1)
            pe.wait_ge(s["keys_copied"], ONE + C)
            pe.wait_ge(s["vals_copied"], ONE + 2 * B)

            def attention(part, a, r, b):
                cur = current[r]
                if part == 1:
                    pe.wait_ge(s["slots_square"], ONE + a + 1)
                    pe.wait_ge(s["mass_ln"], ONE + TW * a)
                    for t in range(TW):
                        for c in range(C):
                            mm = pe.matmul(bank[4 + t][0:M, :], mean_w[:, 0:M], ssq[:, c, t * W:(t + 1) * W],
                                           start=c == 0, stop=c == C - 1)
                        mm.then_inc(s["ms_done"], 1)
                    pe.wait_ge(s["scaled"], ONE + TW * a)
                    pe.wait_ge(s["key_ready"], ONE + a + 1)
                    for t in range(TW):
                        for c in range(C):
                            mm = pe.matmul(bank[6 + t][0:M, :], key_b[:, c, :], cur[:, c, bass.ds(b * S + t * W, W)],
                                           start=c == 0, stop=c == C - 1)
                        mm.then_inc(s["scores_done"], 1)
                if part == 3:
                    pe.wait_ge(s["attn_done"], ONE + a + 1)
                    pe.wait_ge(s["ms_ln"], ONE + TW * (a + 1))
                    for t in range(TW):
                        pe.matmul(bank[4 + t][0:M, :], ones_m[:], attn[:, t * W:(t + 1) * W], start=True, stop=True) \
                            .then_inc(s["mass_done"], 1)

            def cell(n, r, b, k):
                cur, j = current[r], n * HALVES + k
                m, x = half_tile(b, k)
                rows = [slice(g * D + m * P, g * D + (m + 1) * P) for g in range(3)]

                def hidden(q, g, stop):
                    for c in range(C):
                        mm = pe.matmul(bank[q][:], whhT[:, c, rows[g]], cur[:, c, x], start=c == 0, stop=stop and c == C - 1)
                    return mm
                tx = slice(k // C * W, (k // C + 1) * W)
                pe.wait_ge(s["hid_done"], ONE + j)
                hidden(2, 2, True).then_inc(s["cell_done"], 1)
                for g, read in enumerate((s["reset_done"], s["update_done"])):
                    pe.wait_ge(read, ONE + j)
                    hidden(g, g, False)
                    if k == 0 and g == 0:
                        pe.wait_ge(s["val_ready"], ONE + n + 1)
                        pe.wait_ge(s["attn_normed"], ONE + n + 1)
                    pe.matmul(bank[g][:], val_b[:, rows[g]], prob[:, tx], start=False, stop=True).then_inc(s["cell_done"], 1)
                pe.wait_ge(s["arg_done"], ONE + j)
                pe.matmul(bank[3][:], val_b[:, rows[2]], prob[:, tx], start=True, stop=True).then_inc(s["cell_done"], 1)

            schedule(pe, attention, cell)

        @block.scalar
        def _(act):
            act.wait_ge(here, ONE + 16 * 7)
            act.activation(sq[:], ctxT[:], ACT.Square).then_inc(s["csq_done"], 1)
            act.wait_ge(s["cms_done"], ONE + 1)
            act.activation(root[:], bank[0][:, 0:B * M], ACT.Sqrt, bias=RMS_EPS).then_inc(s["croot_done"], 1)
            for k, dst in enumerate((kT, vT)):
                for m in range(C):
                    act.wait_ge(s["kv_done"], ONE + 2 * k + m + 1)
                    act.copy(dst[:, m, :], bank[1 + 2 * k + m][:, 0:B * M]).then_inc(s["kv_copied"], 1)
            for b in range(B):
                for h in range(2):
                    n = 2 * b + h
                    act.wait_ge(s["vals_done"], ONE + n + 1)
                    act.copy(vals[:, b, h * (G3 // 2):(h + 1) * (G3 // 2)], bank[1 + n % 2][0:M, 0:G3 // 2]) \
                        .then_inc(s["vals_copied"], 1)
            act.wait_ge(s["bias_ready"], ONE + 4)

            def attention(part, a, r, b):
                if part == 0:
                    if r >= 1:
                        act.wait_ge(s["slots_done"], LATE + HALVES * (a - B + 1))
                    act.wait_ge(s["ms_done"], ONE + TW * a)
                    act.activation(ssq[:], current[r][:, :, bass.ds(b * S, S)], ACT.Square).then_inc(s["slots_square"], 1)
                if part == 1:
                    for t in range(TW):
                        x = slice(t * W, (t + 1) * W)
                        act.wait_ge(s["ms_done"], ONE + TW * a + t + 1)
                        act.wait_ge(s["scaled"], ONE + TW * a)
                        act.activation(srs[:, x], bank[4 + t][0:M, :], ACT.Ln, bias=eps[0:M, 1:2]).then_inc(s["ms_ln"], 1)
                    for t in range(TW):
                        x = slice(t * W, (t + 1) * W)
                        act.wait_ge(s["ms_ln"], ONE + TW * a + t + 1)
                        act.activation(srs[:, x], srs[:, x], ACT.Exp, scale=-0.5).then_inc(s["srs_done"], 1)
                if part == 2:
                    act.wait_ge(s["minus_done"], ONE + a + 1)
                    act.wait_ge(s["mass_done"], ONE + TW * a)
                    act.wait_ge(s["attn_normed"], ONE + a)
                    act.activation(attn[:], score[:], ACT.Exp, bias=nmx[:], accum_out=zsum[:]).then_inc(s["prob_done"], 1)
                if part == 3:
                    for t in range(TW):
                        x = slice(t * W, (t + 1) * W)
                        act.wait_ge(s["mass_done"], ONE + TW * a + t + 1)
                        act.wait_ge(s["attn_normed"], ONE + a)
                        act.activation(minv[:, x], bank[4 + t][0:M, :], ACT.Ln, bias=eps[0:M, 1:2]).then_inc(s["mass_ln"], 1)
                    act.wait_ge(s["mass_ln"], ONE + TW * (a + 1))
                    act.activation(minv[:], minv[:], ACT.Exp, scale=-1.0).then_inc(s["minv_done"], 1)

            def cell(n, r, b, k):
                m, j = k % C, n * HALVES + k
                act.wait_ge(s["cell_done"], ONE + 4 * j + 1)
                act.wait_ge(s["slots_done"], LATE + j - 1)
                act.activation(hid[:, k % 2, :], bank[2][:], ACT.Identity, bias=bias[:, 6 + m:7 + m], scale=0.5) \
                    .then_inc(s["hid_done"], 1)
                act.wait_ge(s["cell_done"], ONE + 4 * j + 2)
                act.activation(gate_r[:, k % 2, :], bank[0][:], ACT.Tanh, bias=bias[:, m:m + 1], scale=0.5).then_inc(s["reset_done"], 1)
                act.wait_ge(s["cell_done"], ONE + 4 * j + 3)
                act.activation(gate_z[:, k % 2, :], bank[1][:], ACT.Tanh, bias=bias[:, C + m:C + m + 1], scale=0.5) \
                    .then_inc(s["update_done"], 1)
                act.wait_ge(s["arg_done"], ONE + j + 1)
                act.activation(new[:, k % 2, :], arg[:, k % 2, :], ACT.Tanh).then_inc(s["new_done"], 1)

            schedule(act, attention, cell)

        @block.gpsimd
        def _(pool):
            pool.sem_inc(s["dif2_done"], LATE - ONE)
            pool.sem_inc(s["slots_done"], LATE - ONE)
            pool.wait_ge(s["keys_copied"], ONE + C)
            pool.wait_ge(s["vals_copied"], ONE + 2 * B)

            def attention(part, a, r, b):
                if part == 0:
                    pool.wait_ge(s["scores_done"], ONE + TW * a)
                    pool.sem_inc(s["carrier"], 1)
                    pool.tensor_copy(key_b[:], keys[:, :, bass.ds(b * M, M)]).then_inc(s["key_ready"], 1)
                    pool.wait_ge(s["key_ready"], ONE + a + 1)

            def cell(n, r, b, k):
                if k == 0:
                    pool.wait_ge(s["cell_done"], ONE + 4 * HALVES * n)
                    pool.sem_inc(s["carrier"], 1)
                    pool.tensor_copy(val_b[:], vals[:, bass.ds(b, 1), :].rearrange("p o x -> p (o x)")).then_inc(s["val_ready"], 1)
                    pool.wait_ge(s["val_ready"], ONE + n + 1)
                m, x = half_tile(b, k)
                j = n * HALVES + k
                pool.wait_ge(s["new_done"], ONE + j + 1)
                pool.wait_ge(s["dif2_done"], LATE + j - 1)
                pool.sem_inc(s["carrier"], 1)
                pool.tensor_tensor(dif[:, k % 2, :], current[r][:, m, x], new[:, k % 2, :], ALU.subtract).then_inc(s["dif_done"], 1)

            schedule(pool, attention, cell)

        @block.vector
        def _(dve):
            dve.wait_ge(here, ONE + 16 * 7)
            dve.memset(ones_m[:], 1.0).then_inc(s["ones_set"], 1)
            dve.tensor_tensor(bias[:, 0:4], vecs[:, 4:8], vecs[:, 10:14], ALU.add).then_inc(s["bias_ready"], 1)
            dve.wait_ge(s["bias_ready"], ONE + 1)
            dve.tensor_scalar(bias[:, 0:4], bias[:, 0:4], 0.5, None, ALU.mult).then_inc(s["bias_ready"], 1)
            dve.tensor_copy(bias[:, 4:6], vecs[:, 8:10]).then_inc(s["bias_ready"], 1)
            dve.tensor_scalar(bias[:, 6:8], vecs[:, 14:16], 0.5, None, ALU.mult).then_inc(s["bias_ready"], 1)
            dve.wait_ge(s["croot_done"], ONE + 1)
            dve.reciprocal(rinv[:], root[:]).then_inc(s["cinv_done"], 1)
            dve.wait_ge(s["cinv_done"], ONE + 1)
            for c in range(C):
                dve.scalar_tensor_tensor(out=pn[:, c, :], in0=ctxT[:, c, :], scalar=vecs[:, C + c:C + c + 1],
                                         in1=rinv[:], op0=ALU.mult, op1=ALU.mult).then_inc(s["pn_done"], 1)
            for m in range(C):
                dve.wait_ge(s["keys_done"], ONE + m + 1)
                dve.tensor_scalar(keys[:, m, :], bank[5 + m][:, 0:B * M], vecs[:, m:m + 1], float(D) ** -0.5,
                                  ALU.mult, ALU.mult).then_inc(s["keys_copied"], 1)
            dve.wait_ge(s["bias_ready"], ONE + 4)

            def attention(part, a, r, b):
                if part == 1:
                    dve.wait_ge(s["prob_done"], ONE + a)
                    for t in range(TW):
                        x = slice(t * W, (t + 1) * W)
                        dve.wait_ge(s["srs_done"], ONE + TW * a + t + 1)
                        dve.wait_ge(s["scores_done"], ONE + TW * a + t + 1)
                        dve.tensor_tensor(score[:, x], bank[6 + t][0:M, :], srs[:, x], ALU.mult).then_inc(s["scaled"], 1)
                    dve.wait_ge(s["scaled"], ONE + TW * (a + 1))
                    dve.tensor_reduce(mx[:], score[:], AX.X, ALU.max).then_inc(s["top_done"], 1)
                    dve.wait_ge(s["top_done"], ONE + a + 1)
                    dve.tensor_scalar(nmx[:], mx[:], -1.0, None, ALU.mult).then_inc(s["minus_done"], 1)
                if part == 2:
                    dve.wait_ge(s["prob_done"], ONE + a + 1)
                    dve.reciprocal(zinv[:], zsum[:]).then_inc(s["zinv_done"], 1)
                    dve.wait_ge(s["zinv_done"], ONE + a + 1)
                    dve.tensor_scalar(attn[:], attn[:], zinv[:], None, ALU.mult).then_inc(s["attn_done"], 1)
                if part == 3:
                    dve.wait_ge(s["minv_done"], ONE + a + 1)
                    dve.wait_ge(s["cell_done"], ONE + 4 * HALVES * a)
                    dve.tensor_tensor(prob[:], attn[:], minv[:], ALU.mult).then_inc(s["attn_normed"], 1)

            def cell(n, r, b, k):
                m, x = half_tile(b, k)
                j = n * HALVES + k
                dve.wait_ge(s["reset_done"], ONE + j + 1)
                dve.wait_ge(s["hid_done"], ONE + j + 1)
                dve.scalar_tensor_tensor(out=pre[:, k % 2, :], in0=gate_r[:, k % 2, :], scalar=1.0,
                                         in1=hid[:, k % 2, :], op0=ALU.add, op1=ALU.mult).then_inc(s["pre_done"], 1)
                dve.wait_ge(s["pre_done"], ONE + j + 1)
                dve.wait_ge(s["cell_done"], ONE + 4 * j + 4)
                dve.scalar_tensor_tensor(out=arg[:, k % 2, :], in0=bank[3][:], scalar=bias[:, 4 + m:5 + m],
                                         in1=pre[:, k % 2, :], op0=ALU.add, op1=ALU.add).then_inc(s["arg_done"], 1)
                dve.wait_ge(s["dif_done"], ONE + j + 1)
                dve.wait_ge(s["update_done"], ONE + j + 1)
                dve.scalar_tensor_tensor(out=dif2[:, k % 2, :], in0=gate_z[:, k % 2, :], scalar=1.0,
                                         in1=dif[:, k % 2, :], op0=ALU.add, op1=ALU.mult).then_inc(s["dif2_done"], 1)
                dve.wait_ge(s["dif2_done"], LATE + j + 1)
                dve.scalar_tensor_tensor(out=slots[r % 2][:, m, x], in0=dif2[:, k % 2, :], scalar=0.5,
                                         in1=new[:, k % 2, :], op0=ALU.mult, op1=ALU.add).then_inc(s["slots_done"], 1)
                if r == ROUNDS - 1 and k == HALVES - 1:
                    dve.wait_ge(s["slots_done"], LATE + HALVES * (n + 1))
                    row = bass.ds(b * S, S)
                    dve.tensor_tensor(xf[:, :, row], xf[:, :, row], slots[r % 2][:, :, row], ALU.add).then_inc(s["x_added"], 1)

            schedule(dve, attention, cell)
            dve.wait_ge(s["x_added"], ONE + B)
    st.close()


def quantised_ffn(nc, xf, io, eps):
    TT = 128
    N = T // TT
    HALF = INNER // 2
    X = 4
    MAGIC = 1.5 * 2.0 ** 23
    st = Stage(nc, "ffn0")
    wf = [st.sb(f"w_float{k}", [P, 2 * INNER]) for k in range(3)]
    wq = [st.sb(f"w_tern{k}", [P, 2 * INNER], BF16) for k in range(3)]
    wabs = st.sb("w_abs", [P, 2 * INNER])
    wr = st.sb("w_rounded", [P, 2 * INNER])
    wsum, wmean, wscale = st.sb("w_sum", [P, 3]), st.sb("w_mean", [P, 3]), st.sb("w_scale", [P, 3])
    wmean127 = st.sb("w_mean_127", [P, 3])
    count_w = st.sb("count_w", [P, P])
    magic = st.sb("magic", [P, 1])
    identf, identb = st.sb("identity", [P, P]), st.sb("identity_b", [P, P], BF16)
    xc = st.sb("x_tile", [P, X, C, TT])
    xr, xq = st.sb("x_rounded", [P, D]), st.sb("x_quantised", [P, D], BF16)
    xqT = st.sb("x_quantisedT", [P, X, C, TT], BF16)
    sg, h = st.sb("silu", [P, INNER]), st.sb("h", [P, INNER])
    hr, hq = st.sb("h_rounded", [P, INNER]), st.sb("h_quantised", [P, INNER], BF16)
    hqT = st.sb("h_quantisedT", [P, CI, TT], BF16)
    o = st.sb("o", [P, D])
    xm = st.sb("x_scales", [P, X, 6])
    hm = st.sb("h_scales", [P, 2, 5])
    ps_x = st.ps("xT", [P, D])
    ps_q = st.ps("xqT_bank", [P, C, TT], BF16)
    ps_g = [st.ps(f"gate{k}") for k in range(2)]
    ps_u = [st.ps(f"up{k}") for k in range(2)]
    ps_h = st.ps("hqT_bank", [P, CI, TT], BF16)
    ps_o = st.ps("out", [P, 2, D])
    names = ("here consts wsum_done wtot_done wm_done wstep wq_done x_copied x_turned xmax xstep xr_done xq_done xq_turned "
             "xqT_done gu_done silu_done h_done hmax hstep hr_done hq_done h_turned hqT_done down_done o_done o_turned "
             "added h_half").split()
    s = {n: st.sem(n) for n in names}

    def cols(n):
        return bass.ts(n, TT)

    st.start_counters()
    with nc.Block() as block:
        @block.sync
        def _(sp):
            for k, name in enumerate(("q_gateT", "q_upT", "q_downT")):
                sp.dma_start(wf[k][:], io[name].rearrange("p c n -> p (c n)")).then_inc(s["here"], 16)
            sp.dma_start(identf[:], io["identity"]).then_inc(s["here"], 16)

        @block.tensor
        def _(pe):
            pe.wait_ge(s["wsum_done"], ONE + 3)
            pe.wait_ge(s["consts"], ONE + 3)
            pe.matmul(ps_x[:, 0:3], count_w[:], wsum[:], start=True, stop=True).then_inc(s["wtot_done"], 1)
            pe.wait_ge(s["wq_done"], ONE + 3)
            pe.wait_ge(s["wm_done"], ONE + 1)

            def turn_x(n, u):
                pe.wait_ge(s["x_copied"], ONE + n + 1)
                pe.wait_ge(s["xr_done"], ONE + n)
                pe.wait_ge(s["xmax"], ONE + n)
                for c in range(C):
                    mm = pe.transpose(ps_x[:, c * TT:(c + 1) * TT], xc[:, u, c, :], identf[:])
                mm.then_inc(s["x_turned"], 1)

            def turn_xq(n):
                pe.wait_ge(s["xq_done"], ONE + n + 1)
                pe.wait_ge(s["xqT_done"], ONE + n)
                for c in range(C):
                    mm = pe.transpose(ps_q[:, c, :], xq[:, c * TT:(c + 1) * TT], identb[:])
                mm.then_inc(s["xq_turned"], 1)

            def gate_up(n, u):
                pe.wait_ge(s["xqT_done"], ONE + n + 1)
                pe.wait_ge(s["h_done"], ONE + n)
                pe.wait_ge(s["silu_done"], ONE + 2 * n)
                for bank, w in ((ps_g, wq[0]), (ps_u, wq[1])):
                    for f in range(2):
                        for c in range(C):
                            mm = pe.matmul(bank[f][:], xqT[:, u, c, :], w[:, c * INNER + f * HALF:c * INNER + (f + 1) * HALF],
                                           start=c == 0, stop=c == C - 1)
                        mm.then_inc(s["gu_done"], 1)

            def turn_hq(n):
                pe.wait_ge(s["hq_done"], ONE + n + 1)
                pe.wait_ge(s["hqT_done"], ONE + n)
                for c in range(CI):
                    mm = pe.transpose(ps_h[:, c, :], hq[:, c * TT:(c + 1) * TT], identb[:])
                mm.then_inc(s["h_turned"], 1)

            def down(n):
                pe.wait_ge(s["hqT_done"], ONE + n + 1)
                pe.wait_ge(s["o_done"], ONE + n)
                pe.wait_ge(s["added"], ONE + n)
                for c in range(CI):
                    mm = pe.matmul(ps_o[:, 0, :], hqT[:, c, :], wq[2][:, c * D:(c + 1) * D], start=c == 0, stop=c == CI - 1)
                mm.then_inc(s["down_done"], 1)

            def turn_o(n):
                pe.wait_ge(s["o_done"], ONE + n + 1)
                for c in range(C):
                    mm = pe.transpose(ps_o[:, 1, c * TT:(c + 1) * TT], o[:, c * TT:(c + 1) * TT], identf[:])
                mm.then_inc(s["o_turned"], 1)

            def step(n, j, left=X):
                if left >= 1:
                    gate_up(n + 1, (j + 1) % X)
                if left >= 3:
                    turn_x(n + 3, (j + 3) % X)
                turn_hq(n)
                down(n)
                if left >= 3:
                    turn_xq(n + 3)
                turn_o(n)

            for n in range(3):
                turn_x(n, n)
                turn_xq(n)
            gate_up(0, 0)
            with pe.Fori(0, N // X - 1) as i:
                for j in range(X):
                    step(X * i + j, j)
            for j in range(X):
                step(N - X + j, j, X - 1 - j)

        @block.scalar
        def _(act):
            for k in range(3):
                act.wait_ge(s["here"], ONE + 16 * 4)
                if k:
                    act.wait_ge(s["wsum_done"], ONE + k)
                act.activation(wabs[:], wf[k][:], ACT.Abs, accum_out=wsum[:, k:k + 1]).then_inc(s["wsum_done"], 1)
            act.wait_ge(s["consts"], ONE + 4)

            def copy_x(n, u):
                act.wait_ge(s["x_turned"], ONE + n)
                act.copy(xc[:, u, :, :], xf[:, :, cols(n)]).then_inc(s["x_copied"], 1)

            def round_x(n, u):
                act.wait_ge(s["xstep"], ONE + 5 * n + 5)
                act.wait_ge(s["xq_done"], ONE + n)
                act.activation(xr[:], ps_x[:], ACT.Identity, bias=magic[:], scale=xm[:, u, 3:4]).then_inc(s["xr_done"], 1)

            def copy_xq(n, u):
                act.wait_ge(s["xq_turned"], ONE + n + 1)
                act.copy(xqT[:, u, :, :], ps_q[:]).then_inc(s["xqT_done"], 1)

            def silu(n, u):
                act.wait_ge(s["h_done"], ONE + n)
                for f in range(2):
                    act.wait_ge(s["gu_done"], ONE + 4 * n + f + 1)
                    act.activation(sg[:, f * HALF:(f + 1) * HALF], ps_g[f][:], ACT.Silu, scale=xm[:, u, 4:5]) \
                        .then_inc(s["silu_done"], 1)

            def round_h(n, u):
                act.wait_ge(s["hstep"], ONE + 4 * n + 4)
                act.wait_ge(s["hq_done"], ONE + n)
                act.activation(hr[:], h[:], ACT.Identity, bias=magic[:], scale=hm[:, u, 3:4]).then_inc(s["hr_done"], 1)

            def copy_hq(n):
                act.wait_ge(s["h_turned"], ONE + n + 1)
                act.wait_ge(s["down_done"], ONE + n)
                act.copy(hqT[:], ps_h[:]).then_inc(s["hqT_done"], 1)

            def scale_o(n, u):
                act.wait_ge(s["down_done"], ONE + n + 1)
                act.wait_ge(s["o_turned"], ONE + n)
                act.activation(o[:], ps_o[:, 0, :], ACT.Copy, scale=hm[:, u, 4:5]).then_inc(s["o_done"], 1)

            def step(n, j, left=X):
                if left >= 1:
                    silu(n + 1, (j + 1) % X)
                copy_hq(n)
                if left >= 4:
                    copy_x(n + 4, j)
                if left >= 1:
                    round_h(n + 1, (j + 1) % 2)
                if left >= 3:
                    round_x(n + 3, (j + 3) % X)
                scale_o(n, j % 2)
                if left >= 3:
                    copy_xq(n + 3, (j + 3) % X)

            for n in range(3):
                copy_x(n, n)
                round_x(n, n)
                copy_xq(n, n)
            copy_x(3, 3)
            silu(0, 0)
            round_h(0, 0)
            with act.Fori(0, N // X - 1) as i:
                for j in range(X):
                    step(X * i + j, j)
            for j in range(X):
                step(N - X + j, j, X - 1 - j)

        @block.gpsimd
        def _(pool):
            pool.memset(count_w[:], 1.0 / (INNER * D)).then_inc(s["consts"], 1)
            pool.memset(magic[:], MAGIC).then_inc(s["consts"], 1)
            pool.wait_ge(s["here"], ONE + 16 * 4)
            pool.tensor_copy(identb[:], identf[:]).then_inc(s["consts"], 1)

        @block.vector
        def _(dve):
            dve.wait_ge(s["wtot_done"], ONE + 1)
            dve.tensor_scalar(wmean[:], ps_x[:, 0:3], 1e-5, None, ALU.max).then_inc(s["wm_done"], 1)
            dve.wait_ge(s["wm_done"], ONE + 1)
            dve.reciprocal(wscale[:], wmean[:]).then_inc(s["wstep"], 1)
            dve.tensor_scalar(wmean127[:], wmean[:], 1.0 / 127.0, None, ALU.mult).then_inc(s["wstep"], 1)
            dve.wait_ge(s["wstep"], ONE + 2)
            for k in range(3):
                if k:
                    dve.wait_ge(s["wq_done"], ONE + k)
                dve.tensor_scalar(wr[:], wf[k][:], wscale[:, k:k + 1], MAGIC, ALU.mult, ALU.add).then_inc(s["wstep"], 1)
                dve.wait_ge(s["wstep"], ONE + 3 + 2 * k)
                dve.tensor_scalar(wr[:], wr[:], -MAGIC, 1.0, ALU.add, ALU.min).then_inc(s["wstep"], 1)
                dve.wait_ge(s["wstep"], ONE + 4 + 2 * k)
                dve.tensor_scalar(wq[k][:], wr[:], -1.0, None, ALU.max).then_inc(s["wq_done"], 1)
            dve.memset(xm[:], 1.0).then_inc(s["consts"], 1)
            dve.wait_ge(s["consts"], ONE + 4)

            def scales(n, u, m, mx, step, outs):
                k = 3 + len(outs)
                def next_step(a, c):
                    a.then_inc(step, 1)
                    dve.wait_ge(step, ONE + k * n + c)
                next_step(dve.tensor_scalar(m[:, u, 1:2], m[:, u, 0:1], 1e-5, None, ALU.max), 1)
                next_step(dve.reciprocal(m[:, u, 2:3], m[:, u, 1:2]), 2)
                dve.tensor_scalar(m[:, u, 3:4], m[:, u, 2:3], 127.0, None, ALU.mult).then_inc(step, 1)
                for i, w in enumerate(outs):
                    dve.tensor_scalar(m[:, u, 4 + i:5 + i], m[:, u, 1:2], wmean127[:, w:w + 1], None, ALU.mult).then_inc(step, 1)

            def scale_x(n, u):
                dve.wait_ge(s["x_turned"], ONE + n + 1)
                dve.tensor_reduce(xm[:, u, 0:1], ps_x[:], AX.X, ALU.max, apply_absolute_value=True).then_inc(s["xmax"], 1)
                dve.wait_ge(s["xmax"], ONE + n + 1)
                scales(n, u, xm, s["xmax"], s["xstep"], (0, 1))

            def quant_x(n):
                dve.wait_ge(s["xr_done"], ONE + n + 1)
                dve.wait_ge(s["xq_turned"], ONE + n)
                dve.tensor_scalar(xq[:], xr[:], -MAGIC, 127.0, ALU.add, ALU.min).then_inc(s["xq_done"], 1)

            def gated(n, u):
                dve.wait_ge(s["hr_done"], ONE + n)
                dve.wait_ge(s["hmax"], ONE + n)
                dve.wait_ge(s["xstep"], ONE + 5 * n + 5)
                for f in range(2):
                    dve.wait_ge(s["gu_done"], ONE + 4 * n + 3 + f)
                    dve.wait_ge(s["silu_done"], ONE + 2 * n + f + 1)
                    half = slice(f * HALF, (f + 1) * HALF)
                    mm = dve.scalar_tensor_tensor(out=h[:, half], in0=ps_u[f][:], scalar=xm[:, u, 5:6], in1=sg[:, half],
                                                  op0=ALU.mult, op1=ALU.mult)
                    mm.then_inc(s["h_done" if f else "h_half"], 1)
                dve.wait_ge(s["h_half"], ONE + n + 1)
                dve.wait_ge(s["h_done"], ONE + n + 1)
                dve.tensor_reduce(hm[:, u % 2, 0:1], h[:], AX.X, ALU.max, apply_absolute_value=True).then_inc(s["hmax"], 1)
                dve.wait_ge(s["hmax"], ONE + n + 1)
                scales(n, u % 2, hm, s["hmax"], s["hstep"], (2,))

            def add(n):
                dve.wait_ge(s["o_turned"], ONE + n + 1)
                dve.tensor_tensor(xf[:, :, cols(n)], xf[:, :, cols(n)],
                                  ps_o[:, 1, :].rearrange("p (c t) -> p c t", c=C), ALU.add).then_inc(s["added"], 1)

            def quant_h(n):
                dve.wait_ge(s["hr_done"], ONE + n + 1)
                dve.wait_ge(s["h_turned"], ONE + n)
                dve.tensor_scalar(hq[:], hr[:], -MAGIC, 127.0, ALU.add, ALU.min).then_inc(s["hq_done"], 1)

            def step(n, j, left=X):
                if left >= 1:
                    gated(n + 1, (j + 1) % X)
                if left >= 3:
                    scale_x(n + 3, (j + 3) % X)
                if left >= 1:
                    quant_h(n + 1)
                if left >= 3:
                    quant_x(n + 3)
                add(n)

            for n in range(3):
                scale_x(n, n)
                quant_x(n)
            gated(0, 0)
            quant_h(0)
            with dve.Fori(0, N // X - 1) as i:
                for j in range(X):
                    step(X * i + j, j)
            for j in range(X):
                step(N - X + j, j, X - 1 - j)
    st.close()


def sparse_attention(nc, xf, io, eps):
    QT, NQ, PAD = 128, S // 128, 64
    NB, SEL = S // 16, 16
    CS, WK = NB + SEL, PAD + QT
    WIN, KEYS = NB + WK, CS + WK
    G = 4
    NG = H // G
    VA = DH + 1
    OW = 3 * G * VA
    NEG = -1e30
    st = Stage(nc, "nsa")
    names_w = ("wq", "wqs", "wk", "wks", "wv", "wo")
    w = {n: st.sb(n, [P, C, D]) for n in names_w}
    wg, bg = st.sb("wg", [P, C, 3]), st.sb("bg", [P, 3])
    bo = st.sb("bo", [P, C])
    cos, sin = st.sb("cos", [P, S]), st.sb("sin", [P, S])
    wkc, wvc = st.sb("wk_comp", [P, 16]), st.sb("wv_comp", [P, 1])
    pe, peT = st.sb("pe", [16, D]), st.sb("peT", [P, C, 16])
    parity = st.sb("head_parity", [P, 2])
    mask_f = st.sb("mask_float", [P, KEYS])
    mask = st.sb("mask", [P, NQ, KEYS], BF16)
    ident, identb = st.sb("identity", [P, P]), st.sb("identity_b", [P, P], BF16)
    block_of = st.sb("block_of", [P, NQ, NB])
    comp_w = st.sb("comp_w", [P, NQ, NB])
    pe_w = st.sb("pe_w", [16, NB])
    token_no = st.sb("token_number", [P, NQ])
    offset = st.sb("sel_offset", [P, G * SEL])
    own_sel = st.sb("own_selected", [G * SEL, G])
    ones = st.sb("ones", [1, P])
    xb = st.sb("x_row", [P, C, PAD + S])
    t1, t2 = st.sb("rope_cos", [P, 2, W]), st.sb("rope_sin", [P, 2, W])
    qT = st.sb("qT", [P, C, S])
    kr = st.sb("kT", [P, C, S])
    keo = st.sb("k_even_odd", [P, C, 2, PAD + S])
    kcomp = st.sb("k_comp", [P, C, CS])
    kw_prod = st.sb("k_weighted", [P, S])
    pe_k = st.sb("pe_weighted", [P, C, 16])
    pe_sum = st.sb("pe_sum", [P, C])
    ktok = st.sb("k_token", [P, NQ, D])
    v = st.sb("v", [P, NQ, H, VA])
    vprev = st.sb("v_before", [P, NQ, H, VA])
    vsel = st.sb("v_selected", [G * SEL, NG, G, VA])
    qsum = st.sb("q_sum", [P, C])
    imp = st.sb("importance", [1, NB])
    top = st.sb("top_values", [1, 8])
    top_i = st.sb("top_index", [1, 8], mybir.dt.uint32)
    pos0 = st.sb("top_start", [1, 2])
    pos = st.sb("sel_position", [P, G * SEL])
    sel = st.sb("sel_onehot", [P, NQ, G * SEL])
    gl, ge = st.sb("gate_logit", [P, NQ, 3]), st.sb("gate_exp", [P, NQ, 3])
    gmx, gsum, ginv = (st.sb(n, [P, NQ]) for n in ("gate_top", "gate_sum", "gate_inverse"))
    gate = st.sb("gate", [P, NQ, 3 * G])
    q_t = st.sb("q_tile", [P, 2, C, QT])
    k_t = st.sb("k_tile", [P, 2, C * 2, KEYS])
    v_t, vcp_t = st.sb("v_tile", [P, 2, H, 2 * VA]), st.sb("v_comp_before_tile", [P, 2, H, 2 * VA])
    m_t = st.sb("mask_tile", [P, 2, KEYS], BF16)
    mx = st.sb("top", [P, 2, 3, G])
    prob = st.sb("prob", [P, 2, G * KEYS])
    pT, pTs = st.sb("probT", [P, 2, 2, G * QT]), st.sb("prob_selT", [G * SEL, 2, QT])
    outs = st.sb("outs", [P, 2, NG, OW])
    den, rden, rg = (st.sb(n, [P, NG * 3 * G]) for n in ("sum", "sum_inverse", "branch_weight"))
    wo3 = st.sb("weighted", [P, NG, 3 * G, DH])
    two = st.sb("comp_and_window", [P, NG, G, DH])
    att = st.sb("attention", [P, D])
    attT = st.sb("attentionT", [P, C, QT])
    S_ = st.ps("scores", [P, G, W])
    T_ = st.ps("turned", [P, 3, W])
    O_ = st.ps("out", [P, W])
    loads = ([(w[n][:], "nsa_" + n) for n in names_w] + [(wg[:], "nsa_wg"), (bg[:], "nsa_bg"), (bo[:], "nsa_bo"), (cos[:], "nsa_cos"),
             (sin[:], "nsa_sin"), (wkc[:], "nsa_wk_comp"), (wvc[:], "nsa_wv_comp"), (pe[:], "nsa_pe"), (peT[:], "nsa_peT"),
             (parity[:], "nsa_parity"), (ident[:], "identity"), (block_of[:], "nsa_block_of"), (token_no[:], "nsa_token"),
             (offset[:], "nsa_offset"), (own_sel[:], "nsa_own_sel")])
    names = ("here mask_here mask_cast consts cw pew x_copied rope_mm ropec ropes roped k_split v_mm v_moved kc_w kc_red kc_added "
             "cv_mm cv_moved qsum_done imp_mm imp_moved top_done topi_done posf pos_mm pos_done sel_done mask_done ktok_mm ktok_moved "
             "selk_mm selk_moved kc_split g_mm g_logit g_top g_shift g_exp g_sum g_inv gate_done vsel_done vcs_moved tile_copied scores_done "
             "max_done clamp_done shifted exp_done turned pT_moved pv_done o_moved den_done rden_done rg_done weighted two_done att_done att_turned "
             "attT_moved wo_done x_added peT_w pe_sum pew0 ones_set carrier").split()
    s = {n: st.sem(n) for n in names}

    def head(g, j):
        return g // 2, 8 * (g // 2) + 2 * j + g % 2, g % 2

    LAST = NQ * NG - 1

    def schedule(eng, b, slot):
        for c in range(2 * NG):
            slot(b * NQ, 0, c, c)
        eng.sem_inc(s["carrier"], 1)
        with eng.Fori(0, NQ // 2 - 1) as i:
            for c in range(2 * NG):
                slot(b * NQ + 2 * i + 2, 2 * i + 2, c, 2 * NG + c)
        for c in range(4):
            slot(b * NQ + NQ, NQ, c, LAST + 1 + c)

    st.start_counters()
    LATE = ONE + 1
    AHEAD = ONE + NG

    with nc.Block() as block:
        @block.sync
        def _(sp):
            for dst, src in loads:
                sp.dma_start(dst, io[src]).then_inc(s["here"], 16)
            with sp.Fori(0, NQ) as i:
                sp.wait_ge(s["mask_cast"], ONE + i)
                sp.dma_start(mask_f[:], io["nsa_mask"][:, i, :]).then_inc(s["mask_here"], 16)

        @block.tensor
        def _(pe_):
            pe_.wait_ge(s["here"], ONE + 16 * len(loads))
            pe_.wait_ge(s["consts"], ONE + 9)
            pe_.wait_ge(s["cw"], ONE + NQ)
            pe_.wait_ge(s["pew"], ONE + 1)
            with pe_.Fori(0, B) as b:
                pe_.wait_ge(s["x_copied"], ONE + b + 1)
                for r in range(8):
                    which, m, t = r // 4, (r // 2) % 2, r % 2
                    if r >= 2:
                        pe_.wait_ge(s["ropes"], ONE + b * 8 + r - 1)
                    for k, name in enumerate((("wq", "wqs"), ("wk", "wks"))[which]):
                        for c in range(C):
                            mm = pe_.matmul((S_ if r % 2 else T_)[:, k, :], w[name][:, c, m * P:(m + 1) * P],
                                            xb[:, c, PAD + t * W:PAD + (t + 1) * W], start=c == 0, stop=c == C - 1)
                    mm.then_inc(s["rope_mm"], 1)
                for i in range(NQ):
                    if i >= 2:
                        pe_.wait_ge(s["v_moved"], ONE + b * 2 * NQ + 2 * (i - 1))
                    for c in range(C):
                        mm = pe_.matmul(S_[:, 2 + i % 2, 0:D], xb[:, c, PAD + i * QT:PAD + (i + 1) * QT], w["wv"][:, c, :],
                                        start=c == 0, stop=c == C - 1)
                    mm.then_inc(s["v_mm"], 1)
                    for c in range(C):
                        mm = pe_.matmul(S_[P - PAD:P, 2 + i % 2, D:2 * D], xb[:, c, i * QT:i * QT + PAD], w["wv"][:, c, :],
                                        start=c == 0, stop=c == C - 1)
                    mm.then_inc(s["v_mm"], 1)
                pe_.wait_ge(s["ropes"], ONE + b * 8 + 8)
                for i in range(NQ):
                    for c in range(C):
                        mm = pe_.matmul(O_[:, 3 * i:3 * i + 3], xb[:, c, PAD + i * QT:PAD + (i + 1) * QT], wg[:, c, :],
                                        start=c == 0, stop=c == C - 1)
                mm.then_inc(s["g_mm"], 1)
                pe_.wait_ge(s["qsum_done"], ONE + b * C + C)
                pe_.wait_ge(s["kc_added"], ONE + b * C + C)
                for c in range(C):
                    mm = pe_.matmul(S_[0:1, 0, 0:NB], qsum[:, c:c + 1], kcomp[:, c, 0:NB], start=c == 0, stop=c == C - 1)
                mm.then_inc(s["imp_mm"], 1)
                pe_.wait_ge(s["roped"], ONE + b * 8 + 8)
                for i in range(NQ):
                    if i >= 2:
                        pe_.wait_ge(s["ktok_moved"], ONE + b * NQ + i - 1)
                    for c in range(C):
                        mm = pe_.transpose(T_[:, i % 2, c * P:(c + 1) * P], kr[:, c, i * QT:(i + 1) * QT], ident[:])
                    mm.then_inc(s["ktok_mm"], 1)
                pe_.wait_ge(s["posf"], ONE + b + 1)
                pe_.matmul(S_[:, 1, 0:2], ones[:], pos0[:], start=True, stop=True).then_inc(s["pos_mm"], 1)
                pe_.wait_ge(s["v_moved"], ONE + (b + 1) * 2 * NQ)
                for i in range(NQ):
                    pe_.matmul(S_[0:NB, 2, 0:D], comp_w[:, i, :], v[:, i, :, 0:DH], start=i == 0, stop=False)
                pe_.matmul(S_[0:NB, 2, 0:D], pe_w[:], pe[:], start=False, stop=True).then_inc(s["cv_mm"], 1)
                pe_.wait_ge(s["sel_done"], ONE + b * NQ + NQ)
                pe_.wait_ge(s["ktok_moved"], ONE + (b + 1) * NQ)
                for i in range(NQ):
                    mm = pe_.matmul(S_[0:G * SEL, 3, 0:D], sel[:, i, :], v[:, i, :, 0:DH], start=i == 0, stop=i == NQ - 1)
                mm.then_inc(s["cv_mm"], 1)
                for c in range(C):
                    for i in range(NQ):
                        mm = pe_.matmul(T_[:, 2, c * SEL:(c + 1) * SEL], ktok[:, i, c * P:(c + 1) * P], sel[:, i, 0:SEL],
                                        start=i == 0, stop=i == NQ - 1)
                mm.then_inc(s["selk_mm"], 1)
                pe_.wait_ge(s["kc_split"], ONE + 8 * (b + 1))
                pe_.wait_ge(s["vsel_done"], ONE + NG * (b + 1))
                pe_.wait_ge(s["vcs_moved"], ONE + 2 * (b + 1))
                pe_.wait_ge(s["mask_done"], ONE + b * NQ + NQ)
                pe_.wait_ge(s["gate_done"], ONE + 3 * (b + 1))

                pe_.sem_inc(s["carrier"], 1)
                def scores(n, c):
                    t, g, u = c // NG, c % NG, c // NG % 2
                    if g == 0:
                        pe_.wait_ge(s["tile_copied"], ONE + (n + t) * 5 + 5)
                    pe_.wait_ge(s["shifted"], ONE + 3 * (n * NG + c))
                    for j in range(G):
                        pe_.matmul(S_[:, j, 0:KEYS], identb[:], m_t[:, u, :], start=True, stop=False)
                    for j in range(G):
                        c, _, par = head(g, j)
                        rows = slice(32 * j, 32 * j + 32)
                        mm = pe_.matmul(S_[:, j, 0:KEYS], q_t[rows, u, c, :], k_t[rows, u, 2 * c + par, :], start=False, stop=True)
                    mm.then_inc(s["scores_done"], 1)

                def turn(n, c):
                    u = c % 2
                    pe_.wait_ge(s["exp_done"], ONE + n * NG + c + 1)
                    pe_.wait_ge(s["pT_moved"], ONE + 2 * (n * NG + c))
                    for half in range(2):
                        for j in range(G):
                            o = j * WIN + half * P
                            pe_.transpose(T_[:, half, j * QT:(j + 1) * QT], prob[:, u, o:o + P], ident[:])
                    pe_.transpose(T_[0:G * SEL, 2, 0:QT], prob[:, u, G * WIN:], ident[:]).then_inc(s["turned"], 1)

                def weigh(n, c):
                    t, g, u = c // NG, c % NG, c // NG % 2
                    pe_.wait_ge(s["pT_moved"], ONE + 2 * (n * NG + c) + 2)
                    pe_.wait_ge(s["o_moved"], ONE + n * NG + c)
                    for j in range(G):
                        _, h, _ = head(g, j)
                        q = slice(j * QT, (j + 1) * QT)
                        out = O_[:, 2 * j * VA:2 * (j + 1) * VA]
                        pe_.matmul(out, pT[:, c % 2, 0, q], vcp_t[:, u, h, :], start=True, stop=False)
                        pe_.matmul(out, pT[:, c % 2, 1, q], v_t[:, u, h, :], start=False, stop=True)
                    pe_.matmul(O_[:, 2 * G * VA:OW], pTs[:, c % 2, :], vsel[:, g, :, :].rearrange("p h d -> p (h d)"),
                               start=True, stop=True).then_inc(s["pv_done"], 1)

                def turn_out(n, t, c):
                    pe_.wait_ge(s["att_done"], ONE + n + t + 1)
                    pe_.wait_ge(s["pT_moved"], ONE + 2 * (n * NG + c) + 2)
                    for c in range(C):
                        mm = pe_.transpose(T_[:, 0, c * QT:(c + 1) * QT], att[:, c * P:(c + 1) * P], ident[:])
                    mm.then_inc(s["att_turned"], 1)

                def through_wo(n, t):
                    pe_.wait_ge(s["attT_moved"], ONE + n + t + 1)
                    for m in range(C):
                        for c in range(C):
                            mm = pe_.matmul(T_[:, 1, m * QT:(m + 1) * QT], w["wo"][:, c, m * P:(m + 1) * P], attT[:, c, :],
                                            start=c == 0, stop=c == C - 1)
                    mm.then_inc(s["wo_done"], 1)

                def slot(n, t, c, p):
                    if p <= LAST:
                        scores(n, c)
                    if p >= 7 and c % NG == 3:
                        through_wo(n, (c - 7) // NG)
                    if 2 <= p <= LAST + 2:
                        weigh(n, c - 2)
                    if 1 <= p <= LAST + 1:
                        if p >= 7 and c % NG == 3:
                            pe_.wait_ge(s["x_added"], ONE + C * (n + (c - 7) // NG + 1))
                        turn(n, c - 1)
                    if p >= 6 and c % NG == 2:
                        turn_out(n, (c - 6) // NG, c - 1 - max(p - 1 - LAST, 0))

                schedule(pe_, b, slot)
                pe_.wait_ge(s["x_added"], ONE + C * NQ * (b + 1))

        @block.scalar
        def _(act):
            act.wait_ge(s["here"], ONE + 16 * len(loads))
            act.wait_ge(s["consts"], ONE + 9)
            with act.Fori(0, B) as b:
                act.wait_ge(s["x_added"], ONE + b * C * NQ)
                act.copy(xb[:, :, PAD:], xf[:, :, bass.ts(b, S)]).then_inc(s["x_copied"], 1)
                for r in range(4):
                    m, t = r // 2, r % 2
                    x = slice(t * W, (t + 1) * W)
                    act.wait_ge(s["roped"], ONE + b * 8 + 5 + r)
                    for par in range(2):
                        act.activation(keo[:, m, par, PAD + t * W:PAD + (t + 1) * W], kr[:, m, x], ACT.Copy,
                                       scale=parity[:, par:par + 1]).then_inc(s["k_split"], 1)
                for i in range(NQ):
                    act.wait_ge(s["v_mm"], ONE + b * 2 * NQ + 2 * i + 2)
                    act.copy(v[:, i, :, 0:DH], S_[:, 2 + i % 2, 0:D].rearrange("p (h d) -> p h d", h=H)).then_inc(s["v_moved"], 1)
                    act.copy(vprev[P - PAD:P, i, :, 0:DH], S_[P - PAD:P, 2 + i % 2, D:2 * D].rearrange("p (h d) -> p h d", h=H)).then_inc(s["v_moved"], 1)
                act.wait_ge(s["imp_mm"], ONE + b + 1)
                act.copy(imp[:], S_[0:1, 0, 0:NB]).then_inc(s["imp_moved"], 1)
                for i in range(NQ):
                    act.wait_ge(s["ktok_mm"], ONE + b * NQ + i + 1)
                    act.copy(ktok[:, i, :], T_[:, i % 2, 0:D]).then_inc(s["ktok_moved"], 1)
                act.wait_ge(s["g_shift"], ONE + b + 1)
                act.activation(ge[:], gl[:], ACT.Exp).then_inc(s["g_exp"], 1)
                act.wait_ge(s["cv_mm"], ONE + 2 * b + 1)
                for u in range(2):
                    act.copy(vcp_t[0:NB, u, :, 0:DH], S_[0:NB, 2, 0:D].rearrange("p (h d) -> p h d", h=H)).then_inc(s["vcs_moved"], 1)
                act.wait_ge(s["selk_mm"], ONE + b + 1)
                act.copy(kcomp[:, :, NB:CS], T_[:, 2, 0:C * SEL].rearrange("p (c m) -> p c m", c=C)).then_inc(s["selk_moved"], 1)
                act.wait_ge(s["selk_moved"], ONE + b + 1)
                act.wait_ge(s["kc_added"], ONE + (b + 1) * C)
                for u in range(2):
                    for par in range(2):
                        dst = k_t[:, u].rearrange("p (c e) k -> p c e k", c=C)[:, :, par, :]
                        for at, part in ((slice(0, NB), slice(0, NB)), (slice(WIN, KEYS), slice(NB, CS))):
                            act.activation(dst[:, :, at], kcomp[:, :, part], ACT.Copy, scale=parity[:, par:par + 1]).then_inc(s["kc_split"], 1)
                act.sem_inc(s["carrier"], 1)
                def exps(n, c):
                    act.wait_ge(s["shifted"], ONE + 3 * (n * NG + c) + 3)
                    act.activation(prob[:, c % 2, :], prob[:, c % 2, :], ACT.Exp, scale=float(DH) ** -0.5).then_inc(s["exp_done"], 1)

                def move(n, c):
                    act.wait_ge(s["turned"], ONE + n * NG + c + 1)
                    act.wait_ge(s["pv_done"], AHEAD + n * NG + c - 1)
                    act.copy(pT[:, c % 2, :, :], T_[:, 0:2, :]).then_inc(s["pT_moved"], 1)
                    act.copy(pTs[:, c % 2, :], T_[0:G * SEL, 2, 0:QT]).then_inc(s["pT_moved"], 1)

                def keep(n, c):
                    t, g = c // NG, c % NG
                    act.wait_ge(s["pv_done"], AHEAD + n * NG + c + 1)
                    if g == 0:
                        act.wait_ge(s["weighted"], LATE + n + t - 1)
                    act.copy(outs[:, t % 2, g, :], O_[:, 0:OW]).then_inc(s["o_moved"], 1)

                def move_out(n, t):
                    act.wait_ge(s["att_turned"], ONE + n + t + 1)
                    act.copy(attT[:], T_[:, 0, 0:C * QT].rearrange("p (c q) -> p c q", c=C)).then_inc(s["attT_moved"], 1)

                def slot(n, t, c, p):
                    if p <= LAST:
                        exps(n, c)
                    if 2 <= p <= LAST + 2:
                        keep(n, c - 2)
                    if 1 <= p <= LAST + 1:
                        move(n, c - 1)
                    if p >= 6 and c % NG == 2:
                        move_out(n, (c - 6) // NG)

                schedule(act, b, slot)

        @block.gpsimd
        def _(pool):
            pool.sem_inc(s["pv_done"], AHEAD - ONE)
            pool.sem_inc(s["weighted"], LATE - ONE)
            for t in (v[:, :, :, DH:VA], vprev[:, :, :, DH:VA]):
                pool.memset(t, 1.0).then_inc(s["consts"], 1)
            for t in (vcp_t[:], v_t[:], xb[:, :, 0:PAD], keo[:, :, :, 0:PAD]):
                pool.memset(t, 0.0).then_inc(s["consts"], 1)
            pool.wait_ge(s["consts"], ONE + 6)
            pool.memset(vcp_t[0:NB, :, :, DH:VA], 1.0).then_inc(s["consts"], 1)
            pool.wait_ge(s["consts"], ONE + 7)
            pool.wait_ge(s["here"], ONE + 16 * len(loads))
            pool.tensor_copy(identb[:], ident[:]).then_inc(s["consts"], 1)
            pool.wait_ge(s["consts"], ONE + 8)
            pool.tensor_copy(vsel[:, :, :, DH:VA], own_sel[:].unsqueeze(1).unsqueeze(3).to_broadcast([G * SEL, NG, G, 1])) \
                .then_inc(s["consts"], 1)
            pool.wait_ge(s["consts"], ONE + 9)
            pool.sem_inc(s["carrier"], 1)
            with pool.Fori(0, NQ) as i:
                pool.wait_ge(s["mask_here"], ONE + 16 * i + 16)
                pool.sem_inc(s["carrier"], 1)
                pool.tensor_copy(mask[:, bass.ds(i, 1), :].rearrange("p o k -> p (o k)"), mask_f[:]).then_inc(s["mask_cast"], 1)
            with pool.Fori(0, B) as b:
                pool.wait_ge(s["k_split"], ONE + 8 * b + 8)
                pool.wait_ge(s["roped"], ONE + 8 * b + 8)
                pool.wait_ge(s["v_moved"], ONE + 2 * NQ * (b + 1))
                pool.wait_ge(s["mask_done"], ONE + b * NQ + NQ)
                pool.wait_ge(s["gate_done"], ONE + 3 * (b + 1))
                pool.sem_inc(s["carrier"], 1)
                with pool.Fori(0, NQ // 2) as i:
                    for u in range(2):
                        t = i * 2 + u
                        n = b * NQ + t
                        pool.wait_ge(s["pv_done"], AHEAD + n * NG - NG)
                        pool.sem_inc(s["carrier"], 1)
                        pool.tensor_copy(q_t[:, u], qT[:, :, bass.ts(t, QT)]).then_inc(s["tile_copied"], 1)
                        pool.tensor_copy(k_t[:, u, :, NB:WIN], keo[:].rearrange("p c e k -> p (c e) k")[:, :, bass.ds(t * QT, WK)]).then_inc(s["tile_copied"], 1)
                        pool.tensor_copy(v_t[:, u, :, VA:], v[:, bass.ds(t, 1), :, :].rearrange("p o h d -> p (o h) d")).then_inc(s["tile_copied"], 1)
                        pool.tensor_copy(m_t[:, u], mask[:, bass.ds(t, 1), :].rearrange("p o k -> p (o k)")).then_inc(s["tile_copied"], 1)
                        pool.wait_ge(s["tile_copied"], ONE + 5 * n + 4)
                        pool.sem_inc(s["carrier"], 1)
                        pool.tensor_copy(vcp_t[P - PAD:P, u, :, VA:], vprev[P - PAD:P, bass.ds(t, 1), :, :].rearrange("p o h d -> p (o h) d")).then_inc(s["tile_copied"], 1)
                        pool.wait_ge(s["tile_copied"], ONE + 5 * n + 5)
                        pool.sem_inc(s["carrier"], 1)

        @block.vector
        def _(dve):
            dve.memset(ones[:], 1.0).then_inc(s["ones_set"], 1)
            dve.wait_ge(s["ones_set"], ONE + 1)
            dve.wait_ge(s["here"], ONE + 16 * len(loads))
            dve.tensor_scalar(comp_w[:].rearrange("p i n -> p (i n)"), block_of[:].rearrange("p i n -> p (i n)"), wvc[:, 0:1], None,
                              ALU.mult).then_inc(s["cw"], NQ)
            dve.wait_ge(s["cw"], ONE + NQ)
            dve.memset(pe_w[:], 1.0).then_inc(s["pew0"], 1)
            dve.wait_ge(s["pew0"], ONE + 1)
            dve.tensor_scalar(pe_w[:], pe_w[:], wvc[0:16, 0:1], None, ALU.mult).then_inc(s["pew"], 1)
            dve.tensor_tensor(pe_k[:], peT[:], wkc[:].unsqueeze(1).to_broadcast([P, C, 16]), ALU.mult).then_inc(s["peT_w"], 1)
            dve.wait_ge(s["peT_w"], ONE + 1)
            dve.tensor_reduce(pe_sum[:], pe_k[:], AX.X, ALU.add).then_inc(s["pe_sum"], 1)
            dve.wait_ge(s["pe_sum"], ONE + 1)
            with dve.Fori(0, B) as b:
                for r in range(8):
                    which, m, t = r // 4, (r // 2) % 2, r % 2
                    x = slice(t * W, (t + 1) * W)
                    src = S_ if r % 2 else T_
                    dve.wait_ge(s["rope_mm"], ONE + b * 8 + r + 1)
                    dve.wait_ge(s["roped"], ONE + b * 8 + max(r - 1, 0))
                    dve.tensor_tensor(t1[:, r % 2, :], src[:, 0, :], cos[:, x], ALU.mult).then_inc(s["ropec"], 1)
                    dve.tensor_tensor(t2[:, r % 2, :], src[:, 1, :], sin[:, x], ALU.mult).then_inc(s["ropes"], 1)
                    dve.wait_ge(s["ropes"], ONE + b * 8 + r + 1)
                    dve.wait_ge(s["ropec"], ONE + b * 8 + r + 1)
                    dve.tensor_tensor((kr if which else qT)[:, m, x], t1[:, r % 2, :], t2[:, r % 2, :], ALU.add).then_inc(s["roped"], 1)
                dve.wait_ge(s["roped"], ONE + b * 8 + 8)
                dve.wait_ge(s["imp_mm"], ONE + b)
                dve.wait_ge(s["kc_split"], ONE + 8 * b)
                for c in range(C):
                    dve.tensor_reduce(qsum[:, c:c + 1], qT[:, c, :], AX.X, ALU.add).then_inc(s["qsum_done"], 1)
                    dve.wait_ge(s["kc_red"], ONE + b * C + c)
                    dve.tensor_tensor(kw_prod[:].rearrange("p (n k) -> p n k", k=16), kr[:, c, :].rearrange("p (n k) -> p n k", k=16),
                                      wkc[:].unsqueeze(1).to_broadcast([P, NB, 16]), ALU.mult).then_inc(s["kc_w"], 1)
                    dve.wait_ge(s["kc_w"], ONE + b * C + c + 1)
                    dve.tensor_reduce(kcomp[:, c, 0:NB], kw_prod[:].rearrange("p (n k) -> p n k", k=16), AX.X, ALU.add).then_inc(s["kc_red"], 1)
                    dve.wait_ge(s["kc_red"], ONE + b * C + c + 1)
                    dve.tensor_scalar(kcomp[:, c, 0:NB], kcomp[:, c, 0:NB], pe_sum[:, c:c + 1], None, ALU.add).then_inc(s["kc_added"], 1)
                dve.wait_ge(s["g_mm"], ONE + b + 1)
                dve.tensor_tensor(gl[:], O_[:, 0:3 * NQ].rearrange("p (i g) -> p i g", g=3), bg[:].unsqueeze(1).to_broadcast([P, NQ, 3]),
                                  ALU.add).then_inc(s["g_logit"], 1)
                dve.wait_ge(s["g_logit"], ONE + b + 1)
                dve.tensor_reduce(gmx[:], gl[:], AX.X, ALU.max).then_inc(s["g_top"], 1)
                dve.wait_ge(s["g_top"], ONE + b + 1)
                dve.tensor_tensor(gl[:], gl[:], gmx[:].unsqueeze(2).to_broadcast([P, NQ, 3]), ALU.subtract).then_inc(s["g_shift"], 1)
                dve.wait_ge(s["imp_moved"], ONE + b + 1)
                dve.sem_inc(s["carrier"], 1)
                dve.max(top[:], imp[:]).then_inc(s["top_done"], 1)
                dve.wait_ge(s["top_done"], ONE + b + 1)
                dve.sem_inc(s["carrier"], 1)
                dve.max_index(top_i[:], top[:], imp[:]).then_inc(s["topi_done"], 1)
                dve.wait_ge(s["topi_done"], ONE + b + 1)
                dve.tensor_scalar(pos0[:], top_i[:, 0:2], 16.0, None, ALU.mult).then_inc(s["posf"], 1)
                dve.wait_ge(s["pos_mm"], ONE + b + 1)
                dve.tensor_tensor(pos[:].rearrange("p (h a e) -> p h a e", h=G, a=2), offset[:].rearrange("p (h a e) -> p h a e", h=G, a=2),
                                  S_[:, 1, 0:2].unsqueeze(1).unsqueeze(3).to_broadcast([P, G, 2, SEL // 2]), ALU.add).then_inc(s["pos_done"], 1)
                dve.wait_ge(s["pos_done"], ONE + b + 1)
                for i in range(NQ):
                    dve.tensor_scalar(sel[:, i, :], pos[:], token_no[:, i:i + 1], None, ALU.is_equal).then_inc(s["sel_done"], 1)
                dve.wait_ge(s["mask_cast"], ONE + NQ)
                for i in range(NQ):
                    dve.tensor_scalar(mask[:, i, WIN:KEYS], pos[:, 0:SEL], token_no[:, i:i + 1], NEG, ALU.is_gt, ALU.mult).then_inc(s["mask_done"], 1)
                dve.wait_ge(s["g_exp"], ONE + b + 1)
                dve.tensor_reduce(gsum[:], ge[:], AX.X, ALU.add).then_inc(s["g_sum"], 1)
                dve.wait_ge(s["g_sum"], ONE + b + 1)
                dve.reciprocal(ginv[:], gsum[:]).then_inc(s["g_inv"], 1)
                dve.wait_ge(s["g_inv"], ONE + b + 1)
                for branch, cols in enumerate((slice(0, 2 * G, 2), slice(2 * G, 3 * G), slice(1, 2 * G, 2))):
                    dve.tensor_tensor(gate[:, :, cols], ge[:, :, branch:branch + 1].to_broadcast([P, NQ, G]),
                                      ginv[:].unsqueeze(2).to_broadcast([P, NQ, G]), ALU.mult).then_inc(s["gate_done"], 1)
                dve.wait_ge(s["cv_mm"], ONE + 2 * b + 2)
                for g in range(NG):
                    c, _, par = head(g, 0)
                    src = S_[0:G * SEL, 3, c * P:(c + 1) * P].rearrange("p (h e d) -> p h e d", h=G, e=2)[:, :, par, :]
                    dve.tensor_tensor(vsel[:, g, :, 0:DH], src, own_sel[:].unsqueeze(2).to_broadcast([G * SEL, G, DH]), ALU.mult) \
                        .then_inc(s["vsel_done"], 1)
                dve.wait_ge(s["gate_done"], ONE + 3 * (b + 1))
                dve.sem_inc(s["carrier"], 1)
                def shift(n, c, p):
                    u = c % 2
                    dve.wait_ge(s["scores_done"], ONE + n * NG + c + 1)
                    dve.wait_ge(s["shifted"], ONE + 3 * (n * NG + c))
                    dve.wait_ge(s["turned"], ONE + n * NG + c - min(p, 1))
                    branches = (slice(0, NB), slice(WIN, KEYS), slice(NB, WIN))
                    for r, cols in enumerate(branches):
                        dve.tensor_reduce(mx[:, u, r, :], S_[:, :, cols], AX.X, ALU.max).then_inc(s["max_done"], 1)
                    dve.wait_ge(s["max_done"], ONE + 3 * (n * NG + c) + 3)
                    dve.tensor_scalar(mx[:, u, :, :], mx[:, u, :, :], NEG / 10, None, ALU.max).then_inc(s["clamp_done"], 1)
                    dve.wait_ge(s["clamp_done"], ONE + n * NG + c + 1)
                    main = prob[:, u, 0:G * WIN].rearrange("p (h k) -> p h k", h=G)
                    dst = (main[:, :, 0:NB], prob[:, u, G * WIN:].rearrange("p (h k) -> p h k", h=G), main[:, :, NB:WIN])
                    for r, cols in enumerate(branches):
                        dve.tensor_tensor(dst[r], S_[:, :, cols], mx[:, u, r, :].unsqueeze(2).to_broadcast([P, G, cols.stop - cols.start]),
                                          ALU.subtract).then_inc(s["shifted"], 1)

                def combine(n, t, row_tile):
                    n = n + t
                    o = outs[:, t % 2].rearrange("p g (r x) -> p (g r) x", x=VA)
                    dve.wait_ge(s["o_moved"], ONE + (n + 1) * NG)
                    dve.tensor_scalar(den[:], o[:, :, DH], 1e-30, None, ALU.max).then_inc(s["den_done"], 1)
                    dve.wait_ge(s["den_done"], ONE + n + 1)
                    dve.reciprocal(rden[:], den[:]).then_inc(s["rden_done"], 1)
                    dve.wait_ge(s["rden_done"], ONE + n + 1)
                    dve.tensor_tensor(rg[:].rearrange("p (g r) -> p g r", g=NG), rden[:].rearrange("p (g r) -> p g r", g=NG),
                                      gate[:, bass.ds(row_tile, 1), :].to_broadcast([P, NG, 3 * G]), ALU.mult).then_inc(s["rg_done"], 1)
                    dve.wait_ge(s["rg_done"], ONE + n + 1)
                    dve.tensor_tensor(wo3[:].rearrange("p g r d -> p (g r) d"), o[:, :, 0:DH], rg[:].unsqueeze(2).to_broadcast([P, NG * 3 * G, DH]),
                                      ALU.mult).then_inc(s["weighted"], 1)
                    dve.wait_ge(s["weighted"], LATE + n + 1)
                    pair = wo3[:, :, 0:2 * G, :].rearrange("p g (h r) d -> p g h r d", r=2)
                    for g in range(NG):
                        dve.tensor_tensor(two[:, g], pair[:, g, :, 0, :], pair[:, g, :, 1, :], ALU.add).then_inc(s["two_done"], 1)
                    dve.wait_ge(s["two_done"], ONE + NG * (n + 1))
                    dve.wait_ge(s["att_turned"], ONE + n)
                    dve.tensor_tensor(att[:].rearrange("p (g x) -> p g x", g=NG), two[:].rearrange("p g h d -> p g (h d)"),
                                      wo3[:, :, 2 * G:, :].rearrange("p g h d -> p g (h d)"), ALU.add).then_inc(s["att_done"], 1)

                def add(n, t):
                    dve.wait_ge(s["wo_done"], ONE + n + t + 1)
                    for c in range(C):
                        x = xf[:, c, bass.ds((n + t) * QT, QT)]
                        dve.scalar_tensor_tensor(out=x, in0=T_[:, 1, c * QT:(c + 1) * QT], scalar=bo[:, c:c + 1], in1=x,
                                                 op0=ALU.add, op1=ALU.add).then_inc(s["x_added"], 1)

                def slot(n, t, c, p):
                    if p <= LAST:
                        shift(n, c, p)
                    if p >= 5 and c % NG == 1:
                        combine(n, (c - 5) // NG, t + (c - 5) // NG)
                    if p >= 7 and c % NG == 3:
                        add(n, (c - 7) // NG)

                schedule(dve, b, slot)
    st.close()


def mesa_attention(nc, xf, io, eps):
    L = 128
    SEG = 2
    NGRP = T // (L * SEG)
    SYS = SEG * H
    TRI = DH * (DH + 1) // 2

    def off(i):
        return DH * i - i * (i - 1) // 2

    st = Stage(nc, "mesa")
    wqk, wv = st.sb("wqk", [P, C, 2 * D]), st.sb("wv", [P, C, D])
    wfb, gw1, gw2 = st.sb("wfb", [P, C, 2 * H]), st.sb("gw1", [P, C, DH]), st.sb("gw2", [DH, D])
    wo = st.sb("wo_n", [P, C, D])
    normw = st.sb("norm_w", [P, C])
    delta, restart = st.sb("delta", [P, H]), st.sb("restart", [P, T // L])
    delta_n = st.sb("delta_segment", [P, T // L, H])
    lb = st.sb("lambda", [P, DH, H])
    lam = lb
    upto, after = st.sb("upto", [P, L]), st.sb("after", [P, L])
    negf, negb = st.sb("neg_float", [P, L]), st.sb("neg", [P, L], BF16)
    ident, identb = st.sb("identity", [P, P]), st.sb("identity_b", [P, P], BF16)
    parity, expand = st.sb("parity", [P, 2]), st.sb("expand", [H, C, P])
    own = st.sb("own_block", [P, C, P])
    c_small = st.sb("small", [P, 2 * H])
    c_one = st.sb("one", [P, H])
    c_minus = st.sb("minus_one", [P, H])
    c_eps4 = st.sb("eps4", [P, H])
    xs = st.sb("x_seg", [P, C, L])
    sqk = st.sb("qk_square", [P, 2 * H, DH])
    qk, z16 = st.sb("qk", [P, 2 * D]), st.sb("z_f", [P, H])
    ta, tb, tc_, ssum = (st.sb(n, [P, 2 * H, k]) for n, k in (("sum8", 8), ("sum4", 4), ("sum2", 2), ("sum1", 1)))
    rln, rn = st.sb("qk_norm_ln", [P, 2 * H]), st.sb("qk_inverse", [P, 2 * H])
    g1T = st.sb("g1T", [DH, L])
    zf, zabs, zexp, zln, zmin, zneg = (st.sb(n, [P, H]) for n in ("zf", "zf_abs", "zf_exp", "zf_ln", "zf_relu", "zf_sum"))
    eb, eb1, beta = (st.sb(n, [P, H]) for n in ("eb", "eb1", "beta"))
    kn = st.sb("k", [P, H, DH])
    eG = st.sb("decay_to_end", [P, H])
    kk = st.sb("kk", [P, H, TRI])
    lfU = st.sb("log_f_upto", [P, H, L])
    ef_row = lfU[0:1]
    h_rows = st.sb("state_rows", [P, H, TRI])
    h_last, h_row = h_rows[96:P], h_rows[0:1]
    dec = st.sb("decay", [P, 2, SEG, 4, 4, L])
    kb = st.sb("k_beta", [P, 2, SEG, D])
    kd = st.sb("k_decayed", [P, 2, SEG, D])
    vs = st.sb("v", [P, 2, SEG, D])
    g1p = st.sb("gate", [P, 2, SEG, D])
    lf = st.sb("log_f", [P, 2, SEG, H])
    eF = st.sb("decay_from_start", [P, 2, SEG, H])
    eFT = st.sb("decay_from_startT", [H, 2, SEG, L])
    A = st.sb("A", [P, 2, TRI, SYS])
    Y = st.sb("Y", [P, 2, DH, SYS])
    mult = st.sb("multipliers", [P, 2, DH, SYS])
    CHUNK = 2 * DH - 3
    prod = st.sb("product", [P, 2, CHUNK, SYS])
    prod_y = st.sb("product_y", [P, DH, SYS])
    piv, rinv = st.sb("pivot", [P, SYS]), st.sb("pivot_inverse", [P, DH, SYS])
    red, num = st.sb("known_part", [P, SYS]), st.sb("numerator", [P, SYS])
    qs = st.sb("solution", [P, D])
    kbT, qsT = st.sb("k_betaT", [P, C, 2, L]), st.sb("solutionT", [P, C, L])
    oi, o, og = (st.sb(n, [P, H, DH]) for n in ("o_inter", "o", "o_gated"))
    on, osq = oi, o
    la = og[:].rearrange("p h d -> p (h d)").rearrange("p (d h) -> p d h", h=H)
    t8, t4, t2, t1 = (st.sb(n, [P, H, k]) for n, k in (("osum8", 8), ("osum4", 4), ("osum2", 2), ("osum1", 1)))
    oln, orn = st.sb("o_mean_ln", [P, H]), st.sb("o_inverse", [P, H])
    onT = st.sb("o_normedT", [P, C, L])
    state, s_own = (st.sb(n, [P, C, P]) for n in ("state", "state_new"))
    pm, o7 = st.sb("weights", [P, 2, 4 * L]), st.sb("o_parts", [P, 2, H, DH])
    st5, wo6 = st.sb("state_parts", [P, D + C]), st.sb("wo_out", [P, C, L])
    bk = [st.ps(f"bank{k}") for k in range(8)]
    loads = [(wqk[:], "mesa_wqk"), (wv[:], "mesa_wv"), (wfb[:], "mesa_wfb"), (gw1[:], "mesa_gw1"), (gw2[:], "mesa_gw2"),
             (wo[:], "mesa_wo"), (normw[:], "mesa_norm"), (delta[:], "mesa_delta"), (restart[:], "mesa_restart"), (la, "mesa_lambda"),
             (upto[:], "mesa_upto"), (after[:], "mesa_after"), (negf[:], "mesa_neg"), (ident[:], "identity"),
             (parity[:], "nsa_parity"), (expand[:], "mesa_expand"), (own[:], "mesa_own")]
    names = ("here consts lam1 lam2 lam_done wo_ready carrier "
             "xs_done v_mm qk_mm proj_mm gate_mm sqk_done g1_moved eb_done v_moved tanh_done zf_done zabs_done zexp_done zln_done zmin_done "
             "zneg_done lf_done eb1_done beta_done sum8 sum4 sum2 sum1 rln_done rn_done y_done kn_done kb_done kk_done f_mm ef_done eg_done eft_done "
             "ef_row_here kd_done lfu_done gate1_done d_mm dec_done a_mm a_moved h_row_here "
             "solved e "
             "qs_done o_turned kbt_done qst_done o_smm pm_done intra_mm inter_mm oi_done o_done og_done osq_done "
             "qk_moved z_moved s_moved o7_moved st_moved wo_moved os8 os4 os2 os1 oln_done orn_done on_done on_turned ont_done wo_mm x_added st_mm st_own st_dec st_done").split()
    s = {n: st.sem(n) for n in names}

    def head(g, j):
        return 8 * (j // 2) + 2 * g + j % 2

    def grouped(t, g):
        return t.rearrange("p (c a e) t -> p c a e t", c=2, a=4)[:, :, g, :, :]

    NP_ = 4

    def schedule(eng, core, ends):
        def group(g, ahead, u):
            n = None if g is None else g * SEG
            p = None if ahead is None else ahead * SEG
            plus = lambda m, k: None if m is None else m + k
            core(n, None, p, u, 0, None, g, None)
            ends(n, p, u, 0, n)
            core(plus(n, 1), p, plus(p, 1), u, 1, 0, g, g)
            ends(plus(n, 1), plus(p, 1), u, 1, plus(n, 1))
            core(None, plus(p, 1), None, u, None, 1, g, None)

        group(None, 0, 0)
        group(None, 1, 1)
        eng.sem_inc(s["carrier"], 1)
        with eng.Fori(0, NGRP // 2 - 1) as i:
            for u in range(2):
                group(2 * i + u, 2 * i + 2 + u, u)
        group(NGRP - 2, None, 0)
        group(NGRP - 1, None, 1)

    st.start_counters()
    with nc.Block() as block:
        @block.sync
        def _(sp):
            for dst, src in loads:
                sp.dma_start(dst, io[src]).then_inc(s["here"], 16)

            def carry(g, u, q):
                n = g * SEG + q
                sp.wait_ge(s["a_mm"], ONE + 8 * n)
                sp.sem_inc(s["carrier"], 1)
                sp.wait_ge(s["eft_done"], ONE + n + 1)
                sp.sem_inc(s["carrier"], 1)
                sp.wait_ge(s["d_mm"], ONE + 4 * n + 4)
                sp.sem_inc(s["carrier"], 1)
                sp.dma_start(ef_row, eFT[:, u, q, :]).then_inc(s["ef_row_here"], 16)
                sp.wait_ge(s["a_mm"], ONE + 8 * n + 8)
                sp.sem_inc(s["carrier"], 1)
                sp.wait_ge(s["a_moved"], ONE + 16 * n + 16)
                sp.dma_start(h_row, h_last[31:32, :, :]).then_inc(s["h_row_here"], 16)
            with sp.Fori(0, NGRP // 2) as i:
                for u in range(2):
                    for q in range(SEG):
                        carry(2 * i + u, u, q)
            sp.wait_ge(s["h_row_here"], ONE + 16 * NGRP * SEG)

        @block.tensor
        def _(pe):
            pe.wait_ge(s["here"], ONE + 16 * len(loads))
            pe.wait_ge(s["consts"], ONE + 9)
            pe.wait_ge(s["wo_ready"], ONE + C)

            def project(n):
                pe.wait_ge(s["xs_done"], ONE + n + 1)
                pe.wait_ge(s["dec_done"], ONE + NP_ * n)
                for c in range(C):
                    mm = pe.matmul(bk[0][:], xs[:, c, :], wqk[:, c, :], start=c == 0, stop=c == C - 1)
                mm.then_inc(s["qk_mm"], 1)
                for c in range(C):
                    mm = pe.matmul(bk[1][:, 0:D], xs[:, c, :], wv[:, c, :], start=c == 0, stop=c == C - 1)
                mm.then_inc(s["v_mm"], 1)

            def project_small(n):
                pe.wait_ge(s["a_moved"], ONE + 16 * n)
                for c in range(C):
                    pe.matmul(bk[2][:, 0:2 * H], xs[:, c, :], wfb[:, c, :], start=c == 0, stop=c == C - 1)
                for c in range(C):
                    mm = pe.matmul(bk[3][0:DH, 0:L], gw1[:, c, :], xs[:, c, :], start=c == 0, stop=c == C - 1)
                mm.then_inc(s["proj_mm"], 1)

            def gate(n):
                pe.wait_ge(s["g1_moved"], ONE + n + 1)
                pe.matmul(bk[1][:, D:2 * D], g1T[:], gw2[:], start=True, stop=True).then_inc(s["gate_mm"], 1)

            def sums(n, u, q):
                pe.wait_ge(s["lf_done"], ONE + n + 1)
                pe.matmul(bk[3][:, 0:H], upto[:], lf[:, u, q, :], start=True, stop=True)
                pe.matmul(bk[3][:, H:2 * H], after[:], lf[:, u, q, :], start=True, stop=True)
                pe.matmul(bk[3][0:H, 2 * H:2 * H + L], lf[:, u, q, :], upto[:], start=True, stop=True).then_inc(s["f_mm"], 1)

            def log_decay(n, d):
                if d == 0:
                    pe.wait_ge(s["qk_moved"], ONE + n + 1)
                    pe.wait_ge(s["sqk_done"], ONE + n + 1)
                elif d == 1:
                    pe.wait_ge(s["v_moved"], ONE + n + 1)
                    pe.wait_ge(s["tanh_done"], ONE + n + 1)
                else:
                    pe.wait_ge(s["dec_done"], ONE + NP_ * n + d - 1)
                pe.wait_ge(s["lfu_done"], ONE + H * n + 4 * (d + 1))
                pe.matmul(bk[d % 2][:], after[:], grouped(lfU[:], d), start=True, stop=False)
                pe.matmul(bk[d % 2][:], identb[:], negb[:].unsqueeze(1).to_broadcast([P, 4, L]), start=False, stop=True) \
                    .then_inc(s["d_mm"], 1)

            def matrices(n, u, q, d):
                if d == 0:
                    pe.wait_ge(s["kk_done"], ONE + DH * (n + 1))
                    pe.wait_ge(s["eft_done"], ONE + n + 1)
                    pe.wait_ge(s["eb_done"], ONE + n + 1)
                    pe.wait_ge(s["ef_row_here"], ONE + 16 * (n + 1))
                    pe.wait_ge(s["h_row_here"], ONE + 16 * n)
                pe.wait_ge(s["dec_done"], ONE + NP_ * n + d + 1)
                for k in (2 * d, 2 * d + 1):
                    if k >= 2:
                        pe.wait_ge(s["a_moved"], ONE + 16 * n + 2 * (k - 1))
                    for e in range(2):
                        j = 2 * (k % 2) + e
                        h = head(d, j)
                        dst = bk[2 + k % 2][:, e * TRI:(e + 1) * TRI]
                        pe.matmul(dst, dec[:, u, q, d, j, :], kk[:, h, :], start=True, stop=False)
                        mm = pe.matmul(dst, ef_row[:, h, :], h_row[:, h, :], start=False, stop=True)
                    mm.then_inc(s["a_mm"], 1)

            def turn_solution(n, u, q):
                pe.wait_ge(s["wo_moved"], ONE + n)
                pe.wait_ge(s["qs_done"], ONE + n + 1)
                for c in range(C):
                    pe.transpose(bk[6][:, c * P:(c + 1) * P], kb[:, u, q, c * P:(c + 1) * P], ident[:])
                for c in range(C):
                    mm = pe.transpose(bk[6][:, D + c * P:D + (c + 1) * P], qs[:, c * P:(c + 1) * P], ident[:])
                mm.then_inc(s["o_turned"], 1)

            def scores(n, d):
                if d == 0:
                    pe.wait_ge(s["kbt_done"], ONE + 2 * n + 2)
                    pe.wait_ge(s["qst_done"], ONE + n + 1)
                    pe.wait_ge(s["st_moved"], ONE + n)
                    pe.wait_ge(s["s_moved"], ONE + 4 * n)
                elif d >= 2:
                    pe.wait_ge(s["s_moved"], ONE + 4 * n + d - 1)
                for j in range(4):
                    mm = pe.matmul(bk[4 + d % 2][:, j * L:(j + 1) * L], kbT[32 * d:32 * d + 32, j // 2, j % 2, :],
                                   qsT[32 * d:32 * d + 32, j // 2, :], start=True, stop=True)
                mm.then_inc(s["o_smm"], 1)

            def from_state(n):
                pe.wait_ge(s["o7_moved"], ONE + n)
                pe.wait_ge(s["st_done"], ONE + n)
                for c in range(C):
                    mm = pe.matmul(bk[7][:, c * P:(c + 1) * P], qsT[:, c, :], state[:, c, :], start=True, stop=True)
                mm.then_inc(s["inter_mm"], 1)

            def from_segment(n, u, q, d):
                pe.wait_ge(s["pm_done"], ONE + 4 * n + d + 1)
                for j in range(4):
                    h = head(d, j)
                    mm = pe.matmul(bk[7][:, D + h * DH:D + (h + 1) * DH], pm[:, d % 2, j * L:(j + 1) * L],
                                   vs[:, u, q, h * DH:(h + 1) * DH], start=True, stop=True)
                mm.then_inc(s["intra_mm"], 1)

            def next_state(n, u, q):
                pe.wait_ge(s["s_moved"], ONE + 4 * n + 4)
                for c in range(C):
                    pe.matmul(bk[5][:, c * P:(c + 1) * P], kd[:, u, q, c * P:(c + 1) * P], vs[:, u, q, c * P:(c + 1) * P],
                              start=True, stop=True)
                for c in range(C):
                    mm = pe.matmul(bk[5][:, D + c:D + c + 1], expand[:, c, :], eFT[:, u, q, L - 1:L], start=True, stop=True)
                mm.then_inc(s["st_mm"], 1)

            def turn_out(n):
                pe.wait_ge(s["on_done"], ONE + n + 1)
                for c in range(C):
                    mm = pe.transpose(bk[6][:, c * P:(c + 1) * P], on[:].rearrange("p h d -> p (h d)")[:, c * P:(c + 1) * P], ident[:])
                mm.then_inc(s["on_turned"], 1)

            def through_wo(n):
                pe.wait_ge(s["ont_done"], ONE + n + 1)
                for m in range(C):
                    for c in range(C):
                        mm = pe.matmul(bk[6][:, D + m * L:D + (m + 1) * L], wo[:, c, m * P:(m + 1) * P], onT[:, c, :],
                                       start=c == 0, stop=c == C - 1)
                mm.then_inc(s["wo_mm"], 1)

            def core(n, p, a, u, q, pq, group, solved_before):
                if n is not None:
                    turn_solution(n, u, q)
                if p is not None:
                    for d in range(4):
                        log_decay(p, d)
                        if n is not None and d == 1:
                            scores(n, 0)
                elif n is not None:
                    scores(n, 0)
                if n is not None:
                    from_state(n)
                for d in range(4):
                    if n is not None and d < 3:
                        scores(n, d + 1)
                    if p is not None:
                        matrices(p, u, pq, d)
                    if n is not None:
                        from_segment(n, u, q, d)
                    if a is not None and d == 1:
                        project(a)
                        if p is None:
                            project_small(a)
                    if a is not None and p is None and d == 2:
                        gate(a)
                if n is not None:
                    next_state(n, u, q)

            def ends(n, p, u, q, before):
                if p is not None:
                    if q == 1:
                        project_small(p)
                        gate(p)
                    sums(p, u, q)
                if n is not None:
                    turn_out(n)
                    through_wo(n)

            schedule(pe, core, ends)

        @block.scalar
        def _(act):
            act.wait_ge(s["here"], ONE + 16 * len(loads))
            act.wait_ge(s["consts"], ONE + 9)
            act.activation(lb[:], la, ACT.Abs).then_inc(s["lam1"], 1)
            act.wait_ge(s["lam1"], ONE + 1)
            act.activation(lb[:], lb[:], ACT.Exp, scale=-1.0).then_inc(s["lam1"], 1)
            act.wait_ge(s["lam1"], ONE + 2)
            act.activation(lb[:], lb[:], ACT.Ln, bias=eps[:, 3:4]).then_inc(s["lam1"], 1)
            for c in range(C):
                act.activation(wo[:, c, :], wo[:, c, :], ACT.Copy, scale=normw[:, c:c + 1]).then_inc(s["wo_ready"], 1)

            def take_x(n):
                act.wait_ge(s["v_mm"], ONE + n)
                act.wait_ge(s["proj_mm"], ONE + n)
                act.copy(xs[:], xf[:, :, bass.ts(n, L)]).then_inc(s["xs_done"], 1)

            def project(n):
                act.wait_ge(s["qk_mm"], ONE + n + 1)
                act.wait_ge(s["sum8"], ONE + n)
                act.activation(sqk[:].rearrange("p h d -> p (h d)"), bk[0][:], ACT.Square).then_inc(s["sqk_done"], 1)
                act.wait_ge(s["proj_mm"], ONE + n + 1)
                act.wait_ge(s["zf_done"], ONE + n)
                act.copy(z16[:], bk[2][:, 0:H]).then_inc(s["z_moved"], 1)
                act.wait_ge(s["gate_mm"], ONE + n)
                act.copy(g1T[:], bk[3][0:DH, 0:L]).then_inc(s["g1_moved"], 1)
                act.wait_ge(s["eb1_done"], ONE + n)
                act.activation(eb[:], bk[2][:, H:2 * H], ACT.Exp, scale=-1.0).then_inc(s["eb_done"], 1)
                act.wait_ge(s["zf_done"], ONE + n + 1)
                act.activation(zabs[:], zf[:], ACT.Abs).then_inc(s["zabs_done"], 1)
                act.wait_ge(s["zneg_done"], ONE + n)
                act.activation(zmin[:], zf[:], ACT.Relu, scale=-1.0).then_inc(s["zmin_done"], 1)
                act.wait_ge(s["zabs_done"], ONE + n + 1)
                act.activation(zexp[:], zabs[:], ACT.Exp, scale=-1.0).then_inc(s["zexp_done"], 1)
                act.wait_ge(s["y_done"], ONE + n)
                act.wait_ge(s["kn_done"], ONE + n)
                act.copy(qk[:], bk[0][:]).then_inc(s["qk_moved"], 1)

            def logs(n):
                act.wait_ge(s["zexp_done"], ONE + n + 1)
                act.activation(zln[:], zexp[:], ACT.Ln, bias=eps[:, 3:4]).then_inc(s["zln_done"], 1)
                act.wait_ge(s["eb_done"], ONE + n + 1)
                act.wait_ge(s["beta_done"], ONE + n)
                act.activation(eb1[:], eb[:], ACT.Ln, bias=eps[:, 3:4]).then_inc(s["eb1_done"], 1)
                act.wait_ge(s["sum1"], ONE + n + 1)
                act.wait_ge(s["rn_done"], ONE + n)
                act.activation(rln[:], ssum[:].rearrange("p h o -> p (h o)"), ACT.Ln, bias=c_small[:, 0:1]).then_inc(s["rln_done"], 1)

            def exps(n):
                act.wait_ge(s["eb1_done"], ONE + n + 1)
                act.wait_ge(s["kb_done"], ONE + n)
                act.activation(beta[:], eb1[:], ACT.Exp, scale=-1.0).then_inc(s["beta_done"], 1)
                act.wait_ge(s["rln_done"], ONE + n + 1)
                act.activation(rn[:], rln[:], ACT.Exp, scale=-0.5).then_inc(s["rn_done"], 1)

            def spread_log_forget(n, u, q):
                act.wait_ge(s["a_mm"], ONE + 8 * n)
                act.wait_ge(s["lf_done"], ONE + n + 1)
                for h in [head(d, j) for d in range(4) for j in range(4)]:
                    act.activation(lfU[:, h, :], upto[:], ACT.Copy, scale=lf[:, u, q, h:h + 1]).then_inc(s["lfu_done"], 1)

            def from_sums(n, u, q, before):
                act.wait_ge(s["gate_mm"], ONE + n + 1)
                act.wait_ge(s["v_mm"], ONE + n + 1)
                if before is not None:
                    act.wait_ge(s["st_mm"], ONE + before + 1)
                    act.wait_ge(s["intra_mm"], ONE + 4 * (before + 1))
                    act.wait_ge(s["og_done"], ONE + before + 1)
                act.copy(vs[:, u, q, :], bk[1][:, 0:D]).then_inc(s["v_moved"], 1)
                act.activation(g1p[:, u, q, :], bk[1][:, D:2 * D], ACT.Tanh, scale=0.5).then_inc(s["tanh_done"], 1)
                act.wait_ge(s["f_mm"], ONE + n + 1)
                act.activation(eF[:, u, q, :], bk[3][:, 0:H], ACT.Exp).then_inc(s["ef_done"], 1)
                act.wait_ge(s["kd_done"], ONE + n)
                act.activation(eG[:], bk[3][:, H:2 * H], ACT.Exp).then_inc(s["eg_done"], 1)
                act.activation(eFT[:, u, q, :], bk[3][0:H, 2 * H:2 * H + L], ACT.Exp).then_inc(s["eft_done"], 1)

            def decays(n, u, q, d):
                if d == 0:
                    act.wait_ge(s["a_mm"], ONE + 8 * n)
                act.wait_ge(s["d_mm"], ONE + 4 * n + d + 1)
                act.activation(dec[:, u, q, d, :, :].rearrange("p j t -> p (j t)"), bk[d % 2][:], ACT.Exp).then_inc(s["dec_done"], 1)

            def matrices(n, u, q, d, solved_before):
                if d == 0:
                    if solved_before is not None:
                        act.wait_ge(s["solved"], ONE + solved_before + 1)
                    act.wait_ge(s["h_row_here"], ONE + 16 * n)
                for k in (2 * d, 2 * d + 1):
                    h0 = head(d, 2 * (k % 2))
                    act.wait_ge(s["a_mm"], ONE + 8 * n + k + 1)
                    src = bk[2 + k % 2][:, 0:2 * TRI].rearrange("p (e m) -> p e m", e=2)
                    act.copy(A[:, u, :, q * H + h0:q * H + h0 + 2].rearrange("p m e -> p e m"), src).then_inc(s["a_moved"], 1)
                    act.copy(h_last[:, h0:h0 + 2, :], src[96:P]).then_inc(s["a_moved"], 1)

            def take_solution(n, u, q):
                act.wait_ge(s["o_turned"], ONE + n)
                act.copy(qs[:].rearrange("p (h d) -> p h d", h=H), Y[:, u, :, q * H:(q + 1) * H].rearrange("p d h -> p h d")) \
                    .then_inc(s["qs_done"], 1)

            def turn_solution(n):
                act.wait_ge(s["o_turned"], ONE + n + 1)
                act.wait_ge(s["o_smm"], ONE + 4 * n)
                act.wait_ge(s["inter_mm"], ONE + n)
                for e in range(2):
                    act.activation(kbT[:, :, e, :], bk[6][:, 0:D].rearrange("p (c t) -> p c t", c=C), ACT.Copy,
                                   scale=parity[:, e:e + 1]).then_inc(s["kbt_done"], 1)
                act.copy(qsT[:], bk[6][:, D:2 * D].rearrange("p (c t) -> p c t", c=C)).then_inc(s["qst_done"], 1)

            def scores(n, d):
                act.wait_ge(s["o_smm"], ONE + 4 * n + d + 1)
                act.wait_ge(s["intra_mm"], ONE + 4 * n + max(d - 1, 0))
                act.copy(pm[:, d % 2, :], bk[4 + d % 2][:]).then_inc(s["s_moved"], 1)

            def outputs(n):
                act.wait_ge(s["intra_mm"], ONE + 4 * n + 4)
                act.wait_ge(s["inter_mm"], ONE + n + 1)
                act.wait_ge(s["o_done"], ONE + n)
                act.copy(o7[:].rearrange("p a h d -> p (a h d)"), bk[7][:]).then_inc(s["o7_moved"], 1)
                act.wait_ge(s["st_mm"], ONE + n + 1)
                act.wait_ge(s["st_done"], ONE + n)
                act.copy(st5[:], bk[5][:, 0:D + C]).then_inc(s["st_moved"], 1)

            def square(n):
                act.wait_ge(s["og_done"], ONE + n + 1)
                act.wait_ge(s["os8"], ONE + n)
                act.activation(osq[:], og[:], ACT.Square).then_inc(s["osq_done"], 1)

            def norm_log(n):
                act.wait_ge(s["os1"], ONE + n + 1)
                act.wait_ge(s["orn_done"], ONE + n)
                act.activation(oln[:], t1[:].rearrange("p h o -> p (h o)"), ACT.Ln, bias=c_eps4[:, 0:1], scale=1.0 / DH) \
                    .then_inc(s["oln_done"], 1)

            def norm_exp(n):
                act.wait_ge(s["oln_done"], ONE + n + 1)
                act.wait_ge(s["on_done"], ONE + n)
                act.activation(orn[:], oln[:], ACT.Exp, scale=-0.5).then_inc(s["orn_done"], 1)

            def out(n):
                act.wait_ge(s["on_turned"], ONE + n + 1)
                act.wait_ge(s["wo_mm"], ONE + n)
                act.copy(onT[:], bk[6][:, 0:D].rearrange("p (c t) -> p c t", c=C)).then_inc(s["ont_done"], 1)
                act.wait_ge(s["wo_mm"], ONE + n + 1)
                act.wait_ge(s["x_added"], ONE + n)
                act.copy(wo6[:], bk[6][:, D:2 * D].rearrange("p (c t) -> p c t", c=C)).then_inc(s["wo_moved"], 1)

            def core(n, p, a, u, q, pq, group, solved_before):
                if n is not None:
                    if q == 0:
                        act.wait_ge(s["solved"], ONE + group + 1)
                    take_solution(n, u, q)
                    turn_solution(n)
                if a is not None:
                    take_x(a)
                if p is not None:
                    for d in range(4):
                        decays(p, u, pq, d)
                        if n is not None and d == 1:
                            scores(n, 0)
                elif n is not None:
                    scores(n, 0)
                for d in range(4):
                    if n is not None and d < 3:
                        scores(n, d + 1)
                    if p is not None:
                        matrices(p, u, pq, d, solved_before)
                    elif a is not None:
                        if d == 1:
                            project(a)
                        elif d == 2:
                            logs(a)
                        elif d == 3:
                            exps(a)
                if n is not None:
                    outputs(n)
                if a is not None and p is None:
                    spread_log_forget(a, u, 0)

            def ends(n, p, u, q, before):
                if n is not None:
                    square(n)
                if p is not None and q == 1:
                    project(p)
                    logs(p)
                if n is not None:
                    norm_log(n)
                if p is not None and q == 1:
                    exps(p)
                if n is not None:
                    norm_exp(n)
                if p is not None:
                    if q == 1:
                        spread_log_forget(p, u, q)
                    from_sums(p, u, q, before)
                if n is not None:
                    out(n)

            schedule(act, core, ends)

        @block.gpsimd
        def _(pool):
            pool.memset(c_small[:], 1e-6).then_inc(s["consts"], 1)
            pool.memset(c_one[:], 1.0).then_inc(s["consts"], 1)
            pool.memset(c_minus[:], -1.0).then_inc(s["consts"], 1)
            pool.memset(c_eps4[:], 4e-5).then_inc(s["consts"], 1)
            pool.wait_ge(s["here"], ONE + 16 * len(loads))
            pool.tensor_copy(negb[:], negf[:]).then_inc(s["consts"], 1)
            pool.tensor_copy(identb[:], ident[:]).then_inc(s["consts"], 1)
            pool.memset(h_row, 0.0).then_inc(s["consts"], 1)
            pool.memset(state[:], 0.0).then_inc(s["consts"], 1)
            pool.wait_ge(s["consts"], ONE + 8)
            pool.tensor_tensor(delta_n[:], delta[:].unsqueeze(1).to_broadcast([P, T // L, H]),
                               restart[:].unsqueeze(2).to_broadcast([P, T // L, H]), ALU.add).then_inc(s["consts"], 1)
            pool.wait_ge(s["consts"], ONE + 9)

            def op(out, a, b, alu, done, n=None):
                pool.tensor_tensor(out, a, b, alu).then_inc(s[done], 1)
                if n is not None:
                    pool.wait_ge(s[done], ONE + n)

            def bc(t, k):
                return t.unsqueeze(2).to_broadcast([P, t.shape[1], k])

            def by_head(t):
                return t.rearrange("p (h d) -> p h d", h=H)

            def project(n, u, q):
                pool.wait_ge(s["z_moved"], ONE + n + 1)
                pool.sem_inc(s["carrier"], 1)
                op(zf[:], z16[:], delta_n[:, bass.ds(n, 1), :].rearrange("p o h -> p (o h)"), ALU.add, "zf_done", n + 1)
                pool.wait_ge(s["sqk_done"], ONE + n + 1)
                op(ta[:], sqk[:, :, 0:8], sqk[:, :, 8:16], ALU.add, "sum8", n + 1)
                op(tb[:], ta[:, :, 0:4], ta[:, :, 4:8], ALU.add, "sum4", n + 1)
                op(tc_[:], tb[:, :, 0:2], tb[:, :, 2:4], ALU.add, "sum2", n + 1)
                op(ssum[:], tc_[:, :, 0:1], tc_[:, :, 1:2], ALU.add, "sum1", n + 1)

            def log_forget(n, u, q):
                pool.wait_ge(s["zln_done"], ONE + n + 1)
                pool.wait_ge(s["zmin_done"], ONE + n + 1)
                op(zneg[:], zmin[:], zln[:], ALU.add, "zneg_done", n + 1)
                op(lf[:, u, q, :], zneg[:], c_minus[:], ALU.mult, "lf_done", n + 1)

            def keys(n, u, q, before):
                sysm = slice(q * H, (q + 1) * H)
                pool.wait_ge(s["qk_moved"], ONE + n + 1)
                pool.wait_ge(s["rn_done"], ONE + n + 1)
                if before is not None:
                    pool.wait_ge(s["qs_done"], ONE + before + 1)
                    pool.wait_ge(s["o_turned"], ONE + before + 1)
                    pool.wait_ge(s["st_mm"], ONE + before + 1)
                op(Y[:, u, :, sysm].rearrange("p d h -> p h d"), by_head(qk[:, 0:D]), bc(rn[:, 0:H], DH), ALU.mult, "y_done")
                op(kn[:], by_head(qk[:, D:2 * D]), bc(rn[:, H:2 * H], DH), ALU.mult, "kn_done", n + 1)
                pool.wait_ge(s["beta_done"], ONE + n + 1)
                kbv = by_head(kb[:, u, q, :])
                op(kbv, kn[:], bc(beta[:], DH), ALU.mult, "kb_done", n + 1)
                pool.wait_ge(s["a_mm"], ONE + 8 * n)
                for i in range(DH):
                    op(kk[:, :, off(i):off(i) + DH - i], kbv[:, :, i:i + 1].to_broadcast([P, H, DH - i]), kn[:, :, i:], ALU.mult, "kk_done")
                pool.wait_ge(s["eg_done"], ONE + n + 1)
                op(by_head(kd[:, u, q, :]), kbv, bc(eG[:], DH), ALU.mult, "kd_done")
                pool.wait_ge(s["tanh_done"], ONE + n + 1)
                op(by_head(g1p[:, u, q, :]), by_head(g1p[:, u, q, :]), bc(c_one[:], DH), ALU.add, "gate1_done", n + 1)
                pool.wait_ge(s["kk_done"], ONE + DH * (n + 1))
                pool.wait_ge(s["y_done"], ONE + n + 1)
                pool.wait_ge(s["kd_done"], ONE + n + 1)

            def weights(n, u, q, ds):
                for d in ds:
                    pool.wait_ge(s["s_moved"], ONE + 4 * n + d + 1)
                    op(pm[:, d % 2, :], pm[:, d % 2, :], dec[:, u, q, d, :, :].rearrange("p j t -> p (j t)"), ALU.mult, "pm_done")

            def outputs(n, u, q):
                pool.wait_ge(s["o7_moved"], ONE + n + 1)
                pool.wait_ge(s["on_turned"], ONE + n)
                op(oi[:], o7[:, 0], bc(eF[:, u, q, :], DH), ALU.mult, "oi_done", n + 1)
                op(o[:], o7[:, 1], oi[:], ALU.add, "o_done", n + 1)
                op(og[:], o[:], by_head(g1p[:, u, q, :]), ALU.mult, "og_done", n + 1)
                pool.wait_ge(s["st_moved"], ONE + n + 1)
                pool.wait_ge(s["inter_mm"], ONE + n + 1)
                op(s_own[:], st5[:, 0:D].rearrange("p (c k) -> p c k", c=C), own[:], ALU.mult, "st_own", n + 1)
                op(state[:], state[:], st5[:, D:D + C].unsqueeze(2).to_broadcast([P, C, P]), ALU.mult, "st_dec", n + 1)
                op(state[:], state[:], s_own[:], ALU.add, "st_done", n + 1)

            def square_sums(n):
                pool.wait_ge(s["osq_done"], ONE + n + 1)
                op(t8[:], osq[:, :, 0:8], osq[:, :, 8:16], ALU.add, "os8", n + 1)
                op(t4[:], t8[:, :, 0:4], t8[:, :, 4:8], ALU.add, "os4", n + 1)
                op(t2[:], t4[:, :, 0:2], t4[:, :, 2:4], ALU.add, "os2", n + 1)
                op(t1[:], t2[:, :, 0:1], t2[:, :, 1:2], ALU.add, "os1", n + 1)

            def normed(n):
                pool.wait_ge(s["orn_done"], ONE + n + 1)
                op(on[:], og[:], bc(orn[:], DH), ALU.mult, "on_done", n + 1)

            def add(n):
                pool.wait_ge(s["wo_moved"], ONE + n + 1)
                pool.sem_inc(s["carrier"], 1)
                x = xf[:, :, bass.ts(n, L)]
                pool.tensor_tensor(x, wo6[:], x, ALU.add).then_inc(s["x_added"], 1)

            def core(n, p, a, u, q, pq, group, solved_before):
                early = p is None and a is not None
                if n is not None:
                    weights(n, u, q, (0, 1))
                if early:
                    project(a, u, 0)
                if n is not None:
                    weights(n, u, q, (2, 3))
                if early:
                    log_forget(a, u, 0)
                if n is not None:
                    outputs(n, u, q)

            def ends(n, p, u, q, before):
                if p is not None and q == 1:
                    project(p, u, q)
                if n is not None:
                    square_sums(n)
                if p is not None and q == 1:
                    log_forget(p, u, q)
                if n is not None:
                    normed(n)
                if p is not None:
                    keys(p, u, q, before)
                if n is not None:
                    add(n)

            schedule(pool, core, ends)

        @block.vector
        def _(dve):
            dve.wait_ge(s["lam1"], ONE + 3)
            dve.scalar_tensor_tensor(out=lam[:], in0=la, scalar=0.0, in1=lb[:], op0=ALU.max, op1=ALU.add).then_inc(s["lam2"], 1)
            dve.wait_ge(s["lam2"], ONE + 1)
            dve.tensor_scalar(lam[:], lam[:], 0.25, None, ALU.add).then_inc(s["lam_done"], 1)
            dve.wait_ge(s["lam_done"], ONE + 1)

            def chunks(k):
                runs, size = [], CHUNK
                for i in range(k + 1, DH):
                    if size + DH - i > CHUNK:
                        runs.append([])
                        size = 0
                    runs[-1].append(i)
                    size += DH - i
                return runs

            def solve(g, u, base):
                count = [0]

                def step(ins):
                    ins.then_inc(s["e"], 1)
                    count[0] += 1
                    return count[0]

                def upto_step(k):
                    dve.wait_ge(s["e"], ONE + base + k)

                Au, Yu = A[:, u], Y[:, u]
                dve.wait_ge(s["a_moved"], ONE + (g + 1) * SEG * 16)
                dve.wait_ge(s["y_done"], ONE + (g + 1) * SEG)
                row_done = {}
                y_last = 0
                free = {}

                def row(k):
                    return Au[:, off(k):off(k) + DH - k, :]

                def pivot(k):
                    upto_step(row_done.get(k, 0))
                    a = step(dve.tensor_tensor(piv[:].rearrange("p (q h) -> p q h", h=H), row(k)[:, 0, :].rearrange("p (q h) -> p q h", h=H),
                                               lam[:, k:k + 1, :].to_broadcast([P, SEG, H]), ALU.add))
                    yield
                    upto_step(a)
                    a = step(dve.reciprocal(rinv[:, k, :], piv[:]))
                    yield
                    m = DH - 1 - k
                    upto_step(a)
                    if m:
                        a = step(dve.tensor_tensor(mult[:, k % 2, 0:m, :], row(k)[:, 1:, :], rinv[:, k:k + 1, :].to_broadcast([P, m, SYS]), ALU.mult))
                    pivot_done[k] = a

                pivot_done = {}
                for _ in pivot(0):
                    pass
                for k in range(DH - 1):
                    m = DH - 1 - k
                    mu = mult[:, k % 2]
                    upto_step(pivot_done[k])
                    if y_last:
                        upto_step(y_last)
                    py = step(dve.tensor_tensor(prod_y[:, 0:m, :], mu[:, 0:m, :], Yu[:, k:k + 1, :].to_broadcast([P, m, SYS]), ALU.mult))
                    ahead = pivot(k + 1)
                    groups = chunks(k)
                    made = []
                    for c in range(len(groups) + 1):
                        if c < len(groups):
                            at = 0
                            for i in groups[c]:
                                upto_step(free.get(c % 2, 0))
                                a = step(dve.tensor_tensor(prod[:, c % 2, at:at + DH - i, :], row(k)[:, i - k:, :],
                                                           mu[:, i - k - 1:i - k, :].to_broadcast([P, DH - i, SYS]), ALU.mult))
                                at += DH - i
                            made.append((a, at))
                        if c >= 1:
                            done, size = made[c - 1]
                            first = groups[c - 1][0]
                            upto_step(done)
                            dst = Au[:, off(first):off(first) + size, :]
                            a = step(dve.tensor_tensor(dst, dst, prod[:, (c - 1) % 2, 0:size, :], ALU.subtract))
                            free[(c - 1) % 2] = a
                            for i in groups[c - 1]:
                                row_done[i] = a
                            if c == 1:
                                upto_step(py)
                                y_last = step(dve.tensor_tensor(Yu[:, k + 1:, :], Yu[:, k + 1:, :], prod_y[:, 0:m, :], ALU.subtract))
                            else:
                                next(ahead, None)
                    for _ in ahead:
                        pass
                a = pivot_done[DH - 1]
                upto_step(a)
                upto_step(y_last)
                x_done = step(dve.tensor_tensor(Yu[:, DH - 1, :], Yu[:, DH - 1, :], rinv[:, DH - 1, :], ALU.mult))
                known = part = y_last
                for k in range(DH - 2, -1, -1):
                    m = DH - 1 - k
                    upto_step(x_done)
                    near = step(dve.tensor_tensor(piv[:], Au[:, off(k) + 1, :], Yu[:, k + 1, :], ALU.mult))
                    if k:
                        fa = step(dve.tensor_tensor(prod[:, k % 2, 0:m, :], Au[:, off(k - 1) + 2:off(k - 1) + DH - k + 1, :], Yu[:, k + 1:, :], ALU.mult))
                    upto_step(max(near, part))
                    a = step(dve.tensor_tensor(num[:], Yu[:, k, :], piv[:], ALU.subtract))
                    if k:
                        upto_step(fa)
                        known = step(dve.tensor_reduce(red[:], prod[:, k % 2, 0:m, :].rearrange("p j s -> p s j"), AX.X, ALU.add))
                    upto_step(a)
                    x_done = step(dve.tensor_tensor(Yu[:, k, :], num[:], rinv[:, k, :], ALU.mult))
                    if k:
                        upto_step(known)
                        part = step(dve.tensor_tensor(Yu[:, k - 1, :], Yu[:, k - 1, :], red[:], ALU.subtract))
                upto_step(x_done)
                dve.sem_inc(s["solved"], 1)
                return count[0]

            STEPS = sum(2 + (k < DH - 1) * (3 + DH - 1 - k + len(chunks(k))) for k in range(DH)) + 1 + 6 * (DH - 1) - 3
            with dve.Fori(0, NGRP // 2) as i:
                for u in range(2):
                    assert solve(2 * i + u, u, (2 * i + u) * STEPS) == STEPS
    st.close()



def decoder(nc, io, x_out):
    whole = Stage(nc, "all")
    xf = whole.sb("x", [P, C, T])
    mean_w = whole.sb("mean_w", [P, P])
    eps = whole.sb("eps", [P, 4])
    const_set = whole.sem("const_set")
    with nc.Block() as block:
        @block.vector
        def _(dve):
            dve.memset(mean_w[:], 1.0 / D).then_inc(const_set, 1)
            dve.memset(eps[:, 0:1], EPS_LN).then_inc(const_set, 1)
            dve.memset(eps[:, 1:2], 1e-6).then_inc(const_set, 1)
            dve.memset(eps[:, 2:3], 0.0).then_inc(const_set, 1)
            dve.memset(eps[:, 3:4], 1.0).then_inc(const_set, 1)
    load_stream(nc, xf, io["x"])
    if 1 in STAGES:
        mesa_attention(nc, xf, io, eps)
        layer_norm(nc, "ln0a", xf, mean_w, eps)
    if 2 in STAGES:
        context_mixture(nc, xf, io["ctx"], io["ctxT"])
        layer_norm(nc, "ln0b", xf, mean_w, eps)
    if 3 in STAGES:
        quantised_ffn(nc, xf, io, eps)
        layer_norm(nc, "ln0c", xf, mean_w, eps)
    if 4 in STAGES:
        sparse_attention(nc, xf, io, eps)
        layer_norm(nc, "ln1a", xf, mean_w, eps)
    if 5 in STAGES:
        slot_attention(nc, xf, io, mean_w, eps)
        layer_norm(nc, "ln1b", xf, mean_w, eps)
    if 6 in STAGES:
        ternary_ffn(nc, xf, io["w1T"], io["w2T"], io["h1T"], io["h2T"], io["w3T"], io["ffn1_scales"])
        layer_norm(nc, "ln1c", xf, mean_w, eps)
    store_stream(nc, xf, x_out)
    whole.close()



def rows_in_chunks(w):
    k, n = w.shape
    return np.ascontiguousarray(w.reshape(k // P, P, n).transpose(1, 0, 2))


def columns(v):
    return v.reshape(-1, P).T


def lay_out(a):
    n = {k: np.asarray(v) for k, v in a.items()}
    io = {
        "x": np.ascontiguousarray(n["x"].reshape(T, C, P).transpose(2, 1, 0)),
        "ctx": np.ascontiguousarray(n["ctx_1024"].transpose(1, 0, 2)),
        "ctxT": np.ascontiguousarray(n["ctx_1024"].reshape(B * M, C, P).transpose(2, 1, 0)),
    }
    if 6 in STAGES:
        for k, w in (("w1T", "w1_w"), ("w2T", "w2_w"), ("h1T", "h1_w"), ("h2T", "h2_w"), ("w3T", "w3_w")):
            io[k] = rows_in_chunks(n["L1_ffn_" + w].T)
        io["ffn1_scales"] = np.ascontiguousarray(np.concatenate(
            [columns(n["L1_ffn_" + w]) for w in ("w1_s", "w2_s", "h1_s", "h2_s", "w3_s")], axis=1))
    if 5 in STAGES:
        for k, w in (("slot_wkT", "Wk"), ("slot_wvT", "Wv"), ("slot_wihT", "gru_wih"), ("slot_whhT", "gru_whh")):
            io[k] = rows_in_chunks(n["L1_xattn_" + w].T)
        io["slot_wq"] = rows_in_chunks(n["L1_xattn_Wq"])
        io["slot_vectors"] = np.ascontiguousarray(np.concatenate(
            [columns(n["L1_xattn_" + w]) for w in ("slot_norm_w", "input_norm_w", "gru_bih", "gru_bhh")], axis=1))
    if 3 in STAGES:
        for k, w in (("q_gateT", "w_gate"), ("q_upT", "w_up"), ("q_downT", "w_down")):
            io[k] = rows_in_chunks(n["L0_ffn_" + w].T)
    io["identity"] = np.eye(P, dtype=np.float32)
    if 4 in STAGES:
        for k, w in (("nsa_wq", "Wq"), ("nsa_wk", "Wk"), ("nsa_wv", "Wv"), ("nsa_wo", "Wo"), ("nsa_wg", "Wg")):
            io[k] = rows_in_chunks(n["L1_attn_" + w])
        h = 8 * (np.arange(16) // 8) + 2 * (np.arange(16) % 4) + np.arange(16) // 4 % 2
        io["nsa_wo"] = rows_in_chunks(n["L1_attn_Wo"].reshape(16, 16, D)[h].reshape(D, D))
        swapped = np.arange(D) ^ 1
        io["nsa_wqs"], io["nsa_wks"] = io["nsa_wq"][:, :, swapped], io["nsa_wk"][:, :, swapped]
        io["nsa_bg"] = np.ascontiguousarray(np.broadcast_to(n["L1_attn_bg"], (P, 3)))
        io["nsa_bo"] = np.ascontiguousarray(columns(n["L1_attn_bo"]))
        io["nsa_wk_comp"] = np.ascontiguousarray(np.broadcast_to(n["L1_attn_wk_comp"], (P, 16)))
        io["nsa_wv_comp"] = np.ascontiguousarray(np.tile(n["L1_attn_wv_comp"], P // 16)[:, None])
        io["nsa_pe"] = n["L1_attn_pe"]
        io["nsa_peT"] = rows_in_chunks(n["L1_attn_pe"].T)
        inv = (1.0 / np.float32(10000.0) ** (np.arange(DH // 2, dtype=np.float32) * np.float32(2.0) / np.float32(DH))).astype(np.float32)
        ang = np.arange(S, dtype=np.float32)[None, :] * np.repeat(inv, 2)[:, None]
        io["nsa_cos"] = np.tile(np.cos(ang), (P // DH, 1)).astype(np.float32)
        sign = np.tile(np.array([-1.0, 1.0], np.float32), DH // 2)[:, None]
        io["nsa_sin"] = np.tile(sign * np.sin(ang), (P // DH, 1)).astype(np.float32)
        token = np.arange(P)[:, None] + P * np.arange(S // P)[None, :]
        io["nsa_token"] = token.astype(np.float32)
        io["nsa_offset"] = np.tile(np.arange(8, dtype=np.float32), (P, 8))
        io["nsa_own_sel"] = (np.arange(64)[:, None] // 16 == np.arange(4)).astype(np.float32)
        io["nsa_block_of"] = (token[:, :, None] // 16 == np.arange(S // 16)).astype(np.float32)
        seen = np.zeros((P, S // P, 64 + 16 + 192), bool)
        seen[:, :, 0:64] = (np.arange(64) + 1) * 16 <= token[:, :, None]
        key = 128 * np.arange(S // P)[None, :, None] - 64 + np.arange(192)
        seen[:, :, 64:256] = (key >= 0) & (key <= token[:, :, None]) & (key > token[:, :, None] - 64)
        io["nsa_mask"] = np.where(seen, 0.0, -1e30).astype(np.float32)
    if 1 in STAGES:
        io["mesa_wqk"] = rows_in_chunks(np.concatenate([n["L0_attn_Wq"], n["L0_attn_Wk"]], axis=1))
        io["mesa_wfb"] = rows_in_chunks(np.concatenate([n["L0_attn_Wf"], n["L0_attn_Wbet"]], axis=1))
        for k, w in (("mesa_wv", "Wv"), ("mesa_gw1", "gate_w1"), ("mesa_wo", "Wo")):
            io[k] = rows_in_chunks(n["L0_attn_" + w])
        io["mesa_gw2"] = n["L0_attn_gate_w2"]
        io["mesa_norm"] = np.ascontiguousarray(columns(n["L0_attn_norm_weight"]))
        io["mesa_delta"] = np.ascontiguousarray(np.broadcast_to(n["L0_attn_delta"], (P, H)))
        io["mesa_restart"] = np.where((np.arange(P)[:, None] == 0) & (np.arange(T // P) % (S // P) == 0), -30000.0, 0.0).astype(np.float32)
        io["mesa_lambda"] = np.ascontiguousarray(np.broadcast_to(n["L0_attn_lamb_params"].reshape(H, DH).T, (P, DH, H)))
        r, c = np.arange(P)[:, None], np.arange(P)[None, :]
        io["mesa_upto"] = (r <= c).astype(np.float32)
        io["mesa_after"] = (r > c).astype(np.float32)
        io["mesa_neg"] = np.where(r <= c, 0.0, -30000.0).astype(np.float32)
        io["mesa_own"] = np.ascontiguousarray(np.broadcast_to(((r // DH) == (c // DH)).astype(np.float32)[:, None, :], (P, C, P)))
        io["mesa_expand"] = (np.arange(H)[:, None, None] == 8 * np.arange(C)[:, None] + np.arange(P) // DH).astype(np.float32)
    io["nsa_parity"] = ((np.arange(P)[:, None] // DH) % 2 == np.arange(2)).astype(np.float32)
    return io


def kernel(**inputs):
    import concourse.bacc as bacc
    from concourse.bass_utils import run_bass_kernel_spmd

    nc = bacc.Bacc("TRN2", target_bir_lowering=False, num_devices=1)
    arrays = lay_out(inputs)
    io = {k: nc.dram_tensor("in_" + k, v.shape, mybir.dt.from_np(v.dtype), kind="ExternalInput").ap() for k, v in arrays.items()}
    x_out = nc.dram_tensor("x_out", (P, C, T), F32, kind="ExternalOutput").ap()
    decoder(nc, io, x_out)
    r = run_bass_kernel_spmd(nc, [{"in_" + k: v for k, v in arrays.items()}], core_ids=[0])
    y = r.results[0]["x_out"]
    return y.transpose(2, 1, 0).reshape(B, S, D)
```
